# Optimizing a Trainium2 kernel written in Bass

```python
import numpy as np
import jax
import jax.numpy as jnp

def _softmax(x, axis=-1):
    return jax.nn.softmax(x, axis=axis)

def _gelu(x):
    return jax.nn.gelu(x, approximate=True)

def _silu(x):
    return jax.nn.silu(x)

def _sigmoid(x):
    return jax.nn.sigmoid(x)

def _layernorm(x, axis=-1, eps=1e-05):
    m = jnp.mean(x, axis=axis, keepdims=True)
    v = jnp.var(x, axis=axis, keepdims=True)
    return (x - m) / jnp.sqrt(v + eps)

def _scatter_add(tgt, idx, src, axis=0):
    return tgt.at[idx].add(src)

def _segment_sum(src, seg, n):
    return jax.ops.segment_sum(src, seg, n)
kernel_name = 'mk_decoder_preln_d4_seqx_r8_04c5a1'

def setup_inputs(seed: int=0):
    np.random.seed(seed)
    _w = jnp.asarray

    def _rec_inputs():
        import jax
        import jax.numpy as jnp
        _rk = jax.random.key(seed)
        x = -9.806e-05 + 1 * jax.random.normal(jax.random.fold_in(_rk, 1), (4, 512, 128), jnp.float32)
        _lenS = 512 - jax.random.randint(jax.random.fold_in(_rk, 7), (4,), 0, max(1, 512 // 4) + 1, jnp.int32)
        _lenS2 = 154 - jax.random.randint(jax.random.fold_in(_rk, 8), (4,), 0, max(1, 154 // 4) + 1, jnp.int32)
        _ctx_1024P = jax.random.normal(jax.random.fold_in(_rk, 11), (4, 16, 128), jnp.float32)
        _ctx_1024c = jax.random.dirichlet(jax.random.fold_in(_rk, 511), 0.3 * jnp.ones((16,), jnp.float32), (4, 154))
        _ctx_1024t = jnp.einsum('bsk,bkd->bsd', _ctx_1024c, _ctx_1024P)
        _ctx_1024t = _ctx_1024t * jax.lax.rsqrt(jnp.mean(jnp.square(_ctx_1024t)) + 1e-12) * 0.953939
        ctx_1024 = -1.52775e-05 + 0.999936 * (_ctx_1024t + 0.3 * jax.random.normal(jax.random.fold_in(_rk, 611), (4, 154, 128), jnp.float32))
        _validS = jnp.arange(512)[None, :] < _lenS[:, None]
        _validS2 = jnp.arange(154)[None, :] < _lenS2[:, None]
        _causal = jnp.tril(jnp.ones((512, 512), dtype=bool))
        mask_BxSxS2_bf0 = jnp.logical_not(jnp.ones((4, 512, 154), dtype=bool))
        mask_SxS2_bk1 = jnp.broadcast_to(_validS2[0:1, :], (512, 154))
        return (x, ctx_1024, mask_BxSxS2_bf0, mask_SxS2_bk1)
    x, ctx_1024, mask_BxSxS2_bf0, mask_SxS2_bk1 = _rec_inputs()

    def _L0_attn_setup():
        import jax, jax.numpy as jnp
        import numpy as np
        EPS = 1e-06
        N_HEADS = 16

        def _project_static(x):
            sp = jnp.clip(x[..., 1:], -8.0, 8.0)
            x0 = jnp.sqrt(1.0 + jnp.sum(sp * sp, axis=-1, keepdims=True) + EPS)
            return jnp.concatenate([x0, sp], axis=-1)

        def _inner_static(x, y):
            return -x[..., 0] * y[..., 0] + jnp.sum(x[..., 1:] * y[..., 1:], axis=-1)

        def _log_map_approx(x, y):
            y = _project_static(y)
            xy = _inner_static(x, y)
            xy = jnp.minimum(xy, -(1.0 + EPS))[..., None]
            d = jnp.maximum(jnp.arccosh(jnp.maximum(-xy, 1.0 + EPS)), 0.001)
            dirv = y + xy * x
            dn = jnp.sqrt(jnp.maximum(_inner_static(dirv, dirv), EPS))[..., None]
            return d * dirv / (dn + EPS)

        def _dynamic_metric(x, mu, W1, b1, W2, b2):
            d = x.shape[-1]
            eta = jnp.ones((d,), x.dtype).at[0].set(-1.0)
            v = x - mu
            h = jnp.tanh(jnp.tanh(v @ W1.T + b1) @ W2.T + b2) * 0.1
            g = eta + h
            return jnp.concatenate([-jnp.abs(g[..., :1]), jnp.abs(g[..., 1:])], axis=-1)
        key = jax.random.key(seed)
        ks = jax.random.split(key, 9)
        B, T, d = (2, 256, 128)
        s = 0.02
        return {'x': jax.random.normal(ks[0], (B, T, d), jnp.float32), 'W1': jax.random.normal(ks[1], (2 * d, d), jnp.float32) * s, 'b1': jax.random.normal(ks[2], (2 * d,), jnp.float32) * s, 'W2': jax.random.normal(ks[3], (d, 2 * d), jnp.float32) * s, 'b2': jax.random.normal(ks[4], (d,), jnp.float32) * s, 'Wq': jax.random.normal(ks[5], (d, d), jnp.float32) * s, 'Wk': jax.random.normal(ks[6], (d, d), jnp.float32) * s, 'Wv': jax.random.normal(ks[7], (d, d), jnp.float32) * s, 'Wo': jax.random.normal(ks[8], (d, d), jnp.float32) * s}
    _L0_attn_all = _L0_attn_setup()
    _L0_attn_in = {k: v for k, v in _L0_attn_all.items() if k in ('W1', 'b1', 'W2', 'b2', 'Wq', 'Wk', 'Wv', 'Wo')}
    del _L0_attn_all

    def _L0_xattn_setup():
        import jax, jax.numpy as jnp
        import numpy as np
        D = 128
        NUM_ITERS = 3
        EPS = 1e-06
        SCALE = D ** (-0.5)

        def rmsnorm(x, w, eps=EPS):
            return x * jax.lax.rsqrt(jnp.mean(x * x, axis=-1, keepdims=True) + eps) * w

        def gru_cell(x, h, wih, whh, bih, bhh):
            gx = x @ wih.T + bih
            gh = h @ whh.T + bhh
            xr, xz, xn = jnp.split(gx, 3, axis=-1)
            hr, hz, hn = jnp.split(gh, 3, axis=-1)
            r = jax.nn.sigmoid(xr + hr)
            z = jax.nn.sigmoid(xz + hz)
            n = jnp.tanh(xn + r * hn)
            return (1.0 - z) * n + z * h
        key = jax.random.key(seed)
        ks = jax.random.split(key, 8)
        B, K, M, d = (8, 64, 512, D)
        w_std = d ** (-0.5)
        return {'slots': jax.random.normal(ks[0], (B, K, d), jnp.float32), 'P': jax.random.normal(ks[1], (B, M, d), jnp.float32), 'Wq': jax.random.normal(ks[2], (d, d), jnp.float32) * w_std, 'Wk': jax.random.normal(ks[3], (d, d), jnp.float32) * w_std, 'Wv': jax.random.normal(ks[4], (d, d), jnp.float32) * w_std, 'gru_wih': jax.random.normal(ks[5], (3 * d, d), jnp.float32) * w_std, 'gru_whh': jax.random.normal(ks[6], (3 * d, d), jnp.float32) * w_std, 'gru_bih': jnp.zeros((3 * d,), jnp.float32), 'gru_bhh': jnp.zeros((3 * d,), jnp.float32), 'slot_norm_w': jnp.ones((d,), jnp.float32), 'input_norm_w': jnp.ones((d,), jnp.float32)}
    _L0_xattn_all = _L0_xattn_setup()
    _L0_xattn_in = {k: v for k, v in _L0_xattn_all.items() if k in ('Wq', 'Wk', 'Wv', 'gru_wih', 'gru_whh', 'gru_bih', 'gru_bhh', 'slot_norm_w', 'input_norm_w')}
    del _L0_xattn_all

    def _L0_ffn_setup():
        import jax, jax.numpy as jnp
        import numpy as np
        E = 64
        K = 6
        CAP = 64
        ROUTE_SCALE = 1.0
        key = jax.random.key(seed)
        ks = jax.random.split(key, 9)
        B, S, D, I = (2, 128, 128, 88)
        SI = 2 * I
        s = 0.02
        return {'x': jax.random.normal(ks[0], (B, S, D), jnp.float32), 'gate_w': jax.random.normal(ks[1], (E, D), jnp.float32) * s, 'gate_b': jnp.zeros((E,), jnp.float32), 'w1': jax.random.normal(ks[2], (E, I, D), jnp.float32) * s, 'w2': jax.random.normal(ks[3], (E, D, I), jnp.float32) * s, 'w3': jax.random.normal(ks[4], (E, I, D), jnp.float32) * s, 'ws1': jax.random.normal(ks[5], (SI, D), jnp.float32) * s, 'ws2': jax.random.normal(ks[6], (D, SI), jnp.float32) * s, 'ws3': jax.random.normal(ks[7], (SI, D), jnp.float32) * s}
    _L0_ffn_all = _L0_ffn_setup()
    _L0_ffn_in = {k: v for k, v in _L0_ffn_all.items() if k in ('gate_w', 'gate_b', 'w1', 'w2', 'w3', 'ws1', 'ws2', 'ws3')}
    del _L0_ffn_all

    def _L1_attn_setup():
        import jax, jax.numpy as jnp
        import numpy as np
        B, S, D, H, DOUT = (4, 256, 128, 4, 128)
        key = jax.random.key(seed)
        ks = jax.random.split(key, 11)
        x = jax.random.normal(ks[0], (B, S, D), dtype=jnp.float32)
        phase = jax.random.normal(ks[1], (H, D), dtype=jnp.float32) * 0.02
        sc = 1.0 / np.sqrt(D)
        Wq = jax.random.normal(ks[2], (D, H * D), dtype=jnp.float32) * sc
        bq = jnp.zeros((H * D,), dtype=jnp.float32)
        Wk = jax.random.normal(ks[3], (D, H * D), dtype=jnp.float32) * sc
        bk = jnp.zeros((H * D,), dtype=jnp.float32)
        Wv = jax.random.normal(ks[4], (D, H * D), dtype=jnp.float32) * sc
        bv = jnp.zeros((H * D,), dtype=jnp.float32)
        Wo = jax.random.normal(ks[5], (H * D, DOUT), dtype=jnp.float32) / np.sqrt(H * D)
        bo = jnp.zeros((DOUT,), dtype=jnp.float32)
        return {'x': x, 'phase': phase, 'Wq': Wq, 'bq': bq, 'Wk': Wk, 'bk': bk, 'Wv': Wv, 'bv': bv, 'Wo': Wo, 'bo': bo}
    _L1_attn_all = _L1_attn_setup()
    _L1_attn_in = {k: v for k, v in _L1_attn_all.items() if k in ('phase', 'Wq', 'bq', 'Wk', 'bk', 'Wv', 'bv', 'Wo', 'bo')}
    del _L1_attn_all

    def _L1_xattn_setup():
        import jax, jax.numpy as jnp
        import numpy as np
        D_MODEL = 128
        NUM_HEADS = 16
        D_K = D_MODEL // NUM_HEADS

        def _split_heads(x):
            B, S, _ = x.shape
            return x.reshape(B, S, NUM_HEADS, D_K).transpose(0, 2, 1, 3)
        key = jax.random.key(seed)
        ks = jax.random.split(key, 8)
        B, S = (2, 256)
        scale = 1.0 / np.sqrt(D_MODEL)
        return {'query': jax.random.normal(ks[0], (B, S, D_MODEL), jnp.float32), 'key': jax.random.normal(ks[1], (B, S, D_MODEL), jnp.float32), 'value': jax.random.normal(ks[2], (B, S, D_MODEL), jnp.float32), 'mask': jnp.zeros((B, S, S), dtype=bool), 'W_Q': jax.random.normal(ks[3], (D_MODEL, D_MODEL), jnp.float32) * scale, 'W_K': jax.random.normal(ks[4], (D_MODEL, D_MODEL), jnp.float32) * scale, 'W_V': jax.random.normal(ks[5], (D_MODEL, D_MODEL), jnp.float32) * scale, 'W_O': jax.random.normal(ks[6], (D_MODEL, D_MODEL), jnp.float32) * scale}
    _L1_xattn_all = _L1_xattn_setup()
    _L1_xattn_in = {k: v for k, v in _L1_xattn_all.items() if k in ('W_Q', 'W_K', 'W_V', 'W_O')}
    del _L1_xattn_all

    def _L1_ffn_setup():
        import jax, jax.numpy as jnp
        import numpy as np
        B, S, D, F, E, K = (2, 256, 128, 512, 8, 2)
        key = jax.random.key(seed)
        ks = jax.random.split(key, 5)
        x = jax.random.normal(ks[0], (B, S, D), dtype=jnp.float32)
        Wg = jax.random.normal(ks[1], (D, E), dtype=jnp.float32) * 0.02
        W1 = jax.random.normal(ks[2], (E, D, F), dtype=jnp.float32) * 0.02
        b1 = jnp.zeros((E, F), dtype=jnp.float32)
        W2 = jax.random.normal(ks[3], (E, F, D), dtype=jnp.float32) * 0.02
        b2 = jnp.zeros((E, D), dtype=jnp.float32)
        return {'x': x, 'Wg': Wg, 'W1': W1, 'b1': b1, 'W2': W2, 'b2': b2}
    _L1_ffn_all = _L1_ffn_setup()
    _L1_ffn_in = {k: v for k, v in _L1_ffn_all.items() if k in ('Wg', 'W1', 'b1', 'W2', 'b2')}
    del _L1_ffn_all

    def _L2_attn_setup():
        import math
        import jax, jax.numpy as jnp
        import numpy as np
        B, C, D = (4, 256, 128)
        DQ = DV = 64
        H = 16
        key = jax.random.key(seed)
        kx, kq, kk, kv, kw = jax.random.split(key, 5)
        x = jax.random.normal(kx, (B, C, D), dtype=jnp.float32)
        Q = jax.random.normal(kq, (DQ, D, H), dtype=jnp.float32) / math.sqrt(D)
        K = jax.random.normal(kk, (DQ, D, H), dtype=jnp.float32) / math.sqrt(D)
        V = jax.random.normal(kv, (DV, D, H), dtype=jnp.float32) / math.sqrt(D)
        W = jax.random.normal(kw, (D, DV, H), dtype=jnp.float32) / math.sqrt(DV)
        return {'x': x, 'Q': Q, 'K': K, 'V': V, 'W': W}
    _L2_attn_all = _L2_attn_setup()
    _L2_attn_in = {k: v for k, v in _L2_attn_all.items() if k in ('Q', 'K', 'V', 'W')}
    del _L2_attn_all

    def _L2_xattn_setup():
        import jax, jax.numpy as jnp
        import numpy as np
        from jax import lax
        BIG = jnp.float32(1e+30)

        def _pairwise_euclidean(a, b):
            aa = jnp.sum(a * a, axis=-1)[:, None]
            bb = jnp.sum(b * b, axis=-1)[None, :]
            ab = a @ b.T
            return jnp.sqrt(jnp.maximum(aa + bb - 2.0 * ab, 0.0))

        def _dtw_cost(D):
            row0 = jnp.cumsum(D[0])

            def row_step(prev_row, d_row):
                first = d_row[0] + prev_row[0]

                def col_step(left, inp):
                    d_ij, up, diag = inp
                    r = d_ij + jnp.minimum(jnp.minimum(up, left), diag)
                    return (r, r)
                _, rest = lax.scan(col_step, first, (d_row[1:], prev_row[1:], prev_row[:-1]))
                row = jnp.concatenate([first[None], rest])
                return (row, row)
            _, rows = lax.scan(row_step, row0, D[1:])
            return jnp.concatenate([row0[None], rows], axis=0)

        def _backtrack(R, T1, T2):
            L = T1 + T2 - 1

            def step(carry, _):
                i, j, done = carry
                valid = jnp.logical_not(done)
                cd = jnp.where((i > 0) & (j > 0), R[jnp.maximum(i - 1, 0), jnp.maximum(j - 1, 0)], BIG)
                cu = jnp.where(i > 0, R[jnp.maximum(i - 1, 0), j], BIG)
                cl = jnp.where(j > 0, R[i, jnp.maximum(j - 1, 0)], BIG)
                choice = jnp.argmin(jnp.stack([cd, cu, cl]))
                ni = jnp.where(choice <= 1, i - 1, i)
                nj = jnp.where((choice == 0) | (choice == 2), j - 1, j)
                at_origin = (i == 0) & (j == 0)
                ni = jnp.where(at_origin, 0, ni)
                nj = jnp.where(at_origin, 0, nj)
                return ((ni, nj, done | at_origin), (i, j, valid))
            init = (jnp.int32(T1 - 1), jnp.int32(T2 - 1), jnp.bool_(False))
            _, (i_idx, j_idx, valid) = lax.scan(step, init, None, length=L)
            return (i_idx, j_idx, valid)

        def _align_one(small, large):
            T_small, d = small.shape
            T_large = large.shape[0]
            D = _pairwise_euclidean(small, large)
            R = _dtw_cost(D)
            i_idx, j_idx, valid = _backtrack(R, T_small, T_large)
            contrib = small[i_idx] * valid[:, None].astype(small.dtype)
            expanded = jnp.zeros((T_large, d), dtype=small.dtype).at[j_idx].add(contrib)
            return expanded
        key = jax.random.key(seed)
        k1, k2 = jax.random.split(key)
        teacher = jax.random.normal(k1, (16, 50, 128), dtype=jnp.float32)
        student = jax.random.normal(k2, (16, 75, 128), dtype=jnp.float32)
        return {'teacher_features': teacher, 'student_features': student}
    _L2_xattn_all = _L2_xattn_setup()
    _L2_xattn_in = {k: v for k, v in _L2_xattn_all.items() if k in ()}
    del _L2_xattn_all

    def _L2_ffn_setup():
        import math
        import jax, jax.numpy as jnp
        import numpy as np
        B, L, D, F_FF, E = (4, 256, 128, 512, 8)
        TOP_K = 1
        CAPACITY_FACTOR = 1.25
        key = jax.random.key(seed)
        ks = jax.random.split(key, 4)
        h = jax.random.normal(ks[0], (B, L, D), dtype=jnp.float32)
        gate_w = jax.random.normal(ks[1], (E, D), dtype=jnp.float32) * 0.02
        gate_b = jnp.zeros((E,), dtype=jnp.float32)
        w1 = jax.random.normal(ks[2], (E, D, F_FF), dtype=jnp.float32) * 0.02
        b1 = jnp.zeros((E, F_FF), dtype=jnp.float32)
        w2 = jax.random.normal(ks[3], (E, F_FF, D), dtype=jnp.float32) * 0.02
        b2 = jnp.zeros((E, D), dtype=jnp.float32)
        return {'h': h, 'gate_w': gate_w, 'gate_b': gate_b, 'w1': w1, 'b1': b1, 'w2': w2, 'b2': b2}
    _L2_ffn_all = _L2_ffn_setup()
    _L2_ffn_in = {k: v for k, v in _L2_ffn_all.items() if k in ('gate_w', 'gate_b', 'w1', 'b1', 'w2', 'b2')}
    del _L2_ffn_all

    def _L3_attn_setup():
        import jax, jax.numpy as jnp
        import numpy as np
        HEAD_NUM = 16
        key = jax.random.key(seed)
        ks = jax.random.split(key, 9)
        B, S, D = (4, 256, 128)

        def xavier(k, shape):
            limit = jnp.sqrt(6.0 / (shape[0] + shape[1]))
            return jax.random.uniform(k, shape, jnp.float32, -limit, limit)
        return {'x': jax.random.normal(ks[0], (B, S, D), jnp.float32), 'Wq': xavier(ks[1], (D, D)), 'bq': jnp.zeros((D,), jnp.float32), 'Wk': xavier(ks[2], (D, D)), 'bk': jnp.zeros((D,), jnp.float32), 'Wv': xavier(ks[3], (D, D)), 'bv': jnp.zeros((D,), jnp.float32), 'Wo': xavier(ks[4], (D, D)), 'bo': jnp.zeros((D,), jnp.float32)}
    _L3_attn_all = _L3_attn_setup()
    _L3_attn_in = {k: v for k, v in _L3_attn_all.items() if k in ('Wq', 'bq', 'Wk', 'bk', 'Wv', 'bv', 'Wo', 'bo')}
    del _L3_attn_all

    def _L3_xattn_setup():
        import jax, jax.numpy as jnp
        import numpy as np
        D = 128
        H = 16
        HD = D // H
        SCALE = 1.0 / np.sqrt(HD)

        def _split_heads(x):
            B, S, _ = x.shape
            return x.reshape(B, S, H, HD).transpose(0, 2, 1, 3)
        key = jax.random.key(seed)
        ks = jax.random.split(key, 12)
        B, S = (4, 256)
        inp = {'queries': jax.random.normal(ks[0], (B, S, D), jnp.float32), 'keys': jax.random.normal(ks[1], (B, S, D), jnp.float32), 'values': jax.random.normal(ks[2], (B, S, D), jnp.float32), 'mask': jax.random.randint(ks[3], (S, S), 0, 2).astype(bool), 'Wq': jax.random.normal(ks[4], (D, D), jnp.float32) * 0.02, 'bq': jax.random.normal(ks[5], (D,), jnp.float32) * 0.02, 'Wk': jax.random.normal(ks[6], (D, D), jnp.float32) * 0.02, 'bk': jax.random.normal(ks[7], (D,), jnp.float32) * 0.02, 'Wv': jax.random.normal(ks[8], (D, D), jnp.float32) * 0.02, 'bv': jax.random.normal(ks[9], (D,), jnp.float32) * 0.02, 'Wo': jax.random.normal(ks[10], (D, D), jnp.float32) * 0.02, 'bo': jax.random.normal(ks[11], (D,), jnp.float32) * 0.02}
        return inp
    _L3_xattn_all = _L3_xattn_setup()
    _L3_xattn_in = {k: v for k, v in _L3_xattn_all.items() if k in ('Wq', 'bq', 'Wk', 'bk', 'Wv', 'bv', 'Wo', 'bo')}
    del _L3_xattn_all

    def _L3_ffn_setup():
        import jax, jax.numpy as jnp
        import numpy as np
        BLOCK = 16
        _GRID = jnp.array([0.0, 0.5, 1.0, 1.5, 2.0, 3.0, 4.0, 6.0], dtype=jnp.float32)
        _MID = jnp.array([0.25, 0.75, 1.25, 1.75, 2.5, 3.5, 5.0], dtype=jnp.float32)

        def fp4_quant_dequant(x):
            shape = x.shape
            xb = x.reshape(shape[:-1] + (shape[-1] // BLOCK, BLOCK))
            scale = jnp.max(jnp.abs(xb), axis=-1, keepdims=True) / 6.0
            scale = jnp.maximum(scale, jnp.float32(1e-12))
            xn = xb / scale
            idx = jnp.searchsorted(_MID, jnp.abs(xn))
            q = _GRID[idx] * jnp.sign(xn) * scale
            return q.reshape(shape)

        def fp4_linear(x, w):
            xq = fp4_quant_dequant(x)
            wq = fp4_quant_dequant(w)
            return jnp.einsum('bsk,nk->bsn', xq, wq)
        key = jax.random.key(seed)
        k1, k2, k3, k4 = jax.random.split(key, 4)
        H, I = (128, 352)
        x = jax.random.normal(k1, (4, 512, H), dtype=jnp.float32)
        w_gate = jax.random.normal(k2, (I, H), dtype=jnp.float32) * 0.02
        w_up = jax.random.normal(k3, (I, H), dtype=jnp.float32) * 0.02
        w_down = jax.random.normal(k4, (H, I), dtype=jnp.float32) * 0.02
        return {'x': x, 'w_gate': w_gate, 'w_up': w_up, 'w_down': w_down}
    _L3_ffn_all = _L3_ffn_setup()
    _L3_ffn_in = {k: v for k, v in _L3_ffn_all.items() if k in ('w_gate', 'w_up', 'w_down')}
    del _L3_ffn_all
    return {'x': x, 'ctx_1024': ctx_1024, 'mask_BxSxS2_bf0': mask_BxSxS2_bf0, 'mask_SxS2_bk1': mask_SxS2_bk1, 'L0_attn_W1': _L0_attn_in['W1'], 'L0_attn_b1': _L0_attn_in['b1'], 'L0_attn_W2': _L0_attn_in['W2'], 'L0_attn_b2': _L0_attn_in['b2'], 'L0_attn_Wq': _L0_attn_in['Wq'], 'L0_attn_Wk': _L0_attn_in['Wk'], 'L0_attn_Wv': _L0_attn_in['Wv'], 'L0_attn_Wo': _L0_attn_in['Wo'], 'L0_xattn_Wq': _L0_xattn_in['Wq'], 'L0_xattn_Wk': _L0_xattn_in['Wk'], 'L0_xattn_Wv': _L0_xattn_in['Wv'], 'L0_xattn_gru_wih': _L0_xattn_in['gru_wih'], 'L0_xattn_gru_whh': _L0_xattn_in['gru_whh'], 'L0_xattn_gru_bih': _L0_xattn_in['gru_bih'], 'L0_xattn_gru_bhh': _L0_xattn_in['gru_bhh'], 'L0_xattn_slot_norm_w': _L0_xattn_in['slot_norm_w'], 'L0_xattn_input_norm_w': _L0_xattn_in['input_norm_w'], 'L0_ffn_gate_w': _L0_ffn_in['gate_w'], 'L0_ffn_gate_b': _L0_ffn_in['gate_b'], 'L0_ffn_w1': _L0_ffn_in['w1'], 'L0_ffn_w2': _L0_ffn_in['w2'], 'L0_ffn_w3': _L0_ffn_in['w3'], 'L0_ffn_ws1': _L0_ffn_in['ws1'], 'L0_ffn_ws2': _L0_ffn_in['ws2'], 'L0_ffn_ws3': _L0_ffn_in['ws3'], 'L1_attn_phase': _L1_attn_in['phase'], 'L1_attn_Wq': _L1_attn_in['Wq'], 'L1_attn_bq': _L1_attn_in['bq'], 'L1_attn_Wk': _L1_attn_in['Wk'], 'L1_attn_bk': _L1_attn_in['bk'], 'L1_attn_Wv': _L1_attn_in['Wv'], 'L1_attn_bv': _L1_attn_in['bv'], 'L1_attn_Wo': _L1_attn_in['Wo'], 'L1_attn_bo': _L1_attn_in['bo'], 'L1_xattn_W_Q': _L1_xattn_in['W_Q'], 'L1_xattn_W_K': _L1_xattn_in['W_K'], 'L1_xattn_W_V': _L1_xattn_in['W_V'], 'L1_xattn_W_O': _L1_xattn_in['W_O'], 'L1_ffn_Wg': _L1_ffn_in['Wg'], 'L1_ffn_W1': _L1_ffn_in['W1'], 'L1_ffn_b1': _L1_ffn_in['b1'], 'L1_ffn_W2': _L1_ffn_in['W2'], 'L1_ffn_b2': _L1_ffn_in['b2'], 'L2_attn_Q': _L2_attn_in['Q'], 'L2_attn_K': _L2_attn_in['K'], 'L2_attn_V': _L2_attn_in['V'], 'L2_attn_W': _L2_attn_in['W'], 'L2_ffn_gate_w': _L2_ffn_in['gate_w'], 'L2_ffn_gate_b': _L2_ffn_in['gate_b'], 'L2_ffn_w1': _L2_ffn_in['w1'], 'L2_ffn_b1': _L2_ffn_in['b1'], 'L2_ffn_w2': _L2_ffn_in['w2'], 'L2_ffn_b2': _L2_ffn_in['b2'], 'L3_attn_Wq': _L3_attn_in['Wq'], 'L3_attn_bq': _L3_attn_in['bq'], 'L3_attn_Wk': _L3_attn_in['Wk'], 'L3_attn_bk': _L3_attn_in['bk'], 'L3_attn_Wv': _L3_attn_in['Wv'], 'L3_attn_bv': _L3_attn_in['bv'], 'L3_attn_Wo': _L3_attn_in['Wo'], 'L3_attn_bo': _L3_attn_in['bo'], 'L3_xattn_Wq': _L3_xattn_in['Wq'], 'L3_xattn_bq': _L3_xattn_in['bq'], 'L3_xattn_Wk': _L3_xattn_in['Wk'], 'L3_xattn_bk': _L3_xattn_in['bk'], 'L3_xattn_Wv': _L3_xattn_in['Wv'], 'L3_xattn_bv': _L3_xattn_in['bv'], 'L3_xattn_Wo': _L3_xattn_in['Wo'], 'L3_xattn_bo': _L3_xattn_in['bo'], 'L3_ffn_w_gate': _L3_ffn_in['w_gate'], 'L3_ffn_w_up': _L3_ffn_in['w_up'], 'L3_ffn_w_down': _L3_ffn_in['w_down']}

def reference(x, ctx_1024, mask_BxSxS2_bf0, mask_SxS2_bk1, L0_attn_W1, L0_attn_b1, L0_attn_W2, L0_attn_b2, L0_attn_Wq, L0_attn_Wk, L0_attn_Wv, L0_attn_Wo, L0_xattn_Wq, L0_xattn_Wk, L0_xattn_Wv, L0_xattn_gru_wih, L0_xattn_gru_whh, L0_xattn_gru_bih, L0_xattn_gru_bhh, L0_xattn_slot_norm_w, L0_xattn_input_norm_w, L0_ffn_gate_w, L0_ffn_gate_b, L0_ffn_w1, L0_ffn_w2, L0_ffn_w3, L0_ffn_ws1, L0_ffn_ws2, L0_ffn_ws3, L1_attn_phase, L1_attn_Wq, L1_attn_bq, L1_attn_Wk, L1_attn_bk, L1_attn_Wv, L1_attn_bv, L1_attn_Wo, L1_attn_bo, L1_xattn_W_Q, L1_xattn_W_K, L1_xattn_W_V, L1_xattn_W_O, L1_ffn_Wg, L1_ffn_W1, L1_ffn_b1, L1_ffn_W2, L1_ffn_b2, L2_attn_Q, L2_attn_K, L2_attn_V, L2_attn_W, L2_ffn_gate_w, L2_ffn_gate_b, L2_ffn_w1, L2_ffn_b1, L2_ffn_w2, L2_ffn_b2, L3_attn_Wq, L3_attn_bq, L3_attn_Wk, L3_attn_bk, L3_attn_Wv, L3_attn_bv, L3_attn_Wo, L3_attn_bo, L3_xattn_Wq, L3_xattn_bq, L3_xattn_Wk, L3_xattn_bk, L3_xattn_Wv, L3_xattn_bv, L3_xattn_Wo, L3_xattn_bo, L3_ffn_w_gate, L3_ffn_w_up, L3_ffn_w_down):
    import jax
    import jax.numpy as jnp

    def _L0_attn_ref(x, W1, b1, W2, b2, Wq, Wk, Wv, Wo):
        import jax, jax.numpy as jnp
        import numpy as np
        EPS = 1e-06
        N_HEADS = 16

        def _project_static(x):
            sp = jnp.clip(x[..., 1:], -8.0, 8.0)
            x0 = jnp.sqrt(1.0 + jnp.sum(sp * sp, axis=-1, keepdims=True) + EPS)
            return jnp.concatenate([x0, sp], axis=-1)

        def _inner_static(x, y):
            return -x[..., 0] * y[..., 0] + jnp.sum(x[..., 1:] * y[..., 1:], axis=-1)

        def _log_map_approx(x, y):
            y = _project_static(y)
            xy = _inner_static(x, y)
            xy = jnp.minimum(xy, -(1.0 + EPS))[..., None]
            d = jnp.maximum(jnp.arccosh(jnp.maximum(-xy, 1.0 + EPS)), 0.001)
            dirv = y + xy * x
            dn = jnp.sqrt(jnp.maximum(_inner_static(dirv, dirv), EPS))[..., None]
            return d * dirv / (dn + EPS)

        def _dynamic_metric(x, mu, W1, b1, W2, b2):
            d = x.shape[-1]
            eta = jnp.ones((d,), x.dtype).at[0].set(-1.0)
            v = x - mu
            h = jnp.tanh(jnp.tanh(v @ W1.T + b1) @ W2.T + b2) * 0.1
            g = eta + h
            return jnp.concatenate([-jnp.abs(g[..., :1]), jnp.abs(g[..., 1:])], axis=-1)
        B, T, d = x.shape
        h, dh = (N_HEADS, d // N_HEADS)
        mu = jnp.zeros((d,), x.dtype).at[0].set(1.0)
        mu = jnp.broadcast_to(mu, (B, T, d))
        v = _log_map_approx(mu, x)
        q = (v @ Wq.T).reshape(B, T, h, dh).transpose(0, 2, 1, 3)
        k = (v @ Wk.T).reshape(B, T, h, dh).transpose(0, 2, 1, 3)
        vv = (v @ Wv.T).reshape(B, T, h, dh).transpose(0, 2, 1, 3)
        g_x = _dynamic_metric(x, mu, W1, b1, W2, b2)
        gh = g_x.reshape(B, T, h, dh).transpose(0, 2, 1, 3)
        sc = jnp.einsum('bhqd,bhkd->bhqk', q * gh, k) / jnp.sqrt(jnp.asarray(dh, x.dtype))
        at = jax.nn.softmax(sc, axis=-1)
        out = jnp.einsum('bhqk,bhkd->bhqd', at, vv).transpose(0, 2, 1, 3).reshape(B, T, d)
        out = out @ Wo.T
        return _project_static(_project_static(mu) + out * 0.1)

    def _L0_xattn_ref(slots, P, Wq, Wk, Wv, gru_wih, gru_whh, gru_bih, gru_bhh, slot_norm_w, input_norm_w):
        import jax, jax.numpy as jnp
        import numpy as np
        D = 128
        NUM_ITERS = 3
        EPS = 1e-06
        SCALE = D ** (-0.5)

        def rmsnorm(x, w, eps=EPS):
            return x * jax.lax.rsqrt(jnp.mean(x * x, axis=-1, keepdims=True) + eps) * w

        def gru_cell(x, h, wih, whh, bih, bhh):
            gx = x @ wih.T + bih
            gh = h @ whh.T + bhh
            xr, xz, xn = jnp.split(gx, 3, axis=-1)
            hr, hz, hn = jnp.split(gh, 3, axis=-1)
            r = jax.nn.sigmoid(xr + hr)
            z = jax.nn.sigmoid(xz + hz)
            n = jnp.tanh(xn + r * hn)
            return (1.0 - z) * n + z * h
        Pn = rmsnorm(P, input_norm_w)
        k_proj = Pn @ Wk.T
        v_proj = Pn @ Wv.T
        for _ in range(NUM_ITERS):
            sn = rmsnorm(slots, slot_norm_w)
            q_proj = sn @ Wq.T
            scores = jnp.einsum('bkd,bmd->bkm', q_proj, k_proj) * SCALE
            attn = jax.nn.softmax(scores, axis=-2)
            attn = attn / (jnp.sum(attn, axis=-1, keepdims=True) + EPS)
            updates = jnp.einsum('bkm,bmd->bkd', attn, v_proj)
            slots = gru_cell(updates, slots, gru_wih, gru_whh, gru_bih, gru_bhh)
        return slots

    def _L0_ffn_ref(x, gate_w, gate_b, w1, w2, w3, ws1, ws2, ws3):
        import jax, jax.numpy as jnp
        import numpy as np
        E = 64
        K = 6
        CAP = 64
        ROUTE_SCALE = 1.0
        shape = x.shape
        D = shape[-1]
        xf = x.reshape(-1, D)
        T = xf.shape[0]
        scores = jax.nn.softmax(xf @ gate_w.T, axis=-1)
        _, idx = jax.lax.top_k(scores + gate_b, K)
        weights = jnp.take_along_axis(scores, idx, axis=1) * ROUTE_SCALE
        flat_e = idx.reshape(-1)
        order = jnp.argsort(flat_e)
        se = flat_e[order]
        counts = jnp.bincount(flat_e, length=E)
        starts = jnp.cumsum(counts) - counts
        pos = jnp.arange(T * K) - starts[se]
        tok = order // K
        xb = jnp.zeros((E, CAP, D), xf.dtype).at[se, pos].set(xf[tok], mode='drop')
        h = jax.nn.silu(jnp.einsum('ecd,eid->eci', xb, w1)) * jnp.einsum('ecd,eid->eci', xb, w3)
        yb = jnp.einsum('eci,edi->ecd', h, w2)
        valid = (pos < CAP).astype(xf.dtype)
        contrib = yb[se, jnp.minimum(pos, CAP - 1)]
        wf = weights.reshape(-1)[order] * valid
        y = jnp.zeros_like(xf).at[tok].add(contrib * wf[:, None])
        z = jax.nn.silu(xf @ ws1.T) * (xf @ ws3.T) @ ws2.T
        return (y + z).reshape(shape)

    def _L1_attn_ref(x, phase, Wq, bq, Wk, bk, Wv, bv, Wo, bo):
        import jax, jax.numpy as jnp
        import numpy as np
        B, S, D, H, DOUT = (4, 256, 128, 4, 128)
        b, s, d = x.shape
        h = phase.shape[0]
        q = (x @ Wq + bq).reshape(b, s, h, d)
        k = (x @ Wk + bk).reshape(b, s, h, d)
        v = (x @ Wv + bv).reshape(b, s, h, d)
        c, sn = (jnp.cos(phase), jnp.sin(phase))
        qr, qi = (q * c, q * sn)
        kr, ki = (k * c, k * sn)
        scale = 1.0 / np.sqrt(d)
        scores = (jnp.einsum('bshd,bsgd->bshg', qr, kr) + jnp.einsum('bshd,bsgd->bshg', qi, ki)) * scale
        attn = jax.nn.softmax(scores, axis=-1)
        out = jnp.einsum('bshg,bsgd->bshd', attn, v)
        out = jnp.swapaxes(out, 1, 2).reshape(b, s, h * d)
        return out @ Wo + bo

    def _L1_xattn_ref(query, key, value, mask, W_Q, W_K, W_V, W_O):
        import jax, jax.numpy as jnp
        import numpy as np
        D_MODEL = 128
        NUM_HEADS = 16
        D_K = D_MODEL // NUM_HEADS

        def _split_heads(x):
            B, S, _ = x.shape
            return x.reshape(B, S, NUM_HEADS, D_K).transpose(0, 2, 1, 3)
        Q = _split_heads(jnp.einsum('bsd,ed->bse', query, W_Q))
        K = _split_heads(jnp.einsum('bsd,ed->bse', key, W_K))
        V = _split_heads(jnp.einsum('bsd,ed->bse', value, W_V))
        scores = jnp.einsum('bhqd,bhkd->bhqk', Q, K) / jnp.sqrt(jnp.float32(D_K))
        m = mask[:, None, :, :]
        scores = jnp.where(m, -jnp.inf, scores)
        attn = jax.nn.softmax(scores, axis=-1)
        attn = jnp.where(jnp.isnan(attn), 0.0, attn)
        out = jnp.einsum('bhqk,bhkd->bhqd', attn, V)
        B, H, S, _ = out.shape
        out = out.transpose(0, 2, 1, 3).reshape(B, S, D_MODEL)
        return jnp.einsum('bsd,ed->bse', out, W_O)

    def _L1_ffn_ref(x, Wg, W1, b1, W2, b2):
        import jax, jax.numpy as jnp
        import numpy as np
        B, S, D, F, E, K = (2, 256, 128, 512, 8, 2)
        b, s, d = x.shape
        e = Wg.shape[1]
        T = b * s
        C = 2 * K * T // e
        xt = x.reshape(T, d)
        logits = xt.astype(jnp.float32) @ Wg.astype(jnp.float32)
        gates = jax.nn.softmax(logits, axis=-1)
        idx1 = jnp.argmax(gates, axis=-1)
        mask1 = jax.nn.one_hot(idx1, e, dtype=gates.dtype)
        gate1 = jnp.sum(gates * mask1, axis=-1)
        logits2 = jnp.where(mask1 > 0, -jnp.inf, logits)
        idx2 = jnp.argmax(logits2, axis=-1)
        mask2 = jax.nn.one_hot(idx2, e, dtype=gates.dtype)
        gate2 = jnp.sum(gates * mask2, axis=-1)
        denom = gate1 + gate2 + 1e-09
        w1 = gate1 / denom
        w2 = gate2 / denom
        p1 = jnp.cumsum(mask1, axis=0) - mask1
        pos1 = jnp.sum(p1 * mask1, axis=-1).astype(jnp.int32)
        off = jnp.sum(mask1, axis=0)
        p2 = jnp.cumsum(mask2, axis=0) - mask2 + off[None, :]
        pos2 = jnp.sum(p2 * mask2, axis=-1).astype(jnp.int32)
        keep1 = (pos1 < C).astype(xt.dtype)
        keep2 = (pos2 < C).astype(xt.dtype)
        pos1 = jnp.clip(pos1, 0, C - 1)
        pos2 = jnp.clip(pos2, 0, C - 1)
        xe = jnp.zeros((e, C, d), dtype=xt.dtype)
        xe = xe.at[idx1, pos1].add(xt * keep1[:, None])
        xe = xe.at[idx2, pos2].add(xt * keep2[:, None])
        h = jax.nn.gelu(jnp.einsum('ecd,edf->ecf', xe, W1) + b1[:, None, :], approximate=False)
        ye = jnp.einsum('ecf,efd->ecd', h, W2) + b2[:, None, :]
        out = ye[idx1, pos1] * (w1 * keep1)[:, None] + ye[idx2, pos2] * (w2 * keep2)[:, None]
        return out.reshape(b, s, d)

    def _L2_attn_ref(x, Q, K, V, W):
        import math
        import jax, jax.numpy as jnp
        import numpy as np
        B, C, D = (4, 256, 128)
        DQ = DV = 64
        H = 16
        d_query, d_embed, num_heads = Q.shape
        d_value = V.shape[0]
        sq = math.sqrt(d_query / d_embed)
        sv = math.sqrt(d_value / d_embed)
        q = jnp.einsum('qdh,bcd->bhcq', Q, x) * sq
        k = jnp.einsum('qdh,bcd->bhcq', K, x) * sq
        v = jnp.einsum('vdh,bcd->bhcv', V, x) * sv
        att = jnp.einsum('bhcq,bhCq->bhcC', q, k) / d_query
        T = x.shape[1]
        causal = jnp.arange(T)[:, None] >= jnp.arange(T)[None, :]
        att = jnp.where(causal, att, -jnp.inf)
        p = jax.nn.softmax(att, axis=-1)
        y = jnp.einsum('bhcC,bhCv->bhcv', p, v)
        z = jnp.einsum('dvh,bhcv->bcd', W, y) * (math.sqrt(d_embed / d_value) / num_heads)
        return z

    def _L2_xattn_ref(teacher_features, student_features):
        import jax, jax.numpy as jnp
        import numpy as np
        from jax import lax
        BIG = jnp.float32(1e+30)

        def _pairwise_euclidean(a, b):
            aa = jnp.sum(a * a, axis=-1)[:, None]
            bb = jnp.sum(b * b, axis=-1)[None, :]
            ab = a @ b.T
            return jnp.sqrt(jnp.maximum(aa + bb - 2.0 * ab, 0.0))

        def _dtw_cost(D):
            row0 = jnp.cumsum(D[0])

            def row_step(prev_row, d_row):
                first = d_row[0] + prev_row[0]

                def col_step(left, inp):
                    d_ij, up, diag = inp
                    r = d_ij + jnp.minimum(jnp.minimum(up, left), diag)
                    return (r, r)
                _, rest = lax.scan(col_step, first, (d_row[1:], prev_row[1:], prev_row[:-1]))
                row = jnp.concatenate([first[None], rest])
                return (row, row)
            _, rows = lax.scan(row_step, row0, D[1:])
            return jnp.concatenate([row0[None], rows], axis=0)

        def _backtrack(R, T1, T2):
            L = T1 + T2 - 1

            def step(carry, _):
                i, j, done = carry
                valid = jnp.logical_not(done)
                cd = jnp.where((i > 0) & (j > 0), R[jnp.maximum(i - 1, 0), jnp.maximum(j - 1, 0)], BIG)
                cu = jnp.where(i > 0, R[jnp.maximum(i - 1, 0), j], BIG)
                cl = jnp.where(j > 0, R[i, jnp.maximum(j - 1, 0)], BIG)
                choice = jnp.argmin(jnp.stack([cd, cu, cl]))
                ni = jnp.where(choice <= 1, i - 1, i)
                nj = jnp.where((choice == 0) | (choice == 2), j - 1, j)
                at_origin = (i == 0) & (j == 0)
                ni = jnp.where(at_origin, 0, ni)
                nj = jnp.where(at_origin, 0, nj)
                return ((ni, nj, done | at_origin), (i, j, valid))
            init = (jnp.int32(T1 - 1), jnp.int32(T2 - 1), jnp.bool_(False))
            _, (i_idx, j_idx, valid) = lax.scan(step, init, None, length=L)
            return (i_idx, j_idx, valid)

        def _align_one(small, large):
            T_small, d = small.shape
            T_large = large.shape[0]
            D = _pairwise_euclidean(small, large)
            R = _dtw_cost(D)
            i_idx, j_idx, valid = _backtrack(R, T_small, T_large)
            contrib = small[i_idx] * valid[:, None].astype(small.dtype)
            expanded = jnp.zeros((T_large, d), dtype=small.dtype).at[j_idx].add(contrib)
            return expanded
        return jax.vmap(_align_one)(teacher_features, student_features)

    def _L2_ffn_ref(h, gate_w, gate_b, w1, b1, w2, b2):
        import math
        import jax, jax.numpy as jnp
        import numpy as np
        B, L, D, F_FF, E = (4, 256, 128, 512, 8)
        TOP_K = 1
        CAPACITY_FACTOR = 1.25
        Bh, Lh, Dh = h.shape
        T = Bh * Lh
        capacity = max(1, math.ceil(CAPACITY_FACTOR * (T * TOP_K / E)))
        x = h.reshape(T, Dh)
        logits = x @ gate_w.T + gate_b
        probs = jax.nn.softmax(logits, axis=-1)
        idx = jnp.argmax(probs, axis=-1)
        top_prob = jnp.max(probs, axis=-1)
        one_hot = jax.nn.one_hot(idx, E, dtype=jnp.int32)
        pos = jnp.take_along_axis(jnp.cumsum(one_hot, axis=0), idx[:, None], axis=1)[:, 0] - 1
        keep = pos < capacity
        safe_pos = jnp.where(keep, pos, 0)
        buf = jnp.zeros((E, capacity, Dh), dtype=x.dtype)
        buf = buf.at[idx, safe_pos].add(x * keep[:, None].astype(x.dtype))
        hdn = jax.nn.relu(jnp.einsum('ecd,edf->ecf', buf, w1) + b1[:, None, :])
        eout = jnp.einsum('ecf,efd->ecd', hdn, w2) + b2[:, None, :]
        gathered = eout[idx, safe_pos]
        out = gathered * (top_prob * keep.astype(x.dtype))[:, None]
        return out.reshape(Bh, Lh, Dh)

    def _L3_attn_ref(x, Wq, bq, Wk, bk, Wv, bv, Wo, bo):
        import jax, jax.numpy as jnp
        import numpy as np
        HEAD_NUM = 16
        B, S, D = x.shape
        H = HEAD_NUM
        hd = D // H

        def proj(W, b):
            return (x @ W.T + b).reshape(B, S, H, hd).transpose(0, 2, 1, 3)
        Q, K, V = (proj(Wq, bq), proj(Wk, bk), proj(Wv, bv))
        scale = 1.0 / jnp.sqrt(jnp.float32(hd))
        scores = jnp.einsum('bhqd,bhkd->bhqk', Q, K) * scale
        attn = jax.nn.softmax(scores, axis=-1)
        out = jnp.einsum('bhqk,bhkd->bhqd', attn, V)
        out = out.transpose(0, 2, 1, 3).reshape(B, S, D)
        return out @ Wo.T + bo

    def _L3_xattn_ref(queries, keys, values, mask, Wq, bq, Wk, bk, Wv, bv, Wo, bo):
        import jax, jax.numpy as jnp
        import numpy as np
        D = 128
        H = 16
        HD = D // H
        SCALE = 1.0 / np.sqrt(HD)

        def _split_heads(x):
            B, S, _ = x.shape
            return x.reshape(B, S, H, HD).transpose(0, 2, 1, 3)
        q = _split_heads(queries @ Wq + bq)
        k = _split_heads(keys @ Wk + bk)
        v = _split_heads(values @ Wv + bv)
        scores = jnp.einsum('bhqd,bhkd->bhqk', q, k) * SCALE
        neg = jnp.finfo(scores.dtype).min
        scores = jnp.where(mask[None, None, :, :], scores, neg)
        probs = jax.nn.softmax(scores, axis=-1)
        ctx = jnp.einsum('bhqk,bhkd->bhqd', probs, v)
        B, _, Sq, _ = ctx.shape
        combined = ctx.transpose(0, 2, 1, 3).reshape(B, Sq, D)
        return combined @ Wo + bo

    def _L3_ffn_ref(x, w_gate, w_up, w_down):
        import jax, jax.numpy as jnp
        import numpy as np
        BLOCK = 16
        _GRID = jnp.array([0.0, 0.5, 1.0, 1.5, 2.0, 3.0, 4.0, 6.0], dtype=jnp.float32)
        _MID = jnp.array([0.25, 0.75, 1.25, 1.75, 2.5, 3.5, 5.0], dtype=jnp.float32)

        def fp4_quant_dequant(x):
            shape = x.shape
            xb = x.reshape(shape[:-1] + (shape[-1] // BLOCK, BLOCK))
            scale = jnp.max(jnp.abs(xb), axis=-1, keepdims=True) / 6.0
            scale = jnp.maximum(scale, jnp.float32(1e-12))
            xn = xb / scale
            idx = jnp.searchsorted(_MID, jnp.abs(xn))
            q = _GRID[idx] * jnp.sign(xn) * scale
            return q.reshape(shape)

        def fp4_linear(x, w):
            xq = fp4_quant_dequant(x)
            wq = fp4_quant_dequant(w)
            return jnp.einsum('bsk,nk->bsn', xq, wq)
        gate = fp4_linear(x, w_gate)
        y = fp4_linear(x, w_up)
        h = jax.nn.silu(gate) * y
        return fp4_linear(h, w_down)
    x = x + _L0_attn_ref(_layernorm(x, axis=-1), L0_attn_W1, L0_attn_b1, L0_attn_W2, L0_attn_b2, L0_attn_Wq, L0_attn_Wk, L0_attn_Wv, L0_attn_Wo)
    x = x + _L0_xattn_ref(_layernorm(x, axis=-1), ctx_1024, L0_xattn_Wq, L0_xattn_Wk, L0_xattn_Wv, L0_xattn_gru_wih, L0_xattn_gru_whh, L0_xattn_gru_bih, L0_xattn_gru_bhh, L0_xattn_slot_norm_w, L0_xattn_input_norm_w)
    x = x + _L0_ffn_ref(_layernorm(x, axis=-1), L0_ffn_gate_w, L0_ffn_gate_b, L0_ffn_w1, L0_ffn_w2, L0_ffn_w3, L0_ffn_ws1, L0_ffn_ws2, L0_ffn_ws3)
    x = x + _L1_attn_ref(_layernorm(x, axis=-1), L1_attn_phase, L1_attn_Wq, L1_attn_bq, L1_attn_Wk, L1_attn_bk, L1_attn_Wv, L1_attn_bv, L1_attn_Wo, L1_attn_bo)
    x = x + _L1_xattn_ref(_layernorm(x, axis=-1), ctx_1024, ctx_1024, mask_BxSxS2_bf0, L1_xattn_W_Q, L1_xattn_W_K, L1_xattn_W_V, L1_xattn_W_O)
    x = x + _L1_ffn_ref(_layernorm(x, axis=-1), L1_ffn_Wg, L1_ffn_W1, L1_ffn_b1, L1_ffn_W2, L1_ffn_b2)
    x = x + _L2_attn_ref(_layernorm(x, axis=-1), L2_attn_Q, L2_attn_K, L2_attn_V, L2_attn_W)
    x = x + _L2_xattn_ref(ctx_1024, _layernorm(x, axis=-1))
    x = x + _L2_ffn_ref(_layernorm(x, axis=-1), L2_ffn_gate_w, L2_ffn_gate_b, L2_ffn_w1, L2_ffn_b1, L2_ffn_w2, L2_ffn_b2)
    x = x + _L3_attn_ref(_layernorm(x, axis=-1), L3_attn_Wq, L3_attn_bq, L3_attn_Wk, L3_attn_bk, L3_attn_Wv, L3_attn_bv, L3_attn_Wo, L3_attn_bo)
    x = x + _L3_xattn_ref(_layernorm(x, axis=-1), ctx_1024, ctx_1024, mask_SxS2_bk1, L3_xattn_Wq, L3_xattn_bq, L3_xattn_Wk, L3_xattn_bk, L3_xattn_Wv, L3_xattn_bv, L3_xattn_Wo, L3_xattn_bo)
    x = x + _L3_ffn_ref(_layernorm(x, axis=-1), L3_ffn_w_gate, L3_ffn_w_up, L3_ffn_w_down)
    return x

_drawn_inputs = setup_inputs


def setup_inputs(seed=0):
    import zlib

    import numpy as np

    out = dict(_drawn_inputs(seed))
    spreads = {'L0_xattn_gru_bih': (0.0, 0.1),
     'L0_xattn_gru_bhh': (0.0, 0.1),
     'L0_xattn_slot_norm_w': (1.0, 0.2),
     'L0_xattn_input_norm_w': (1.0, 0.2),
     'L0_ffn_gate_b': (0.0, 0.8),
     'L1_attn_bq': (0.0, 0.1),
     'L1_attn_bk': (0.0, 0.345),
     'L1_attn_bv': (0.0, 0.1),
     'L1_attn_bo': (0.0, 0.1),
     'L1_ffn_b1': (0.0, 0.1),
     'L1_ffn_b2': (0.0, 0.1),
     'L2_ffn_gate_b': (0.0, 0.8),
     'L2_ffn_b1': (0.0, 0.8),
     'L2_ffn_b2': (0.0, 0.8),
     'L3_attn_bq': (0.0, 0.8),
     'L3_attn_bk': (0.0, 2.0),
     'L3_attn_bv': (0.0, 0.1),
     'L3_attn_bo': (0.0, 0.1)}
    factors = {'L0_attn_W1': 8.0,
     'L0_attn_b1': 200.0,
     'L0_attn_W2': 8.0,
     'L0_attn_b2': 200.0,
     'L0_attn_Wq': 8.0,
     'L0_attn_Wk': 8.0,
     'L0_attn_Wv': 8.0,
     'L0_attn_Wo': 8.0,
     'L0_ffn_gate_w': 8.0,
     'L0_ffn_w1': 8.0,
     'L0_ffn_w2': 8.0,
     'L0_ffn_w3': 8.0,
     'L0_ffn_ws2': 8.0,
     'L1_attn_phase': 8.0,
     'L2_attn_K': 8.0,
     'L2_ffn_gate_w': 5.792,
     'L2_ffn_w1': 8.0,
     'L2_ffn_w2': 8.0,
     'L3_xattn_Wq': 8.0,
     'L3_xattn_bq': 8.0,
     'L3_xattn_Wk': 8.0,
     'L3_xattn_bk': 200.0,
     'L3_xattn_Wv': 3.845,
     'L3_xattn_bv': 8.0,
     'L3_xattn_Wo': 4.463,
     'L3_xattn_bo': 4.799,
     'L3_ffn_w_gate': 8.0,
     'L3_ffn_w_up': 8.0,
     'L3_ffn_w_down': 8.0}
    for name, (base, spread) in spreads.items():
        noise = np.random.default_rng([zlib.crc32(name.encode()), seed]).standard_normal(out[name].shape)
        drawn = base * np.exp(spread * noise) if base else spread * noise
        out[name] = jnp.asarray(drawn.astype(out[name].dtype))
    for name, factor in factors.items():
        out[name] = (out[name] * factor).astype(out[name].dtype)
    return out
```

```python
from collections import namedtuple
from contextlib import ExitStack, contextmanager
from itertools import count

import numpy as np

import concourse.bass as bass
from concourse import mybir

ALU = mybir.AluOpType
ACT = mybir.ActivationFunctionType
AX = mybir.AxisListType
F32 = mybir.dt.float32
BF16 = mybir.dt.bfloat16
U32 = mybir.dt.uint32
I32 = mybir.dt.int32
U8 = mybir.dt.uint8

P = 128
D = 128
B = 4
S = 512
QT = S // P
NT = B * QT
SC = 154
SERIAL = count()
MASKED = -1.0e30


def named(**items):
    return namedtuple("Named", list(items))(**items)


def ctx_tiles():
    return [(0, P), (P, SC - P)]


@contextmanager
def stage_semaphores(nc, *names):
    with ExitStack() as held:
        sems = {n: held.enter_context(nc.semaphore(n)) for n in names}
        yield named(**sems)
        with nc.Block() as block:
            @block.sync
            def _(sp):
                for s in sems.values():
                    sp.sem_clear(s)


@contextmanager
def buffers(nc, **shapes):
    stage = next(SERIAL)
    with ExitStack() as held:
        yield named(**{n: held.enter_context(nc.sbuf_tensor(f"{n}_{stage}", list(s), t))
                                 for n, (s, t) in shapes.items()})


def load(nc, pairs):
    with stage_semaphores(nc, "loaded") as s:
        with nc.Block() as block:
            @block.sync
            def _(sp):
                for n, (dst, src) in enumerate(pairs):
                    sp.dma_start(dst, src, allow_slow_non_contiguous=True).then_inc(s.loaded, 16)
                sp.wait_ge(s.loaded, 16 * len(pairs))


def constants(nc, g):
    with stage_semaphores(nc, "filled", "selected") as s:
        with nc.Block() as block:
            @block.gpsimd
            def _(pool):
                pool.memset(g.ident[:], 0.0).then_inc(s.filled, 1)
                pool.memset(g.ones[:], 1.0).then_inc(s.filled, 1)
                pool.memset(g.ones_bf[:], 1.0).then_inc(s.filled, 1)
                pool.memset(g.before[:], 1.0).then_inc(s.filled, 1)
                pool.memset(g.causal[:], 0.0).then_inc(s.filled, 1)
                pool.memset(g.eta[:], 1.0).then_inc(s.filled, 1)
                pool.memset(g.minus_e0[:], 0.0).then_inc(s.filled, 1)
                pool.wait_ge(s.filled, 7)
                pool.affine_select(out=g.ident[:], in_=g.ident[:], compare_op=ALU.not_equal, fill=1.0, base=0,
                                   pattern=[[-1, P]], channel_multiplier=1).then_inc(s.selected, 1)
                pool.affine_select(out=g.before[:], in_=g.before[:], compare_op=ALU.is_gt, fill=0.0, base=0,
                                   pattern=[[1, P]], channel_multiplier=-1).then_inc(s.selected, 1)
                pool.affine_select(out=g.causal[:], in_=g.causal[:], compare_op=ALU.is_ge, fill=MASKED, base=0,
                                   pattern=[[-1, P]], channel_multiplier=1).then_inc(s.selected, 1)
                pool.memset(g.eta[0:1, 0:1], -1.0).then_inc(s.filled, 1)
                pool.memset(g.minus_e0[0:1, :], -1.0).then_inc(s.filled, 1)
                pool.wait_ge(s.selected, 1)
                pool.tensor_copy(g.ident_bf[:], g.ident[:]).then_inc(s.selected, 1)
                pool.wait_ge(s.selected, 4)
                pool.wait_ge(s.filled, 9)


def layernorm(nc, g):
    with (
        buffers(nc, stats=((P, QT, 6), F32), mv=((P, QT, 2), F32), rstd=((P, QT), F32), normed=((P, QT, D), F32)) as u,
        nc.Fori(0, B) as b,
        stage_semaphores(nc, "stats_done", "mean_done", "var_done", "sd_done", "rstd_done", "normed_done",
                         "turned", "feature_major_done", "token_major_done") as s,
        nc.Block() as block,
    ):
        @block.vector
        def _(dve):
            for j in range(QT):
                dve.bn_stats(u.stats[:, j, :], g.x[:, bass.ds(b * QT + j, 1), :]).then_inc(s.stats_done, 1)
            for j in range(QT):
                dve.wait_ge(s.stats_done, j + 1)
                dve.bn_aggr(u.mv[:, j, :], u.stats[:, j, :]).then_inc(s.mean_done, 1)
            dve.wait_ge(s.mean_done, QT)
            dve.tensor_scalar(u.rstd[:], u.mv[:, :, 1], 1e-5, None, ALU.add).then_inc(s.var_done, 1)
            dve.wait_ge(s.sd_done, 1)
            dve.reciprocal(u.rstd[:], u.rstd[:]).then_inc(s.rstd_done, 1)
            dve.wait_ge(s.rstd_done, 1)
            for j in range(QT):
                dve.tensor_scalar(u.normed[:, j, :], g.x[:, bass.ds(b * QT + j, 1), :], u.mv[:, j, 0:1],
                                  u.rstd[:, j:j + 1], ALU.subtract, ALU.mult).then_inc(s.normed_done, 1)

        @block.scalar
        def _(act):
            act.wait_ge(s.var_done, 1)
            act.activation(u.rstd[:], u.rstd[:], ACT.Sqrt).then_inc(s.sd_done, 1)
            act.wait_ge(s.turned, 1)
            act.activation(g.xnT[:, bass.ds(b * S, S)], g.psum[:, 0, :], ACT.Copy).then_inc(s.feature_major_done, 1)

        @block.gpsimd
        def _(pool):
            pool.wait_ge(s.normed_done, QT)
            pool.tensor_copy(g.xn[:, bass.ds(b * QT, QT), :], u.normed[:]).then_inc(s.token_major_done, 1)

        @block.tensor
        def _(pe):
            for j in range(QT):
                pe.wait_ge(s.normed_done, j + 1)
                last = pe.transpose(g.psum[:, 0, j * P:(j + 1) * P], u.normed[:, j, :], g.ident[:])
            last.then_inc(s.turned, 1)


def turn_to_features(nc, g, src, dstT):
    with (
        buffers(nc, fixed=((P, QT, D), F32)) as u,
        nc.Fori(0, B) as b,
        stage_semaphores(nc, "fixed_done", "turned", "feature_major_done") as s,
        nc.Block() as block,
    ):
        @block.vector
        def _(dve):
            dve.tensor_copy(u.fixed[:], src[:, bass.ds(b * QT, QT), :]).then_inc(s.fixed_done, 1)

        @block.tensor
        def _(pe):
            pe.wait_ge(s.fixed_done, 1)
            for j in range(QT):
                last = pe.transpose(g.psum[:, 0, j * P:(j + 1) * P], u.fixed[:, j, :], g.ident[:])
            last.then_inc(s.turned, 1)

        @block.scalar
        def _(act):
            act.wait_ge(s.turned, 1)
            act.activation(dstT[:, bass.ds(b * S, S)], g.psum[:, 0, :], ACT.Copy).then_inc(s.feature_major_done, 1)


def attention(nc, g, *, w, H, dh, hp, keys, kv_src, scale, q_src=None, causal=False, mask=None, metric=None,
              add_to=None, store=None, out_scale=1.0, zero_if_all_masked=False, bq=None, bk=None, bv=None, bo=None):
    G = H * hp // P
    per = P // hp
    dv = dh
    HV = H * dv
    OC = HV // P
    KT = len(keys)
    SK = keys[-1][0] + keys[-1][1]
    VN = max(1, HV // 512)
    VW = HV // VN
    q_src = q_src if q_src is not None else g.xnT
    jobs_v = [(t, n) for t in range(KT) for n in range(VN)]
    NQK = 2 * G
    NJOBS = NQK + len(jobs_v)
    NB = QT * H

    shapes = dict(srcq=((P, S), F32), srck=((P, SK), F32), qT=((P, G, S), F32), kT=((P, G, SK), F32),
                  v=((P, KT, HV), F32), probs=((P, 3, S), F32), probsT=((P, 2, KT * P), F32),
                  nmax=((P, QT, H), F32), rsum=((P, QT, H), F32), rinv=((P, 2, H), F32),
                  o=((P, 2, HV), F32), oT=((P, 2, HV), F32))
    if mask is not None:
        shapes["mask_add"] = ((P, QT, SK), BF16)
        shapes["live"] = ((P, 2, H), F32)
    if metric is not None:
        shapes.update(metric_src=((P, S), F32), hidden=((P, 2, S), F32), gx=((P, 2, S), F32))
    with (
        buffers(nc, **shapes) as u,
        nc.Fori(0, B) as b,
        stage_semaphores(nc, "src_done", "product_done", "even_out", "odd_out", "mask_done",
                         "scores_done", "max_done", "probs_done", "probs_turned", "probsT_done", "heads_done",
                         "rinv_done", "o_done", "o_turned", "oT_done", "projected", "stored", "chain",
                         "metric_in", "hidden_mm", "hidden_done", "gx_mm", "gx_tanh", "gx_done") as s,
    ):
        with nc.Block() as block:
            @block.vector
            def _(dve):
                dve.tensor_copy(u.srcq[:], q_src[:, bass.ds(b * S, S)]).then_inc(s.src_done, 1)
                dve.tensor_copy(u.srck[:], kv_src[:, bass.ds(b * SK, SK)]).then_inc(s.src_done, 1)
                if metric is not None:
                    dve.tensor_scalar(u.metric_src[:], g.xnT[:, bass.ds(b * S, S)], g.minus_e0[:, 0:1], None,
                                      ALU.add).then_inc(s.metric_in, 1)
                if mask is not None:
                    kind, m = mask
                    src = m[:, bass.ds(b * QT, QT), :] if kind == "drop" else m[:]
                    if kind == "drop":
                        dve.tensor_scalar(u.mask_add[:], src, MASKED, None, ALU.mult).then_inc(s.mask_done, 1)
                    else:
                        dve.tensor_scalar(u.mask_add[:], src, -1.0, -MASKED, ALU.add, ALU.mult).then_inc(s.mask_done, 1)
                for n in range(1, NJOBS, 2):
                    dve.wait_ge(s.product_done, n + 1)
                    if n < NQK:
                        i = n // 2
                        dst = u.kT[:, i, :]
                        if bk is not None:
                            ins = dve.tensor_scalar(dst, g.psum[:, n % 8, 0:SK], bk[:, i:i + 1], None, ALU.add)
                        else:
                            ins = dve.tensor_copy(dst, g.psum[:, n % 8, 0:SK])
                    else:
                        t, c = jobs_v[n - NQK]
                        rows = keys[t][1]
                        ins = dve.tensor_copy(u.v[0:rows, t, c * VW:(c + 1) * VW], g.psum[0:rows, n % 8, 0:VW])
                    ins.then_inc(s.odd_out, 1)

            @block.scalar
            def _(act):
                for n in range(0, NJOBS, 2):
                    act.wait_ge(s.product_done, n + 1)
                    if n < NQK:
                        i = n // 2
                        bias = bq[:, i:i + 1] if bq is not None else 0.0
                        ins = act.activation(u.qT[:, i, :], g.psum[:, n % 8, :], ACT.Identity, bias=bias, scale=scale)
                    else:
                        t, c = jobs_v[n - NQK]
                        rows = keys[t][1]
                        ins = act.activation(u.v[0:rows, t, c * VW:(c + 1) * VW], g.psum[0:rows, n % 8, 0:VW], ACT.Copy)
                    ins.then_inc(s.even_out, 1)

            @block.tensor
            def _(pe):
                pe.wait_ge(s.src_done, 2)
                for n in range(NJOBS):
                    if n >= 8 and n % 2 == 0:
                        pe.wait_ge(s.even_out, n // 2 - 3)
                    if n >= 8 and n % 2 == 1:
                        pe.wait_ge(s.odd_out, n // 2 - 3)
                    if n < NQK:
                        i = n // 2
                        if n % 2 == 0:
                            last = pe.matmul(g.psum[:, n % 8, :], w.wq[:, i, :], u.srcq[:], start=True, stop=True)
                        else:
                            last = pe.matmul(g.psum[:, n % 8, 0:SK], w.wk[:, i, :], u.srck[:], start=True, stop=True)
                    else:
                        t, c = jobs_v[n - NQK]
                        at, rows = keys[t]
                        out = g.psum[0:rows, n % 8, 0:VW]
                        last = pe.matmul(out, u.srck[:, at:at + rows], w.wv[:, c * VW:(c + 1) * VW],
                                         start=True, stop=bv is None)
                        if bv is not None:
                            last = pe.matmul(out, g.ones[0:1, 0:rows], bv[0:1, c * VW:(c + 1) * VW],
                                             start=False, stop=True)
                    last.then_inc(s.product_done, 1)

        if metric is not None:
            with nc.Block() as block:
                @block.tensor
                def _(pe):
                    for c in range(2):
                        pe.matmul(g.psum[:, c, :], metric.w1[:, c, :], u.metric_src[:], start=True,
                                  stop=True).then_inc(s.hidden_mm, 1)
                    pe.wait_ge(s.hidden_done, 2)
                    for i in range(G):
                        if i >= 2:
                            pe.wait_ge(s.gx_tanh, i - 1)
                        pe.matmul(g.psum[:, 2 + i % 2, :], metric.w2[:, 0, i, :], u.hidden[:, 0, :], start=True, stop=False)
                        pe.matmul(g.psum[:, 2 + i % 2, :], metric.w2[:, 1, i, :], u.hidden[:, 1, :], start=False,
                                  stop=True).then_inc(s.gx_mm, 1)

                @block.scalar
                def _(act):
                    for c in range(2):
                        act.wait_ge(s.hidden_mm, c + 1)
                        act.activation(u.hidden[:, c, :], g.psum[:, c, :], ACT.Tanh,
                                       bias=metric.b1[:, c:c + 1]).then_inc(s.hidden_done, 1)
                    for i in range(G):
                        act.wait_ge(s.gx_mm, i + 1)
                        if i >= 2:
                            act.wait_ge(s.gx_done, i - 1)
                        act.activation(u.gx[:, i % 2, :], g.psum[:, 2 + i % 2, :], ACT.Tanh,
                                       bias=metric.b2[:, i:i + 1]).then_inc(s.gx_tanh, 1)

                @block.vector
                def _(dve):
                    for i in range(G):
                        eta = g.eta[:, i:i + 1]
                        gx = u.gx[:, i % 2, :]
                        dve.wait_ge(s.gx_tanh, i + 1)
                        dve.tensor_scalar(gx, gx, 0.1, eta, ALU.mult, ALU.add).then_inc(s.chain, 1)
                        dve.wait_ge(s.chain, 2 * i + 1)
                        dve.scalar_tensor_tensor(out=gx, in0=gx, scalar=-1.0, in1=gx, op0=ALU.mult,
                                                 op1=ALU.max).then_inc(s.chain, 1)
                        dve.wait_ge(s.chain, 2 * i + 2)
                        dve.scalar_tensor_tensor(out=u.qT[:, i, :], in0=gx, scalar=eta, in1=u.qT[:, i, :], op0=ALU.mult,
                                                 op1=ALU.mult).then_inc(s.gx_done, 1)

        SCORES, TURNED, OUT, OTURN, FINAL = 0, 2, 4, 6, 7

        def width(n):
            return (n // H + 1) * P if causal else SK

        def tiles(n):
            return n // H + 1 if causal else KT

        def out_bank(q, lo, hi):
            if OC == 1:
                return g.psum[:, OUT + q % 2, lo:hi]
            return g.psum[:, OUT + lo // 512, lo % 512:lo % 512 + hi - lo]

        with nc.Block() as block:
            @block.tensor
            def _(pe):
                def scores(n):
                    q, h = n // H, n % H
                    rows = slice(hp * (h % per), hp * (h % per) + hp)
                    N = width(n)
                    if n >= 2:
                        pe.wait_ge(s.probs_done, n - 1)
                    out = g.psum[:, SCORES + n % 2, 0:N]
                    masked = mask is not None
                    last = pe.matmul(out, u.qT[rows, h // per, q * P:(q + 1) * P], u.kT[rows, h // per, 0:N],
                                     start=True, stop=not (masked or causal), tile_position=(rows.start, 0))
                    if masked:
                        last = pe.matmul(out, g.ident_bf[:], u.mask_add[:, q, :], start=False, stop=True)
                    if causal:
                        last = pe.matmul(g.psum[:, SCORES + n % 2, N - P:N], g.ident_bf[:], g.causal[:],
                                         start=False, stop=True)
                    last.then_inc(s.scores_done, 1)

                def turn(n):
                    pe.wait_ge(s.probs_done, n + 1)
                    if n >= 2:
                        pe.wait_ge(s.probsT_done, n - 1)
                    for t in range(tiles(n)):
                        at, rows = keys[t]
                        last = pe.transpose(g.psum[0:rows, TURNED + n % 2, t * P:(t + 1) * P],
                                            u.probs[:, n % 3, at:at + rows], g.ident[:])
                    last.then_inc(s.probs_turned, 1)

                def heads(n):
                    q, h = n // H, n % H
                    pe.wait_ge(s.probsT_done, n + 1)
                    if h == 0 and (q >= 2 or (q >= 1 and OC > 1)):
                        pe.wait_ge(s.o_done, q - 1 if OC == 1 else q)
                    for t in range(tiles(n)):
                        rows = keys[t][1]
                        last = pe.matmul(out_bank(q, h * dv, (h + 1) * dv), u.probsT[0:rows, n % 2, t * P:(t + 1) * P],
                                         u.v[0:rows, t, h * dv:(h + 1) * dv], start=t == 0, stop=t == tiles(n) - 1)
                    last.then_inc(s.heads_done, 1)

                def project(q):
                    pe.wait_ge(s.o_done, q + 1)
                    for c0 in range(0, OC, 4):
                        n = q * ((OC + 3) // 4) + c0 // 4
                        if n >= 1:
                            pe.wait_ge(s.oT_done, n)
                        for c in range(c0, min(OC, c0 + 4)):
                            last = pe.transpose(g.psum[:, OTURN, (c % 4) * P:(c % 4 + 1) * P],
                                                u.o[:, q % 2, c * P:(c + 1) * P], g.ident[:])
                        last.then_inc(s.o_turned, 1)
                    pe.wait_ge(s.oT_done, (q + 1) * ((OC + 3) // 4))
                    if q >= 1:
                        pe.wait_ge(s.stored, q)
                    for c in range(OC):
                        last = pe.matmul(g.psum[:, FINAL, 0:D], u.oT[:, q % 2, c * P:(c + 1) * P], w.wo[:, c, :],
                                         start=c == 0, stop=c == OC - 1 and bo is None)
                    if bo is not None:
                        last = pe.matmul(g.psum[:, FINAL, 0:D], g.ones[0:1, :], bo[0:1, :], start=False, stop=True)
                    last.then_inc(s.projected, 1)

                if mask is not None:
                    pe.wait_ge(s.mask_done, 1)
                for n in range(NB + 3):
                    if n < NB:
                        scores(n)
                    if 2 <= n < NB + 2:
                        turn(n - 2)
                    if n >= 3:
                        heads(n - 3)
                    if n >= 6 and (n - 6) % H == H - 1:
                        project((n - 6) // H)
                project(QT - 1)

            @block.vector
            def _(dve):
                def maximum(n):
                    dve.wait_ge(s.scores_done, n + 1)
                    dve.tensor_reduce(u.nmax[:, n // H, n % H:n % H + 1], g.psum[:, SCORES + n % 2, 0:width(n)], AX.X,
                                      ALU.max, negate=True).then_inc(s.max_done, 1)

                def copy_turned(n):
                    dve.wait_ge(s.probs_turned, n + 1)
                    if n >= 2:
                        dve.wait_ge(s.heads_done, n - 1)
                    full = [t for t in range(tiles(n)) if keys[t][1] == P]
                    ins = dve.tensor_copy(u.probsT[:, n % 2, 0:len(full) * P],
                                          g.psum[:, TURNED + n % 2, 0:len(full) * P])
                    if len(full) < tiles(n):
                        t, rows = tiles(n) - 1, keys[tiles(n) - 1][1]
                        ins = dve.tensor_copy(u.probsT[0:rows, n % 2, t * P:(t + 1) * P],
                                              g.psum[0:rows, TURNED + n % 2, t * P:(t + 1) * P])
                    ins.then_inc(s.probsT_done, 1)

                def normalise(q):
                    dve.wait_ge(s.heads_done, H * (q + 1))
                    if q >= 2:
                        dve.wait_ge(s.projected, q - 1)
                    dve.wait_ge(s.probs_done, H * (q + 1))
                    dve.reciprocal(u.rinv[:, q % 2, :], u.rsum[:, q, :]).then_inc(s.rinv_done, 1)
                    per_q = 1
                    if zero_if_all_masked:
                        dve.tensor_scalar(u.live[:, q % 2, :], u.nmax[:, q, :], -MASKED / 2, None,
                                          ALU.is_lt).then_inc(s.rinv_done, 1)
                        dve.wait_ge(s.rinv_done, 3 * q + 2)
                        dve.tensor_tensor(u.rinv[:, q % 2, :], u.rinv[:, q % 2, :], u.live[:, q % 2, :],
                                          ALU.mult).then_inc(s.rinv_done, 1)
                        per_q = 3
                    dve.wait_ge(s.rinv_done, per_q * (q + 1))
                    step = min(HV, 512)
                    for lo in range(0, HV, step):
                        hs = step // dv
                        h0 = lo // dv
                        ins = dve.tensor_tensor(
                            u.o[:, q % 2, lo:lo + step].rearrange("p (h d) -> p h d", d=dv),
                            out_bank(q, lo, lo + step).rearrange("p (h d) -> p h d", d=dv),
                            u.rinv[:, q % 2, h0:h0 + hs].unsqueeze(2).to_broadcast([P, hs, dv]), ALU.mult)
                    ins.then_inc(s.o_done, 1)

                def put(q):
                    dve.wait_ge(s.projected, q + 1)
                    if add_to is not None:
                        at = add_to[:, bass.ds(b * QT + q, 1), :]
                        dve.scalar_tensor_tensor(out=at, in0=g.psum[:, FINAL, 0:D].unsqueeze(1), scalar=out_scale, in1=at,
                                                 op0=ALU.mult, op1=ALU.add).then_inc(s.stored, 1)
                    else:
                        dve.tensor_scalar(store[:, bass.ds(b * QT + q, 1), :], g.psum[:, FINAL, 0:D].unsqueeze(1), out_scale,
                                          None, ALU.mult).then_inc(s.stored, 1)

                for n in range(NB + 3):
                    if n < NB:
                        maximum(n)
                    if 2 <= n < NB + 2:
                        copy_turned(n - 2)
                    if n >= 3 and (n - 3) % H == H - 1:
                        normalise((n - 3) // H)
                    if n >= 8 and (n - 8) % H == H - 1:
                        put((n - 8) // H)
                put(QT - 1)

            @block.scalar
            def _(act):
                def copy_o(q):
                    for c0 in range(0, OC, 4):
                        n = q * ((OC + 3) // 4) + c0 // 4
                        act.wait_ge(s.o_turned, n + 1)
                        if q >= 2:
                            act.wait_ge(s.projected, q - 1)
                        wd = min(4, OC - c0) * P
                        act.activation(u.oT[:, q % 2, c0 * P:c0 * P + wd], g.psum[:, OTURN, 0:wd],
                                       ACT.Copy).then_inc(s.oT_done, 1)

                for n in range(NB + 3):
                    if n < NB:
                        act.wait_ge(s.max_done, n + 1)
                        if n >= 3:
                            act.wait_ge(s.probs_turned, n - 2)
                        act.activation(u.probs[:, n % 3, 0:width(n)], g.psum[:, SCORES + n % 2, 0:width(n)], ACT.Exp,
                                       bias=u.nmax[:, n // H, n % H:n % H + 1],
                                       accum_out=u.rsum[:, n // H, n % H:n % H + 1]).then_inc(s.probs_done, 1)
                    if n >= 6 and (n - 6) % H == H - 1:
                        copy_o((n - 6) // H)
                copy_o(QT - 1)


ALL_KEYS = [(t * P, P) for t in range(QT)]


def log_map(nc, g, dst):
    EPS = 1e-6
    with (
        buffers(nc, sq=((P, NT, D), F32), n2=((P, NT), F32), y0=((P, NT), F32), z=((P, NT), F32), t0=((P, NT), F32),
                a=((P, NT), F32), c=((P, NT), F32)) as u,
        stage_semaphores(nc, "step", "rooted") as s,
        nc.Block() as block,
    ):
        @block.vector
        def _(dve):
            steps = [0]

            def done(ins):
                steps[0] += 1
                ins.then_inc(s.step, 1)
                dve.wait_ge(s.step, steps[0])

            tail = dst[:, :, 1:D]
            done(dve.tensor_scalar(tail, g.xn[:, :, 1:D], -8.0, 8.0, ALU.max, ALU.min))
            done(dve.tensor_tensor(u.sq[:, :, 1:D], tail, tail, ALU.mult))
            done(dve.tensor_reduce(u.n2[:], u.sq[:, :, 1:D], AX.X, ALU.add))
            done(dve.tensor_scalar(u.y0[:], u.n2[:], 1.0, EPS, ALU.add, ALU.add))
            dve.wait_ge(s.rooted, 1)
            done(dve.tensor_scalar(u.z[:], u.y0[:], 1.0 + EPS, None, ALU.max))
            done(dve.tensor_tensor(u.t0[:], u.y0[:], u.z[:], ALU.subtract))
            done(dve.tensor_tensor(u.c[:], u.t0[:], u.t0[:], ALU.mult))
            done(dve.tensor_tensor(u.c[:], u.n2[:], u.c[:], ALU.subtract))
            done(dve.tensor_scalar(u.c[:], u.c[:], EPS, None, ALU.max))
            done(dve.tensor_tensor(u.a[:], u.z[:], u.z[:], ALU.mult))
            done(dve.tensor_scalar(u.a[:], u.a[:], -1.0, None, ALU.add))
            dve.wait_ge(s.rooted, 3)
            done(dve.tensor_tensor(u.a[:], u.a[:], u.z[:], ALU.add))
            dve.wait_ge(s.rooted, 4)
            done(dve.tensor_scalar(u.a[:], u.a[:], 1e-3, None, ALU.max))
            done(dve.tensor_scalar(u.c[:], u.c[:], EPS, None, ALU.add))
            done(dve.reciprocal(u.c[:], u.c[:]))
            done(dve.tensor_tensor(u.a[:], u.a[:], u.c[:], ALU.mult))
            done(dve.tensor_copy(dst[:, :, 0], u.t0[:]))
            done(dve.tensor_tensor(dst[:], dst[:], u.a[:].unsqueeze(2).to_broadcast([P, NT, D]), ALU.mult))

        @block.scalar
        def _(act):
            act.wait_ge(s.step, 4)
            act.activation(u.y0[:], u.y0[:], ACT.Sqrt).then_inc(s.rooted, 1)
            act.wait_ge(s.step, 11)
            act.activation(u.c[:], u.c[:], ACT.Sqrt).then_inc(s.rooted, 1)
            act.activation(u.a[:], u.a[:], ACT.Sqrt).then_inc(s.rooted, 1)
            act.wait_ge(s.step, 12)
            act.activation(u.a[:], u.a[:], ACT.Ln).then_inc(s.rooted, 1)


def project_and_add(nc, g, o):
    EPS = 1e-6
    with (
        buffers(nc, sq=((P, NT, D), F32), n2=((P, NT), F32)) as u,
        stage_semaphores(nc, "step", "rooted") as s,
        nc.Block() as block,
    ):
        @block.vector
        def _(dve):
            dve.tensor_scalar(o[:, :, 1:D], o[:, :, 1:D], -8.0, 8.0, ALU.max, ALU.min).then_inc(s.step, 1)
            dve.wait_ge(s.step, 1)
            dve.tensor_tensor(u.sq[:, :, 1:D], o[:, :, 1:D], o[:, :, 1:D], ALU.mult).then_inc(s.step, 1)
            dve.wait_ge(s.step, 2)
            dve.tensor_reduce(u.n2[:], u.sq[:, :, 1:D], AX.X, ALU.add).then_inc(s.step, 1)
            dve.wait_ge(s.step, 3)
            dve.tensor_scalar(u.n2[:], u.n2[:], 1.0, EPS, ALU.add, ALU.add).then_inc(s.step, 1)
            dve.wait_ge(s.rooted, 1)
            dve.tensor_tensor(g.x[:], g.x[:], o[:], ALU.add).then_inc(s.step, 1)

        @block.scalar
        def _(act):
            act.wait_ge(s.step, 4)
            act.activation(o[:, :, 0], u.n2[:], ACT.Sqrt).then_inc(s.rooted, 1)


H16, DH8, G4 = 16, 8, 4
HG = H16 // G4
HW = P // HG
PARTS = 3
STACK = PARTS * PARTS * DH8
MAX_AT = 96
MAX_END = MAX_AT + PARTS * HG


def split_projections(nc, g, w, q_src, kv_src, scale, SK, bq, bk, metric):
    shapes = dict(q=((P, S), F32), k=((P, SK), F32), q_left=((P, S), F32), k_left=((P, SK), F32),
                  q_parts=((P, PARTS, S), BF16), k_parts=((P, PARTS, SK), BF16))
    if metric is not None:
        shapes.update(metric_src=((P, S), F32), hidden=((P, 2, S), F32), gx=((P, S), F32))
    Q, K, HID, GX = 0, 1, 2, 4
    with (
        buffers(nc, **shapes) as u,
        nc.Fori(0, B) as b,
        stage_semaphores(nc, "q_mm", "k_mm", "q_out", "q_ready", "k_ready", "k_first", "k_rest", "k_second", "k_done",
                         "q_first", "q_rest", "q_second", "q_done", "metric_in", "hidden_mm", "hidden_done", "gx_mm",
                         "gx_tanh", "chain", "written") as s,
        nc.Block() as block,
    ):
        @block.tensor
        def _(pe):
            pe.matmul(g.psum[:, K, 0:SK], w.wk[:], kv_src[:, bass.ds(b * SK, SK)], start=True,
                      stop=True).then_inc(s.k_mm, 1)
            if metric is not None:
                pe.wait_ge(s.metric_in, 1)
                for c in range(2):
                    pe.matmul(g.psum[:, HID + c, :], metric.w1[:, c, :], u.metric_src[:], start=True,
                              stop=True).then_inc(s.hidden_mm, 1)
            pe.matmul(g.psum[:, Q, :], w.wq[:], q_src[:, bass.ds(b * S, S)], start=True, stop=True).then_inc(s.q_mm, 1)
            if metric is not None:
                for c in range(2):
                    pe.wait_ge(s.hidden_done, c + 1)
                    last = pe.matmul(g.psum[:, GX, :], metric.w2[:, c, :], u.hidden[:, c, :], start=c == 0, stop=c == 1)
                last.then_inc(s.gx_mm, 1)

        @block.scalar
        def _(act):
            act.wait_ge(s.k_mm, 1)
            act.activation(u.k[:], g.psum[:, K, 0:SK], ACT.Identity, bias=bk[:, 0:1] if bk is not None else 0.0
                           ).then_inc(s.k_ready, 1)
            act.wait_ge(s.k_ready, 1)
            act.activation(u.k_parts[:, 0, :], u.k[:], ACT.Copy).then_inc(s.k_first, 1)
            if metric is not None:
                for c in range(2):
                    act.wait_ge(s.hidden_mm, c + 1)
                    act.activation(u.hidden[:, c, :], g.psum[:, HID + c, :], ACT.Tanh,
                                   bias=metric.b1[:, c:c + 1]).then_inc(s.hidden_done, 1)
            act.wait_ge(s.q_mm, 1)
            act.activation(u.q[:], g.psum[:, Q, :], ACT.Identity, bias=bq[:, 0:1] if bq is not None else 0.0,
                           scale=scale).then_inc(s.q_out, 1)
            if metric is not None:
                act.wait_ge(s.gx_mm, 1)
                act.activation(u.gx[:], g.psum[:, GX, :], ACT.Tanh, bias=metric.b2[:, 0:1]).then_inc(s.gx_tanh, 1)
                act.wait_ge(s.q_ready, 1)
            else:
                act.wait_ge(s.q_out, 1)
            act.activation(u.q_parts[:, 0, :], u.q[:], ACT.Copy).then_inc(s.q_first, 1)
            act.wait_ge(s.k_rest, 1)
            act.activation(u.k_parts[:, 1, :], u.k_left[:], ACT.Copy).then_inc(s.k_second, 1)
            act.wait_ge(s.q_rest, 1)
            act.activation(u.q_parts[:, 1, :], u.q_left[:], ACT.Copy).then_inc(s.q_second, 1)

        @block.vector
        def _(dve):
            if metric is not None:
                dve.tensor_scalar(u.metric_src[:], g.xnT[:, bass.ds(b * S, S)], g.minus_e0[:, 0:1], None,
                                  ALU.add).then_inc(s.metric_in, 1)
            dve.wait_ge(s.k_first, 1)
            dve.tensor_tensor(u.k_left[:], u.k[:], u.k_parts[:, 0, :], ALU.subtract).then_inc(s.k_rest, 1)
            if metric is not None:
                dve.wait_ge(s.gx_tanh, 1)
                dve.tensor_scalar(u.gx[:], u.gx[:], 0.1, g.eta[:, 0:1], ALU.mult, ALU.add).then_inc(s.chain, 1)
                dve.wait_ge(s.chain, 1)
                dve.scalar_tensor_tensor(out=u.gx[:], in0=u.gx[:], scalar=-1.0, in1=u.gx[:], op0=ALU.mult,
                                         op1=ALU.max).then_inc(s.chain, 1)
                dve.wait_ge(s.chain, 2)
                dve.wait_ge(s.q_out, 1)
                dve.scalar_tensor_tensor(out=u.q[:], in0=u.gx[:], scalar=g.eta[:, 0:1], in1=u.q[:], op0=ALU.mult,
                                         op1=ALU.mult).then_inc(s.q_ready, 1)
            dve.wait_ge(s.q_first, 1)
            dve.tensor_tensor(u.q_left[:], u.q[:], u.q_parts[:, 0, :], ALU.subtract).then_inc(s.q_rest, 1)
            dve.wait_ge(s.k_second, 1)
            dve.tensor_tensor(u.k_parts[:, 2, :], u.k_left[:], u.k_parts[:, 1, :], ALU.subtract).then_inc(s.k_done, 1)
            dve.wait_ge(s.q_second, 1)
            dve.tensor_tensor(u.q_parts[:, 2, :], u.q_left[:], u.q_parts[:, 1, :], ALU.subtract).then_inc(s.q_done, 1)

        @block.sync
        def _(sp):
            sp.wait_ge(s.k_done, 1)
            sp.dma_start(g.k_parts[bass.ds(b, 1), :, :, 0:SK].rearrange("o c p s -> (o p) c s"),
                         u.k_parts[:]).then_inc(s.written, 16)
            sp.wait_ge(s.q_done, 1)
            sp.dma_start(g.q_parts[bass.ds(b, 1)].rearrange("o c p s -> (o p) c s"), u.q_parts[:]).then_inc(s.written, 16)
            sp.wait_ge(s.written, 32)


def prepare_stacks(nc, g, u):
    with stage_semaphores(nc, "zeroed", "selected", "filled") as s, nc.Block() as block:
        @block.gpsimd
        def _(pool):
            pool.memset(u.ks[64:96], 0.0).then_inc(s.filled, 1)
            pool.wait_ge(s.filled, 1)

        @block.vector
        def _(dve):
            dve.memset(u.qs[64:96], 0.0).then_inc(s.zeroed, 1)
            dve.memset(u.mp[:], 0.0).then_inc(s.zeroed, 1)
            dve.memset(u.v[:], 0.0).then_inc(s.zeroed, 1)
            dve.tensor_reduce(u.sel[MAX_AT:MAX_END], g.ident[MAX_AT:MAX_END, MAX_AT:MAX_END].rearrange(
                "p (a j) -> p j a", j=HG), AX.X, ALU.add).then_inc(s.selected, 1)
            dve.wait_ge(s.zeroed, 3)
            dve.memset(u.v[:, :, :, DH8:DH8 + 1].rearrange("p k h c -> p (k h) c"), 1.0).then_inc(s.zeroed, 1)
            dve.wait_ge(s.zeroed, 4)

        @block.scalar
        def _(act):
            act.wait_ge(s.selected, 1)
            SK = u.ks.shape[2]
            for gi in range(G4):
                act.activation(u.ks[MAX_AT:MAX_END, gi * HG:(gi + 1) * HG, :],
                               u.sel[MAX_AT:MAX_END].unsqueeze(2).to_broadcast([PARTS * HG, HG, SK]),
                               ACT.Copy).then_inc(s.selected, 1)
            act.wait_ge(s.selected, 1 + G4)


def narrow_attention(nc, g, *, w, keys, kv_src, scale, q_src=None, mask=None, metric=None, add_to=None, store=None,
                     out_scale=1.0, zero_if_all_masked=False, bq=None, bk=None, bv=None, bo=None):
    KT = len(keys)
    SK = keys[-1][0] + keys[-1][1]
    PER = QT // KT
    PERG = KT * HG
    NBLK = G4 * PERG
    RING = 2 * HG
    STACK_DMAS = 2 * PARTS * PARTS
    q_src = q_src if q_src is not None else g.xnT
    split_projections(nc, g, w, q_src, kv_src, scale, SK, bq, bk, metric)

    shapes = dict(qs=((P, H16, S), BF16), ks=((P, H16, SK), BF16), srck=((P, SK), F32), v=((P, KT, H16, HW), F32),
                  probs=((P, RING, S), F32), nmax=((P, G4, QT, HG), F32), left=((P, QT, HG), F32),
                  mp=((P, QT, MAX_END), BF16), sel=((P, HG), F32), outs=((P, 2, S), F32), rinv=((P, 2, QT, HG), F32),
                  o=((P, QT, D), F32), oT=((P, QT * P), F32))
    if mask is not None:
        shapes.update(mask_add=((P, QT, SK), BF16), mask_addT=((P, KT, S), BF16), live=((P, QT, HG), F32))
    SCORES, LOGITS, OUT, MAXT, MISC = 0, 2, 4, 6, 7
    with buffers(nc, **shapes) as u:
        prepare_stacks(nc, g, u)
        with (
            nc.Fori(0, B) as b,
            stage_semaphores(nc, "stack0", "stack1", "stack2", "stack3", "src_done", "v_mm", "v_done", "mask_done",
                             "scores_done", "max_done", "split", "parts_done", "maxima_turned", "maxima_done",
                             "logits_done", "probs_done", "heads_done", "outputs_copied", "outputs_turned", "chain",
                             "normalised", "o_turned", "oT_done", "projected", "stored") as s,
            nc.Block() as block,
        ):
            stacks = [s.stack0, s.stack1, s.stack2, s.stack3]

            @block.sync
            def _(sp):
                for gi in range(G4):
                    rows = slice(gi * HG * DH8, (gi + 1) * HG * DH8)
                    hs = slice(gi * HG, (gi + 1) * HG)
                    for a in range(PARTS):
                        for c in range(PARTS):
                            at = (a * PARTS + c) * DH8
                            for stack, parts, part, N in ((u.qs, g.q_parts, a, S), (u.ks, g.k_parts, c, SK)):
                                sp.dma_start(stack[at:at + DH8, hs, :], parts[bass.ds(b, 1), part, rows, 0:N].rearrange(
                                    "o (h d) s -> (o d) h s", d=DH8)).then_inc(stacks[gi], 16)

            @block.tensor
            def _(pe):
                def values():
                    pe.wait_ge(s.src_done, 1)
                    for t, (at, rows) in enumerate(keys):
                        out = g.psum[0:rows, MISC, t * P:(t + 1) * P]
                        last = pe.matmul(out, u.srck[:, at:at + rows], w.wv[:], start=True, stop=bv is None)
                        if bv is not None:
                            last = pe.matmul(out, g.ones[0:1, 0:rows], bv[0:1, :], start=False, stop=True)
                    last.then_inc(s.v_mm, 1)

                def scores(n):
                    gi, kt, j = n // PERG, n // HG % KT, n % HG
                    if n % PERG == 0:
                        pe.wait_ge(stacks[gi], 16 * STACK_DMAS)
                    if n >= 2:
                        pe.wait_ge(s.max_done, n - 1)
                    for i in range(PER):
                        q = kt * PER + i
                        out = g.psum[:, SCORES + n % 2, i * SK:(i + 1) * SK]
                        last = pe.matmul(out, u.qs[0:STACK, gi * HG + j, q * P:(q + 1) * P],
                                         u.ks[0:STACK, gi * HG + j, :], start=True, stop=mask is None)
                        if mask is not None:
                            last = pe.matmul(out, g.ident_bf[:], u.mask_add[:, q, :], start=False, stop=True)
                    last.then_inc(s.scores_done, 1)

                def turn_maxima(gi):
                    pe.wait_ge(s.parts_done, gi + 1)
                    if gi >= 1:
                        pe.wait_ge(s.maxima_done, gi)
                    for q in range(QT):
                        last = pe.matmul(g.psum[0:MAX_END, MAXT, q * P:(q + 1) * P], u.mp[:, q, :], g.ident_bf[:],
                                         start=True, stop=True)
                    last.then_inc(s.maxima_turned, 1)

                def logits(n):
                    gi, kt, j = n // PERG, n // HG % KT, n % HG
                    at, rows = keys[kt]
                    if n % PERG == 0:
                        pe.wait_ge(s.maxima_done, gi + 1)
                    if n >= 2:
                        pe.wait_ge(s.probs_done, n - 1)
                    out = g.psum[0:rows, LOGITS + n % 2, :]
                    last = pe.matmul(out, u.ks[0:MAX_END, gi * HG + j, at:at + rows], u.qs[0:MAX_END, gi * HG + j, :],
                                     start=True, stop=mask is None)
                    if mask is not None:
                        last = pe.matmul(out, g.ident_bf[0:rows, 0:rows], u.mask_addT[0:rows, kt, :],
                                         start=False, stop=True)
                    last.then_inc(s.logits_done, 1)

                def heads(m):
                    gi, kt = m // KT, m % KT
                    rows = keys[kt][1]
                    pe.wait_ge(s.probs_done, HG * (m + 1))
                    if m == 0:
                        pe.wait_ge(s.v_done, 1)
                    if kt == 0 and gi >= 2:
                        pe.wait_ge(s.outputs_copied, gi - 1)
                    for j in range(HG):
                        last = pe.matmul(g.psum[j * HW:(j + 1) * HW, OUT + gi % 2, :], u.v[0:rows, kt, gi * HG + j, :],
                                         u.probs[0:rows, (m * HG + j) % RING, :], start=kt == 0, stop=kt == KT - 1,
                                         tile_position=(0, j * HW))
                    last.then_inc(s.heads_done, 1)

                def turn_outputs(gi):
                    pe.wait_ge(s.outputs_copied, gi + 1)
                    if gi == 0:
                        pe.wait_ge(s.v_done, 1)
                    else:
                        pe.wait_ge(s.normalised, gi)
                    for q in range(QT):
                        last = pe.transpose(g.psum[:, MISC, q * P:(q + 1) * P], u.outs[:, gi % 2, q * P:(q + 1) * P],
                                            g.ident[:])
                    last.then_inc(s.outputs_turned, 1)

                values()
                if mask is not None:
                    pe.wait_ge(s.mask_done, 1 + KT)
                for n in range(PERG):
                    scores(n)
                turn_maxima(0)
                for n in range(NBLK):
                    gi, m = n // PERG, n // HG
                    logits(n)
                    if n + PERG < NBLK:
                        scores(n + PERG)
                    if n % HG == HG - 1:
                        if m >= 1:
                            heads(m - 1)
                        if m % KT == KT - 1 and gi + 1 < G4:
                            turn_maxima(gi + 1)
                        if m >= KT + 1 and (m - 1) % KT == 0:
                            turn_outputs((m - 1) // KT - 1)
                heads(NBLK // HG - 1)
                turn_outputs(G4 - 1)
                pe.wait_ge(s.normalised, G4)
                pe.wait_ge(s.maxima_done, G4)
                for q in range(QT):
                    last = pe.transpose(g.psum[:, MAXT, q * P:(q + 1) * P], u.o[:, q, :], g.ident[:])
                last.then_inc(s.o_turned, 1)
                pe.wait_ge(s.oT_done, 1)
                for q in range(QT):
                    out = g.psum[:, MISC, q * P:(q + 1) * P]
                    last = pe.matmul(out, u.oT[:, q * P:(q + 1) * P], w.wo[:], start=True, stop=bo is None)
                    if bo is not None:
                        last = pe.matmul(out, g.ones[0:1, :], bo[0:1, :], start=False, stop=True)
                last.then_inc(s.projected, 1)

            @block.vector
            def _(dve):
                def maximum(n):
                    gi, kt, j = n // PERG, n // HG % KT, n % HG
                    dve.wait_ge(s.scores_done, n + 1)
                    dve.tensor_reduce(u.nmax[:, gi, kt * PER:(kt + 1) * PER, j],
                                      g.psum[:, SCORES + n % 2, 0:PER * SK].rearrange("p (i k) -> p i k", k=SK), AX.X,
                                      ALU.max, negate=True).then_inc(s.max_done, 1)

                def split_maxima(gi):
                    part = [u.mp[:, :, MAX_AT + a * HG:MAX_AT + (a + 1) * HG] for a in range(PARTS)]
                    dve.wait_ge(s.max_done, PERG * (gi + 1))
                    if gi >= 1:
                        dve.wait_ge(s.maxima_turned, gi)
                    dve.tensor_copy(part[0], u.nmax[:, gi]).then_inc(s.split, 1)
                    dve.wait_ge(s.split, 3 * gi + 1)
                    dve.tensor_tensor(u.left[:], u.nmax[:, gi], part[0], ALU.subtract).then_inc(s.split, 1)
                    dve.wait_ge(s.split, 3 * gi + 2)
                    dve.tensor_copy(part[1], u.left[:]).then_inc(s.split, 1)
                    dve.wait_ge(s.split, 3 * gi + 3)
                    dve.tensor_tensor(part[2], u.left[:], part[1], ALU.subtract).then_inc(s.parts_done, 1)

                def normalise(gi):
                    turned = g.psum[:, MISC, :].rearrange("p (q j r) -> p q j r", q=QT, r=HW)
                    rinv = u.rinv[:, gi % 2]
                    steps = 3 if zero_if_all_masked else 1
                    dve.wait_ge(s.outputs_turned, gi + 1)
                    dve.reciprocal(rinv, turned[:, :, :, DH8]).then_inc(s.chain, 1)
                    if zero_if_all_masked:
                        dve.tensor_scalar(u.live[:], u.nmax[:, gi], -MASKED / 2, None, ALU.is_lt).then_inc(s.chain, 1)
                        dve.wait_ge(s.chain, steps * gi + 2)
                        dve.tensor_tensor(rinv, rinv, u.live[:], ALU.mult).then_inc(s.chain, 1)
                    dve.wait_ge(s.chain, steps * (gi + 1))
                    for q in range(QT):
                        ins = dve.tensor_tensor(
                            u.o[:, q, gi * HG * DH8:(gi + 1) * HG * DH8].rearrange("p (j r) -> p j r", r=DH8),
                            turned[:, q, :, 0:DH8], rinv[:, q].unsqueeze(2).to_broadcast([P, HG, DH8]), ALU.mult)
                    ins.then_inc(s.normalised, 1)

                dve.tensor_copy(u.srck[:], kv_src[:, bass.ds(b * SK, SK)]).then_inc(s.src_done, 1)
                if mask is not None:
                    kind, m, mT = mask
                    op = (MASKED, None, ALU.mult) if kind == "drop" else (-1.0, -MASKED, ALU.add, ALU.mult)
                    per_batch = kind == "drop"
                    dve.tensor_scalar(u.mask_add[:], m[:, bass.ds(b * QT, QT), :] if per_batch else m[:],
                                      *op).then_inc(s.mask_done, 1)
                    for t, (_, rows) in enumerate(keys):
                        src = mT[0:rows, bass.ds(b * KT + t, 1), :] if per_batch else mT[0:rows, t:t + 1, :]
                        dve.tensor_scalar(u.mask_addT[0:rows, t:t + 1, :], src, *op).then_inc(s.mask_done, 1)
                for n in range(PERG):
                    maximum(n)
                split_maxima(0)
                for n in range(NBLK):
                    gi, m = n // PERG, n // HG
                    if n + PERG < NBLK:
                        maximum(n + PERG)
                    if n % HG == HG - 1:
                        if m % KT == KT - 1 and gi + 1 < G4:
                            split_maxima(gi + 1)
                        if m >= KT + 1 and (m - 1) % KT == 0:
                            normalise((m - 1) // KT - 1)
                normalise(G4 - 1)
                dve.wait_ge(s.projected, 1)
                result = g.psum[:, MISC, :].rearrange("p (q d) -> p q d", d=D)
                if add_to is not None:
                    at = add_to[:, bass.ds(b * QT, QT), :]
                    dve.tensor_tensor(at, result, at, ALU.add).then_inc(s.stored, 1)
                else:
                    dve.tensor_scalar(store[:, bass.ds(b * QT, QT), :], result, out_scale, None,
                                      ALU.mult).then_inc(s.stored, 1)

            @block.scalar
            def _(act):
                def copy_maxima(gi):
                    act.wait_ge(s.maxima_turned, gi + 1)
                    act.activation(u.qs[MAX_AT:MAX_END, gi * HG:(gi + 1) * HG, :],
                                   g.psum[MAX_AT:MAX_END, MAXT, :].unsqueeze(1).to_broadcast([PARTS * HG, HG, S]),
                                   ACT.Copy).then_inc(s.maxima_done, 1)

                def exponentials(n):
                    rows = keys[n // HG % KT][1]
                    act.wait_ge(s.logits_done, n + 1)
                    if n >= RING:
                        act.wait_ge(s.heads_done, (n - RING) // HG + 1)
                    act.activation(u.probs[0:rows, n % RING, :], g.psum[0:rows, LOGITS + n % 2, :],
                                   ACT.Exp).then_inc(s.probs_done, 1)

                def copy_outputs(gi):
                    act.wait_ge(s.heads_done, KT * (gi + 1))
                    if gi >= 2:
                        act.wait_ge(s.outputs_turned, gi - 1)
                    act.activation(u.outs[:, gi % 2, :], g.psum[:, OUT + gi % 2, :],
                                   ACT.Copy).then_inc(s.outputs_copied, 1)

                act.wait_ge(s.v_mm, 1)
                for t, (_, rows) in enumerate(keys):
                    ins = act.activation(u.v[0:rows, t, :, 0:DH8],
                                         g.psum[0:rows, MISC, t * P:(t + 1) * P].rearrange("p (h d) -> p h d", d=DH8),
                                         ACT.Copy)
                ins.then_inc(s.v_done, 1)
                copy_maxima(0)
                for n in range(NBLK):
                    gi, m = n // PERG, n // HG
                    exponentials(n)
                    if n % HG == HG - 1:
                        if m % KT == KT - 1 and gi + 1 < G4:
                            copy_maxima(gi + 1)
                        if m >= KT and m % KT == 0:
                            copy_outputs(m // KT - 1)
                copy_outputs(G4 - 1)
                act.wait_ge(s.o_turned, 1)
                act.activation(u.oT[:], g.psum[:, MAXT, :], ACT.Copy).then_inc(s.oT_done, 1)


def row(ap):
    return ap.rearrange("(a n) -> a n", a=1)


def column(ap):
    return ap.rearrange("(n a) -> n a", a=1)


def layer0_attention(nc, g, a):
    layernorm(nc, g)
    with (
        buffers(nc, wq=((P, P), F32), wk=((P, P), F32), wv=((P, D), F32), wo=((P, D), F32),
                w1=((P, 2, P), F32), w2=((P, 2, P), F32), b1=((P, 2), F32), b2=((P, 1), F32),
                vmap=((P, NT, D), F32), vT=((P, NT * P), F32)) as u,
    ):
        load(nc, [(u.wv[:], a["L0_attn_WvT"]), (u.wo[:], a["L0_attn_WoT"]),
                  (u.wq[:], a["L0_attn_WqT"]), (u.wk[:], a["L0_attn_WkT"]),
                  (u.w1[:], a["L0_attn_W1T"].rearrange("k (c m) -> k c m", c=2)),
                  (u.b1[:], a["L0_attn_b1"].rearrange("(c p) -> p c", c=2)),
                  (u.w2[:], a["L0_attn_W2T"].rearrange("(c p) m -> p c m", c=2)), (u.b2[:], column(a["L0_attn_b2"]))])
        log_map(nc, g, u.vmap)
        turn_to_features(nc, g, u.vmap, u.vT)
        narrow_attention(nc, g, w=u, keys=ALL_KEYS, kv_src=u.vT, q_src=u.vT, scale=DH8 ** -0.5,
                         metric=named(w1=u.w1, w2=u.w2, b1=u.b1, b2=u.b2), store=u.vmap, out_scale=0.1)
        project_and_add(nc, g, u.vmap)


def layer1_cross(nc, g, a):
    layernorm(nc, g)
    keys = ctx_tiles()
    KT = len(keys)
    with buffers(nc, wq=((P, P), F32), wk=((P, P), F32), wv=((P, D), F32), wo=((P, D), F32),
                 mask=((P, NT, SC), U8), maskT=((P, B * KT, S), U8)) as u:
        maskT = u.maskT[:].rearrange("p (b t) s -> p b t s", t=KT)
        load(nc, [(u.wv[:], a["L1_xattn_W_VT"]), (u.wo[:], a["L1_xattn_W_OT"]), (u.wq[:], a["L1_xattn_W_QT"]),
                  (u.wk[:], a["L1_xattn_W_KT"]),
                  (u.mask[:], a["mask_BxSxS2_bf0"].rearrange("b (t p) k -> p (b t) k", p=P))]
             + [(maskT[0:rows, :, t, :], a["mask_BxSxS2_bf0T"][:, at:at + rows, :].rearrange("b k s -> k b s"))
                for t, (at, rows) in enumerate(keys)])
        narrow_attention(nc, g, w=u, keys=keys, kv_src=g.ctxT, scale=DH8 ** -0.5,
                         mask=("drop", u.mask, u.maskT), zero_if_all_masked=True, add_to=g.x)


def layer3_attention(nc, g, a):
    layernorm(nc, g)
    with buffers(nc, wq=((P, P), F32), wk=((P, P), F32), wv=((P, D), F32), wo=((P, D), F32),
                 bq=((P, 1), F32), bqs=((P, 1), F32), bk=((P, 1), F32), bv=((1, D), F32), bo=((1, D), F32)) as u:
        load(nc, [(u.wv[:], a["L3_attn_WvT"]), (u.wo[:], a["L3_attn_WoT"]), (u.bv[:], row(a["L3_attn_bv"])),
                  (u.bo[:], row(a["L3_attn_bo"])), (u.wq[:], a["L3_attn_WqT"]), (u.wk[:], a["L3_attn_WkT"]),
                  (u.bq[:], column(a["L3_attn_bq"])), (u.bk[:], column(a["L3_attn_bk"]))])
        scale_bias(nc, u.bqs, u.bq, DH8 ** -0.5)
        narrow_attention(nc, g, w=u, keys=ALL_KEYS, kv_src=g.xnT, scale=DH8 ** -0.5, add_to=g.x,
                         bq=u.bqs, bk=u.bk, bv=u.bv, bo=u.bo)


def layer3_cross(nc, g, a):
    layernorm(nc, g)
    keys = ctx_tiles()
    with buffers(nc, wq=((P, P), F32), wk=((P, P), F32), wv=((P, D), F32), wo=((P, D), F32),
                 mask=((P, QT, SC), U8), maskT=((P, len(keys), S), U8), bq=((P, 1), F32), bqs=((P, 1), F32),
                 bk=((P, 1), F32), bv=((1, D), F32), bo=((1, D), F32)) as u:
        load(nc, [(u.wv[:], a["L3_xattn_Wv"]), (u.wo[:], a["L3_xattn_Wo"]), (u.bv[:], row(a["L3_xattn_bv"])),
                  (u.bo[:], row(a["L3_xattn_bo"])), (u.wq[:], a["L3_xattn_Wq"]), (u.wk[:], a["L3_xattn_Wk"]),
                  (u.bq[:], column(a["L3_xattn_bq"])), (u.bk[:], column(a["L3_xattn_bk"])),
                  (u.mask[:], a["mask_SxS2_bk1"].rearrange("(t p) k -> p t k", p=P))]
             + [(u.maskT[0:rows, t, :], a["mask_SxS2_bk1T"][at:at + rows, :]) for t, (at, rows) in enumerate(keys)])
        scale_bias(nc, u.bqs, u.bq, DH8 ** -0.5)
        narrow_attention(nc, g, w=u, keys=keys, kv_src=g.ctxT, scale=DH8 ** -0.5,
                         mask=("keep", u.mask, u.maskT), add_to=g.x, bq=u.bqs, bk=u.bk, bv=u.bv, bo=u.bo)


def layer2_attention(nc, g, a):
    DQ = 64
    layernorm(nc, g)
    with buffers(nc, wq=((P, 8, P), F32), wk=((P, 8, P), F32), wv=((P, H16 * DQ), F32), wo=((P, 8, D), F32)) as u:
        load(nc, [(u.wq[:], a["L2_attn_QT"].rearrange("k (g m) -> k g m", g=8)),
                  (u.wk[:], a["L2_attn_KT"].rearrange("k (g m) -> k g m", g=8)),
                  (u.wv[:], a["L2_attn_VT"]), (u.wo[:], a["L2_attn_WT"].rearrange("(c p) d -> p c d", p=P))])
        root = (DQ / D) ** 0.5
        attention(nc, g, w=u, H=H16, dh=DQ, hp=DQ, keys=ALL_KEYS, kv_src=g.xnT, scale=root * root / DQ, causal=True,
                  add_to=g.x, out_scale=root * (D / DQ) ** 0.5 / H16)


def scale_bias(nc, dst, src, by):
    with stage_semaphores(nc, "scaled") as s, nc.Block() as block:
        @block.vector
        def _(dve):
            dve.tensor_scalar(dst[:], src[:], by, None, ALU.mult).then_inc(s.scaled, 1)
            dve.wait_ge(s.scaled, 1)


def slots_from_context(nc, g, a):
    ROUNDS, EPS = 3, 1e-6
    BEFORE = ["h_in", "ctx_in", "ctx_sq", "ctx_mean", "ctx_eps", "ctx_root", "ctx_inv", "ctx_normed", "kv_mm",
              "k_out", "v0_out", "v1_out"]
    ROUND = ["sq", "mean", "eps", "root", "inv", "normed", "q_mm", "q_out", "scores", "max0", "max1", "exp0", "exp1",
             "sinv0", "sinv1", "norm0", "norm1", "update_mm", "total_eps", "total_inv", "update", "gates_mm", "r", "z",
             "rh", "nx", "n", "h_n", "zh_n", "h"]
    layernorm(nc, g)
    with buffers(nc, wq=((P, D), F32), wk=((P, D), F32), wv=((P, D), F32), wih=((P, 3 * D), F32), whh=((P, 3 * D), F32),
                 bih=((P, 3), F32), bhh=((P, 3), F32), bsum=((P, 3), F32), w_slot=((P, 1), F32), w_in=((P, 1), F32),
                 h=((P, S), F32), cT=((P, SC), F32), sq=((P, S), F32), inv=((P, S), F32), sn=((P, S), F32),
                 pn=((P, SC), F32), kT=((P, SC), F32), v=((P, 2, D), F32), qT=((P, S), F32), nmax=((P, 2), F32),
                 sums=((P, 2), F32), at=((P, 2, S), F32), up=((P, S), F32), r=((P, S), F32), z=((P, S), F32),
                 n=((P, S), F32), d=((P, S), F32), mean=((P, P), F32)) as u:
        load(nc, [(u.wq[:], a["L0_xattn_WqT"]), (u.wk[:], a["L0_xattn_WkT"]), (u.wv[:], a["L0_xattn_WvT"]),
                  (u.wih[:], a["L0_xattn_gru_wihT"]), (u.whh[:], a["L0_xattn_gru_whhT"]),
                  (u.bih[:], a["L0_xattn_gru_bih"].rearrange("(c p) -> p c", p=P)),
                  (u.bhh[:], a["L0_xattn_gru_bhh"].rearrange("(c p) -> p c", p=P)),
                  (u.w_slot[:], a["L0_xattn_slot_norm_w"].rearrange("(p a) -> p a", a=1)),
                  (u.w_in[:], a["L0_xattn_input_norm_w"].rearrange("(p a) -> p a", a=1))])
        with stage_semaphores(nc, "set_up") as s, nc.Block() as block:
            @block.vector
            def _(dve):
                dve.memset(u.mean[:], 1.0 / D).then_inc(s.set_up, 1)
                dve.tensor_tensor(u.bsum[:], u.bih[:], u.bhh[:], ALU.add).then_inc(s.set_up, 1)
                dve.wait_ge(s.set_up, 2)
        keys = ctx_tiles()
        PS = g.psum
        with (
            nc.Fori(0, B) as b,
            stage_semaphores(nc, "step", "turned", "added") as s,
        ):
            def after(name, i=None):
                return BEFORE.index(name) + 1 if i is None else len(BEFORE) + i * len(ROUND) + ROUND.index(name) + 1

            with nc.Block() as block:
                @block.vector
                def _(dve):
                    def step(ins, name, i=None):
                        ins.then_inc(s.step, 1)
                        dve.wait_ge(s.step, after(name, i))

                    step(dve.tensor_copy(u.h[:], g.xnT[:, bass.ds(b * S, S)]), "h_in")
                    step(dve.tensor_copy(u.cT[:], g.ctxT[:, bass.ds(b * SC, SC)]), "ctx_in")
                    step(dve.tensor_tensor(u.sq[:, 0:SC], u.cT[:], u.cT[:], ALU.mult), "ctx_sq")
                    dve.wait_ge(s.step, after("ctx_mean"))
                    step(dve.tensor_scalar(u.inv[:, 0:SC], PS[:, 0, 0:SC], EPS, None, ALU.add), "ctx_eps")
                    dve.wait_ge(s.step, after("ctx_root"))
                    step(dve.reciprocal(u.inv[:, 0:SC], u.inv[:, 0:SC]), "ctx_inv")
                    step(dve.scalar_tensor_tensor(out=u.pn[:], in0=u.cT[:], scalar=u.w_in[:, 0:1], in1=u.inv[:, 0:SC],
                                                  op0=ALU.mult, op1=ALU.mult), "ctx_normed")
                    dve.wait_ge(s.step, after("v1_out"))
                    for i in range(ROUNDS):
                        step(dve.tensor_tensor(u.sq[:], u.h[:], u.h[:], ALU.mult), "sq", i)
                        dve.wait_ge(s.step, after("mean", i))
                        step(dve.tensor_scalar(u.inv[:], PS[:, 0, :], EPS, None, ALU.add), "eps", i)
                        dve.wait_ge(s.step, after("root", i))
                        step(dve.reciprocal(u.inv[:], u.inv[:]), "inv", i)
                        step(dve.scalar_tensor_tensor(out=u.sn[:], in0=u.h[:], scalar=u.w_slot[:, 0:1], in1=u.inv[:],
                                                      op0=ALU.mult, op1=ALU.mult), "normed", i)
                        dve.wait_ge(s.step, after("scores", i))
                        for t, (_, rows) in enumerate(keys):
                            step(dve.tensor_reduce(u.nmax[0:rows, t:t + 1], PS[0:rows, 2 + t, :], AX.X, ALU.max,
                                                   negate=True), f"max{t}", i)
                        dve.wait_ge(s.step, after("exp1", i))
                        for t, (_, rows) in enumerate(keys):
                            step(dve.reciprocal(u.sums[0:rows, t:t + 1], u.sums[0:rows, t:t + 1]), f"sinv{t}", i)
                        for t, (_, rows) in enumerate(keys):
                            step(dve.tensor_scalar(u.at[0:rows, t, :], u.at[0:rows, t, :], u.sums[0:rows, t:t + 1],
                                                   None, ALU.mult), f"norm{t}", i)
                        dve.wait_ge(s.step, after("update_mm", i))
                        step(dve.tensor_scalar(u.inv[:], PS[:, 5, :], EPS, None, ALU.add), "total_eps", i)
                        step(dve.reciprocal(u.inv[:], u.inv[:]), "total_inv", i)
                        step(dve.tensor_tensor(u.up[:], PS[:, 4, :], u.inv[:], ALU.mult), "update", i)
                        dve.wait_ge(s.step, after("z", i))
                        step(dve.scalar_tensor_tensor(out=u.d[:], in0=PS[:, 7, :], scalar=u.bhh[:, 2:3], in1=u.r[:],
                                                      op0=ALU.add, op1=ALU.mult), "rh", i)
                        step(dve.tensor_tensor(u.n[:], u.d[:], PS[:, 6, :], ALU.add), "nx", i)
                        dve.wait_ge(s.step, after("n", i))
                        step(dve.tensor_tensor(u.d[:], u.h[:], u.n[:], ALU.subtract), "h_n", i)
                        step(dve.tensor_tensor(u.d[:], u.d[:], u.z[:], ALU.mult), "zh_n", i)
                        step(dve.tensor_tensor(u.h[:], u.n[:], u.d[:], ALU.add), "h", i)
                    dve.wait_ge(s.turned, 1)
                    at = g.x[:, bass.ds(b * QT, QT), :]
                    dve.tensor_tensor(at, at, PS[:, 1, :].rearrange("p (t d) -> p t d", d=D), ALU.add).then_inc(s.added, 1)

                @block.scalar
                def _(act):
                    act.wait_ge(s.step, after("ctx_eps"))
                    act.activation(u.inv[:, 0:SC], u.inv[:, 0:SC], ACT.Sqrt).then_inc(s.step, 1)
                    act.wait_ge(s.step, after("kv_mm"))
                    act.activation(u.kT[:], PS[:, 1, 0:SC], ACT.Copy).then_inc(s.step, 1)
                    for t, (_, rows) in enumerate(keys):
                        act.wait_ge(s.step, after("k_out") + t)
                        act.activation(u.v[0:rows, t, :], PS[0:rows, 2 + t, 0:D], ACT.Copy).then_inc(s.step, 1)
                    for i in range(ROUNDS):
                        act.wait_ge(s.step, after("eps", i))
                        act.activation(u.inv[:], u.inv[:], ACT.Sqrt).then_inc(s.step, 1)
                        act.wait_ge(s.step, after("q_mm", i))
                        act.activation(u.qT[:], PS[:, 1, :], ACT.Copy, scale=D ** -0.5).then_inc(s.step, 1)
                        for t, (_, rows) in enumerate(keys):
                            act.wait_ge(s.step, after("max1", i) + t)
                            act.activation(u.at[0:rows, t, :], PS[0:rows, 2 + t, :], ACT.Exp, bias=u.nmax[0:rows, t:t + 1],
                                           accum_out=u.sums[0:rows, t:t + 1]).then_inc(s.step, 1)
                        act.wait_ge(s.step, after("gates_mm", i))
                        act.activation(u.r[:], PS[:, 2, :], ACT.Sigmoid, bias=u.bsum[:, 0:1]).then_inc(s.step, 1)
                        act.wait_ge(s.step, after("r", i))
                        act.activation(u.z[:], PS[:, 3, :], ACT.Sigmoid, bias=u.bsum[:, 1:2]).then_inc(s.step, 1)
                        act.wait_ge(s.step, after("nx", i))
                        act.activation(u.n[:], u.n[:], ACT.Tanh, bias=u.bih[:, 2:3]).then_inc(s.step, 1)

                @block.tensor
                def _(pe):
                    pe.wait_ge(s.step, after("ctx_sq"))
                    pe.matmul(PS[:, 0, 0:SC], u.mean[:], u.sq[:, 0:SC], start=True, stop=True).then_inc(s.step, 1)
                    pe.wait_ge(s.step, after("ctx_normed"))
                    pe.matmul(PS[:, 1, 0:SC], u.wk[:], u.pn[:], start=True, stop=True)
                    for t, (at, rows) in enumerate(keys):
                        last = pe.matmul(PS[0:rows, 2 + t, 0:D], u.pn[:, at:at + rows], u.wv[:], start=True, stop=True)
                    last.then_inc(s.step, 1)
                    for i in range(ROUNDS):
                        pe.wait_ge(s.step, after("sq", i))
                        pe.matmul(PS[:, 0, :], u.mean[:], u.sq[:], start=True, stop=True).then_inc(s.step, 1)
                        pe.wait_ge(s.step, after("normed", i))
                        pe.matmul(PS[:, 1, :], u.wq[:], u.sn[:], start=True, stop=True).then_inc(s.step, 1)
                        pe.wait_ge(s.step, after("q_out", i))
                        for t, (at, rows) in enumerate(keys):
                            last = pe.matmul(PS[0:rows, 2 + t, :], u.kT[:, at:at + rows], u.qT[:], start=True, stop=True)
                        last.then_inc(s.step, 1)
                        pe.wait_ge(s.step, after("norm1", i))
                        for t, (_, rows) in enumerate(keys):
                            pe.matmul(PS[:, 4, :], u.v[0:rows, t, :], u.at[0:rows, t, :], start=t == 0, stop=t == 1)
                        for t, (_, rows) in enumerate(keys):
                            last = pe.matmul(PS[:, 5, :], g.ones[0:rows, :], u.at[0:rows, t, :], start=t == 0, stop=t == 1)
                        last.then_inc(s.step, 1)
                        pe.wait_ge(s.step, after("update", i))
                        for c in range(2):
                            pe.matmul(PS[:, 2 + c, :], u.wih[:, c * D:(c + 1) * D], u.up[:], start=True, stop=False)
                            pe.matmul(PS[:, 2 + c, :], u.whh[:, c * D:(c + 1) * D], u.h[:], start=False, stop=True)
                        pe.matmul(PS[:, 6, :], u.wih[:, 2 * D:3 * D], u.up[:], start=True, stop=True)
                        pe.matmul(PS[:, 7, :], u.whh[:, 2 * D:3 * D], u.h[:], start=True, stop=True).then_inc(s.step, 1)
                    pe.wait_ge(s.step, after("h", ROUNDS - 1))
                    for j in range(QT):
                        last = pe.transpose(PS[:, 1, j * P:(j + 1) * P], u.h[:, j * P:(j + 1) * P], g.ident[:])
                    last.then_inc(s.turned, 1)


def layer1_attention(nc, g, a):
    H = 4
    PAIRS = H * H
    layernorm(nc, g)
    with buffers(nc, wq=((P, H * D), F32), wk=((P, H * D), F32), wv=((P, H * D), F32), wo=((P, H, D), F32),
                 bq=((P, H), F32), bk=((P, H), F32), bv=((1, H * D), F32), bo=((1, D), F32), phase=((P, H), F32),
                 cos=((P, H), F32), sin=((P, H), F32), turn=((P, H), F32), whole=((P, H), I32), cc=((P, H, H), F32),
                 ss=((P, H, H), F32), pick=((P, PAIRS, PAIRS), F32),
                 src=((P, S), F32), qT=((P, H, S), F32), kT=((P, H, S), F32), v=((P, QT, H * D), F32),
                 prod=((P, 2, S), F32), sT=((PAIRS, S), F32), sc=((P, QT * H, H), F32), mx=((P, QT * H), F32),
                 o=((P, QT, H * D), F32), oT=((P, H, S), F32)) as u:
        load(nc, [(u.wq[:], a["L1_attn_Wq"]), (u.wk[:], a["L1_attn_Wk"]), (u.wv[:], a["L1_attn_Wv"]),
                  (u.wo[:], a["L1_attn_Wo"].rearrange("(c p) n -> p c n", p=P)),
                  (u.bq[:], a["L1_attn_bq"].rearrange("(h p) -> p h", p=P)),
                  (u.bk[:], a["L1_attn_bk"].rearrange("(h p) -> p h", p=P)), (u.bv[:], row(a["L1_attn_bv"])),
                  (u.bo[:], row(a["L1_attn_bo"])), (u.phase[:], a["L1_attn_phaseT"])])
        with stage_semaphores(nc, "step", "sined") as s, nc.Block() as block:
            @block.vector
            def _(dve):
                steps = [0]

                def done(ins):
                    steps[0] += 1
                    ins.then_inc(s.step, 1)
                    dve.wait_ge(s.step, steps[0])

                for n, (dst, shift) in enumerate(((u.sin, 0.0), (u.cos, 0.25))):
                    done(dve.tensor_scalar(u.turn[:], u.phase[:], 1 / (2 * np.pi), shift, ALU.mult, ALU.add))
                    done(dve.tensor_copy(u.whole[:], u.turn[:]))
                    done(dve.tensor_copy(dst[:], u.whole[:]))
                    done(dve.tensor_tensor(dst[:], u.turn[:], dst[:], ALU.subtract))
                    done(dve.tensor_scalar(dst[:], dst[:], 0.5, -0.5, ALU.min, ALU.max))
                done(dve.memset(u.pick[:], 0.0))
                dve.wait_ge(s.sined, 2)
                row_of = [P, H, H]
                done(dve.tensor_tensor(u.cc[:], u.cos[:].unsqueeze(2).to_broadcast(row_of),
                                       u.cos[:].unsqueeze(1).to_broadcast(row_of), ALU.mult))
                done(dve.tensor_tensor(u.ss[:], u.sin[:].unsqueeze(2).to_broadcast(row_of),
                                       u.sin[:].unsqueeze(1).to_broadcast(row_of), ALU.mult))
                done(dve.tensor_tensor(u.cc[:], u.cc[:], u.ss[:], ALU.add))
                done(dve.tensor_scalar(u.pick[:].rearrange("p a b -> p (a b)")[:, 0:PAIRS * PAIRS:PAIRS + 1],
                                       u.cc[:].rearrange("p a b -> p (a b)"), D ** -0.5, None, ALU.mult))

            @block.scalar
            def _(act):
                act.wait_ge(s.step, 5)
                act.activation(u.sin[:], u.sin[:], ACT.Sin, scale=float(2 * np.pi * (1 - 2e-7))).then_inc(s.sined, 1)
                act.wait_ge(s.step, 10)
                act.activation(u.cos[:], u.cos[:], ACT.Sin, scale=float(2 * np.pi * (1 - 2e-7))).then_inc(s.sined, 1)
        PS = g.psum
        with (
            nc.Fori(0, B) as b,
            stage_semaphores(nc, "src_done", "q_mm", "q_out", "k_mm", "k_out", "v_mm", "v_out", "prod_done", "pair_mm",
                             "sT_done", "s_turned", "step", "exp_done", "heads_done", "o_turned", "oT_done", "projected",
                             "added") as s,
            nc.Block() as block,
        ):
            @block.tensor
            def _(pe):
                pe.wait_ge(s.src_done, 1)
                for h in range(H):
                    pe.matmul(PS[:, h, :], u.wq[:, h * D:(h + 1) * D], u.src[:], start=True, stop=True).then_inc(s.q_mm, 1)
                for h in range(H):
                    pe.matmul(PS[:, 4 + h, :], u.wk[:, h * D:(h + 1) * D], u.src[:], start=True, stop=True).then_inc(s.k_mm, 1)
                for t in range(QT):
                    pe.wait_ge(s.q_out, t + 1)
                    pe.matmul(PS[:, t, :], u.src[:, t * P:(t + 1) * P], u.wv[:], start=True, stop=False)
                    pe.matmul(PS[:, t, :], g.ones[0:1, :], u.bv[0:1, :], start=False, stop=True).then_inc(s.v_mm, 1)
                pe.wait_ge(s.k_out, 1)
                for p in range(PAIRS):
                    pe.wait_ge(s.prod_done, p + 1)
                    pe.matmul(PS[0:PAIRS, 4, :], u.pick[:, p, :], u.prod[:, p % 2, :], start=p == 0,
                              stop=p == PAIRS - 1).then_inc(s.pair_mm, 1)
                pe.wait_ge(s.sT_done, 1)
                pe.wait_ge(s.k_out, 2)
                for t in range(QT):
                    last = pe.transpose(PS[:, 5, t * PAIRS:(t + 1) * PAIRS], u.sT[:, t * P:(t + 1) * P],
                                        g.ident[0:PAIRS, 0:PAIRS])
                last.then_inc(s.s_turned, 1)
                pe.wait_ge(s.v_out, QT)
                for t in range(QT):
                    pe.wait_ge(s.heads_done, H * (t + 1))
                    for h in range(H):
                        last = pe.transpose(PS[:, t, h * P:(h + 1) * P], u.o[:, t, h * D:(h + 1) * D], g.ident[:])
                    last.then_inc(s.o_turned, 1)
                pe.wait_ge(s.oT_done, QT)
                pe.wait_ge(s.step, 1)
                pe.wait_ge(s.k_out, 4)
                for h in range(H):
                    out = PS[:, 6, h * D:(h + 1) * D]
                    for c in range(H):
                        pe.matmul(out, u.oT[:, h, c:S:H], u.wo[:, c, :], start=c == 0, stop=False)
                    last = pe.matmul(out, g.ones[0:1, :], u.bo[0:1, :], start=False, stop=True)
                last.then_inc(s.projected, 1)

            @block.scalar
            def _(act):
                for h in range(H):
                    act.wait_ge(s.q_mm, h + 1)
                    act.activation(u.qT[:, h, :], PS[:, h, :], ACT.Identity, bias=u.bq[:, h:h + 1]).then_inc(s.q_out, 1)
                for t in range(QT):
                    act.wait_ge(s.v_mm, t + 1)
                    act.activation(u.v[:, t, :], PS[:, t, :], ACT.Copy).then_inc(s.v_out, 1)
                act.wait_ge(s.pair_mm, PAIRS)
                act.activation(u.sT[:], PS[0:PAIRS, 4, :], ACT.Copy).then_inc(s.sT_done, 1)
                act.wait_ge(s.step, 2)
                act.activation(u.sc[:], u.sc[:], ACT.Exp).then_inc(s.exp_done, 1)
                for t in range(QT):
                    act.wait_ge(s.o_turned, t + 1)
                    act.activation(u.oT[:, :, t * P:(t + 1) * P], PS[:, t, :].rearrange("p (h m) -> p h m", h=H),
                                   ACT.Copy).then_inc(s.oT_done, 1)

            @block.vector
            def _(dve):
                dve.tensor_copy(u.src[:], g.xnT[:, bass.ds(b * S, S)]).then_inc(s.src_done, 1)
                for h in range(H):
                    dve.wait_ge(s.k_mm, h + 1)
                    dve.tensor_scalar(u.kT[:, h, :], PS[:, 4 + h, :], u.bk[:, h:h + 1], None, ALU.add).then_inc(s.k_out, 1)
                dve.wait_ge(s.k_out, H)
                for p in range(PAIRS):
                    dve.wait_ge(s.q_out, p // H + 1)
                    if p >= 2:
                        dve.wait_ge(s.pair_mm, p - 1)
                    dve.tensor_tensor(u.prod[:, p % 2, :], u.qT[:, p // H, :], u.kT[:, p % H, :],
                                      ALU.mult).then_inc(s.prod_done, 1)
                steps = [0]

                def done(ins):
                    steps[0] += 1
                    ins.then_inc(s.step, 1)
                    dve.wait_ge(s.step, steps[0])

                wide = [P, QT * H, H]
                scores = PS[:, 5, 0:QT * PAIRS].rearrange("p (q e) -> p q e", e=H)
                dve.wait_ge(s.s_turned, 1)
                done(dve.tensor_reduce(u.mx[:], scores, AX.X, ALU.max))
                done(dve.tensor_tensor(u.sc[:], scores, u.mx[:].unsqueeze(2).to_broadcast(wide), ALU.subtract))
                dve.wait_ge(s.exp_done, 1)
                done(dve.tensor_reduce(u.mx[:], u.sc[:], AX.X, ALU.add))
                done(dve.reciprocal(u.mx[:], u.mx[:]))
                done(dve.tensor_tensor(u.sc[:], u.sc[:], u.mx[:].unsqueeze(2).to_broadcast(wide), ALU.mult))
                for t in range(QT):
                    dve.wait_ge(s.v_out, t + 1)
                    for e in range(H):
                        for h in range(H):
                            out, val = u.o[:, t, h * D:(h + 1) * D], u.v[:, t, e * D:(e + 1) * D]
                            wt = u.sc[:, t * H + h, e:e + 1]
                            if e == 0:
                                ins = dve.tensor_scalar(out, val, wt, None, ALU.mult)
                            else:
                                ins = dve.scalar_tensor_tensor(out=out, in0=val, scalar=wt, in1=out, op0=ALU.mult,
                                                               op1=ALU.add)
                            if e == H - 1:
                                ins.then_inc(s.heads_done, 1)
                            else:
                                ins.then_inc(s.step, 1)
                                steps[0] += 1
                        if e < H - 1:
                            dve.wait_ge(s.step, steps[0])
                dve.wait_ge(s.projected, 1)
                at = g.x[:, bass.ds(b * QT, QT), :]
                dve.tensor_tensor(at, at, PS[:, 6, :].rearrange("p (t d) -> p t d", d=D), ALU.add).then_inc(s.added, 1)


def route(nc, g, u, E, K, gate, gate_b, bias_in_logits):
    PER = 512 // E
    with (
        buffers(nc, top=((P, NT, 8), F32), where=((P, NT, 8), U32), wheref=((P, NT, 8), F32),
                select=((P, NT, E), F32), mx=((P, NT), F32), which=((P, E), I32), whichf=((P, E), F32)) as w,
        stage_semaphores(nc, "logits_done", "step", "exp_done", "top_done", "found", "counted") as s,
        nc.Block() as block,
    ):
        banks = [g.psum[:, n, :].rearrange("p (t e) -> p t e", e=E) for n in range(-(-NT // PER))]
        spread = [P, NT, E]

        @block.tensor
        def _(pe):
            for t in range(NT):
                out = banks[t // PER][:, t % PER, :]
                last = pe.matmul(out, g.xnT[:, t * P:(t + 1) * P], gate[:], start=True, stop=not bias_in_logits)
                if bias_in_logits:
                    last = pe.matmul(out, g.ones[0:1, :], gate_b[0:1, :], start=False, stop=True)
            if gate_b is not None and not bias_in_logits:
                last = pe.matmul(g.psum[:, 7, 0:E], g.ones[0:1, :], gate_b[0:1, :], start=True, stop=True)
            last.then_inc(s.logits_done, 1)

        @block.gpsimd
        def _(pool):
            pool.iota(w.which[:], pattern=[[1, E]], base=0, channel_multiplier=0).then_inc(s.counted, 1)
            pool.wait_ge(s.counted, 1)
            pool.tensor_copy(w.whichf[:], w.which[:]).then_inc(s.counted, 1)

        @block.scalar
        def _(act):
            act.wait_ge(s.step, 2 * len(banks))
            act.activation(u.ex[:], u.ex[:], ACT.Exp).then_inc(s.exp_done, 1)

        @block.vector
        def _(dve):
            steps = [0]

            def done(ins):
                steps[0] += 1
                ins.then_inc(s.step, 1)
                dve.wait_ge(s.step, steps[0])

            dve.wait_ge(s.logits_done, 1)
            for n, bank in enumerate(banks):
                some = slice(n * PER, min(NT, (n + 1) * PER))
                wide = some.stop - some.start
                done(dve.tensor_reduce(w.mx[:, some], bank[:, 0:wide, :], AX.X, ALU.max))
                done(dve.tensor_tensor(u.ex[:, some, :], bank[:, 0:wide, :],
                                       w.mx[:, some].unsqueeze(2).to_broadcast([P, wide, E]), ALU.subtract))
            dve.wait_ge(s.exp_done, 1)
            done(dve.tensor_reduce(u.inv_z[:], u.ex[:], AX.X, ALU.add))
            done(dve.reciprocal(u.inv_z[:], u.inv_z[:]))
            if bias_in_logits or gate_b is None:
                for n, bank in enumerate(banks):
                    some = slice(n * PER, min(NT, (n + 1) * PER))
                    done(dve.tensor_copy(w.select[:, some, :], bank[:, 0:some.stop - some.start, :]))
            else:
                done(dve.tensor_tensor(u.ex[:], u.ex[:], u.inv_z[:].unsqueeze(2).to_broadcast(spread), ALU.mult))
                done(dve.tensor_tensor(w.select[:], u.ex[:], g.psum[:, 7, 0:E].unsqueeze(1).to_broadcast(spread), ALU.add))
            for t in range(NT):
                dve.max(w.top[:, t, :], w.select[:, t, :]).then_inc(s.top_done, 1)
            for t in range(NT):
                dve.wait_ge(s.top_done, t + 1)
                dve.max_index(w.where[:, t, :], w.top[:, t, :], w.select[:, t, :]).then_inc(s.found, 1)
            dve.wait_ge(s.found, NT)
            done(dve.tensor_copy(w.wheref[:], w.where[:]))
            dve.wait_ge(s.counted, 2)
            for k in range(K):
                ins = dve.tensor_tensor(u.pick[:, k, :, :], w.whichf[:].unsqueeze(1).to_broadcast(spread),
                                        w.wheref[:, :, k].unsqueeze(2).to_broadcast(spread), ALU.is_equal)
                ins.then_inc(s.step, 1)
            steps[0] += K
            dve.wait_ge(s.step, steps[0])


def count_before(nc, g, u, E, chosen, pos, after=None):
    N = NT * E
    with (
        buffers(nc, prefix=((P, NT, E), BF16), total=((P, E), F32), total_bf=((P, E), BF16)) as w,
        stage_semaphores(nc, "prefix_done", "total_done", "counted", "pos_done") as s,
        nc.Block() as block,
    ):
        @block.vector
        def _(dve):
            dve.memset(w.prefix[:, 0, :], 0.0).then_inc(s.prefix_done, 1)
            for t in range(1, NT):
                dve.wait_ge(s.prefix_done, t)
                dve.tensor_tensor(w.prefix[:, t, :], w.prefix[:, t - 1, :], chosen[:, t - 1, :],
                                  ALU.add).then_inc(s.prefix_done, 1)
            if after is not None:
                dve.tensor_reduce(w.total[:], after[:].rearrange("p t e -> p e t"), AX.X, ALU.add).then_inc(s.total_done, 1)
                dve.wait_ge(s.total_done, 1)
                dve.tensor_copy(w.total_bf[:], w.total[:]).then_inc(s.total_done, 1)
            for n in range(0, N, 512):
                wide = min(512, N - n)
                dve.wait_ge(s.counted, n // 512 + 1)
                dve.tensor_copy(pos[:].rearrange("p t e -> p (t e)")[:, n:n + wide],
                                g.psum[:, n // 512, 0:wide]).then_inc(s.pos_done, 1)

        @block.tensor
        def _(pe):
            pe.wait_ge(s.prefix_done, NT)
            if after is not None:
                pe.wait_ge(s.total_done, 2)
            for n in range(0, N, 512):
                wide = min(512, N - n)
                out = g.psum[:, n // 512, 0:wide]
                pe.matmul(out, g.before[:], chosen[:].rearrange("p t e -> p (t e)")[:, n:n + wide], start=True, stop=False)
                last = pe.matmul(out, g.ones_bf[:], w.prefix[:].rearrange("p t e -> p (t e)")[:, n:n + wide],
                                 start=False, stop=after is None)
                if after is not None:
                    last = pe.matmul(out, g.ones_bf[:], w.total_bf[:].unsqueeze(1).to_broadcast([P, wide // E, E]),
                                     start=False, stop=True)
                last.then_inc(s.counted, 1)


def experts(nc, g, u, E, F, func):
    FC = F // P
    with (
        buffers(nc, src=((P, S), F32), coef=((P, QT, E), F32), hidden=((P, 2, FC, S), F32), acc=((P, QT, D), F32)) as w,
        nc.Fori(0, B) as b,
        stage_semaphores(nc, "src_done", "coef_done", "hidden_mm", "hidden_done", "out_mm", "acc_done", "added") as s,
        nc.Block() as block,
    ):
        @block.tensor
        def _(pe):
            def hidden(e):
                for c in range(FC):
                    n = e * FC + c
                    if n >= 3:
                        pe.wait_ge(s.hidden_done, n - 2)
                    pe.matmul(g.psum[:, n % 3, :], u.w1[:, e, c * P:(c + 1) * P], w.src[:], start=True,
                              stop=True).then_inc(s.hidden_mm, 1)

            def out(e):
                pe.wait_ge(s.hidden_done, FC * (e + 1))
                if e >= 2:
                    pe.wait_ge(s.acc_done, QT * (e - 1))
                for j in range(QT):
                    o = g.psum[:, 4 + e % 2, j * D:(j + 1) * D]
                    for c in range(FC):
                        pe.matmul(o, w.hidden[:, e % 2, c, j * P:(j + 1) * P], u.w2[:, e, c, :], start=c == 0, stop=False)
                    last = pe.matmul(o, g.ones[0:1, :], u.b2[0:1, e * D:(e + 1) * D], start=False, stop=True)
                last.then_inc(s.out_mm, 1)

            pe.wait_ge(s.src_done, 1)
            for e in range(E + 1):
                if e < E:
                    hidden(e)
                if e >= 1:
                    out(e - 1)

        @block.scalar
        def _(act):
            for n in range(E * FC):
                e, c = n // FC, n % FC
                act.wait_ge(s.hidden_mm, n + 1)
                if e >= 2:
                    act.wait_ge(s.out_mm, e - 1)
                act.activation(w.hidden[:, e % 2, c, :], g.psum[:, n % 3, :], func,
                               bias=u.b1[:, n:n + 1]).then_inc(s.hidden_done, 1)

        @block.vector
        def _(dve):
            dve.tensor_copy(w.src[:], g.xnT[:, bass.ds(b * S, S)]).then_inc(s.src_done, 1)
            dve.tensor_copy(w.coef[:], u.coef[:, bass.ds(b * QT, QT), :]).then_inc(s.coef_done, 1)
            dve.memset(w.acc[:], 0.0).then_inc(s.coef_done, 1)
            dve.wait_ge(s.coef_done, 2)
            for e in range(E):
                dve.wait_ge(s.out_mm, e + 1)
                if e >= 1:
                    dve.wait_ge(s.acc_done, QT * e)
                for j in range(QT):
                    dve.scalar_tensor_tensor(out=w.acc[:, j, :], in0=g.psum[:, 4 + e % 2, j * D:(j + 1) * D],
                                             scalar=w.coef[:, j, e:e + 1], in1=w.acc[:, j, :], op0=ALU.mult,
                                             op1=ALU.add).then_inc(s.acc_done, 1)
            dve.wait_ge(s.acc_done, QT * E)
            at = g.x[:, bass.ds(b * QT, QT), :]
            dve.tensor_tensor(at, at, w.acc[:], ALU.add).then_inc(s.added, 1)


def mixture8(nc, g, a, K, capacity, names, func):
    E, F = 8, 512
    gate, gate_b, w1, b1, w2, b2 = names
    layernorm(nc, g)
    with buffers(nc, w1=((P, E, F), F32), w2=((P, E, F // P, D), F32), b1=((P, E * F // P), F32), b2=((1, E * D), F32),
                 gate=((P, E), F32), gate_b=((1, E), F32), ex=((P, NT, E), F32), inv_z=((P, NT), F32),
                 pick=((P, K, NT, E), F32), coef=((P, NT, E), F32)) as u:
        pairs = [(u.w1[:], a[w1].rearrange("e k f -> k e f")), (u.w2[:], a[w2].rearrange("e (c p) d -> p e c d", p=P)),
                 (u.b1[:], a[b1].rearrange("e (c p) -> p (e c)", p=P)), (u.b2[:], row(a[b2].rearrange("e d -> (e d)"))),
                 (u.gate[:], a[gate])]
        if gate_b:
            pairs.append((u.gate_b[:], row(a[gate_b])))
        load(nc, pairs)
        route(nc, g, u, E, K, u.gate, u.gate_b if gate_b else None, bool(gate_b))
        with buffers(nc, chosen=((P, K, NT, E), BF16), pos=((P, K, NT, E), F32), g1=((P, NT), F32), g2=((P, NT), F32),
                     den=((P, NT), F32), tmp=((P, NT, E), F32)) as w:
            with stage_semaphores(nc, "chosen_done") as s, nc.Block() as block:
                @block.vector
                def _(dve):
                    dve.tensor_copy(w.chosen[:], u.pick[:]).then_inc(s.chosen_done, 1)
                    dve.wait_ge(s.chosen_done, 1)
            for k in range(K):
                count_before(nc, g, u, E, w.chosen[:, k], w.pos[:, k], after=w.chosen[:, 0] if k else None)
            with stage_semaphores(nc, "step") as s, nc.Block() as block:
                @block.vector
                def _(dve):
                    steps = [0]

                    def done(ins):
                        steps[0] += 1
                        ins.then_inc(s.step, 1)
                        dve.wait_ge(s.step, steps[0])

                    spread = [P, NT, E]
                    done(dve.scalar_tensor_tensor(out=u.pick[:], in0=w.pos[:], scalar=float(capacity), in1=u.pick[:],
                                                  op0=ALU.is_lt, op1=ALU.mult))
                    if K == 1:
                        done(dve.tensor_tensor(u.coef[:], u.pick[:, 0], u.inv_z[:].unsqueeze(2).to_broadcast(spread), ALU.mult))
                    else:
                        done(dve.tensor_tensor(w.tmp[:], u.ex[:], w.chosen[:, 1], ALU.mult))
                        done(dve.tensor_reduce(w.g2[:], w.tmp[:], AX.X, ALU.add))
                        done(dve.tensor_tensor(w.g2[:], w.g2[:], u.inv_z[:], ALU.mult))
                        done(dve.tensor_tensor(w.den[:], w.g2[:], u.inv_z[:], ALU.add))
                        done(dve.tensor_scalar(w.den[:], w.den[:], 1e-9, None, ALU.add))
                        done(dve.reciprocal(w.den[:], w.den[:]))
                        done(dve.tensor_tensor(w.g1[:], u.inv_z[:], w.den[:], ALU.mult))
                        done(dve.tensor_tensor(w.g2[:], w.g2[:], w.den[:], ALU.mult))
                        done(dve.tensor_tensor(u.coef[:], u.pick[:, 0], w.g1[:].unsqueeze(2).to_broadcast(spread), ALU.mult))
                        done(dve.tensor_tensor(w.tmp[:], u.pick[:, 1], w.g2[:].unsqueeze(2).to_broadcast(spread), ALU.mult))
                        done(dve.tensor_tensor(u.coef[:], u.coef[:], w.tmp[:], ALU.add))
        experts(nc, g, u, E, F, func)


def layer1_ffn(nc, g, a):
    mixture8(nc, g, a, 2, 2 * 2 * NT * P // 8, ("L1_ffn_Wg", None, "L1_ffn_W1", "L1_ffn_b1", "L1_ffn_W2", "L1_ffn_b2"),
             ACT.Gelu)


def layer2_ffn(nc, g, a):
    mixture8(nc, g, a, 1, -(-5 * NT * P // (4 * 8)), ("L2_ffn_gate_wT", "L2_ffn_gate_b", "L2_ffn_w1", "L2_ffn_b1",
                                                     "L2_ffn_w2", "L2_ffn_b2"), ACT.Relu)


def layer0_ffn(nc, g, a):
    E, K, CAP, I, SI = 64, 6, 64, 88, 176
    ROWS = E * CAP
    FAR = float(1 << 20)
    layernorm(nc, g)
    rows_in, rows_out = g.moe_in, g.moe_out
    with buffers(nc, w13=((P, E, 2 * I), F32), w2=((I, E, D), F32), gate=((P, E), F32), gate_b=((1, E), F32),
                 ws1=((P, SI), F32), ws3=((P, SI), F32), ws2=((P, 2, D), F32), slot_in=((P, NT, K), I32),
                 slot_out=((P, NT, K), I32), weight=((P, NT, K), F32)) as u:
        load(nc, [(u.w13[:, :, 0:I], a["L0_ffn_w1T"]), (u.w13[:, :, I:2 * I], a["L0_ffn_w3T"]), (u.w2[:], a["L0_ffn_w2T"]),
                  (u.gate[:], a["L0_ffn_gate_wT"]), (u.gate_b[:], row(a["L0_ffn_gate_b"])), (u.ws1[:], a["L0_ffn_ws1T"]),
                  (u.ws3[:], a["L0_ffn_ws3T"]), (u.ws2[:, 0, :], a["L0_ffn_ws2T"][0:P, :]),
                  (u.ws2[0:SI - P, 1, :], a["L0_ffn_ws2T"][P:SI, :])])
        with buffers(nc, ex=((P, NT, E), F32), inv_z=((P, NT), F32), pick=((P, K, NT, E), F32), chosen=((P, NT, E), BF16),
                     pos=((P, NT, E), F32), kept=((P, NT, E), F32), tmp=((P, NT, E), F32), slotf=((P, NT, K), F32),
                     first=((P, E), I32)) as w:
            route(nc, g, w, E, K, u.gate, u.gate_b, False)
            with stage_semaphores(nc, "step", "zeroed", "cleared") as s, nc.Block() as block:
                @block.vector
                def _(dve):
                    steps = [0]

                    def done(ins):
                        steps[0] += 1
                        ins.then_inc(s.step, 1)
                        dve.wait_ge(s.step, steps[0])

                    done(dve.tensor_tensor(w.kept[:], w.pick[:, 0], w.pick[:, 1], ALU.add))
                    for k in range(2, K):
                        done(dve.tensor_tensor(w.kept[:], w.kept[:], w.pick[:, k], ALU.add))
                    done(dve.tensor_copy(w.chosen[:], w.kept[:]))
                    dve.memset(w.tmp[:], 0.0).then_inc(s.zeroed, 1)

                @block.sync
                def _(sp):
                    sp.wait_ge(s.zeroed, 1)
                    view = rows_in.rearrange("(p n) d -> p (n d)", p=P)
                    wide = NT * E
                    for n in range(0, ROWS // P * D, wide):
                        sp.dma_start(view[:, n:n + wide], w.tmp[:].rearrange("p t e -> p (t e)")).then_inc(s.cleared, 16)
                    sp.wait_ge(s.cleared, 16 * (ROWS // P * D // wide))
            count_before(nc, g, w, E, w.chosen, w.pos)
            with stage_semaphores(nc, "step", "first_done") as s, nc.Block() as block:
                @block.gpsimd
                def _(pool):
                    pool.iota(w.first[:], pattern=[[CAP, E]], base=0, channel_multiplier=0).then_inc(s.first_done, 1)

                @block.vector
                def _(dve):
                    steps = [0]

                    def done(ins):
                        steps[0] += 1
                        ins.then_inc(s.step, 1)
                        dve.wait_ge(s.step, steps[0])

                    spread = [P, NT, E]
                    done(dve.tensor_scalar(w.kept[:], w.pos[:], float(CAP), None, ALU.is_lt))
                    done(dve.tensor_tensor(w.ex[:], w.ex[:], w.kept[:], ALU.mult))
                    done(dve.tensor_scalar(w.kept[:], w.kept[:], -FAR, FAR, ALU.mult, ALU.add))
                    done(dve.tensor_tensor(w.pos[:], w.pos[:], w.kept[:], ALU.add))
                    dve.wait_ge(s.first_done, 1)
                    done(dve.tensor_tensor(w.pos[:], w.pos[:], w.first[:].unsqueeze(1).to_broadcast(spread), ALU.add))
                    for k in range(K):
                        done(dve.tensor_tensor(w.tmp[:], w.pick[:, k], w.ex[:], ALU.mult))
                        done(dve.tensor_reduce(u.weight[:, :, k], w.tmp[:], AX.X, ALU.add))
                        done(dve.tensor_tensor(w.tmp[:], w.pick[:, k], w.pos[:], ALU.mult))
                        done(dve.tensor_reduce(w.slotf[:, :, k], w.tmp[:], AX.X, ALU.add))
                    done(dve.tensor_copy(u.slot_in[:], w.slotf[:]))
                    done(dve.tensor_scalar(w.slotf[:], w.slotf[:], float(ROWS - 1), None, ALU.min))
                    done(dve.tensor_copy(u.slot_out[:], w.slotf[:]))

        with (
            buffers(nc, tile=((P, D), F32), slots=((P, K), I32)) as w,
            nc.Fori(0, NT) as t,
            stage_semaphores(nc, "fixed") as s,
            nc.Block() as block,
        ):
            @block.vector
            def _(dve):
                dve.tensor_copy(w.tile[:].unsqueeze(1), g.xn[:, bass.ds(t, 1), :]).then_inc(s.fixed, 1)
                dve.tensor_copy(w.slots[:].unsqueeze(1), u.slot_in[:, bass.ds(t, 1), :]).then_inc(s.fixed, 1)

            @block.gpsimd
            def _(pool):
                pool.wait_ge(s.fixed, 2)
                for k in range(K):
                    pool.indirect_dma_start(rows_in, bass.IndirectOffsetOnAxis(ap=w.slots[:, k:k + 1].bitcast(U32), axis=0),
                                            w.tile[:], None, bounds_check=ROWS - 1,
                                            oob_is_err=False).then_inc(g.scattered, 16)
                pool.wait_ge(g.scattered, t * (16 * K) + 16 * K)

        EB = 8
        PS = g.psum
        with (
            buffers(nc, rows=((CAP, EB, D), F32), rT=((P, EB * CAP), F32), gated=((CAP, EB, I), F32),
                    h=((CAP, EB, I), F32), hT=((I, EB * CAP), F32), y=((CAP, EB, D), F32)) as w,
            nc.Fori(0, E // EB) as n,
            stage_semaphores(nc, "rows_in", "turned", "rT_done", "hidden_mm", "silu_done", "h_done", "h_turned",
                             "hT_done", "out_mm", "y_done", "rows_saved") as s,
            nc.Block() as block,
        ):
            @block.sync
            def _(sp):
                sp.dma_start(w.rows[:], rows_in.rearrange("(e c) d -> c e d", c=CAP)[:, bass.ds(n * EB, EB), :]).then_inc(s.rows_in, 16)
                sp.wait_ge(s.y_done, 2)
                sp.dma_start(rows_out.rearrange("(e c) d -> c e d", c=CAP)[:, bass.ds(n * EB, EB), :],
                             w.y[:]).then_inc(s.rows_saved, 16)
                sp.wait_ge(s.rows_saved, 16)

            def hid(e):
                return PS[0:CAP, 1 + e // 2, (e % 2) * 2 * I:(e % 2 + 1) * 2 * I]

            @block.tensor
            def _(pe):
                pe.wait_ge(s.rows_in, 16)
                for e in range(EB):
                    last = pe.transpose(PS[:, 0, e * CAP:(e + 1) * CAP], w.rows[:, e, :], g.ident[0:CAP, 0:CAP])
                last.then_inc(s.turned, 1)
                pe.wait_ge(s.rT_done, 1)
                for e in range(EB):
                    pe.matmul(hid(e).unsqueeze(1), w.rT[:, e * CAP:(e + 1) * CAP], u.w13[:, bass.ds(n * EB + e, 1), :],
                              start=True, stop=True).then_inc(s.hidden_mm, 1)
                for e in range(EB):
                    pe.wait_ge(s.h_done, e // 2 + 1)
                    last = pe.transpose(PS[0:I, 5, e * CAP:(e + 1) * CAP], w.h[:, e, :], g.ident[0:CAP, 0:CAP])
                last.then_inc(s.h_turned, 1)
                pe.wait_ge(s.hT_done, 1)
                for e in range(EB):
                    pe.matmul(PS[0:CAP, 6 + e // 4, (e % 4) * D:(e % 4 + 1) * D].unsqueeze(1), w.hT[:, e * CAP:(e + 1) * CAP],
                              u.w2[:, bass.ds(n * EB + e, 1), :], start=True, stop=True).then_inc(s.out_mm, 1)

            @block.scalar
            def _(act):
                act.wait_ge(s.turned, 1)
                act.activation(w.rT[:], PS[:, 0, :], ACT.Copy).then_inc(s.rT_done, 1)
                for m in range(EB // 2):
                    act.wait_ge(s.hidden_mm, 2 * m + 2)
                    both = PS[0:CAP, 1 + m, 0:4 * I].rearrange("p (e w i) -> p e w i", e=2, w=2)
                    act.activation(w.gated[:, 2 * m:2 * m + 2, :], both[:, :, 0, :], ACT.Silu).then_inc(s.silu_done, 1)
                act.wait_ge(s.h_turned, 1)
                act.activation(w.hT[:], PS[0:I, 5, :], ACT.Copy).then_inc(s.hT_done, 1)
                act.wait_ge(s.out_mm, 4)
                act.activation(w.y[:, 0:4, :], PS[0:CAP, 6, :].rearrange("p (e d) -> p e d", d=D), ACT.Copy).then_inc(s.y_done, 1)

            @block.vector
            def _(dve):
                for m in range(EB // 2):
                    dve.wait_ge(s.silu_done, m + 1)
                    both = PS[0:CAP, 1 + m, 0:4 * I].rearrange("p (e w i) -> p e w i", e=2, w=2)
                    dve.tensor_tensor(w.h[:, 2 * m:2 * m + 2, :], w.gated[:, 2 * m:2 * m + 2, :], both[:, :, 1, :],
                                      ALU.mult).then_inc(s.h_done, 1)
                dve.wait_ge(s.out_mm, 8)
                dve.tensor_copy(w.y[:, 4:8, :], PS[0:CAP, 7, :].rearrange("p (e d) -> p e d", d=D)).then_inc(s.y_done, 1)

        with (
            buffers(nc, got=((P, K, D), F32), slots=((P, K), I32), wt=((P, K), F32)) as w,
            nc.Fori(0, NT) as t,
            stage_semaphores(nc, "fixed", "added") as s,
            nc.Block() as block,
        ):
            @block.gpsimd
            def _(pool):
                pool.wait_ge(s.fixed, 2)
                for k in range(K):
                    pool.indirect_dma_start(w.got[:, k, :], None, rows_out,
                                            bass.IndirectOffsetOnAxis(ap=w.slots[:, k:k + 1].bitcast(U32), axis=0),
                                            bounds_check=ROWS - 1, oob_is_err=False).then_inc(g.gathered, 16)

            @block.vector
            def _(dve):
                dve.tensor_copy(w.slots[:].unsqueeze(1), u.slot_out[:, bass.ds(t, 1), :]).then_inc(s.fixed, 1)
                dve.tensor_copy(w.wt[:].unsqueeze(1), u.weight[:, bass.ds(t, 1), :]).then_inc(s.fixed, 1)
                dve.wait_ge(g.gathered, t * (16 * K) + 16 * K)
                dve.wait_ge(s.fixed, 2)
                at = g.x[:, bass.ds(t, 1), :]
                for k in range(K):
                    if k:
                        dve.wait_ge(s.added, k)
                    dve.scalar_tensor_tensor(out=at, in0=w.got[:, k:k + 1, :], scalar=w.wt[:, k:k + 1], in1=at,
                                             op0=ALU.mult, op1=ALU.add).then_inc(s.added, 1)

        parts = [(0, P), (P, SI - P)]
        with (
            buffers(nc, src=((P, S), F32), gated=((P, 2, S), F32), h=((P, 2, S), F32)) as w,
            nc.Fori(0, B) as b,
            stage_semaphores(nc, "src_done", "hidden_mm", "silu_done", "h_done", "out_mm", "added") as s,
            nc.Block() as block,
        ):
            @block.tensor
            def _(pe):
                pe.wait_ge(s.src_done, 1)
                for c, (at, rows) in enumerate(parts):
                    pe.matmul(PS[0:rows, 2 * c, :], u.ws1[:, at:at + rows], w.src[:], start=True, stop=True)
                    pe.matmul(PS[0:rows, 2 * c + 1, :], u.ws3[:, at:at + rows], w.src[:], start=True,
                              stop=True).then_inc(s.hidden_mm, 1)
                pe.wait_ge(s.h_done, 2)
                for j in range(QT):
                    for c, (_, rows) in enumerate(parts):
                        last = pe.matmul(PS[:, 4, j * D:(j + 1) * D], w.h[0:rows, c, j * P:(j + 1) * P], u.ws2[0:rows, c, :],
                                         start=c == 0, stop=c == 1)
                last.then_inc(s.out_mm, 1)

            @block.scalar
            def _(act):
                for c, (_, rows) in enumerate(parts):
                    act.wait_ge(s.hidden_mm, c + 1)
                    act.activation(w.gated[0:rows, c, :], PS[0:rows, 2 * c, :], ACT.Silu).then_inc(s.silu_done, 1)

            @block.vector
            def _(dve):
                dve.tensor_copy(w.src[:], g.xnT[:, bass.ds(b * S, S)]).then_inc(s.src_done, 1)
                for c, (_, rows) in enumerate(parts):
                    dve.wait_ge(s.silu_done, c + 1)
                    dve.tensor_tensor(w.h[0:rows, c, :], w.gated[0:rows, c, :], PS[0:rows, 2 * c + 1, :],
                                      ALU.mult).then_inc(s.h_done, 1)
                dve.wait_ge(s.out_mm, 1)
                at = g.x[:, bass.ds(b * QT, QT), :]
                dve.tensor_tensor(at, at, PS[:, 4, :].rearrange("p (t d) -> p t d", d=D), ALU.add).then_inc(s.added, 1)


def layer2_warp(nc, g, a):
    W = 16
    KB = S // W
    TIMES = SC + KB - 1
    UNIT = 5
    PADDED = -(-TIMES // (2 * UNIT)) * 2 * UNIT
    BIG = 1e30
    BACK = 4
    layernorm(nc, g)
    with buffers(nc, table=((P, PADDED + 1, W + 1), F32), first=((P, 1), F32), last=((P, 1), F32),
                 inner=((P, 1), F32)) as u:
        with stage_semaphores(nc, "marked") as s, nc.Block() as block:
            @block.vector
            def _(dve):
                dve.tensor_reduce(u.first[:], g.ident[:, 0:P:KB], AX.X, ALU.add).then_inc(s.marked, 1)
                dve.tensor_reduce(u.last[:], g.ident[:, KB - 1:P:KB], AX.X, ALU.add).then_inc(s.marked, 1)
                dve.wait_ge(s.marked, 2)
                dve.tensor_scalar(u.inner[:], u.last[:], -1.0, 1.0, ALU.mult, ALU.add).then_inc(s.marked, 1)
                dve.wait_ge(s.marked, 3)

        with buffers(nc, skewed=((P, PADDED, W + 1), F32)) as v:
            PERB = 3
            with (
                buffers(nc, xsq=((P, NT * P), F32), csq=((P, B * SC), F32), cm2=((P, B * SC), F32),
                        dist=((P, SC, W), F32), wide=((P, PADDED * W), F32)) as w,
                stage_semaphores(nc, "squared", "product_done", "floored", "rooted", "filled", "placed", "spread",
                                 "read") as s,
                nc.Block() as block,
            ):
                @block.gpsimd
                def _(pool):
                    pool.memset(w.wide[:], BIG).then_inc(s.filled, 1)

                @block.vector
                def _(dve):
                    dve.tensor_tensor(w.xsq[:], g.xnT[:], g.xnT[:], ALU.mult).then_inc(s.squared, 1)
                    dve.tensor_tensor(w.csq[:], g.ctxT[:], g.ctxT[:], ALU.mult).then_inc(s.squared, 1)
                    dve.tensor_scalar(w.cm2[:], g.ctxT[:], -2.0, None, ALU.mult).then_inc(s.squared, 1)
                    for n in range(0, W, PERB):
                        m = min(PERB, W - n)
                        dve.wait_ge(s.product_done, n // PERB + 1)
                        dve.tensor_scalar(w.dist[:, :, n:n + m].rearrange("p i j -> p j i"),
                                          g.psum[:, n // PERB, 0:m * SC].rearrange("p (j i) -> p j i", i=SC), 0.0, None,
                                          ALU.max).then_inc(s.floored, 1)
                    dve.wait_ge(s.read, 16)
                    dve.tensor_copy(v.skewed[:, :, 1:W + 1], w.wide[:].rearrange("p (t j) -> p t j", j=W)).then_inc(s.spread, 1)
                    dve.memset(v.skewed[:, :, 0], BIG).then_inc(s.spread, 1)
                    dve.wait_ge(s.spread, 2)
                    dve.tensor_scalar(v.skewed[:, :, 0], v.skewed[:, :, 0], u.first[:, 0:1], None, ALU.mult).then_inc(s.spread, 1)

                @block.tensor
                def _(pe):
                    pe.wait_ge(s.squared, 3)
                    for n in range(W):
                        for b in range(B):
                            rows = slice(KB * b, KB * (b + 1))
                            out = g.psum[rows, n // PERB, (n % PERB) * SC:(n % PERB + 1) * SC]
                            x = slice(b * S + n, (b + 1) * S, W)
                            c = slice(b * SC, (b + 1) * SC)
                            at = (0, KB * b)
                            pe.matmul(out, g.xnT[:, x], w.cm2[:, c], start=True, stop=False, tile_position=at)
                            pe.matmul(out, w.xsq[:, x], g.ones[:, 0:1].to_broadcast([P, SC]), start=False, stop=False,
                                      tile_position=at)
                            last = pe.matmul(out, g.ones[:, 0:KB], w.csq[:, c], start=False, stop=True, tile_position=at)
                        if n % PERB == PERB - 1 or n == W - 1:
                            last.then_inc(s.product_done, 1)

                @block.scalar
                def _(act):
                    act.wait_ge(s.floored, -(-W // PERB))
                    act.activation(w.dist[:], w.dist[:], ACT.Sqrt).then_inc(s.rooted, 1)

                @block.sync
                def _(sp):
                    far = g.warp_skew
                    sp.wait_ge(s.filled, 1)
                    sp.dma_start(far[0:P, :], w.wide[:]).then_inc(s.placed, 16)
                    sp.wait_ge(s.placed, 16)
                    sp.wait_ge(s.rooted, 1)
                    for b in range(B):
                        dst = bass.AP(tensor=far.tensor, offset=far.offset + b * KB * PADDED * W,
                                      ap=[[(PADDED + 1) * W, KB], [1, SC * W]])
                        sp.dma_start(dst, w.dist[KB * b:KB * (b + 1), :, :].rearrange("p i j -> p (i j)")).then_inc(s.placed, 16)
                    sp.wait_ge(s.placed, 16 * (1 + B))
                    sp.dma_start(w.wide[:], far[0:P, :]).then_inc(s.read, 16)

            from_left = [max(0, k - 1) for k in range(KB)]
            with (
                buffers(nc, ring=((P, 2 * UNIT, W + 1), F32), best=((P, W + 1), F32)) as w,
                stage_semaphores(nc, "row_done", "best_done", "free0", "free1") as s,
                nc.Block() as block,
            ):
                free = [s.free0, s.free1]

                @block.vector
                def _(dve):
                    start = w.ring[:, 2 * UNIT - 1, :]
                    dve.memset(start, BIG).then_inc(s.row_done, 1)
                    dve.wait_ge(s.row_done, 1)
                    dve.tensor_scalar(start[:, 0:1], u.first[:], -BIG, BIG, ALU.mult, ALU.add).then_inc(s.row_done, 1)
                    dve.wait_ge(s.row_done, 2)
                    dve.tensor_copy(u.table[:, 0, :], start).then_inc(s.free0, 1)
                    dve.tensor_copy(w.best[:, 0:1], start[:, 0:1]).then_inc(s.free1, 1)
                    dve.wait_ge(s.free0, 1)
                    dve.wait_ge(s.free1, 1)
                    with dve.Fori(0, PADDED // (2 * UNIT)) as it:
                        for n in range(2 * UNIT):
                            before, now = w.ring[:, (n - 1) % (2 * UNIT), :], w.ring[:, n, :]
                            dve.wait_ge(s.row_done, it * (2 * UNIT) + n + 2)
                            dve.tensor_tensor(w.best[:, 1:W + 1], before[:, 0:W], before[:, 1:W + 1],
                                              ALU.min).then_inc(s.best_done, 1)
                            dve.stream_shuffle(w.best[:, 0:1], before[:, W:W + 1], from_left).then_inc(s.best_done, 1)
                            if n % UNIT == 0:
                                dve.wait_ge(free[n // UNIT], it + 1)
                            dve.wait_ge(s.best_done, it * (4 * UNIT) + 2 * n + 2)
                            dve.tensor_tensor_scan(now, w.best[:], v.skewed[:, bass.ds(it * (2 * UNIT) + n, 1), :]
                                                   .rearrange("p a w -> p (a w)"), BIG, ALU.min,
                                                   ALU.add).then_inc(s.row_done, 1)

                @block.scalar
                def _(act):
                    with act.Fori(0, PADDED // (2 * UNIT)) as it:
                        for half in range(2):
                            act.wait_ge(s.row_done, it * (2 * UNIT) + UNIT * (half + 1) + 2)
                            act.activation(u.table[:, bass.ds(it * (2 * UNIT) + UNIT * half + 1, UNIT), :],
                                           w.ring[:, UNIT * half:UNIT * (half + 1), :], ACT.Copy).then_inc(free[half], 1)

        with buffers(nc, take=((P, PADDED, 2 * W), F32), keep=((P, PADDED, 2 * W), F32), path=((P, PADDED, W), F32),
                     unskewed=((P, SC, W), F32)) as v:
            from_right = [min(KB - 1, k + 1) for k in range(KB)]
            with (
                buffers(nc, least=((P, PADDED, W), F32), diag=((P, PADDED, W + 1), F32), up=((P, PADDED, W), F32),
                        left=((P, PADDED, W + 1), F32), edge=((P, PADDED), F32)) as w,
                stage_semaphores(nc, "step") as s,
                nc.Block() as block,
            ):
                @block.vector
                def _(dve):
                    steps = [0]

                    def done(ins):
                        steps[0] += 1
                        ins.then_inc(s.step, 1)
                        dve.wait_ge(s.step, steps[0])

                    R = u.table
                    cd, cu, cl = R[:, 0:PADDED, 0:W], R[:, 0:PADDED, 1:W + 1], R[:, 1:PADDED + 1, 0:W]
                    diag, left = w.diag[:, :, 0:W], w.left[:, :, 0:W]
                    done(dve.tensor_tensor(w.least[:], cu, cl, ALU.min))
                    done(dve.tensor_tensor(diag, cd, w.least[:], ALU.is_le))
                    done(dve.tensor_tensor(w.up[:], cu, cl, ALU.is_le))
                    done(dve.tensor_tensor(w.least[:], w.up[:], diag, ALU.mult))
                    done(dve.tensor_tensor(w.up[:], w.up[:], w.least[:], ALU.subtract))
                    done(dve.tensor_tensor(w.least[:], w.up[:], diag, ALU.add))
                    done(dve.tensor_scalar(left, w.least[:], -1.0, 1.0, ALU.mult, ALU.add))
                    for m in (w.diag, w.left):
                        done(dve.memset(m[:, PADDED - 1, W:W + 1], 0.0))
                        done(dve.tensor_copy(w.edge[:], m[:, :, 0]))
                        done(dve.stream_shuffle(w.edge[:], w.edge[:], from_right))
                        done(dve.tensor_scalar(m[:, 0:PADDED - 1, W], w.edge[:, 1:PADDED], u.inner[:, 0:1], None, ALU.mult))
                    for r in range(W):
                        c = W - r
                        dve.tensor_copy(v.take[:, :, 2 * r], w.diag[:, :, c]).then_inc(s.step, 1)
                        dve.tensor_copy(v.take[:, :, 2 * r + 1], w.up[:, :, c - 1]).then_inc(s.step, 1)
                        dve.tensor_copy(v.keep[:, :, 2 * r], w.left[:, :, c]).then_inc(s.step, 1)
                    dve.memset(v.keep[:].rearrange("p t (r two) -> p t r two", two=2)[:, :, :, 1], 1.0).then_inc(s.step, 1)
                    steps[0] += 3 * W + 1
                    dve.wait_ge(s.step, steps[0])

            RW = 2 * W + 2
            with (
                buffers(nc, ring=((P, 2 * BACK, RW), F32), shares=((P, 2 * W), F32)) as w,
                stage_semaphores(nc, "row_done", "share_done", "free0", "free1", "set_up") as s,
                nc.Block() as block,
            ):
                free = [s.free0, s.free1]
                ring = w.ring[:]
                STEPS = TIMES - 1
                assert STEPS % (2 * BACK) == 0

                def pairs_of(n):
                    return bass.AP(tensor=ring.tensor, offset=ring.offset + n * RW + 1,
                                   ap=[[2 * BACK * RW, P], [2, W], [2, 2]])

                @block.vector
                def _(dve):
                    dve.memset(w.ring[:], 0.0).then_inc(s.set_up, 1)
                    dve.memset(w.shares[:], 0.0).then_inc(s.set_up, 1)
                    dve.wait_ge(s.set_up, 2)
                    dve.tensor_copy(w.shares[:, 1:2], u.last[:]).then_inc(s.set_up, 1)
                    dve.wait_ge(s.set_up, 3)
                    first = w.ring[:, 2 * BACK - 1, :]
                    dve.tensor_tensor_scan(first[:, 2:RW], v.keep[:, TIMES - 1, :], w.shares[:], 0.0, ALU.mult,
                                           ALU.add).then_inc(s.row_done, 1)
                    dve.wait_ge(s.row_done, 1)
                    dve.tensor_copy(v.path[:, TIMES - 1, :], first[:, 3:RW:2]).then_inc(s.free0, 1)
                    dve.tensor_copy(w.shares[:, 0:1], u.last[:]).then_inc(s.free1, 1)
                    dve.wait_ge(s.free0, 1)
                    dve.wait_ge(s.free1, 1)
                    with dve.Fori(0, STEPS // (2 * BACK)) as it:
                        for n in range(2 * BACK):
                            before = (n - 1) % (2 * BACK)
                            time = TIMES - 2 - n
                            dve.wait_ge(s.row_done, it * (2 * BACK) + n + 1)
                            if n % BACK == 0:
                                dve.wait_ge(free[n // BACK], it + 1)
                            dve.tensor_tensor(w.shares[:].rearrange("p (r two) -> p r two", two=2), pairs_of(before),
                                              v.take[:, bass.ds(it * (-2 * BACK) + time + 1, 1), :]
                                              .rearrange("p a (r two) -> p (a r) two", two=2), ALU.mult).then_inc(s.share_done, 1)
                            dve.stream_shuffle(w.ring[:, n, 1:2], w.ring[:, before, RW - 1:RW],
                                               from_right).then_inc(s.share_done, 1)
                            dve.wait_ge(s.share_done, it * (4 * BACK) + 2 * n + 2)
                            dve.tensor_tensor_scan(w.ring[:, n, 2:RW], v.keep[:, bass.ds(it * (-2 * BACK) + time, 1), :]
                                                   .rearrange("p a w -> p (a w)"), w.shares[:], w.ring[:, n, 1:2],
                                                   ALU.mult, ALU.add).then_inc(s.row_done, 1)

                @block.scalar
                def _(act):
                    with act.Fori(0, STEPS // (2 * BACK)) as it:
                        for half in range(2):
                            act.wait_ge(s.row_done, it * (2 * BACK) + BACK * (half + 1) + 1)
                            for n in range(BACK * half, BACK * (half + 1)):
                                ins = act.activation(v.path[:, bass.ds(it * (-2 * BACK) + TIMES - 2 - n, 1), :],
                                                     w.ring[:, n:n + 1, 3:RW:2], ACT.Copy)
                            ins.then_inc(free[half], 1)

            with (
                buffers(nc, onT=((P, 2, B, KB, W), F32), ctx=((P, 2, B, D), F32)) as w,
                stage_semaphores(nc, "saved", "read", "ctx_in", "turned", "on_done", "summed", "added") as s,
                nc.Block() as block,
            ):
                parts = ctx_tiles()

                @block.sync
                def _(sp):
                    for h, (at, rows) in enumerate(parts):
                        sp.dma_start(w.ctx[0:rows, h, :, :], a["ctx"][:, at:at + rows, :].rearrange("b i d -> i b d")).then_inc(s.ctx_in, 16)
                    far = g.warp_skew
                    sp.dma_start(far[0:P, 0:TIMES * W], v.path[:, 0:TIMES, :].rearrange("p t j -> p (t j)")).then_inc(s.saved, 16)
                    sp.wait_ge(s.saved, 16)
                    for b in range(B):
                        src = bass.AP(tensor=far.tensor, offset=far.offset + b * KB * PADDED * W,
                                      ap=[[(PADDED + 1) * W, KB], [1, SC * W]])
                        sp.dma_start(v.unskewed[KB * b:KB * (b + 1), :, :].rearrange("p i j -> p (i j)"), src).then_inc(s.read, 16)

                turns = [(h, r0) for h in range(2) for r0 in range(0, W, 4)]

                @block.tensor
                def _(pe):
                    pe.wait_ge(s.read, 16 * B)
                    for n, (h, r0) in enumerate(turns):
                        at, rows = parts[h]
                        if n >= 4:
                            pe.wait_ge(s.on_done, n - 3)
                        for r in range(r0, r0 + 4):
                            last = pe.transpose(g.psum[0:rows, n % 4, (r - r0) * P:(r - r0 + 1) * P],
                                                v.unskewed[:, at:at + rows, r], g.ident[:])
                        last.then_inc(s.turned, 1)
                    pe.wait_ge(s.on_done, len(turns))
                    pe.wait_ge(s.ctx_in, 32)
                    for b in range(B):
                        for j in range(QT):
                            for h, (_, rows) in enumerate(parts):
                                cells = w.onT[0:rows, h, b, :, :].rearrange("p k w -> p (k w)")[:, j * P:(j + 1) * P]
                                last = pe.matmul(g.psum[:, 4 + b, j * D:(j + 1) * D], cells, w.ctx[0:rows, h, b, :],
                                                 start=h == 0, stop=h == 1)
                        last.then_inc(s.summed, 1)

                @block.vector
                def _(dve):
                    for n, (h, r0) in enumerate(turns):
                        rows = parts[h][1]
                        dve.wait_ge(s.turned, n + 1)
                        for r in range(r0, r0 + 4):
                            ins = dve.tensor_copy(w.onT[0:rows, h, :, :, W - 1 - r],
                                                  g.psum[0:rows, n % 4, (r - r0) * P:(r - r0 + 1) * P]
                                                  .rearrange("p (b k) -> p b k", k=KB))
                        ins.then_inc(s.on_done, 1)
                    for b in range(B):
                        dve.wait_ge(s.summed, b + 1)
                        at = g.x[:, b * QT:(b + 1) * QT, :]
                        dve.tensor_tensor(at, at, g.psum[:, 4 + b, :].rearrange("p (t d) -> p t d", d=D), ALU.add).then_inc(s.added, 1)


def fp4_steps(dve, done, x, out, amax, inv, mag, N):
    spread = [x.shape[0], N, 16]
    done(dve.tensor_reduce(amax, x, AX.X, ALU.max, apply_absolute_value=True))
    done(dve.tensor_scalar(amax, amax, 1.0 / 6.0, 1e-12, ALU.mult, ALU.max))
    done(dve.reciprocal(inv, amax))
    done(dve.tensor_tensor(mag, x, inv.unsqueeze(2).to_broadcast(spread), ALU.mult))
    done(dve.scalar_tensor_tensor(out=mag, in0=mag, scalar=-1.0, in1=mag, op0=ALU.mult, op1=ALU.max))
    done(dve.tensor_scalar(x, x, 0.0, None, ALU.is_ge))
    done(dve.tensor_scalar(out, mag, 5.0, 2.0, ALU.is_gt, ALU.mult))
    for mid in (3.5, 2.5):
        done(dve.scalar_tensor_tensor(out=out, in0=mag, scalar=mid, in1=out, op0=ALU.is_gt, op1=ALU.add))
    done(dve.tensor_scalar(out, out, 2.0, None, ALU.mult))
    for mid in (1.75, 1.25, 0.75, 0.25):
        done(dve.scalar_tensor_tensor(out=out, in0=mag, scalar=mid, in1=out, op0=ALU.is_gt, op1=ALU.add))
    done(dve.scalar_tensor_tensor(out=out, in0=x, scalar=-0.5, in1=out, op0=ALU.add, op1=ALU.mult))
    done(dve.tensor_tensor(out, out, amax.unsqueeze(2).to_broadcast(spread), ALU.mult))


def layer3_ffn(nc, g, a):
    I, Q = 352, 16
    parts = [(0, P), (P, P), (2 * P, I - 2 * P)]
    layernorm(nc, g)
    PS = g.psum
    with buffers(nc, wgT=((P, I), F32), wuT=((P, I), F32), wdT=((P, 3, D), F32), xq=((P, NT, D), F32),
                 xqT=((P, NT * P), F32)) as u:
        NW = 2 * 3 * D // Q + I // Q
        with (
            buffers(nc, w=((P, NW, Q), F32), wq=((P, NW, Q), F32), amax=((P, NW), F32), inv=((P, NW), F32),
                    mag=((P, NW, Q), F32)) as w,
            stage_semaphores(nc, "zeroed", "loaded", "step", "turned", "out_done") as s,
            nc.Block() as block,
        ):
            flat = w.w[:].rearrange("p n q -> p (n q)")
            flatq = w.wq[:].rearrange("p n q -> p (n q)")
            STEPS = 16

            @block.sync
            def _(sp):
                sp.wait_ge(s.zeroed, 1)
                for m, name in enumerate(("L3_ffn_w_gate", "L3_ffn_w_up")):
                    for c, (at, rows) in enumerate(parts):
                        sp.dma_start(flat[0:rows, (3 * m + c) * D:(3 * m + c + 1) * D], a[name][at:at + rows, :]).then_inc(s.loaded, 16)
                sp.dma_start(flat[:, 6 * D:6 * D + I], a["L3_ffn_w_down"]).then_inc(s.loaded, 16)

            @block.vector
            def _(dve):
                dve.memset(w.w[:], 0.0).then_inc(s.zeroed, 1)
                dve.wait_ge(s.loaded, 16 * 7)
                steps = [0]

                def done(ins):
                    steps[0] += 1
                    ins.then_inc(s.step, 1)
                    dve.wait_ge(s.step, steps[0])

                fp4_steps(dve, done, w.w[:], w.wq[:], w.amax[:], w.inv[:], w.mag[:], NW)
                assert steps[0] == STEPS
                dve.wait_ge(s.turned, 1)
                dve.tensor_copy(u.wgT[:], PS[:, 0, 0:I]).then_inc(s.out_done, 1)
                dve.tensor_copy(u.wuT[:], PS[:, 1, 0:I]).then_inc(s.out_done, 1)
                for c, (_, rows) in enumerate(parts):
                    dve.tensor_copy(u.wdT[0:rows, c, :], PS[0:rows, 2, c * P:(c + 1) * P]).then_inc(s.out_done, 1)
                dve.wait_ge(s.out_done, 5)

            @block.tensor
            def _(pe):
                pe.wait_ge(s.step, STEPS)
                for m in range(2):
                    for c, (at, rows) in enumerate(parts):
                        pe.transpose(PS[:, m, at:at + rows], flatq[0:rows, (3 * m + c) * D:(3 * m + c + 1) * D],
                                     g.ident[0:rows, 0:rows])
                for c, (at, rows) in enumerate(parts):
                    last = pe.transpose(PS[0:rows, 2, c * P:(c + 1) * P], flatq[:, 6 * D + at:6 * D + at + rows], g.ident[:])
                last.then_inc(s.turned, 1)

        NX = NT * D // Q
        with (
            buffers(nc, x=((P, NX, Q), F32), amax=((P, NX), F32), inv=((P, NX), F32), mag=((P, NX, Q), F32)) as w,
            stage_semaphores(nc, "step") as s,
            nc.Block() as block,
        ):
            @block.vector
            def _(dve):
                steps = [0]

                def done(ins):
                    steps[0] += 1
                    ins.then_inc(s.step, 1)
                    dve.wait_ge(s.step, steps[0])

                done(dve.tensor_copy(w.x[:].rearrange("p n q -> p (n q)"), g.xn[:].rearrange("p t d -> p (t d)")))
                fp4_steps(dve, done, w.x[:], u.xq[:].rearrange("p t (m q) -> p (t m) q", q=Q), w.amax[:], w.inv[:],
                          w.mag[:], NX)
        turn_to_features(nc, g, u.xq, u.xqT)

        NH = QT * I // Q
        with (
            buffers(nc, src=((P, S), F32), gated=((P, QT, I), F32), h=((P, QT, I), F32), hq=((P, QT, I), F32),
                    hqT=((P, 3, S), F32), amax=((P, NH), F32), inv=((P, NH), F32), mag=((P, NH, Q), F32)) as w,
            nc.Fori(0, B) as b,
            stage_semaphores(nc, "src_done", "hidden_mm", "silu_done", "h_done", "step", "h_turned", "hT_done", "out_mm",
                             "added") as s,
            nc.Block() as block,
        ):
            STEPS = 16

            @block.tensor
            def _(pe):
                pe.wait_ge(s.src_done, 1)
                for j in range(QT):
                    pe.matmul(PS[:, 2 * j, 0:I], w.src[:, j * P:(j + 1) * P], u.wgT[:], start=True, stop=True)
                    pe.matmul(PS[:, 2 * j + 1, 0:I], w.src[:, j * P:(j + 1) * P], u.wuT[:], start=True,
                              stop=True).then_inc(s.hidden_mm, 1)
                pe.wait_ge(s.step, STEPS)
                for c, (at, rows) in enumerate(parts):
                    for j in range(QT):
                        last = pe.transpose(PS[0:rows, c, j * P:(j + 1) * P], w.hq[:, j, at:at + rows], g.ident[:])
                    last.then_inc(s.h_turned, 1)
                pe.wait_ge(s.hT_done, 3)
                for j in range(QT):
                    for c, (_, rows) in enumerate(parts):
                        last = pe.matmul(PS[:, 4, j * D:(j + 1) * D], w.hqT[0:rows, c, j * P:(j + 1) * P],
                                         u.wdT[0:rows, c, :], start=c == 0, stop=c == 2)
                last.then_inc(s.out_mm, 1)

            @block.scalar
            def _(act):
                for j in range(QT):
                    act.wait_ge(s.hidden_mm, j + 1)
                    act.activation(w.gated[:, j, :], PS[:, 2 * j, 0:I], ACT.Silu).then_inc(s.silu_done, 1)
                for c, (_, rows) in enumerate(parts):
                    act.wait_ge(s.h_turned, c + 1)
                    act.activation(w.hqT[0:rows, c, :], PS[0:rows, c, :], ACT.Copy).then_inc(s.hT_done, 1)

            @block.vector
            def _(dve):
                dve.tensor_copy(w.src[:], u.xqT[:, bass.ds(b * S, S)]).then_inc(s.src_done, 1)
                for j in range(QT):
                    dve.wait_ge(s.silu_done, j + 1)
                    dve.tensor_tensor(w.h[:, j, :], w.gated[:, j, :], PS[:, 2 * j + 1, 0:I], ALU.mult).then_inc(s.h_done, 1)
                dve.wait_ge(s.h_done, QT)
                steps = [0]

                def done(ins):
                    steps[0] += 1
                    ins.then_inc(s.step, 1)
                    dve.wait_ge(s.step, steps[0])

                fp4_steps(dve, done, w.h[:].rearrange("p j (m q) -> p (j m) q", q=Q),
                          w.hq[:].rearrange("p j (m q) -> p (j m) q", q=Q), w.amax[:], w.inv[:], w.mag[:], NH)
                dve.wait_ge(s.out_mm, 1)
                at = g.x[:, bass.ds(b * QT, QT), :]
                dve.tensor_tensor(at, at, PS[:, 4, :].rearrange("p (t d) -> p t d", d=D), ALU.add).then_inc(s.added, 1)


LAYERS = [layer0_attention, slots_from_context, layer0_ffn, layer1_attention, layer1_cross, layer1_ffn,
          layer2_attention, layer2_warp, layer2_ffn, layer3_attention, layer3_cross, layer3_ffn]


def decoder(nc, a, out, layers=None):
    with ExitStack() as held:
        def sb(name, shape, dt=F32):
            return held.enter_context(nc.sbuf_tensor(name, shape, dt))

        g = named(
            x=sb("x_tokens", [P, NT, D]), xn=sb("xn_tokens", [P, NT, D]), xnT=sb("xn_features", [P, NT * P]),
            ctxT=sb("ctx_features", [P, B * SC]), ident=sb("ident", [P, P]), ones=sb("ones", [P, P]),
            ident_bf=sb("ident_bf", [P, P], BF16), ones_bf=sb("ones_bf", [P, P], BF16),
            before=sb("before", [P, P], BF16), causal=sb("causal", [P, P], BF16), eta=sb("eta", [P, 1]),
            minus_e0=sb("minus_e0", [P, 1]),
            q_parts=nc.dram_tensor("q_parts", (B, PARTS, P, S), BF16).ap(),
            k_parts=nc.dram_tensor("k_parts", (B, PARTS, P, S), BF16).ap(),
            scattered=held.enter_context(nc.semaphore("scattered")), gathered=held.enter_context(nc.semaphore("gathered")),
            warp_skew=nc.dram_tensor("warp_skew", (P + 1, 190 * 16), F32).ap(),
            moe_in=nc.dram_tensor("expert_rows_in", (64 * 64, D), F32).ap(),
            moe_out=nc.dram_tensor("expert_rows_out", (64 * 64, D), F32).ap(),
            psum=held.enter_context(nc.psum_tensor("psum", [P, 8, 512], F32)))
        xs = a["x"].rearrange("b (t p) d -> p (b t) d", p=P)
        load(nc, [(g.x[:], xs), (g.ctxT[:], a["ctxT"])])
        constants(nc, g)
        for n, layer in enumerate(LAYERS):
            if layers is None or n in layers:
                layer(nc, g, a)
        with stage_semaphores(nc, "saved") as s, nc.Block() as block:
            @block.sync
            def _(sp):
                sp.dma_start(out.rearrange("b (t p) d -> p (b t) d", p=P), g.x[:]).then_inc(s.saved, 16)
                sp.wait_ge(s.saved, 16)


_TURNED = ["L0_attn_W1", "L0_attn_W2", "L0_attn_Wq", "L0_attn_Wk", "L0_attn_Wv", "L0_attn_Wo",
           "L0_xattn_Wq", "L0_xattn_Wk", "L0_xattn_Wv", "L0_xattn_gru_wih", "L0_xattn_gru_whh", "L1_attn_phase",
           "L0_ffn_gate_w", "L0_ffn_ws1", "L0_ffn_ws2", "L0_ffn_ws3", "L2_ffn_gate_w",
           "L1_xattn_W_Q", "L1_xattn_W_K", "L1_xattn_W_V", "L1_xattn_W_O", "L3_attn_Wq", "L3_attn_Wk", "L3_attn_Wv",
           "L3_attn_Wo"]


def laid_out(inputs):
    c = np.ascontiguousarray
    a = {k: np.asarray(v) for k, v in inputs.items()}
    for k in _TURNED:
        a[k + "T"] = c(a.pop(k).T)
    for k in "QKV":
        a[f"L2_attn_{k}T"] = a.pop(f"L2_attn_{k}").transpose(1, 2, 0).reshape(D, -1)
    for k in ("w1", "w2", "w3"):
        a[f"L0_ffn_{k}T"] = a.pop(f"L0_ffn_{k}").transpose(2, 0, 1)
    a["L2_attn_WT"] = a.pop("L2_attn_W").transpose(2, 1, 0).reshape(-1, D)
    for k in ("mask_BxSxS2_bf0", "mask_SxS2_bk1"):
        a[k + "T"] = np.swapaxes(a[k], -1, -2)
    ctx = a.pop("ctx_1024")
    a["ctx"] = ctx
    a["ctxT"] = c(ctx.reshape(B * SC, D).T)
    return {k: c(v) for k, v in a.items()}


def kernel(**inputs):
    import concourse.bacc as _bacc
    from concourse.bass_utils import run_bass_kernel_spmd as _run

    nc = _bacc.Bacc("TRN2", target_bir_lowering=False, num_devices=1)
    arrays = laid_out(inputs)
    aps = {k: nc.dram_tensor("in_" + k, v.shape, mybir.dt.from_np(v.dtype), kind="ExternalInput").ap()
           for k, v in arrays.items()}
    out = nc.dram_tensor("out_0", (B, S, D), F32, kind="ExternalOutput").ap()
    decoder(nc, aps, out)
    r = _run(nc, [{"in_" + k: v for k, v in arrays.items()}], core_ids=[0])
    return r.results[0]["out_0"]
```

```python
from collections import namedtuple
from contextlib import ExitStack, contextmanager
from itertools import count

import numpy as np

import concourse.bass as bass
from concourse import mybir

ALU = mybir.AluOpType
ACT = mybir.ActivationFunctionType
AX = mybir.AxisListType
F32 = mybir.dt.float32
BF16 = mybir.dt.bfloat16
U32 = mybir.dt.uint32
I32 = mybir.dt.int32
U8 = mybir.dt.uint8

P = 128
D = 128
B = 4
S = 512
QT = S // P
NT = B * QT
SC = 154
SERIAL = count()
MASKED = -1.0e30


def named(**items):
    return namedtuple("Named", list(items))(**items)


def ctx_tiles():
    return [(0, P), (P, SC - P)]


@contextmanager
def stage_semaphores(nc, *names):
    with ExitStack() as held:
        sems = {n: held.enter_context(nc.semaphore(n)) for n in names}
        yield named(**sems)
        with nc.Block() as block:
            @block.sync
            def _(sp):
                for s in sems.values():
                    sp.sem_clear(s)


@contextmanager
def buffers(nc, **shapes):
    stage = next(SERIAL)
    with ExitStack() as held:
        yield named(**{n: held.enter_context(nc.sbuf_tensor(f"{n}_{stage}", list(s), t))
                                 for n, (s, t) in shapes.items()})


@contextmanager
def zeroed(nc, tile):
    with stage_semaphores(nc, "zeros_in") as s, nc.Block() as block:
        @block.vector
        def _(dve):
            dve.memset(tile[:], 0.0).then_inc(s.zeros_in, 1)
            dve.wait_ge(s.zeros_in, 1)
    yield tile


def load(nc, pairs):
    with stage_semaphores(nc, "loaded") as s:
        with nc.Block() as block:
            @block.sync
            def _(sp):
                for n, (dst, src) in enumerate(pairs):
                    sp.dma_start(dst, src, allow_slow_non_contiguous=True).then_inc(s.loaded, 16)
                sp.wait_ge(s.loaded, 16 * len(pairs))


def constants(nc, g):
    with stage_semaphores(nc, "filled", "selected") as s:
        with nc.Block() as block:
            @block.gpsimd
            def _(pool):
                pool.memset(g.ident[:], 0.0).then_inc(s.filled, 1)
                pool.memset(g.ones[:], 1.0).then_inc(s.filled, 1)
                pool.memset(g.ones_bf[:], 1.0).then_inc(s.filled, 1)
                pool.memset(g.before[:], 1.0).then_inc(s.filled, 1)
                pool.memset(g.causal[:], 0.0).then_inc(s.filled, 1)
                pool.memset(g.eta[:], 1.0).then_inc(s.filled, 1)
                pool.memset(g.minus_e0[:], 0.0).then_inc(s.filled, 1)
                pool.wait_ge(s.filled, 7)
                pool.affine_select(out=g.ident[:], in_=g.ident[:], compare_op=ALU.not_equal, fill=1.0, base=0,
                                   pattern=[[-1, P]], channel_multiplier=1).then_inc(s.selected, 1)
                pool.affine_select(out=g.before[:], in_=g.before[:], compare_op=ALU.is_gt, fill=0.0, base=0,
                                   pattern=[[1, P]], channel_multiplier=-1).then_inc(s.selected, 1)
                pool.affine_select(out=g.causal[:], in_=g.causal[:], compare_op=ALU.is_ge, fill=MASKED, base=0,
                                   pattern=[[-1, P]], channel_multiplier=1).then_inc(s.selected, 1)
                pool.memset(g.eta[0:1, 0:1], -1.0).then_inc(s.filled, 1)
                pool.memset(g.minus_e0[0:1, :], -1.0).then_inc(s.filled, 1)
                pool.wait_ge(s.selected, 1)
                pool.tensor_copy(g.ident_bf[:], g.ident[:]).then_inc(s.selected, 1)
                pool.wait_ge(s.selected, 4)
                pool.wait_ge(s.filled, 9)


def layernorm(nc, g):
    with (
        buffers(nc, stats=((P, NT, 6), F32), mv=((P, NT, 2), F32), rstd=((P, NT), F32)) as u,
        stage_semaphores(nc, "stats_done", "mean_done", "var_done", "sd_done", "rstd_done", "normed_done",
                         "turned", "feature_major_done") as s,
        nc.Block() as block,
    ):
        def tiles(b):
            return range(b * QT, (b + 1) * QT)

        @block.vector
        def _(dve):
            for b in range(B + 1):
                if b < B:
                    for t in tiles(b):
                        dve.bn_stats(u.stats[:, t, :], g.x[:, t, :]).then_inc(s.stats_done, 1)
                    for t in tiles(b):
                        dve.wait_ge(s.stats_done, t + 1)
                        dve.bn_aggr(u.mv[:, t, :], u.stats[:, t, :]).then_inc(s.mean_done, 1)
                    dve.wait_ge(s.mean_done, QT * (b + 1))
                    dve.tensor_scalar(u.rstd[:, b * QT:(b + 1) * QT], u.mv[:, b * QT:(b + 1) * QT, 1], 1e-5, None,
                                      ALU.add).then_inc(s.var_done, 1)
                if b >= 1:
                    last = slice((b - 1) * QT, b * QT)
                    dve.wait_ge(s.sd_done, b)
                    dve.reciprocal(u.rstd[:, last], u.rstd[:, last]).then_inc(s.rstd_done, 1)
                    dve.wait_ge(s.rstd_done, b)
                    for t in tiles(b - 1):
                        dve.tensor_scalar(g.xn[:, t, :], g.x[:, t, :], u.mv[:, t, 0:1], u.rstd[:, t:t + 1],
                                          ALU.subtract, ALU.mult).then_inc(s.normed_done, 1)

        @block.scalar
        def _(act):
            for b in range(B + 1):
                if b < B:
                    act.wait_ge(s.var_done, b + 1)
                    act.activation(u.rstd[:, b * QT:(b + 1) * QT], u.rstd[:, b * QT:(b + 1) * QT],
                                   ACT.Sqrt).then_inc(s.sd_done, 1)
                if b >= 1:
                    act.wait_ge(s.turned, b)
                    act.activation(g.xnT[:, (b - 1) * S:b * S], g.psum[:, b - 1, :],
                                   ACT.Copy).then_inc(s.feature_major_done, 1)

        @block.tensor
        def _(pe):
            for b in range(B):
                for j in range(QT):
                    pe.wait_ge(s.normed_done, b * QT + j + 1)
                    last = pe.transpose(g.psum[:, b, j * P:(j + 1) * P], g.xn[:, b * QT + j, :], g.ident[:])
                last.then_inc(s.turned, 1)


def turn_to_features(nc, g, src, dstT):
    with (
        buffers(nc, fixed=((P, QT, D), F32)) as u,
        nc.Fori(0, B) as b,
        stage_semaphores(nc, "fixed_done", "turned", "feature_major_done") as s,
        nc.Block() as block,
    ):
        @block.vector
        def _(dve):
            dve.tensor_copy(u.fixed[:], src[:, bass.ds(b * QT, QT), :]).then_inc(s.fixed_done, 1)

        @block.tensor
        def _(pe):
            pe.wait_ge(s.fixed_done, 1)
            for j in range(QT):
                last = pe.transpose(g.psum[:, 0, j * P:(j + 1) * P], u.fixed[:, j, :], g.ident[:])
            last.then_inc(s.turned, 1)

        @block.scalar
        def _(act):
            act.wait_ge(s.turned, 1)
            act.activation(dstT[:, bass.ds(b * S, S)], g.psum[:, 0, :], ACT.Copy).then_inc(s.feature_major_done, 1)


def attention(nc, g, *, w, H, dh, hp, keys, kv_src, scale, q_src=None, causal=False, mask=None, metric=None,
              add_to=None, store=None, out_scale=1.0, zero_if_all_masked=False, bq=None, bk=None, bv=None, bo=None):
    G = H * hp // P
    per = P // hp
    dv = dh
    HV = H * dv
    OC = HV // P
    KT = len(keys)
    SK = keys[-1][0] + keys[-1][1]
    VN = max(1, HV // 512)
    VW = HV // VN
    q_src = q_src if q_src is not None else g.xnT
    jobs_v = [(t, n) for t in range(KT) for n in range(VN)]
    NQK = 2 * G
    NJOBS = NQK + len(jobs_v)
    NB = QT * H

    shapes = dict(srcq=((P, S), F32), srck=((P, SK), F32), qT=((P, G, S), F32), kT=((P, H, SK), F32),
                  v=((P, KT, HV), F32), probs=((P, 3, S), F32), probsT=((P, 2, KT * P), F32),
                  nmax=((P, QT, H), F32), rsum=((P, QT, H), F32), rinv=((P, 2, H), F32),
                  o=((P, 2, HV), F32), oT=((P, 2, HV), F32))
    if mask is not None:
        shapes["mask_add"] = ((P, QT, SK), BF16)
        shapes["live"] = ((P, 2, H), F32)
    if metric is not None:
        shapes.update(metric_src=((P, S), F32), hidden=((P, 2, S), F32), gx=((P, 2, S), F32))
    with (
        buffers(nc, **shapes) as u,
        zeroed(nc, u.kT),
        nc.Fori(0, B) as b,
        stage_semaphores(nc, "src_done", "product_done", "even_out", "odd_out", "mask_done",
                         "scores_done", "max_done", "probs_done", "probs_turned", "probsT_done", "heads_done",
                         "rinv_done", "o_done", "o_turned", "oT_done", "projected", "stored", "chain",
                         "metric_in", "hidden_mm", "hidden_done", "gx_mm", "gx_tanh", "gx_done") as s,
    ):
        with nc.Block() as block:
            @block.vector
            def _(dve):
                dve.tensor_copy(u.srcq[:], q_src[:, bass.ds(b * S, S)]).then_inc(s.src_done, 1)
                dve.tensor_copy(u.srck[:], kv_src[:, bass.ds(b * SK, SK)]).then_inc(s.src_done, 1)
                if metric is not None:
                    dve.tensor_scalar(u.metric_src[:], g.xnT[:, bass.ds(b * S, S)], g.minus_e0[:, 0:1], None,
                                      ALU.add).then_inc(s.metric_in, 1)
                if mask is not None:
                    kind, m = mask
                    src = m[:, bass.ds(b * QT, QT), :] if kind == "drop" else m[:]
                    if kind == "drop":
                        dve.tensor_scalar(u.mask_add[:], src, MASKED, None, ALU.mult).then_inc(s.mask_done, 1)
                    else:
                        dve.tensor_scalar(u.mask_add[:], src, -1.0, -MASKED, ALU.add, ALU.mult).then_inc(s.mask_done, 1)
                for n in range(1, NJOBS, 2):
                    dve.wait_ge(s.product_done, n + 1)
                    if n < NQK:
                        i = n // 2
                        for j in range(per):
                            rows = slice(j * hp, (j + 1) * hp)
                            ins = dve.tensor_copy(u.kT[rows, i * per + j, :], g.psum[rows, n % 8, 0:SK])
                    else:
                        t, c = jobs_v[n - NQK]
                        rows = keys[t][1]
                        ins = dve.tensor_copy(u.v[0:rows, t, c * VW:(c + 1) * VW], g.psum[0:rows, n % 8, 0:VW])
                    ins.then_inc(s.odd_out, 1)

            @block.scalar
            def _(act):
                for n in range(0, NJOBS, 2):
                    act.wait_ge(s.product_done, n + 1)
                    if n < NQK:
                        i = n // 2
                        bias = bq[:, i:i + 1] if bq is not None else 0.0
                        ins = act.activation(u.qT[:, i, :], g.psum[:, n % 8, :], ACT.Identity, bias=bias, scale=scale)
                    else:
                        t, c = jobs_v[n - NQK]
                        rows = keys[t][1]
                        ins = act.activation(u.v[0:rows, t, c * VW:(c + 1) * VW], g.psum[0:rows, n % 8, 0:VW], ACT.Copy)
                    ins.then_inc(s.even_out, 1)

            @block.tensor
            def _(pe):
                pe.wait_ge(s.src_done, 2)
                for n in range(NJOBS):
                    if n >= 8 and n % 2 == 0:
                        pe.wait_ge(s.even_out, n // 2 - 3)
                    if n >= 8 and n % 2 == 1:
                        pe.wait_ge(s.odd_out, n // 2 - 3)
                    if n < NQK:
                        i = n // 2
                        if n % 2 == 0:
                            last = pe.matmul(g.psum[:, n % 8, :], w.wq[:, i, :], u.srcq[:], start=True, stop=True)
                        else:
                            last = pe.matmul(g.psum[:, n % 8, 0:SK], w.wk[:, i, :], u.srck[:], start=True, stop=True)
                    else:
                        t, c = jobs_v[n - NQK]
                        at, rows = keys[t]
                        out = g.psum[0:rows, n % 8, 0:VW]
                        last = pe.matmul(out, u.srck[:, at:at + rows], w.wv[:, c * VW:(c + 1) * VW],
                                         start=True, stop=bv is None)
                        if bv is not None:
                            last = pe.matmul(out, g.ones[0:1, 0:rows], bv[0:1, c * VW:(c + 1) * VW],
                                             start=False, stop=True)
                    last.then_inc(s.product_done, 1)

        if metric is not None:
            with nc.Block() as block:
                @block.tensor
                def _(pe):
                    for c in range(2):
                        pe.matmul(g.psum[:, c, :], metric.w1[:, c, :], u.metric_src[:], start=True,
                                  stop=True).then_inc(s.hidden_mm, 1)
                    pe.wait_ge(s.hidden_done, 2)
                    for i in range(G):
                        if i >= 2:
                            pe.wait_ge(s.gx_tanh, i - 1)
                        pe.matmul(g.psum[:, 2 + i % 2, :], metric.w2[:, 0, i, :], u.hidden[:, 0, :], start=True, stop=False)
                        pe.matmul(g.psum[:, 2 + i % 2, :], metric.w2[:, 1, i, :], u.hidden[:, 1, :], start=False,
                                  stop=True).then_inc(s.gx_mm, 1)

                @block.scalar
                def _(act):
                    for c in range(2):
                        act.wait_ge(s.hidden_mm, c + 1)
                        act.activation(u.hidden[:, c, :], g.psum[:, c, :], ACT.Tanh,
                                       bias=metric.b1[:, c:c + 1]).then_inc(s.hidden_done, 1)
                    for i in range(G):
                        act.wait_ge(s.gx_mm, i + 1)
                        if i >= 2:
                            act.wait_ge(s.gx_done, i - 1)
                        act.activation(u.gx[:, i % 2, :], g.psum[:, 2 + i % 2, :], ACT.Tanh,
                                       bias=metric.b2[:, i:i + 1]).then_inc(s.gx_tanh, 1)

                @block.vector
                def _(dve):
                    for i in range(G):
                        eta = g.eta[:, i:i + 1]
                        gx = u.gx[:, i % 2, :]
                        dve.wait_ge(s.gx_tanh, i + 1)
                        dve.tensor_scalar(gx, gx, 0.1, eta, ALU.mult, ALU.add).then_inc(s.chain, 1)
                        dve.wait_ge(s.chain, 2 * i + 1)
                        dve.scalar_tensor_tensor(out=gx, in0=gx, scalar=-1.0, in1=gx, op0=ALU.mult,
                                                 op1=ALU.max).then_inc(s.chain, 1)
                        dve.wait_ge(s.chain, 2 * i + 2)
                        dve.scalar_tensor_tensor(out=u.qT[:, i, :], in0=gx, scalar=eta, in1=u.qT[:, i, :], op0=ALU.mult,
                                                 op1=ALU.mult).then_inc(s.gx_done, 1)

        SCORES, TURNED, OUT, OTURN, FINAL = 0, 2, 4, 6, 7

        def width(n):
            return (n // H + 1) * P if causal else SK

        def tiles(n):
            return n // H + 1 if causal else KT

        def out_bank(q, lo, hi):
            if OC == 1:
                return g.psum[:, OUT + q % 2, lo:hi]
            return g.psum[:, OUT + lo // 512, lo % 512:lo % 512 + hi - lo]

        with nc.Block() as block:
            @block.tensor
            def _(pe):
                def scores(n):
                    q, h = n // H, n % H
                    N = width(n)
                    if n >= 2:
                        pe.wait_ge(s.probs_done, n - 1)
                    out = g.psum[:, SCORES + n % 2, 0:N]
                    masked = mask is not None
                    last = pe.matmul(out, u.qT[:, h // per, q * P:(q + 1) * P], u.kT[:, h, 0:N],
                                     start=True, stop=not (masked or causal))
                    if masked:
                        last = pe.matmul(out, g.ident_bf[:], u.mask_add[:, q, :], start=False, stop=True)
                    if causal:
                        last = pe.matmul(g.psum[:, SCORES + n % 2, N - P:N], g.ident_bf[:], g.causal[:],
                                         start=False, stop=True)
                    last.then_inc(s.scores_done, 1)

                def turn(n):
                    pe.wait_ge(s.probs_done, n + 1)
                    if n >= 2:
                        pe.wait_ge(s.probsT_done, n - 1)
                    for t in range(tiles(n)):
                        at, rows = keys[t]
                        last = pe.transpose(g.psum[0:rows, TURNED + n % 2, t * P:(t + 1) * P],
                                            u.probs[:, n % 3, at:at + rows], g.ident[:])
                    last.then_inc(s.probs_turned, 1)

                def heads(n):
                    q, h = n // H, n % H
                    pe.wait_ge(s.probsT_done, n + 1)
                    if h == 0 and (q >= 2 or (q >= 1 and OC > 1)):
                        pe.wait_ge(s.o_done, q - 1 if OC == 1 else q)
                    for t in range(tiles(n)):
                        rows = keys[t][1]
                        last = pe.matmul(out_bank(q, h * dv, (h + 1) * dv), u.probsT[0:rows, n % 2, t * P:(t + 1) * P],
                                         u.v[0:rows, t, h * dv:(h + 1) * dv], start=t == 0, stop=t == tiles(n) - 1)
                    last.then_inc(s.heads_done, 1)

                def project(q):
                    pe.wait_ge(s.o_done, q + 1)
                    for c0 in range(0, OC, 4):
                        n = q * ((OC + 3) // 4) + c0 // 4
                        if n >= 1:
                            pe.wait_ge(s.oT_done, n)
                        for c in range(c0, min(OC, c0 + 4)):
                            last = pe.transpose(g.psum[:, OTURN, (c % 4) * P:(c % 4 + 1) * P],
                                                u.o[:, q % 2, c * P:(c + 1) * P], g.ident[:])
                        last.then_inc(s.o_turned, 1)
                    pe.wait_ge(s.oT_done, (q + 1) * ((OC + 3) // 4))
                    if q >= 1:
                        pe.wait_ge(s.stored, q)
                    for c in range(OC):
                        last = pe.matmul(g.psum[:, FINAL, 0:D], u.oT[:, q % 2, c * P:(c + 1) * P], w.wo[:, c, :],
                                         start=c == 0, stop=c == OC - 1 and bo is None)
                    if bo is not None:
                        last = pe.matmul(g.psum[:, FINAL, 0:D], g.ones[0:1, :], bo[0:1, :], start=False, stop=True)
                    last.then_inc(s.projected, 1)

                if mask is not None:
                    pe.wait_ge(s.mask_done, 1)
                for n in range(NB + 3):
                    if n < NB:
                        scores(n)
                    if 2 <= n < NB + 2:
                        turn(n - 2)
                    if n >= 3:
                        heads(n - 3)
                    if n >= 6 and (n - 6) % H == H - 1:
                        project((n - 6) // H)
                project(QT - 1)

            @block.vector
            def _(dve):
                def maximum(n):
                    dve.wait_ge(s.scores_done, n + 1)
                    dve.tensor_reduce(u.nmax[:, n // H, n % H:n % H + 1], g.psum[:, SCORES + n % 2, 0:width(n)], AX.X,
                                      ALU.max, negate=True).then_inc(s.max_done, 1)

                def copy_turned(n):
                    dve.wait_ge(s.probs_turned, n + 1)
                    if n >= 2:
                        dve.wait_ge(s.heads_done, n - 1)
                    full = [t for t in range(tiles(n)) if keys[t][1] == P]
                    ins = dve.tensor_copy(u.probsT[:, n % 2, 0:len(full) * P],
                                          g.psum[:, TURNED + n % 2, 0:len(full) * P])
                    if len(full) < tiles(n):
                        t, rows = tiles(n) - 1, keys[tiles(n) - 1][1]
                        ins = dve.tensor_copy(u.probsT[0:rows, n % 2, t * P:(t + 1) * P],
                                              g.psum[0:rows, TURNED + n % 2, t * P:(t + 1) * P])
                    ins.then_inc(s.probsT_done, 1)

                def normalise(q):
                    dve.wait_ge(s.heads_done, H * (q + 1))
                    if q >= 2:
                        dve.wait_ge(s.projected, q - 1)
                    dve.wait_ge(s.probs_done, H * (q + 1))
                    dve.reciprocal(u.rinv[:, q % 2, :], u.rsum[:, q, :]).then_inc(s.rinv_done, 1)
                    per_q = 1
                    if zero_if_all_masked:
                        dve.tensor_scalar(u.live[:, q % 2, :], u.nmax[:, q, :], -MASKED / 2, None,
                                          ALU.is_lt).then_inc(s.rinv_done, 1)
                        dve.wait_ge(s.rinv_done, 3 * q + 2)
                        dve.tensor_tensor(u.rinv[:, q % 2, :], u.rinv[:, q % 2, :], u.live[:, q % 2, :],
                                          ALU.mult).then_inc(s.rinv_done, 1)
                        per_q = 3
                    dve.wait_ge(s.rinv_done, per_q * (q + 1))
                    step = min(HV, 512)
                    for lo in range(0, HV, step):
                        hs = step // dv
                        h0 = lo // dv
                        ins = dve.tensor_tensor(
                            u.o[:, q % 2, lo:lo + step].rearrange("p (h d) -> p h d", d=dv),
                            out_bank(q, lo, lo + step).rearrange("p (h d) -> p h d", d=dv),
                            u.rinv[:, q % 2, h0:h0 + hs].unsqueeze(2).to_broadcast([P, hs, dv]), ALU.mult)
                    ins.then_inc(s.o_done, 1)

                def put(q):
                    dve.wait_ge(s.projected, q + 1)
                    if add_to is not None:
                        at = add_to[:, bass.ds(b * QT + q, 1), :]
                        dve.scalar_tensor_tensor(out=at, in0=g.psum[:, FINAL, 0:D].unsqueeze(1), scalar=out_scale, in1=at,
                                                 op0=ALU.mult, op1=ALU.add).then_inc(s.stored, 1)
                    else:
                        dve.tensor_scalar(store[:, bass.ds(b * QT + q, 1), :], g.psum[:, FINAL, 0:D].unsqueeze(1), out_scale,
                                          None, ALU.mult).then_inc(s.stored, 1)

                for n in range(NB + 3):
                    if n < NB:
                        maximum(n)
                    if 2 <= n < NB + 2:
                        copy_turned(n - 2)
                    if n >= 3 and (n - 3) % H == H - 1:
                        normalise((n - 3) // H)
                    if n >= 8 and (n - 8) % H == H - 1:
                        put((n - 8) // H)
                put(QT - 1)

            @block.scalar
            def _(act):
                def copy_o(q):
                    for c0 in range(0, OC, 4):
                        n = q * ((OC + 3) // 4) + c0 // 4
                        act.wait_ge(s.o_turned, n + 1)
                        if q >= 2:
                            act.wait_ge(s.projected, q - 1)
                        wd = min(4, OC - c0) * P
                        act.activation(u.oT[:, q % 2, c0 * P:c0 * P + wd], g.psum[:, OTURN, 0:wd],
                                       ACT.Copy).then_inc(s.oT_done, 1)

                for n in range(NB + 3):
                    if n < NB:
                        act.wait_ge(s.max_done, n + 1)
                        if n >= 3:
                            act.wait_ge(s.probs_turned, n - 2)
                        act.activation(u.probs[:, n % 3, 0:width(n)], g.psum[:, SCORES + n % 2, 0:width(n)], ACT.Exp,
                                       bias=u.nmax[:, n // H, n % H:n % H + 1],
                                       accum_out=u.rsum[:, n // H, n % H:n % H + 1]).then_inc(s.probs_done, 1)
                    if n >= 6 and (n - 6) % H == H - 1:
                        copy_o((n - 6) // H)
                copy_o(QT - 1)


ALL_KEYS = [(t * P, P) for t in range(QT)]


def log_map(nc, g, dst):
    EPS = 1e-6
    with (
        buffers(nc, sq=((P, NT, D), F32), n2=((P, NT), F32), y0=((P, NT), F32), z=((P, NT), F32), t0=((P, NT), F32),
                a=((P, NT), F32), c=((P, NT), F32)) as u,
        stage_semaphores(nc, "step", "rooted") as s,
        nc.Block() as block,
    ):
        @block.vector
        def _(dve):
            steps = [0]

            def done(ins):
                steps[0] += 1
                ins.then_inc(s.step, 1)
                dve.wait_ge(s.step, steps[0])

            tail = dst[:, :, 1:D]
            done(dve.tensor_scalar(tail, g.xn[:, :, 1:D], -8.0, 8.0, ALU.max, ALU.min))
            done(dve.tensor_tensor(u.sq[:, :, 1:D], tail, tail, ALU.mult))
            done(dve.tensor_reduce(u.n2[:], u.sq[:, :, 1:D], AX.X, ALU.add))
            done(dve.tensor_scalar(u.y0[:], u.n2[:], 1.0, EPS, ALU.add, ALU.add))
            dve.wait_ge(s.rooted, 1)
            done(dve.tensor_scalar(u.z[:], u.y0[:], 1.0 + EPS, None, ALU.max))
            done(dve.tensor_tensor(u.t0[:], u.y0[:], u.z[:], ALU.subtract))
            done(dve.tensor_tensor(u.c[:], u.t0[:], u.t0[:], ALU.mult))
            done(dve.tensor_tensor(u.c[:], u.n2[:], u.c[:], ALU.subtract))
            done(dve.tensor_scalar(u.c[:], u.c[:], EPS, None, ALU.max))
            done(dve.tensor_tensor(u.a[:], u.z[:], u.z[:], ALU.mult))
            done(dve.tensor_scalar(u.a[:], u.a[:], -1.0, None, ALU.add))
            dve.wait_ge(s.rooted, 3)
            done(dve.tensor_tensor(u.a[:], u.a[:], u.z[:], ALU.add))
            dve.wait_ge(s.rooted, 4)
            done(dve.tensor_scalar(u.a[:], u.a[:], 1e-3, None, ALU.max))
            done(dve.tensor_scalar(u.c[:], u.c[:], EPS, None, ALU.add))
            done(dve.reciprocal(u.c[:], u.c[:]))
            done(dve.tensor_tensor(u.a[:], u.a[:], u.c[:], ALU.mult))
            done(dve.tensor_copy(dst[:, :, 0], u.t0[:]))
            done(dve.tensor_tensor(dst[:], dst[:], u.a[:].unsqueeze(2).to_broadcast([P, NT, D]), ALU.mult))

        @block.scalar
        def _(act):
            act.wait_ge(s.step, 4)
            act.activation(u.y0[:], u.y0[:], ACT.Sqrt).then_inc(s.rooted, 1)
            act.wait_ge(s.step, 11)
            act.activation(u.c[:], u.c[:], ACT.Sqrt).then_inc(s.rooted, 1)
            act.activation(u.a[:], u.a[:], ACT.Sqrt).then_inc(s.rooted, 1)
            act.wait_ge(s.step, 12)
            act.activation(u.a[:], u.a[:], ACT.Ln).then_inc(s.rooted, 1)


def project_and_add(nc, g, o):
    EPS = 1e-6
    with (
        buffers(nc, sq=((P, NT, D), F32), n2=((P, NT), F32)) as u,
        stage_semaphores(nc, "step", "rooted") as s,
        nc.Block() as block,
    ):
        @block.vector
        def _(dve):
            dve.tensor_scalar(o[:, :, 1:D], o[:, :, 1:D], -8.0, 8.0, ALU.max, ALU.min).then_inc(s.step, 1)
            dve.wait_ge(s.step, 1)
            dve.tensor_tensor(u.sq[:, :, 1:D], o[:, :, 1:D], o[:, :, 1:D], ALU.mult).then_inc(s.step, 1)
            dve.wait_ge(s.step, 2)
            dve.tensor_reduce(u.n2[:], u.sq[:, :, 1:D], AX.X, ALU.add).then_inc(s.step, 1)
            dve.wait_ge(s.step, 3)
            dve.tensor_scalar(u.n2[:], u.n2[:], 1.0, EPS, ALU.add, ALU.add).then_inc(s.step, 1)
            dve.wait_ge(s.rooted, 1)
            dve.tensor_tensor(g.x[:], g.x[:], o[:], ALU.add).then_inc(s.step, 1)

        @block.scalar
        def _(act):
            act.wait_ge(s.step, 4)
            act.activation(o[:, :, 0], u.n2[:], ACT.Sqrt).then_inc(s.rooted, 1)


H16, DH8, G4 = 16, 8, 4
HG = H16 // G4
HW = P // HG
PARTS = 3
PAIRED = [(0, 0), (0, 1), (1, 0), (0, 2), (1, 1), (2, 0)]
STACK_DMAS = 2 * len(PAIRED)
MAX_AT = 96
MAX_END = MAX_AT + PARTS * HG


def split_projections(nc, g, w, q_src, kv_src, scale, SK, bq, bk, metric):
    LANES = 2
    lanes = range(LANES)
    shapes = dict(q=((P, LANES, S), F32), k=((P, LANES, SK), F32), q_left=((P, LANES, S), F32),
                  k_left=((P, LANES, SK), F32), q_parts=((P, LANES, PARTS, S), BF16),
                  k_parts=((P, LANES, PARTS, SK), BF16))
    if metric is not None:
        shapes.update(metric_src=((P, LANES, S), F32), hidden=((P, LANES, 2, S), F32), gx=((P, LANES, S), F32))
    K, Q, HID, GX = 0, 1, 2, 0
    with (
        buffers(nc, **shapes) as u,
        nc.Fori(0, B // LANES) as pair,
        stage_semaphores(nc, "q_mm", "k_mm", "q_out", "q_ready", "k_ready", "k_first", "k_rest", "k_second", "k_done",
                         "q_first", "q_rest", "q_second", "q_done", "metric_in", "hidden_mm", "hidden_done", "gx_mm",
                         "gx_tanh", "gx_eta", "gx_abs", "written") as s,
        nc.Block() as block,
    ):
        def bank(c, n):
            return g.psum[:, 4 * c + n, :]

        @block.tensor
        def _(pe):
            for c in lanes:
                pe.matmul(bank(c, K)[:, 0:SK], w.wk[:], kv_src[:, bass.ds((pair * LANES + c) * SK, SK)], start=True,
                          stop=True).then_inc(s.k_mm, 1)
                pe.matmul(bank(c, Q), w.wq[:], q_src[:, bass.ds((pair * LANES + c) * S, S)], start=True,
                          stop=True).then_inc(s.q_mm, 1)
            if metric is not None:
                for c in lanes:
                    pe.wait_ge(s.metric_in, c + 1)
                    for n in range(2):
                        pe.matmul(bank(c, HID + n), metric.w1[:, n, :], u.metric_src[:, c, :], start=True,
                                  stop=True).then_inc(s.hidden_mm, 1)
                for c in lanes:
                    pe.wait_ge(s.k_ready, c + 1)
                    for n in range(2):
                        pe.wait_ge(s.hidden_done, 2 * c + n + 1)
                        last = pe.matmul(bank(c, GX), metric.w2[:, n, :], u.hidden[:, c, n, :], start=n == 0, stop=n == 1)
                    last.then_inc(s.gx_mm, 1)

        @block.scalar
        def _(act):
            for c in lanes:
                act.wait_ge(s.k_mm, c + 1)
                act.activation(u.k[:, c, :], bank(c, K)[:, 0:SK], ACT.Identity,
                               bias=bk[:, 0:1] if bk is not None else 0.0).then_inc(s.k_ready, 1)
                act.wait_ge(s.q_mm, c + 1)
                act.activation(u.q[:, c, :], bank(c, Q), ACT.Identity, bias=bq[:, 0:1] if bq is not None else 0.0,
                               scale=scale).then_inc(s.q_out, 1)
                act.wait_ge(s.k_ready, c + 1)
                act.activation(u.k_parts[:, c, 0, :], u.k[:, c, :], ACT.Copy).then_inc(s.k_first, 1)
            if metric is not None:
                for c in lanes:
                    for n in range(2):
                        act.wait_ge(s.hidden_mm, 2 * c + n + 1)
                        act.activation(u.hidden[:, c, n, :], bank(c, HID + n), ACT.Tanh,
                                       bias=metric.b1[:, n:n + 1]).then_inc(s.hidden_done, 1)
                for c in lanes:
                    act.wait_ge(s.gx_mm, c + 1)
                    act.activation(u.gx[:, c, :], bank(c, GX), ACT.Tanh, bias=metric.b2[:, 0:1]).then_inc(s.gx_tanh, 1)
            for c in lanes:
                act.wait_ge(s.k_rest, c + 1)
                act.activation(u.k_parts[:, c, 1, :], u.k_left[:, c, :], ACT.Copy).then_inc(s.k_second, 1)
                act.wait_ge(s.q_ready if metric is not None else s.q_out, c + 1)
                act.activation(u.q_parts[:, c, 0, :], u.q[:, c, :], ACT.Copy).then_inc(s.q_first, 1)
            for c in lanes:
                act.wait_ge(s.q_rest, c + 1)
                act.activation(u.q_parts[:, c, 1, :], u.q_left[:, c, :], ACT.Copy).then_inc(s.q_second, 1)

        @block.vector
        def _(dve):
            if metric is not None:
                for c in lanes:
                    dve.tensor_scalar(u.metric_src[:, c, :], g.xnT[:, bass.ds((pair * LANES + c) * S, S)],
                                      g.minus_e0[:, 0:1], None, ALU.add).then_inc(s.metric_in, 1)
            for c in lanes:
                dve.wait_ge(s.k_first, c + 1)
                dve.tensor_tensor(u.k_left[:, c, :], u.k[:, c, :], u.k_parts[:, c, 0, :], ALU.subtract).then_inc(s.k_rest, 1)
            for c in lanes:
                if metric is not None:
                    gx = u.gx[:, c, :]
                    dve.wait_ge(s.gx_tanh, c + 1)
                    dve.tensor_scalar(gx, gx, 0.1, g.eta[:, 0:1], ALU.mult, ALU.add).then_inc(s.gx_eta, 1)
                    dve.wait_ge(s.gx_eta, c + 1)
                    dve.scalar_tensor_tensor(out=gx, in0=gx, scalar=-1.0, in1=gx, op0=ALU.mult,
                                             op1=ALU.max).then_inc(s.gx_abs, 1)
                    dve.wait_ge(s.gx_abs, c + 1)
                    dve.wait_ge(s.q_out, c + 1)
                    dve.scalar_tensor_tensor(out=u.q[:, c, :], in0=gx, scalar=g.eta[:, 0:1], in1=u.q[:, c, :],
                                             op0=ALU.mult, op1=ALU.mult).then_inc(s.q_ready, 1)
                dve.wait_ge(s.k_second, c + 1)
                dve.tensor_tensor(u.k_parts[:, c, 2, :], u.k_left[:, c, :], u.k_parts[:, c, 1, :],
                                  ALU.subtract).then_inc(s.k_done, 1)
            for c in lanes:
                dve.wait_ge(s.q_first, c + 1)
                dve.tensor_tensor(u.q_left[:, c, :], u.q[:, c, :], u.q_parts[:, c, 0, :], ALU.subtract).then_inc(s.q_rest, 1)
            for c in lanes:
                dve.wait_ge(s.q_second, c + 1)
                dve.tensor_tensor(u.q_parts[:, c, 2, :], u.q_left[:, c, :], u.q_parts[:, c, 1, :],
                                  ALU.subtract).then_inc(s.q_done, 1)

        @block.sync
        def _(sp):
            def save(parts, src, N, batch):
                sp.dma_start(parts[batch, :, :, 0:N].rearrange("o c p s -> (o p) c s"), src).then_inc(s.written, 16)

            last = LANES - 1
            for c in lanes:
                sp.wait_ge(s.k_done, c + 1)
                save(g.k_parts, u.k_parts[:, c], SK, bass.ds(pair * LANES + c, 1))
            save(g.k_parts, u.k_parts[:, last], SK, slice(B, B + 1))
            for c in lanes:
                sp.wait_ge(s.q_done, c + 1)
                save(g.q_parts, u.q_parts[:, c], S, bass.ds(pair * LANES + c, 1))
            save(g.q_parts, u.q_parts[:, last], S, slice(B, B + 1))
            sp.wait_ge(s.written, 16 * 2 * (LANES + 1))


def prepare_stacks(nc, g):
    with buffers(nc, sel=((P, HG), F32)) as u, stage_semaphores(nc, "filled", "zeroed", "selected") as s, nc.Block() as block:
        @block.gpsimd
        def _(pool):
            pool.memset(g.ks[32:64], 0.0).then_inc(s.filled, 1)
            pool.wait_ge(s.filled, 1)

        @block.vector
        def _(dve):
            dve.tensor_reduce(u.sel[MAX_AT:MAX_END], g.ident[MAX_AT:MAX_END, MAX_AT:MAX_END].rearrange(
                "p (a j) -> p j a", j=HG), AX.X, ALU.add).then_inc(s.selected, 1)
            dve.memset(g.qs[32:64], 0.0).then_inc(s.zeroed, 1)
            dve.memset(g.qs[64:96], 0.0).then_inc(s.zeroed, 1)
            dve.memset(g.ks[64:96], 0.0).then_inc(s.zeroed, 1)
            dve.wait_ge(s.zeroed, 3)

        @block.scalar
        def _(act):
            act.wait_ge(s.selected, 1)
            for gi in range(G4):
                act.activation(g.ks[MAX_AT:MAX_END, gi * HG:(gi + 1) * HG, :],
                               u.sel[MAX_AT:MAX_END].unsqueeze(2).to_broadcast([PARTS * HG, HG, S]),
                               ACT.Copy).then_inc(s.selected, 1)
            act.wait_ge(s.selected, 1 + G4)


def narrow_attention(nc, g, *, w, keys, kv_src, scale, q_src=None, mask=None, metric=None, add_to=None, store=None,
                     out_scale=1.0, zero_if_all_masked=False, bq=None, bk=None, bv=None, bo=None):
    KT = len(keys)
    SK = keys[-1][0] + keys[-1][1]
    PER = QT // KT
    PERG = KT * HG
    NBLK = G4 * PERG
    LEAD = PERG + HG
    RING = 2 * HG
    q_src = q_src if q_src is not None else g.xnT
    split_projections(nc, g, w, q_src, kv_src, scale, SK, bq, bk, metric)

    shapes = dict(srck=((P, SK), F32), v=((P, KT, H16, HW), F32),
                  probs=((P, RING, S), F32), nmax=((P, G4, QT, HG), F32), left=((P, QT, HG), F32),
                  mp=((P, QT, MAX_END), BF16), outs=((P, 2, S), F32), rinv=((P, 2, QT, HG), F32),
                  o=((P, QT, D), F32), oT=((P, QT * P), F32))
    if mask is not None:
        by_batch = mask[0] == "drop"
        MB = B if by_batch else 1
        shapes.update(mask_add=((P, (MB + 1) * QT, SK), BF16), mask_addT=((P, MB * KT, S), BF16),
                      live=((P, QT, HG), F32))
        if by_batch:
            shapes.update(maskT_now=((P, KT, S), BF16))
    SCORES, LOGITS, OUT, MAXT, MISC = 0, 2, 4, 6, 7
    with buffers(nc, **shapes) as u:
        ks = g.ks[:, :, 0:SK]

        with stage_semaphores(nc, "zeroed") as s, nc.Block() as block:
            @block.vector
            def _(dve):
                dve.memset(u.mp[:], 0.0).then_inc(s.zeroed, 1)
                dve.memset(u.v[:], 0.0).then_inc(s.zeroed, 1)
                dve.wait_ge(s.zeroed, 2)
                dve.memset(u.v[:, :, :, DH8:DH8 + 1].rearrange("p k h c -> p (k h) c"), 1.0).then_inc(s.zeroed, 1)
                dve.wait_ge(s.zeroed, 3)

        def load_stack(sp, gi, batch, ready):
            rows = slice(gi * HG * DH8, (gi + 1) * HG * DH8)
            hs = slice(gi * HG, (gi + 1) * HG)
            for n, (qp, kp) in enumerate(PAIRED):
                for stack, parts, part, N in ((g.qs, g.q_parts, qp, S), (ks, g.k_parts, kp, SK)):
                    sp.dma_start(stack[n * DH8:(n + 1) * DH8, hs, :], parts[batch, part, rows, 0:N].rearrange(
                        "o (h d) s -> (o d) h s", d=DH8)).then_inc(ready, 16)

        def score(pe, bank, gi, kt, j, batch):
            for i in range(PER):
                q = kt * PER + i
                out = g.psum[:, bank, i * SK:(i + 1) * SK]
                last = pe.matmul(out, g.qs[0:MAX_AT, gi * HG + j, q * P:(q + 1) * P], ks[0:MAX_AT, gi * HG + j, :],
                                 start=True, stop=mask is None)
                if mask is not None:
                    madd = (u.mask_add[:, q, :] if isinstance(batch, int) or not by_batch
                            else u.mask_add[:, bass.ds(batch * QT + q, 1), :])
                    last = pe.matmul(out, g.ident_bf[:], madd, start=False, stop=True)
            return last

        def maximum(dve, bank, gi, kt, j):
            return dve.tensor_reduce(u.nmax[:, gi, kt * PER:(kt + 1) * PER, j],
                                     g.psum[:, bank, 0:PER * SK].rearrange("p (i k) -> p i k", k=SK), AX.X, ALU.max,
                                     negate=True)

        def split_maxima(dve, gi, split, done, before):
            part = [u.mp[:, :, MAX_AT + a * HG:MAX_AT + (a + 1) * HG] for a in range(PARTS)]
            dve.tensor_copy(part[0], u.nmax[:, gi]).then_inc(split, 1)
            dve.wait_ge(split, before + 1)
            dve.tensor_tensor(u.left[:], u.nmax[:, gi], part[0], ALU.subtract).then_inc(split, 1)
            dve.wait_ge(split, before + 2)
            dve.tensor_copy(part[1], u.left[:]).then_inc(split, 1)
            dve.wait_ge(split, before + 3)
            dve.tensor_tensor(part[2], u.left[:], part[1], ALU.subtract).then_inc(done, 1)

        def turn_maxima(pe):
            for q in range(QT):
                last = pe.matmul(g.psum[0:MAX_END, MAXT, q * P:(q + 1) * P], u.mp[:, q, :], g.ident_bf[:],
                                 start=True, stop=True)
            return last

        def copy_maxima(act, h):
            return act.activation(g.qs[MAX_AT:MAX_END, h, :], g.psum[MAX_AT:MAX_END, MAXT, :], ACT.Copy)

        with (
            stage_semaphores(nc, "stack0", "stack1", "stack2", "masks_done", "scores_done", "max_done", "split", "parts_done",
                             "maxima_turned", "maxima_done") as s,
            nc.Block() as block,
        ):
            @block.sync
            def _(sp):
                load_stack(sp, 0, slice(0, 1), s.stack0)
                load_stack(sp, 1, slice(0, 1), s.stack1)
                load_stack(sp, 2, slice(0, 1), s.stack2)
                sp.wait_ge(s.stack2, 16 * STACK_DMAS)

            @block.tensor
            def _(pe):
                pe.wait_ge(s.stack0, 16 * STACK_DMAS)
                if mask is not None:
                    pe.wait_ge(s.masks_done, 2 + KT)
                for n in range(LEAD):
                    if n == PERG:
                        pe.wait_ge(s.stack1, 16 * STACK_DMAS)
                    if n >= 2:
                        pe.wait_ge(s.max_done, n - 1)
                    score(pe, SCORES + n % 2, n // PERG, n // HG % KT, n % HG, 0).then_inc(s.scores_done, 1)
                pe.wait_ge(s.parts_done, 1)
                turn_maxima(pe).then_inc(s.maxima_turned, 1)

            @block.vector
            def _(dve):
                if mask is not None:
                    kind, m, mT = mask
                    op = (MASKED, None, ALU.mult) if kind == "drop" else (-1.0, -MASKED, ALU.add, ALU.mult)
                    dve.tensor_scalar(u.mask_add[:, 0:MB * QT, :], m[:], *op).then_inc(s.masks_done, 1)
                    dve.tensor_scalar(u.mask_add[:, MB * QT:(MB + 1) * QT, :], m[:, 0:QT, :], *op).then_inc(s.masks_done, 1)
                    for t, (_, rows) in enumerate(keys):
                        dve.tensor_scalar(u.mask_addT[0:rows].rearrange("p (b t) s -> p b t s", t=KT)[:, :, t, :],
                                          mT[0:rows].rearrange("p (b t) s -> p b t s", t=KT)[:, :, t, :],
                                          *op).then_inc(s.masks_done, 1)
                for n in range(LEAD):
                    dve.wait_ge(s.scores_done, n + 1)
                    maximum(dve, SCORES + n % 2, n // PERG, n // HG % KT, n % HG).then_inc(s.max_done, 1)
                dve.wait_ge(s.max_done, PERG)
                split_maxima(dve, 0, s.split, s.parts_done, 0)

            @block.scalar
            def _(act):
                act.wait_ge(s.maxima_turned, 1)
                for h in range(HG):
                    copy_maxima(act, h).then_inc(s.maxima_done, 1)

        with (
            nc.Fori(0, B) as b,
            stage_semaphores(nc, "stack3", "stack0_next", "stack1_next", "stack2_next", "src_done", "v_mm", "v_done",
                             "scores_done", "max_done", "split", "parts_done", "maxima_turned", "maxima_done",
                             "maskT_done", "logits_done", "probs_done", "heads_done", "outputs_copied", "outputs_turned", "chain",
                             "normalised", "o_turned", "oT_done", "projected", "stored") as s,
            nc.Block() as block,
        ):
            @block.sync
            def _(sp):
                load_stack(sp, 3, bass.ds(b, 1), s.stack3)
                for gi, ready in enumerate((s.stack0_next, s.stack1_next, s.stack2_next)):
                    sp.wait_ge(s.probs_done, PERG * (gi + 1))
                    load_stack(sp, gi, bass.ds(b + 1, 1), ready)
                for ready in (s.stack1_next, s.stack2_next):
                    sp.wait_ge(ready, 16 * STACK_DMAS)

            output_quads = [m for m in range(KT + 2, NBLK // HG) if (m - 2) % KT == 0]

            @block.tensor
            def _(pe):
                def values():
                    pe.wait_ge(s.src_done, 1)
                    for t, (at, rows) in enumerate(keys):
                        out = g.psum[0:rows, MISC, t * P:(t + 1) * P]
                        last = pe.matmul(out, u.srck[:, at:at + rows], w.wv[:], start=True, stop=bv is None)
                        if bv is not None:
                            last = pe.matmul(out, g.ones[0:1, 0:rows], bv[0:1, :], start=False, stop=True)
                    last.then_inc(s.v_mm, 1)

                def scores(n):
                    ahead = (n + LEAD) % NBLK
                    if ahead == PERG * (G4 - 1):
                        pe.wait_ge(s.stack3, 16 * STACK_DMAS)
                    if ahead == 0:
                        pe.wait_ge(s.stack0_next, 16 * STACK_DMAS)
                    if ahead == PERG:
                        pe.wait_ge(s.stack1_next, 16 * STACK_DMAS)
                    if n >= 2:
                        pe.wait_ge(s.max_done, n - 1)
                    score(pe, SCORES + n % 2, ahead // PERG, ahead // HG % KT, ahead % HG,
                          b if n + LEAD < NBLK else b + 1).then_inc(s.scores_done, 1)

                def turn_group(k):
                    pe.wait_ge(s.parts_done, k + 1)
                    if k >= 1:
                        pe.wait_ge(s.maxima_done, HG * k)
                    turn_maxima(pe).then_inc(s.maxima_turned, 1)

                def logits(n):
                    gi, kt, j = n // PERG, n // HG % KT, n % HG
                    at, rows = keys[kt]
                    if kt == 0 and gi >= 1:
                        pe.wait_ge(s.maxima_done, HG * (gi - 1) + j + 1)
                    if n == 0 and mask is not None and by_batch:
                        pe.wait_ge(s.maskT_done, 1)
                    if n >= 2:
                        pe.wait_ge(s.probs_done, n - 1)
                    out = g.psum[0:rows, LOGITS + n % 2, :]
                    last = pe.matmul(out, ks[0:MAX_END, gi * HG + j, at:at + rows], g.qs[0:MAX_END, gi * HG + j, :],
                                     start=True, stop=mask is None)
                    if mask is not None:
                        maddT = u.maskT_now[0:rows, kt, :] if by_batch else u.mask_addT[0:rows, kt, :]
                        last = pe.matmul(out, g.ident_bf[0:rows, 0:rows], maddT, start=False, stop=True)
                    last.then_inc(s.logits_done, 1)

                def heads(m):
                    gi, kt = m // KT, m % KT
                    rows = keys[kt][1]
                    pe.wait_ge(s.probs_done, HG * (m + 1))
                    if m == 0:
                        pe.wait_ge(s.v_done, 1)
                    if kt == 0 and gi >= 2:
                        pe.wait_ge(s.outputs_copied, gi - 1)
                    for j in range(HG):
                        last = pe.matmul(g.psum[j * HW:(j + 1) * HW, OUT + gi % 2, :], u.v[0:rows, kt, gi * HG + j, :],
                                         u.probs[0:rows, (m * HG + j) % RING, :], start=kt == 0, stop=kt == KT - 1,
                                         tile_position=(0, j * HW))
                    last.then_inc(s.heads_done, 1)

                def turn_outputs(gi):
                    pe.wait_ge(s.outputs_copied, gi + 1)
                    if gi == 0:
                        pe.wait_ge(s.v_done, 1)
                    else:
                        pe.wait_ge(s.normalised, gi)
                    for q in range(QT):
                        last = pe.transpose(g.psum[:, MISC, q * P:(q + 1) * P], u.outs[:, gi % 2, q * P:(q + 1) * P],
                                            g.ident[:])
                    last.then_inc(s.outputs_turned, 1)

                values()
                for n in range(NBLK):
                    gi, m = n // PERG, n // HG
                    logits(n)
                    scores(n)
                    if n % HG == HG - 1 and m >= 1:
                        heads(m - 1)
                    if n % HG == 1 and m % KT == KT - 1:
                        turn_group(gi)
                    if n % HG == 1 and m in output_quads:
                        turn_outputs(output_quads.index(m))
                heads(NBLK // HG - 1)
                for gi in range(len(output_quads), G4):
                    turn_outputs(gi)
                pe.wait_ge(s.normalised, G4)
                pe.wait_ge(s.maxima_done, HG * G4)
                for q in range(QT):
                    last = pe.transpose(g.psum[:, MAXT, q * P:(q + 1) * P], u.o[:, q, :], g.ident[:])
                last.then_inc(s.o_turned, 1)
                pe.wait_ge(s.oT_done, 1)
                for q in range(QT):
                    out = g.psum[:, MISC, q * P:(q + 1) * P]
                    last = pe.matmul(out, u.oT[:, q * P:(q + 1) * P], w.wo[:], start=True, stop=bo is None)
                    if bo is not None:
                        last = pe.matmul(out, g.ones[0:1, :], bo[0:1, :], start=False, stop=True)
                last.then_inc(s.projected, 1)

            @block.vector
            def _(dve):
                def normalise(gi):
                    turned = g.psum[:, MISC, :].rearrange("p (q j r) -> p q j r", q=QT, r=HW)
                    rinv = u.rinv[:, gi % 2]
                    steps = 3 if zero_if_all_masked else 1
                    dve.wait_ge(s.outputs_turned, gi + 1)
                    dve.reciprocal(rinv, turned[:, :, :, DH8]).then_inc(s.chain, 1)
                    if zero_if_all_masked:
                        dve.tensor_scalar(u.live[:], u.nmax[:, gi], -MASKED / 2, None, ALU.is_lt).then_inc(s.chain, 1)
                        dve.wait_ge(s.chain, steps * gi + 2)
                        dve.tensor_tensor(rinv, rinv, u.live[:], ALU.mult).then_inc(s.chain, 1)
                    dve.wait_ge(s.chain, steps * (gi + 1))
                    for q in range(QT):
                        ins = dve.tensor_tensor(
                            u.o[:, q, gi * HG * DH8:(gi + 1) * HG * DH8].rearrange("p (j r) -> p j r", r=DH8),
                            turned[:, q, :, 0:DH8], rinv[:, q].unsqueeze(2).to_broadcast([P, HG, DH8]), ALU.mult)
                    ins.then_inc(s.normalised, 1)

                if mask is not None and by_batch:
                    for t, (_, rows) in enumerate(keys):
                        ins = dve.tensor_copy(u.maskT_now[0:rows, t:t + 1, :],
                                              u.mask_addT[0:rows, bass.ds(b * KT + t, 1), :])
                    ins.then_inc(s.maskT_done, 1)
                dve.tensor_copy(u.srck[:], kv_src[:, bass.ds(b * SK, SK)]).then_inc(s.src_done, 1)
                for n in range(NBLK):
                    gi, m = n // PERG, n // HG
                    ahead = (n + LEAD) % NBLK
                    dve.wait_ge(s.scores_done, n + 1)
                    maximum(dve, SCORES + n % 2, ahead // PERG, ahead // HG % KT, ahead % HG).then_inc(s.max_done, 1)
                    if n % HG == HG - 1:
                        if m % KT == KT - 2:
                            dve.wait_ge(s.max_done, n + 1)
                            if gi >= 1:
                                dve.wait_ge(s.maxima_turned, gi)
                            split_maxima(dve, (gi + 1) % G4, s.split, s.parts_done, 3 * gi)
                    if n % HG == 2 and m in output_quads:
                        normalise(output_quads.index(m))
                for gi in range(len(output_quads), G4):
                    normalise(gi)
                dve.wait_ge(s.projected, 1)
                result = g.psum[:, MISC, :].rearrange("p (q d) -> p q d", d=D)
                if add_to is not None:
                    at = add_to[:, bass.ds(b * QT, QT), :]
                    dve.tensor_tensor(at, result, at, ALU.add).then_inc(s.stored, 1)
                else:
                    dve.tensor_scalar(store[:, bass.ds(b * QT, QT), :], result, out_scale, None,
                                      ALU.mult).then_inc(s.stored, 1)

            @block.scalar
            def _(act):
                def exponentials(n):
                    rows = keys[n // HG % KT][1]
                    act.wait_ge(s.logits_done, n + 1)
                    if n >= RING:
                        act.wait_ge(s.heads_done, (n - RING) // HG + 1)
                    act.activation(u.probs[0:rows, n % RING, :], g.psum[0:rows, LOGITS + n % 2, :],
                                   ACT.Exp).then_inc(s.probs_done, 1)

                def copy_outputs(gi):
                    act.wait_ge(s.heads_done, KT * (gi + 1))
                    if gi >= 2:
                        act.wait_ge(s.outputs_turned, gi - 1)
                    act.activation(u.outs[:, gi % 2, :], g.psum[:, OUT + gi % 2, :],
                                   ACT.Copy).then_inc(s.outputs_copied, 1)

                act.wait_ge(s.v_mm, 1)
                for t, (_, rows) in enumerate(keys):
                    ins = act.activation(u.v[0:rows, t, :, 0:DH8],
                                         g.psum[0:rows, MISC, t * P:(t + 1) * P].rearrange("p (h d) -> p h d", d=DH8),
                                         ACT.Copy)
                ins.then_inc(s.v_done, 1)
                for n in range(NBLK):
                    gi, m = n // PERG, n // HG
                    exponentials(n)
                    if m % KT == KT - 1 and n % HG >= HG // 2:
                        if n % HG == HG // 2:
                            act.wait_ge(s.maxima_turned, gi + 1)
                        for j in (2 * (n % HG) - HG, 2 * (n % HG) - HG + 1):
                            copy_maxima(act, (gi + 1) % G4 * HG + j).then_inc(s.maxima_done, 1)
                    if n % HG == HG - 1:
                        if m >= KT and m % KT == 0:
                            copy_outputs(m // KT - 1)
                copy_outputs(G4 - 1)
                act.wait_ge(s.o_turned, 1)
                act.activation(u.oT[:], g.psum[:, MAXT, :], ACT.Copy).then_inc(s.oT_done, 1)


def row(ap):
    return ap.rearrange("(a n) -> a n", a=1)


def column(ap):
    return ap.rearrange("(n a) -> n a", a=1)


def layer0_attention(nc, g, a):
    layernorm(nc, g)
    with (
        buffers(nc, wq=((P, P), F32), wk=((P, P), F32), wv=((P, D), F32), wo=((P, D), F32),
                w1=((P, 2, P), F32), w2=((P, 2, P), F32), b1=((P, 2), F32), b2=((P, 1), F32),
                vmap=((P, NT, D), F32), vT=((P, NT * P), F32)) as u,
    ):
        load(nc, [(u.wv[:], a["L0_attn_WvT"]), (u.wo[:], a["L0_attn_WoT"]),
                  (u.wq[:], a["L0_attn_WqT"]), (u.wk[:], a["L0_attn_WkT"]),
                  (u.w1[:], a["L0_attn_W1T"].rearrange("k (c m) -> k c m", c=2)),
                  (u.b1[:], a["L0_attn_b1"].rearrange("(c p) -> p c", c=2)),
                  (u.w2[:], a["L0_attn_W2T"].rearrange("(c p) m -> p c m", c=2)), (u.b2[:], column(a["L0_attn_b2"]))])
        log_map(nc, g, u.vmap)
        turn_to_features(nc, g, u.vmap, u.vT)
        narrow_attention(nc, g, w=u, keys=ALL_KEYS, kv_src=u.vT, q_src=u.vT, scale=DH8 ** -0.5,
                         metric=named(w1=u.w1, w2=u.w2, b1=u.b1, b2=u.b2), store=u.vmap, out_scale=0.1)
        project_and_add(nc, g, u.vmap)


def layer1_cross(nc, g, a):
    layernorm(nc, g)
    keys = ctx_tiles()
    KT = len(keys)
    with buffers(nc, wq=((P, P), F32), wk=((P, P), F32), wv=((P, D), F32), wo=((P, D), F32),
                 mask=((P, NT, SC), U8), maskT=((P, B * KT, S), U8)) as u:
        maskT = u.maskT[:].rearrange("p (b t) s -> p b t s", t=KT)
        load(nc, [(u.wv[:], a["L1_xattn_W_VT"]), (u.wo[:], a["L1_xattn_W_OT"]), (u.wq[:], a["L1_xattn_W_QT"]),
                  (u.wk[:], a["L1_xattn_W_KT"]),
                  (u.mask[:], a["mask_BxSxS2_bf0"].rearrange("b (t p) k -> p (b t) k", p=P))]
             + [(maskT[0:rows, :, t, :], a["mask_BxSxS2_bf0T"][:, at:at + rows, :].rearrange("b k s -> k b s"))
                for t, (at, rows) in enumerate(keys)])
        narrow_attention(nc, g, w=u, keys=keys, kv_src=g.ctxT, scale=DH8 ** -0.5,
                         mask=("drop", u.mask, u.maskT), zero_if_all_masked=True, add_to=g.x)


def layer3_attention(nc, g, a):
    layernorm(nc, g)
    with buffers(nc, wq=((P, P), F32), wk=((P, P), F32), wv=((P, D), F32), wo=((P, D), F32),
                 bq=((P, 1), F32), bqs=((P, 1), F32), bk=((P, 1), F32), bv=((1, D), F32), bo=((1, D), F32)) as u:
        load(nc, [(u.wv[:], a["L3_attn_WvT"]), (u.wo[:], a["L3_attn_WoT"]), (u.bv[:], row(a["L3_attn_bv"])),
                  (u.bo[:], row(a["L3_attn_bo"])), (u.wq[:], a["L3_attn_WqT"]), (u.wk[:], a["L3_attn_WkT"]),
                  (u.bq[:], column(a["L3_attn_bq"])), (u.bk[:], column(a["L3_attn_bk"]))])
        scale_bias(nc, u.bqs, u.bq, DH8 ** -0.5)
        narrow_attention(nc, g, w=u, keys=ALL_KEYS, kv_src=g.xnT, scale=DH8 ** -0.5, add_to=g.x,
                         bq=u.bqs, bk=u.bk, bv=u.bv, bo=u.bo)


def layer3_cross(nc, g, a):
    layernorm(nc, g)
    keys = ctx_tiles()
    with buffers(nc, wq=((P, P), F32), wk=((P, P), F32), wv=((P, D), F32), wo=((P, D), F32),
                 mask=((P, QT, SC), U8), maskT=((P, len(keys), S), U8), bq=((P, 1), F32), bqs=((P, 1), F32),
                 bk=((P, 1), F32), bv=((1, D), F32), bo=((1, D), F32)) as u:
        load(nc, [(u.wv[:], a["L3_xattn_Wv"]), (u.wo[:], a["L3_xattn_Wo"]), (u.bv[:], row(a["L3_xattn_bv"])),
                  (u.bo[:], row(a["L3_xattn_bo"])), (u.wq[:], a["L3_xattn_Wq"]), (u.wk[:], a["L3_xattn_Wk"]),
                  (u.bq[:], column(a["L3_xattn_bq"])), (u.bk[:], column(a["L3_xattn_bk"])),
                  (u.mask[:], a["mask_SxS2_bk1"].rearrange("(t p) k -> p t k", p=P))]
             + [(u.maskT[0:rows, t, :], a["mask_SxS2_bk1T"][at:at + rows, :]) for t, (at, rows) in enumerate(keys)])
        scale_bias(nc, u.bqs, u.bq, DH8 ** -0.5)
        narrow_attention(nc, g, w=u, keys=keys, kv_src=g.ctxT, scale=DH8 ** -0.5,
                         mask=("keep", u.mask, u.maskT), add_to=g.x, bq=u.bqs, bk=u.bk, bv=u.bv, bo=u.bo)


def layer2_attention(nc, g, a):
    DQ = 64
    layernorm(nc, g)
    with buffers(nc, wq=((P, 8, P), F32), wk=((P, 8, P), F32), wv=((P, H16 * DQ), F32), wo=((P, 8, D), F32)) as u:
        load(nc, [(u.wq[:], a["L2_attn_QT"].rearrange("k (g m) -> k g m", g=8)),
                  (u.wk[:], a["L2_attn_KT"].rearrange("k (g m) -> k g m", g=8)),
                  (u.wv[:], a["L2_attn_VT"]), (u.wo[:], a["L2_attn_WT"].rearrange("(c p) d -> p c d", p=P))])
        root = (DQ / D) ** 0.5
        attention(nc, g, w=u, H=H16, dh=DQ, hp=DQ, keys=ALL_KEYS, kv_src=g.xnT, scale=root * root / DQ, causal=True,
                  add_to=g.x, out_scale=root * (D / DQ) ** 0.5 / H16)


def scale_bias(nc, dst, src, by):
    with stage_semaphores(nc, "scaled") as s, nc.Block() as block:
        @block.vector
        def _(dve):
            dve.tensor_scalar(dst[:], src[:], by, None, ALU.mult).then_inc(s.scaled, 1)
            dve.wait_ge(s.scaled, 1)


def slots_from_context(nc, g, a):
    ROUNDS, EPS, LANES = 3, 1e-6, 2
    SCALE = D ** -0.5
    STEPS = dict(
        dve=(["h_in", "ctx_in", "ctx_sq", "ctx_eps", "ctx_inv", "ctx_normed"],
             ["sq", "rms_eps", "rms_inv", "rms_diag", "q", "max0", "max1", "sinv0", "sinv1", "vs0", "vs1", "total_eps",
              "total_inv", "total_diag", "update", "rh", "nx", "h_n", "zh_n", "h"]),
        act=(["ctx_root", "k_out", "v0_out", "v1_out"],
             ["q_out", "rms_root", "exp0", "exp1", "update_out", "r", "z", "n"]),
        pe=(["ctx_mean", "kv_mm"], ["q_mm", "mean", "rms_mm", "scores", "update_mm", "total_mm", "r_mm", "z_mm", "n_mm"]))

    def after(engine, name, i=None):
        first, every = STEPS[engine]
        return first.index(name) + 1 if i is None else len(first) + i * len(every) + every.index(name) + 1

    layernorm(nc, g)
    with buffers(nc, wq=((P, D), F32), wk=((P, D), F32), wv=((P, D), F32), wih=((P, 3 * D), F32), whh=((P, 3 * D), F32),
                 bih=((P, 3), F32), bhh=((P, 3), F32), bsum=((P, 3), F32), w_slot=((P, 1), F32), w_in=((P, 1), F32),
                 mean=((P, P), F32), h=((P, LANES, S), F32), cT=((P, LANES, SC), F32), sq=((P, LANES, S), F32),
                 c_inv=((P, LANES, SC), F32), inv=((P, LANES, QT), F32), diag=((P, LANES, QT, P), F32),
                 pn=((P, LANES, SC), F32), kT=((P, LANES, SC), F32), v=((P, LANES, 2, D), F32),
                 vs=((P, LANES, 2, D), F32), qT=((P, LANES, S), F32), nmax=((P, LANES, 2), F32),
                 sums=((P, LANES, 2), F32), at=((P, LANES, 2, S), F32), up=((P, LANES, S), F32),
                 r=((P, LANES, S), F32), z=((P, LANES, S), F32), n=((P, LANES, S), F32), d=((P, LANES, S), F32)) as u:
        load(nc, [(u.wq[:], a["L0_xattn_WqT"]), (u.wk[:], a["L0_xattn_WkT"]), (u.wv[:], a["L0_xattn_WvT"]),
                  (u.wih[:], a["L0_xattn_gru_wihT"]), (u.whh[:], a["L0_xattn_gru_whhT"]),
                  (u.bih[:], a["L0_xattn_gru_bih"].rearrange("(c p) -> p c", p=P)),
                  (u.bhh[:], a["L0_xattn_gru_bhh"].rearrange("(c p) -> p c", p=P)),
                  (u.w_slot[:], a["L0_xattn_slot_norm_w"].rearrange("(p a) -> p a", a=1)),
                  (u.w_in[:], a["L0_xattn_input_norm_w"].rearrange("(p a) -> p a", a=1))])
        with stage_semaphores(nc, "set_up") as s, nc.Block() as block:
            @block.vector
            def _(dve):
                dve.memset(u.mean[:], 1.0 / D).then_inc(s.set_up, 1)
                dve.tensor_tensor(u.bsum[:], u.bih[:], u.bhh[:], ALU.add).then_inc(s.set_up, 1)
                dve.tensor_scalar(u.wq[:], u.wq[:], u.w_slot[:, 0:1], None, ALU.mult).then_inc(s.set_up, 1)
                dve.wait_ge(s.set_up, 3)
        keys = ctx_tiles()
        PS = g.psum
        with (
            nc.Fori(0, B // LANES) as pair,
            stage_semaphores(nc, "dve0", "dve1", "act0", "act1", "pe0", "pe1", "turned", "added") as s,
            nc.Block() as block,
        ):
            done = dict(dve=(s.dve0, s.dve1), act=(s.act0, s.act1), pe=(s.pe0, s.pe1))
            lanes = range(LANES)
            BK = [[4 * c + k for k in range(4)] for c in lanes]

            @block.vector
            def _(dve):
                step = done["dve"]

                def wait(c, engine, name, i=None):
                    dve.wait_ge(done[engine][c], after(engine, name, i))

                for c in lanes:
                    batch = pair * LANES + c
                    dve.tensor_copy(u.h[:, c, :], g.xnT[:, bass.ds(batch * S, S)]).then_inc(step[c], 1)
                    dve.tensor_copy(u.cT[:, c, :], g.ctxT[:, bass.ds(batch * SC, SC)]).then_inc(step[c], 1)
                for c in lanes:
                    wait(c, "dve", "ctx_in")
                    dve.tensor_tensor(u.sq[:, c, 0:SC], u.cT[:, c, :], u.cT[:, c, :], ALU.mult).then_inc(step[c], 1)
                for c in lanes:
                    wait(c, "pe", "ctx_mean")
                    dve.tensor_scalar(u.c_inv[:, c, :], PS[:, BK[c][0], 0:SC], EPS, None, ALU.add).then_inc(step[c], 1)
                for c in lanes:
                    wait(c, "act", "ctx_root")
                    dve.reciprocal(u.c_inv[:, c, :], u.c_inv[:, c, :]).then_inc(step[c], 1)
                for c in lanes:
                    wait(c, "dve", "ctx_inv")
                    dve.scalar_tensor_tensor(out=u.pn[:, c, :], in0=u.cT[:, c, :], scalar=u.w_in[:, 0:1],
                                             in1=u.c_inv[:, c, :], op0=ALU.mult, op1=ALU.mult).then_inc(step[c], 1)
                for i in range(ROUNDS):
                    for c in lanes:
                        if i == 0:
                            wait(c, "dve", "ctx_normed")
                        else:
                            wait(c, "dve", "h", i - 1)
                        dve.tensor_tensor(u.sq[:, c, :], u.h[:, c, :], u.h[:, c, :], ALU.mult).then_inc(step[c], 1)
                    for c in lanes:
                        wait(c, "pe", "mean", i)
                        dve.tensor_scalar(u.inv[:, c, :], PS[:, BK[c][0], 0:QT], EPS, None, ALU.add).then_inc(step[c], 1)
                    for c in lanes:
                        wait(c, "act", "rms_root", i)
                        dve.reciprocal(u.inv[:, c, :], u.inv[:, c, :]).then_inc(step[c], 1)
                        wait(c, "dve", "rms_inv", i)
                        dve.tensor_tensor(u.diag[:, c], g.ident[:].unsqueeze(1).to_broadcast([P, QT, P]),
                                          u.inv[:, c, :].unsqueeze(2).to_broadcast([P, QT, P]),
                                          ALU.mult).then_inc(step[c], 1)
                    for c in lanes:
                        wait(c, "act", "q_out", i)
                        wait(c, "pe", "rms_mm", i)
                        dve.tensor_tensor(u.qT[:, c, :], u.qT[:, c, :], PS[:, BK[c][0], :], ALU.mult).then_inc(step[c], 1)
                    for c in lanes:
                        wait(c, "pe", "scores", i)
                        for t, (_, rows) in enumerate(keys):
                            dve.tensor_reduce(u.nmax[0:rows, c, t:t + 1], PS[0:rows, BK[c][2 + t], :], AX.X, ALU.max,
                                              negate=True).then_inc(step[c], 1)
                    for c in lanes:
                        for t, (_, rows) in enumerate(keys):
                            wait(c, "act", f"exp{t}", i)
                            dve.reciprocal(u.sums[0:rows, c, t:t + 1], u.sums[0:rows, c, t:t + 1]).then_inc(step[c], 1)
                        for t, (_, rows) in enumerate(keys):
                            wait(c, "dve", f"sinv{t}", i)
                            dve.tensor_scalar(u.vs[0:rows, c, t, :], u.v[0:rows, c, t, :], u.sums[0:rows, c, t:t + 1],
                                              None, ALU.mult).then_inc(step[c], 1)
                    for c in lanes:
                        wait(c, "pe", "update_mm", i)
                        dve.tensor_scalar(u.inv[:, c, :], PS[:, BK[c][0], 0:QT], EPS, None, ALU.add).then_inc(step[c], 1)
                        wait(c, "dve", "total_eps", i)
                        dve.reciprocal(u.inv[:, c, :], u.inv[:, c, :]).then_inc(step[c], 1)
                        wait(c, "dve", "total_inv", i)
                        dve.tensor_tensor(u.diag[:, c], g.ident[:].unsqueeze(1).to_broadcast([P, QT, P]),
                                          u.inv[:, c, :].unsqueeze(2).to_broadcast([P, QT, P]),
                                          ALU.mult).then_inc(step[c], 1)
                    for c in lanes:
                        wait(c, "act", "update_out", i)
                        wait(c, "pe", "total_mm", i)
                        dve.tensor_tensor(u.up[:, c, :], u.up[:, c, :], PS[:, BK[c][0], :], ALU.mult).then_inc(step[c], 1)
                    for c in lanes:
                        wait(c, "act", "r", i)
                        wait(c, "pe", "n_mm", i)
                        dve.scalar_tensor_tensor(out=u.d[:, c, :], in0=PS[:, BK[c][0], :], scalar=u.bhh[:, 2:3],
                                                 in1=u.r[:, c, :], op0=ALU.add, op1=ALU.mult).then_inc(step[c], 1)
                        wait(c, "dve", "rh", i)
                        dve.tensor_tensor(u.n[:, c, :], u.d[:, c, :], PS[:, BK[c][1], :], ALU.add).then_inc(step[c], 1)
                    for c in lanes:
                        wait(c, "act", "n", i)
                        dve.tensor_tensor(u.d[:, c, :], u.h[:, c, :], u.n[:, c, :], ALU.subtract).then_inc(step[c], 1)
                        wait(c, "act", "z", i)
                        wait(c, "dve", "h_n", i)
                        dve.tensor_tensor(u.d[:, c, :], u.d[:, c, :], u.z[:, c, :], ALU.mult).then_inc(step[c], 1)
                        wait(c, "dve", "zh_n", i)
                        dve.tensor_tensor(u.h[:, c, :], u.n[:, c, :], u.d[:, c, :], ALU.add).then_inc(step[c], 1)
                for c in lanes:
                    dve.wait_ge(s.turned, c + 1)
                    at = g.x[:, bass.ds((pair * LANES + c) * QT, QT), :]
                    dve.tensor_tensor(at, at, PS[:, BK[c][0], :].rearrange("p (t d) -> p t d", d=D),
                                      ALU.add).then_inc(s.added, 1)

            @block.scalar
            def _(act):
                step = done["act"]

                def wait(c, engine, name, i=None):
                    act.wait_ge(done[engine][c], after(engine, name, i))

                for c in lanes:
                    wait(c, "dve", "ctx_eps")
                    act.activation(u.c_inv[:, c, :], u.c_inv[:, c, :], ACT.Sqrt).then_inc(step[c], 1)
                for c in lanes:
                    wait(c, "pe", "kv_mm")
                    act.activation(u.kT[:, c, :], PS[:, BK[c][1], 0:SC], ACT.Copy).then_inc(step[c], 1)
                    for t, (_, rows) in enumerate(keys):
                        act.activation(u.v[0:rows, c, t, :], PS[0:rows, BK[c][2 + t], 0:D],
                                       ACT.Copy).then_inc(step[c], 1)
                for i in range(ROUNDS):
                    for c in lanes:
                        wait(c, "pe", "q_mm", i)
                        act.activation(u.qT[:, c, :], PS[:, BK[c][1], :], ACT.Copy, scale=SCALE).then_inc(step[c], 1)
                    for c in lanes:
                        wait(c, "dve", "rms_eps", i)
                        act.activation(u.inv[:, c, :], u.inv[:, c, :], ACT.Sqrt).then_inc(step[c], 1)
                    for c in lanes:
                        for t, (_, rows) in enumerate(keys):
                            wait(c, "dve", f"max{t}", i)
                            act.activation(u.at[0:rows, c, t, :], PS[0:rows, BK[c][2 + t], :], ACT.Exp,
                                           bias=u.nmax[0:rows, c, t:t + 1],
                                           accum_out=u.sums[0:rows, c, t:t + 1]).then_inc(step[c], 1)
                    for c in lanes:
                        wait(c, "pe", "update_mm", i)
                        act.activation(u.up[:, c, :], PS[:, BK[c][1], :], ACT.Copy).then_inc(step[c], 1)
                    for c in lanes:
                        wait(c, "pe", "r_mm", i)
                        act.activation(u.r[:, c, :], PS[:, BK[c][2], :], ACT.Sigmoid,
                                       bias=u.bsum[:, 0:1]).then_inc(step[c], 1)
                        wait(c, "pe", "z_mm", i)
                        act.activation(u.z[:, c, :], PS[:, BK[c][3], :], ACT.Sigmoid,
                                       bias=u.bsum[:, 1:2]).then_inc(step[c], 1)
                    for c in lanes:
                        wait(c, "dve", "nx", i)
                        act.activation(u.n[:, c, :], u.n[:, c, :], ACT.Tanh, bias=u.bih[:, 2:3]).then_inc(step[c], 1)

            @block.tensor
            def _(pe):
                step = done["pe"]

                def wait(c, engine, name, i=None):
                    pe.wait_ge(done[engine][c], after(engine, name, i))

                for c in lanes:
                    wait(c, "dve", "ctx_sq")
                    pe.matmul(PS[:, BK[c][0], 0:SC], u.mean[:], u.sq[:, c, 0:SC], start=True,
                              stop=True).then_inc(step[c], 1)
                for c in lanes:
                    wait(c, "dve", "ctx_normed")
                    pe.matmul(PS[:, BK[c][1], 0:SC], u.wk[:], u.pn[:, c, :], start=True, stop=True)
                    for t, (at, rows) in enumerate(keys):
                        last = pe.matmul(PS[0:rows, BK[c][2 + t], 0:D], u.pn[:, c, at:at + rows], u.wv[:], start=True,
                                         stop=True)
                    last.then_inc(step[c], 1)
                for i in range(ROUNDS):
                    for c in lanes:
                        if i == 0:
                            wait(c, "act", "v1_out")
                        else:
                            wait(c, "dve", "h", i - 1)
                        pe.matmul(PS[:, BK[c][1], :], u.wq[:], u.h[:, c, :], start=True, stop=True).then_inc(step[c], 1)
                        wait(c, "dve", "sq", i)
                        for j in range(QT):
                            last = pe.matmul(PS[:, BK[c][0], j:j + 1], u.sq[:, c, j * P:(j + 1) * P], u.mean[:, 0:1],
                                             start=True, stop=True)
                        last.then_inc(step[c], 1)
                    for c in lanes:
                        wait(c, "dve", "rms_diag", i)
                        pe.matmul(PS[:, BK[c][0], :], g.ones[:], u.diag[:, c].rearrange("p t k -> p (t k)"), start=True,
                                  stop=True).then_inc(step[c], 1)
                    for c in lanes:
                        wait(c, "dve", "q", i)
                        for t, (at, rows) in enumerate(keys):
                            last = pe.matmul(PS[0:rows, BK[c][2 + t], :], u.kT[:, c, at:at + rows], u.qT[:, c, :],
                                             start=True, stop=True)
                        last.then_inc(step[c], 1)
                    for c in lanes:
                        wait(c, "dve", "vs1", i)
                        for j in range(QT):
                            for t, (_, rows) in enumerate(keys):
                                pe.matmul(PS[:, BK[c][0], j:j + 1], u.at[0:rows, c, t, j * P:(j + 1) * P],
                                          u.sums[0:rows, c, t:t + 1], start=t == 0, stop=t == 1)
                        for t, (_, rows) in enumerate(keys):
                            last = pe.matmul(PS[:, BK[c][1], :], u.vs[0:rows, c, t, :], u.at[0:rows, c, t, :],
                                             start=t == 0, stop=t == 1)
                        last.then_inc(step[c], 1)
                        for k in range(2):
                            pe.matmul(PS[:, BK[c][2 + k], :], u.whh[:, k * D:(k + 1) * D], u.h[:, c, :], start=True,
                                      stop=False)
                    for c in lanes:
                        wait(c, "dve", "total_diag", i)
                        pe.matmul(PS[:, BK[c][0], :], g.ones[:], u.diag[:, c].rearrange("p t k -> p (t k)"), start=True,
                                  stop=True).then_inc(step[c], 1)
                    for c in lanes:
                        wait(c, "dve", "update", i)
                        for k in range(2):
                            pe.matmul(PS[:, BK[c][2 + k], :], u.wih[:, k * D:(k + 1) * D], u.up[:, c, :], start=False,
                                      stop=True).then_inc(step[c], 1)
                        pe.matmul(PS[:, BK[c][0], :], u.whh[:, 2 * D:3 * D], u.h[:, c, :], start=True, stop=True)
                        pe.matmul(PS[:, BK[c][1], :], u.wih[:, 2 * D:3 * D], u.up[:, c, :], start=True,
                                  stop=True).then_inc(step[c], 1)
                for c in lanes:
                    wait(c, "dve", "h", ROUNDS - 1)
                    for j in range(QT):
                        last = pe.transpose(PS[:, BK[c][0], j * P:(j + 1) * P], u.h[:, c, j * P:(j + 1) * P], g.ident[:])
                    last.then_inc(s.turned, 1)


def layer1_attention(nc, g, a):
    H = 4
    PAIRS = H * H
    layernorm(nc, g)
    with buffers(nc, wq=((P, H * D), F32), wk=((P, H * D), F32), wv=((P, H * D), F32), wo=((P, H, D), F32),
                 bq=((P, H), F32), bk=((P, H), F32), bv=((1, H * D), F32), bo=((1, D), F32), phase=((P, H), F32),
                 cos=((P, H), F32), sin=((P, H), F32), turn=((P, H), F32), whole=((P, H), I32), cc=((P, H, H), F32),
                 ss=((P, H, H), F32), pick=((P, PAIRS, PAIRS), F32),
                 src=((P, S), F32), qT=((P, H, S), F32), kT=((P, H, S), F32), v=((P, QT, H * D), F32),
                 prod=((P, 2, S), F32), sT=((PAIRS, S), F32), sc=((P, QT * H, H), F32), mx=((P, QT * H), F32),
                 o=((P, QT, H * D), F32), oT=((P, H, S), F32)) as u:
        load(nc, [(u.wq[:], a["L1_attn_Wq"]), (u.wk[:], a["L1_attn_Wk"]), (u.wv[:], a["L1_attn_Wv"]),
                  (u.wo[:], a["L1_attn_Wo"].rearrange("(c p) n -> p c n", p=P)),
                  (u.bq[:], a["L1_attn_bq"].rearrange("(h p) -> p h", p=P)),
                  (u.bk[:], a["L1_attn_bk"].rearrange("(h p) -> p h", p=P)), (u.bv[:], row(a["L1_attn_bv"])),
                  (u.bo[:], row(a["L1_attn_bo"])), (u.phase[:], a["L1_attn_phaseT"])])
        with stage_semaphores(nc, "step", "sined") as s, nc.Block() as block:
            @block.vector
            def _(dve):
                steps = [0]

                def done(ins):
                    steps[0] += 1
                    ins.then_inc(s.step, 1)
                    dve.wait_ge(s.step, steps[0])

                for n, (dst, shift) in enumerate(((u.sin, 0.0), (u.cos, 0.25))):
                    done(dve.tensor_scalar(u.turn[:], u.phase[:], 1 / (2 * np.pi), shift, ALU.mult, ALU.add))
                    done(dve.tensor_copy(u.whole[:], u.turn[:]))
                    done(dve.tensor_copy(dst[:], u.whole[:]))
                    done(dve.tensor_tensor(dst[:], u.turn[:], dst[:], ALU.subtract))
                    done(dve.tensor_scalar(dst[:], dst[:], 0.5, -0.5, ALU.min, ALU.max))
                done(dve.memset(u.pick[:], 0.0))
                dve.wait_ge(s.sined, 2)
                row_of = [P, H, H]
                done(dve.tensor_tensor(u.cc[:], u.cos[:].unsqueeze(2).to_broadcast(row_of),
                                       u.cos[:].unsqueeze(1).to_broadcast(row_of), ALU.mult))
                done(dve.tensor_tensor(u.ss[:], u.sin[:].unsqueeze(2).to_broadcast(row_of),
                                       u.sin[:].unsqueeze(1).to_broadcast(row_of), ALU.mult))
                done(dve.tensor_tensor(u.cc[:], u.cc[:], u.ss[:], ALU.add))
                done(dve.tensor_scalar(u.pick[:].rearrange("p a b -> p (a b)")[:, 0:PAIRS * PAIRS:PAIRS + 1],
                                       u.cc[:].rearrange("p a b -> p (a b)"), D ** -0.5, None, ALU.mult))

            @block.scalar
            def _(act):
                act.wait_ge(s.step, 5)
                act.activation(u.sin[:], u.sin[:], ACT.Sin, scale=float(2 * np.pi * (1 - 2e-7))).then_inc(s.sined, 1)
                act.wait_ge(s.step, 10)
                act.activation(u.cos[:], u.cos[:], ACT.Sin, scale=float(2 * np.pi * (1 - 2e-7))).then_inc(s.sined, 1)
        PS = g.psum
        with (
            nc.Fori(0, B) as b,
            stage_semaphores(nc, "src_done", "q_mm", "q_out", "k_mm", "k_out", "v_mm", "v_out", "prod_done", "pair_mm",
                             "sT_done", "s_turned", "step", "exp_done", "heads_done", "o_turned", "oT_done", "projected",
                             "added") as s,
            nc.Block() as block,
        ):
            @block.tensor
            def _(pe):
                pe.wait_ge(s.src_done, 1)
                for h in range(H):
                    pe.matmul(PS[:, h, :], u.wq[:, h * D:(h + 1) * D], u.src[:], start=True, stop=True).then_inc(s.q_mm, 1)
                for h in range(H):
                    pe.matmul(PS[:, 4 + h, :], u.wk[:, h * D:(h + 1) * D], u.src[:], start=True, stop=True).then_inc(s.k_mm, 1)
                for t in range(QT):
                    pe.wait_ge(s.q_out, t + 1)
                    pe.matmul(PS[:, t, :], u.src[:, t * P:(t + 1) * P], u.wv[:], start=True, stop=False)
                    pe.matmul(PS[:, t, :], g.ones[0:1, :], u.bv[0:1, :], start=False, stop=True).then_inc(s.v_mm, 1)
                pe.wait_ge(s.k_out, 1)
                for p in range(PAIRS):
                    pe.wait_ge(s.prod_done, p + 1)
                    pe.matmul(PS[0:PAIRS, 4, :], u.pick[:, p, :], u.prod[:, p % 2, :], start=p == 0,
                              stop=p == PAIRS - 1).then_inc(s.pair_mm, 1)
                pe.wait_ge(s.sT_done, 1)
                pe.wait_ge(s.k_out, 2)
                for t in range(QT):
                    last = pe.transpose(PS[:, 5, t * PAIRS:(t + 1) * PAIRS], u.sT[:, t * P:(t + 1) * P],
                                        g.ident[0:PAIRS, 0:PAIRS])
                last.then_inc(s.s_turned, 1)
                pe.wait_ge(s.v_out, QT)
                for t in range(QT):
                    pe.wait_ge(s.heads_done, H * (t + 1))
                    for h in range(H):
                        last = pe.transpose(PS[:, t, h * P:(h + 1) * P], u.o[:, t, h * D:(h + 1) * D], g.ident[:])
                    last.then_inc(s.o_turned, 1)
                pe.wait_ge(s.oT_done, QT)
                pe.wait_ge(s.step, 1)
                pe.wait_ge(s.k_out, 4)
                for h in range(H):
                    out = PS[:, 6, h * D:(h + 1) * D]
                    for c in range(H):
                        pe.matmul(out, u.oT[:, h, c:S:H], u.wo[:, c, :], start=c == 0, stop=False)
                    last = pe.matmul(out, g.ones[0:1, :], u.bo[0:1, :], start=False, stop=True)
                last.then_inc(s.projected, 1)

            @block.scalar
            def _(act):
                for h in range(H):
                    act.wait_ge(s.q_mm, h + 1)
                    act.activation(u.qT[:, h, :], PS[:, h, :], ACT.Identity, bias=u.bq[:, h:h + 1]).then_inc(s.q_out, 1)
                for t in range(QT):
                    act.wait_ge(s.v_mm, t + 1)
                    act.activation(u.v[:, t, :], PS[:, t, :], ACT.Copy).then_inc(s.v_out, 1)
                act.wait_ge(s.pair_mm, PAIRS)
                act.activation(u.sT[:], PS[0:PAIRS, 4, :], ACT.Copy).then_inc(s.sT_done, 1)
                act.wait_ge(s.step, 2)
                act.activation(u.sc[:], u.sc[:], ACT.Exp).then_inc(s.exp_done, 1)
                for t in range(QT):
                    act.wait_ge(s.o_turned, t + 1)
                    act.activation(u.oT[:, :, t * P:(t + 1) * P], PS[:, t, :].rearrange("p (h m) -> p h m", h=H),
                                   ACT.Copy).then_inc(s.oT_done, 1)

            @block.vector
            def _(dve):
                dve.tensor_copy(u.src[:], g.xnT[:, bass.ds(b * S, S)]).then_inc(s.src_done, 1)
                for h in range(H):
                    dve.wait_ge(s.k_mm, h + 1)
                    dve.tensor_scalar(u.kT[:, h, :], PS[:, 4 + h, :], u.bk[:, h:h + 1], None, ALU.add).then_inc(s.k_out, 1)
                dve.wait_ge(s.k_out, H)
                for p in range(PAIRS):
                    dve.wait_ge(s.q_out, p // H + 1)
                    if p >= 2:
                        dve.wait_ge(s.pair_mm, p - 1)
                    dve.tensor_tensor(u.prod[:, p % 2, :], u.qT[:, p // H, :], u.kT[:, p % H, :],
                                      ALU.mult).then_inc(s.prod_done, 1)
                steps = [0]

                def done(ins):
                    steps[0] += 1
                    ins.then_inc(s.step, 1)
                    dve.wait_ge(s.step, steps[0])

                wide = [P, QT * H, H]
                scores = PS[:, 5, 0:QT * PAIRS].rearrange("p (q e) -> p q e", e=H)
                dve.wait_ge(s.s_turned, 1)
                done(dve.tensor_reduce(u.mx[:], scores, AX.X, ALU.max))
                done(dve.tensor_tensor(u.sc[:], scores, u.mx[:].unsqueeze(2).to_broadcast(wide), ALU.subtract))
                dve.wait_ge(s.exp_done, 1)
                done(dve.tensor_reduce(u.mx[:], u.sc[:], AX.X, ALU.add))
                done(dve.reciprocal(u.mx[:], u.mx[:]))
                done(dve.tensor_tensor(u.sc[:], u.sc[:], u.mx[:].unsqueeze(2).to_broadcast(wide), ALU.mult))
                for t in range(QT):
                    dve.wait_ge(s.v_out, t + 1)
                    for e in range(H):
                        for h in range(H):
                            out, val = u.o[:, t, h * D:(h + 1) * D], u.v[:, t, e * D:(e + 1) * D]
                            wt = u.sc[:, t * H + h, e:e + 1]
                            if e == 0:
                                ins = dve.tensor_scalar(out, val, wt, None, ALU.mult)
                            else:
                                ins = dve.scalar_tensor_tensor(out=out, in0=val, scalar=wt, in1=out, op0=ALU.mult,
                                                               op1=ALU.add)
                            if e == H - 1:
                                ins.then_inc(s.heads_done, 1)
                            else:
                                ins.then_inc(s.step, 1)
                                steps[0] += 1
                        if e < H - 1:
                            dve.wait_ge(s.step, steps[0])
                dve.wait_ge(s.projected, 1)
                at = g.x[:, bass.ds(b * QT, QT), :]
                dve.tensor_tensor(at, at, PS[:, 6, :].rearrange("p (t d) -> p t d", d=D), ALU.add).then_inc(s.added, 1)


def route(nc, g, u, E, K, gate, gate_b, bias_in_logits):
    PER = 512 // E
    with (
        buffers(nc, top=((P, NT, 8), F32), where=((P, NT, 8), U32), wheref=((P, NT, 8), F32),
                select=((P, NT, E), F32), mx=((P, NT), F32), which=((P, E), I32), whichf=((P, E), F32)) as w,
        stage_semaphores(nc, "logits_done", "step", "exp_done", "top_done", "found", "counted") as s,
        nc.Block() as block,
    ):
        banks = [g.psum[:, n, :].rearrange("p (t e) -> p t e", e=E) for n in range(-(-NT // PER))]
        spread = [P, NT, E]

        @block.tensor
        def _(pe):
            for t in range(NT):
                out = banks[t // PER][:, t % PER, :]
                last = pe.matmul(out, g.xnT[:, t * P:(t + 1) * P], gate[:], start=True, stop=not bias_in_logits)
                if bias_in_logits:
                    last = pe.matmul(out, g.ones[0:1, :], gate_b[0:1, :], start=False, stop=True)
            if gate_b is not None and not bias_in_logits:
                last = pe.matmul(g.psum[:, 7, 0:E], g.ones[0:1, :], gate_b[0:1, :], start=True, stop=True)
            last.then_inc(s.logits_done, 1)

        @block.gpsimd
        def _(pool):
            pool.iota(w.which[:], pattern=[[1, E]], base=0, channel_multiplier=0).then_inc(s.counted, 1)
            pool.wait_ge(s.counted, 1)
            pool.tensor_copy(w.whichf[:], w.which[:]).then_inc(s.counted, 1)

        @block.scalar
        def _(act):
            act.wait_ge(s.step, 2 * len(banks))
            act.activation(u.ex[:], u.ex[:], ACT.Exp).then_inc(s.exp_done, 1)

        @block.vector
        def _(dve):
            steps = [0]

            def done(ins):
                steps[0] += 1
                ins.then_inc(s.step, 1)
                dve.wait_ge(s.step, steps[0])

            dve.wait_ge(s.logits_done, 1)
            for n, bank in enumerate(banks):
                some = slice(n * PER, min(NT, (n + 1) * PER))
                wide = some.stop - some.start
                done(dve.tensor_reduce(w.mx[:, some], bank[:, 0:wide, :], AX.X, ALU.max))
                done(dve.tensor_tensor(u.ex[:, some, :], bank[:, 0:wide, :],
                                       w.mx[:, some].unsqueeze(2).to_broadcast([P, wide, E]), ALU.subtract))
            dve.wait_ge(s.exp_done, 1)
            done(dve.tensor_reduce(u.inv_z[:], u.ex[:], AX.X, ALU.add))
            done(dve.reciprocal(u.inv_z[:], u.inv_z[:]))
            if bias_in_logits or gate_b is None:
                for n, bank in enumerate(banks):
                    some = slice(n * PER, min(NT, (n + 1) * PER))
                    done(dve.tensor_copy(w.select[:, some, :], bank[:, 0:some.stop - some.start, :]))
            else:
                done(dve.tensor_tensor(u.ex[:], u.ex[:], u.inv_z[:].unsqueeze(2).to_broadcast(spread), ALU.mult))
                done(dve.tensor_tensor(w.select[:], u.ex[:], g.psum[:, 7, 0:E].unsqueeze(1).to_broadcast(spread), ALU.add))
            for t in range(NT):
                dve.max(w.top[:, t, :], w.select[:, t, :]).then_inc(s.top_done, 1)
            for t in range(NT):
                dve.wait_ge(s.top_done, t + 1)
                dve.max_index(w.where[:, t, :], w.top[:, t, :], w.select[:, t, :]).then_inc(s.found, 1)
            dve.wait_ge(s.found, NT)
            done(dve.tensor_copy(w.wheref[:], w.where[:]))
            dve.wait_ge(s.counted, 2)
            for k in range(K):
                ins = dve.tensor_tensor(u.pick[:, k, :, :], w.whichf[:].unsqueeze(1).to_broadcast(spread),
                                        w.wheref[:, :, k].unsqueeze(2).to_broadcast(spread), ALU.is_equal)
                ins.then_inc(s.step, 1)
            steps[0] += K
            dve.wait_ge(s.step, steps[0])


def count_before(nc, g, u, E, chosen, pos, after=None):
    N = NT * E
    with (
        buffers(nc, prefix=((P, NT, E), BF16), total=((P, E), F32), total_bf=((P, E), BF16)) as w,
        stage_semaphores(nc, "prefix_done", "total_done", "counted", "pos_done") as s,
        nc.Block() as block,
    ):
        @block.vector
        def _(dve):
            dve.memset(w.prefix[:, 0, :], 0.0).then_inc(s.prefix_done, 1)
            for t in range(1, NT):
                dve.wait_ge(s.prefix_done, t)
                dve.tensor_tensor(w.prefix[:, t, :], w.prefix[:, t - 1, :], chosen[:, t - 1, :],
                                  ALU.add).then_inc(s.prefix_done, 1)
            if after is not None:
                dve.tensor_reduce(w.total[:], after[:].rearrange("p t e -> p e t"), AX.X, ALU.add).then_inc(s.total_done, 1)
                dve.wait_ge(s.total_done, 1)
                dve.tensor_copy(w.total_bf[:], w.total[:]).then_inc(s.total_done, 1)
            for n in range(0, N, 512):
                wide = min(512, N - n)
                dve.wait_ge(s.counted, n // 512 + 1)
                dve.tensor_copy(pos[:].rearrange("p t e -> p (t e)")[:, n:n + wide],
                                g.psum[:, n // 512, 0:wide]).then_inc(s.pos_done, 1)

        @block.tensor
        def _(pe):
            pe.wait_ge(s.prefix_done, NT)
            if after is not None:
                pe.wait_ge(s.total_done, 2)
            for n in range(0, N, 512):
                wide = min(512, N - n)
                out = g.psum[:, n // 512, 0:wide]
                pe.matmul(out, g.before[:], chosen[:].rearrange("p t e -> p (t e)")[:, n:n + wide], start=True, stop=False)
                last = pe.matmul(out, g.ones_bf[:], w.prefix[:].rearrange("p t e -> p (t e)")[:, n:n + wide],
                                 start=False, stop=after is None)
                if after is not None:
                    last = pe.matmul(out, g.ones_bf[:], w.total_bf[:].unsqueeze(1).to_broadcast([P, wide // E, E]),
                                     start=False, stop=True)
                last.then_inc(s.counted, 1)


def experts(nc, g, u, E, F, func):
    FC = F // P
    with (
        buffers(nc, src=((P, S), F32), coef=((P, QT, E), F32), hidden=((P, 2, FC, S), F32), acc=((P, QT, D), F32),
                coefT=((E, S), F32)) as w,
        nc.Fori(0, B) as b,
        stage_semaphores(nc, "src_done", "coef_done", "coef_turned", "coefT_done", "bias_mm", "hidden_mm", "hidden_done", "out_mm", "acc_done", "added") as s,
        nc.Block() as block,
    ):
        @block.tensor
        def _(pe):
            def hidden(e):
                for c in range(FC):
                    n = e * FC + c
                    if n >= 3:
                        pe.wait_ge(s.hidden_done, n - 2)
                    pe.matmul(g.psum[:, n % 3, :], u.w1[:, e, c * P:(c + 1) * P], w.src[:], start=True,
                              stop=True).then_inc(s.hidden_mm, 1)

            def out(e):
                pe.wait_ge(s.hidden_done, FC * (e + 1))
                if e >= 2:
                    pe.wait_ge(s.acc_done, QT * (e - 1))
                for j in range(QT):
                    o = g.psum[:, 4 + e % 2, j * D:(j + 1) * D]
                    for c in range(FC):
                        last = pe.matmul(o, w.hidden[:, e % 2, c, j * P:(j + 1) * P], u.w2[:, e, c, :], start=c == 0,
                                         stop=c == FC - 1)
                last.then_inc(s.out_mm, 1)

            pe.wait_ge(s.src_done, 1)
            hidden(0)
            pe.wait_ge(s.coef_done, 1)
            for j in range(QT):
                last = pe.transpose(g.psum[0:E, 6, j * P:(j + 1) * P], w.coef[:, j, :], g.ident[:])
            last.then_inc(s.coef_turned, 1)
            pe.wait_ge(s.coefT_done, 1)
            for j in range(QT):
                last = pe.matmul(g.psum[:, 7, j * D:(j + 1) * D], w.coefT[:, j * P:(j + 1) * P], u.b2[:], start=True, stop=True)
            last.then_inc(s.bias_mm, 1)
            for e in range(E + 1):
                if 0 < e < E:
                    hidden(e)
                if e >= 1:
                    out(e - 1)

        @block.scalar
        def _(act):
            for n in range(E * FC):
                e, c = n // FC, n % FC
                act.wait_ge(s.hidden_mm, n + 1)
                if e >= 2:
                    act.wait_ge(s.out_mm, e - 1)
                act.activation(w.hidden[:, e % 2, c, :], g.psum[:, n % 3, :], func,
                               bias=u.b1[:, n:n + 1]).then_inc(s.hidden_done, 1)

        @block.vector
        def _(dve):
            dve.tensor_copy(w.src[:], g.xnT[:, bass.ds(b * S, S)]).then_inc(s.src_done, 1)
            dve.tensor_copy(w.coef[:], u.coef[:, bass.ds(b * QT, QT), :]).then_inc(s.coef_done, 1)
            dve.wait_ge(s.coef_turned, 1)
            dve.tensor_copy(w.coefT[:], g.psum[0:E, 6, :]).then_inc(s.coefT_done, 1)
            dve.wait_ge(s.bias_mm, 1)
            dve.tensor_copy(w.acc[:], g.psum[:, 7, :].rearrange("p (t d) -> p t d", d=D)).then_inc(s.coef_done, 1)
            dve.wait_ge(s.coef_done, 2)
            for e in range(E):
                dve.wait_ge(s.out_mm, e + 1)
                if e >= 1:
                    dve.wait_ge(s.acc_done, QT * e)
                for j in range(QT):
                    dve.scalar_tensor_tensor(out=w.acc[:, j, :], in0=g.psum[:, 4 + e % 2, j * D:(j + 1) * D],
                                             scalar=w.coef[:, j, e:e + 1], in1=w.acc[:, j, :], op0=ALU.mult,
                                             op1=ALU.add).then_inc(s.acc_done, 1)
            dve.wait_ge(s.acc_done, QT * E)
            at = g.x[:, bass.ds(b * QT, QT), :]
            dve.tensor_tensor(at, at, w.acc[:], ALU.add).then_inc(s.added, 1)


def mixture8(nc, g, a, K, capacity, names, func):
    E, F = 8, 512
    gate, gate_b, w1, b1, w2, b2 = names
    layernorm(nc, g)
    with buffers(nc, w1=((P, E, F), F32), w2=((P, E, F // P, D), F32), b1=((P, E * F // P), F32), b2=((E, D), F32),
                 gate=((P, E), F32), gate_b=((1, E), F32), ex=((P, NT, E), F32), inv_z=((P, NT), F32),
                 pick=((P, K, NT, E), F32), coef=((P, NT, E), F32)) as u:
        pairs = [(u.w1[:], a[w1].rearrange("e k f -> k e f")), (u.w2[:], a[w2].rearrange("e (c p) d -> p e c d", p=P)),
                 (u.b1[:], a[b1].rearrange("e (c p) -> p (e c)", p=P)), (u.b2[:], a[b2]),
                 (u.gate[:], a[gate])]
        if gate_b:
            pairs.append((u.gate_b[:], row(a[gate_b])))
        load(nc, pairs)
        route(nc, g, u, E, K, u.gate, u.gate_b if gate_b else None, bool(gate_b))
        with buffers(nc, chosen=((P, K, NT, E), BF16), pos=((P, K, NT, E), F32), g1=((P, NT), F32), g2=((P, NT), F32),
                     den=((P, NT), F32), tmp=((P, NT, E), F32)) as w:
            with stage_semaphores(nc, "chosen_done") as s, nc.Block() as block:
                @block.vector
                def _(dve):
                    dve.tensor_copy(w.chosen[:], u.pick[:]).then_inc(s.chosen_done, 1)
                    dve.wait_ge(s.chosen_done, 1)
            for k in range(K):
                count_before(nc, g, u, E, w.chosen[:, k], w.pos[:, k], after=w.chosen[:, 0] if k else None)
            with stage_semaphores(nc, "step") as s, nc.Block() as block:
                @block.vector
                def _(dve):
                    steps = [0]

                    def done(ins):
                        steps[0] += 1
                        ins.then_inc(s.step, 1)
                        dve.wait_ge(s.step, steps[0])

                    spread = [P, NT, E]
                    done(dve.scalar_tensor_tensor(out=u.pick[:], in0=w.pos[:], scalar=float(capacity), in1=u.pick[:],
                                                  op0=ALU.is_lt, op1=ALU.mult))
                    if K == 1:
                        done(dve.tensor_tensor(u.coef[:], u.pick[:, 0], u.inv_z[:].unsqueeze(2).to_broadcast(spread), ALU.mult))
                    else:
                        done(dve.tensor_tensor(w.tmp[:], u.ex[:], w.chosen[:, 1], ALU.mult))
                        done(dve.tensor_reduce(w.g2[:], w.tmp[:], AX.X, ALU.add))
                        done(dve.tensor_tensor(w.g2[:], w.g2[:], u.inv_z[:], ALU.mult))
                        done(dve.tensor_tensor(w.den[:], w.g2[:], u.inv_z[:], ALU.add))
                        done(dve.tensor_scalar(w.den[:], w.den[:], 1e-9, None, ALU.add))
                        done(dve.reciprocal(w.den[:], w.den[:]))
                        done(dve.tensor_tensor(w.g1[:], u.inv_z[:], w.den[:], ALU.mult))
                        done(dve.tensor_tensor(w.g2[:], w.g2[:], w.den[:], ALU.mult))
                        done(dve.tensor_tensor(u.coef[:], u.pick[:, 0], w.g1[:].unsqueeze(2).to_broadcast(spread), ALU.mult))
                        done(dve.tensor_tensor(w.tmp[:], u.pick[:, 1], w.g2[:].unsqueeze(2).to_broadcast(spread), ALU.mult))
                        done(dve.tensor_tensor(u.coef[:], u.coef[:], w.tmp[:], ALU.add))
        experts(nc, g, u, E, F, func)


def layer1_ffn(nc, g, a):
    mixture8(nc, g, a, 2, 2 * 2 * NT * P // 8, ("L1_ffn_Wg", None, "L1_ffn_W1", "L1_ffn_b1", "L1_ffn_W2", "L1_ffn_b2"),
             ACT.Gelu)


def layer2_ffn(nc, g, a):
    E, F, K = 8, 512, 1
    FC = F // P
    CAP = -(-5 * NT * P // (4 * E))
    ROWS = E * CAP
    RT = ROWS // P
    FAR = float(1 << 20)
    PER = 4
    GROUPS = RT // PER
    assert RT * P == ROWS and GROUPS * PER == RT
    layernorm(nc, g)
    rows_in, rows_out = g.moe_in[0:ROWS, :], g.moe_out[0:ROWS, :]
    with buffers(nc, w1=((P, E, F), F32), w2=((P, E, FC, D), F32), b1=((P, E * FC), F32), b2=((P, E), F32),
                 gate=((P, E), F32), gate_b=((1, E), F32), ex=((P, NT, E), F32), inv_z=((P, NT), F32),
                 pick=((P, K, NT, E), F32), slot_in=((P, NT), I32), slot_out=((P, NT), I32), weight=((P, NT), F32)) as u:
        load(nc, [(u.w1[:], a["L2_ffn_w1"].rearrange("e k f -> k e f")),
                  (u.w2[:], a["L2_ffn_w2"].rearrange("e (c p) d -> p e c d", p=P)),
                  (u.b1[:], a["L2_ffn_b1"].rearrange("e (c p) -> p (e c)", p=P)),
                  (u.b2[:], a["L2_ffn_b2"].rearrange("e d -> d e")), (u.gate[:], a["L2_ffn_gate_wT"]),
                  (u.gate_b[:], row(a["L2_ffn_gate_b"]))])
        route(nc, g, u, E, K, u.gate, u.gate_b, True)
        with buffers(nc, chosen=((P, NT, E), BF16), pos=((P, NT, E), F32), tmp=((P, NT, E), F32), kept=((P, NT), F32),
                     slotf=((P, NT), F32), far=((P, NT), F32), first=((P, E), I32), zeros=((P, RT * D), F32)) as w:
            with stage_semaphores(nc, "chosen_done", "first_done", "cleared") as s, nc.Block() as block:
                @block.vector
                def _(dve):
                    dve.tensor_copy(w.chosen[:], u.pick[:, 0]).then_inc(s.chosen_done, 1)
                    dve.memset(w.zeros[:], 0.0).then_inc(s.chosen_done, 1)

                @block.gpsimd
                def _(pool):
                    pool.iota(w.first[:], pattern=[[CAP, E]], base=0, channel_multiplier=0).then_inc(s.first_done, 1)

                @block.sync
                def _(sp):
                    sp.wait_ge(s.chosen_done, 2)
                    sp.dma_start(rows_in.rearrange("(p n) d -> p (n d)", p=P), w.zeros[:]).then_inc(s.cleared, 16)
                    sp.wait_ge(s.cleared, 16)
            count_before(nc, g, u, E, w.chosen, w.pos)
            with stage_semaphores(nc, "step") as s, nc.Block() as block:
                @block.vector
                def _(dve):
                    steps = [0]

                    def done(ins):
                        steps[0] += 1
                        ins.then_inc(s.step, 1)
                        dve.wait_ge(s.step, steps[0])

                    done(dve.scalar_tensor_tensor(out=u.pick[:, 0], in0=w.pos[:], scalar=float(CAP), in1=u.pick[:, 0],
                                                  op0=ALU.is_lt, op1=ALU.mult))
                    done(dve.tensor_tensor(w.tmp[:], w.pos[:], w.first[:].unsqueeze(1).to_broadcast([P, NT, E]), ALU.add))
                    done(dve.tensor_tensor(w.tmp[:], w.tmp[:], u.pick[:, 0], ALU.mult))
                    done(dve.tensor_reduce(w.slotf[:], w.tmp[:], AX.X, ALU.add))
                    done(dve.tensor_reduce(w.kept[:], u.pick[:, 0], AX.X, ALU.add))
                    done(dve.tensor_tensor(u.weight[:], w.kept[:], u.inv_z[:], ALU.mult))
                    done(dve.tensor_scalar(w.far[:], w.kept[:], -FAR, FAR, ALU.mult, ALU.add))
                    done(dve.tensor_tensor(w.slotf[:], w.slotf[:], w.far[:], ALU.add))
                    done(dve.tensor_copy(u.slot_in[:], w.slotf[:]))
                    done(dve.tensor_scalar(w.slotf[:], w.slotf[:], float(ROWS - 1), None, ALU.min))
                    done(dve.tensor_copy(u.slot_out[:], w.slotf[:]))

        with nc.Block() as block:
            @block.gpsimd
            def _(pool):
                for t in range(NT):
                    pool.indirect_dma_start(
                        rows_in, bass.IndirectOffsetOnAxis(ap=u.slot_in[:, t:t + 1].bitcast(U32), axis=0),
                        g.xn[:, t, :], None, bounds_check=ROWS - 1, oob_is_err=False).then_inc(g.scattered_rows, 16)
                pool.wait_ge(g.scattered_rows, 16 * NT)

        with (
            buffers(nc, rows=((P, RT, D), F32), rT=((P, ROWS), F32), hidden=((P, 2, FC, CAP), F32), yT=((P, ROWS), F32),
                    y=((P, RT, D), F32)) as w,
            stage_semaphores(nc, "rows_in0", "rows_in1", "rows_in2", "rows_in3", "rows_in4", "turned", "rT_done",
                             "hidden_mm", "hidden_done", "out_mm", "yT_done", "y_turned", "y_done", "rows_saved") as s,
            nc.Block() as block,
        ):
            TURN, HIDDEN, OUT, BACK = 0, 1, 4, 6
            tiled_in = rows_in.rearrange("(t p) d -> p t d", p=P)
            tiled_out = rows_out.rearrange("(t p) d -> p t d", p=P)
            rows_ready = [s.rows_in0, s.rows_in1, s.rows_in2, s.rows_in3, s.rows_in4]

            def tiles(n):
                return slice(n * PER, (n + 1) * PER)

            def turn_before(e):
                return -(-(e + 1) * CAP // (PER * P))

            @block.sync
            def _(sp):
                for n in range(GROUPS):
                    sp.dma_start(w.rows[:, tiles(n), :], tiled_in[:, tiles(n), :]).then_inc(rows_ready[n], 16)
                for n in range(GROUPS):
                    sp.wait_ge(s.y_done, n + 1)
                    sp.dma_start(tiled_out[:, tiles(n), :], w.y[:, tiles(n), :]).then_inc(s.rows_saved, 16)
                sp.wait_ge(s.rows_saved, 16 * GROUPS)

            @block.tensor
            def _(pe):
                def turn(n):
                    pe.wait_ge(rows_ready[n], 16)
                    if n >= 1:
                        pe.wait_ge(s.rT_done, n)
                    for i in range(PER):
                        last = pe.transpose(g.psum[:, TURN, i * P:(i + 1) * P], w.rows[:, n * PER + i, :], g.ident[:])
                    last.then_inc(s.turned, 1)

                def hidden(e):
                    pe.wait_ge(s.rT_done, turn_before(e))
                    for c in range(FC):
                        n = e * FC + c
                        if n >= 3:
                            pe.wait_ge(s.hidden_done, n - 2)
                        pe.matmul(g.psum[:, HIDDEN + n % 3, 0:CAP], u.w1[:, e, c * P:(c + 1) * P],
                                  w.rT[:, e * CAP:(e + 1) * CAP], start=True, stop=True).then_inc(s.hidden_mm, 1)

                def out(e):
                    pe.wait_ge(s.hidden_done, FC * (e + 1))
                    if e >= 2:
                        pe.wait_ge(s.yT_done, e - 1)
                    for c in range(FC):
                        last = pe.matmul(g.psum[:, OUT + e % 2, 0:CAP], u.w2[:, e, c, :], w.hidden[:, e % 2, c, :],
                                         start=c == 0, stop=c == FC - 1)
                    last.then_inc(s.out_mm, 1)

                def turn_back(n):
                    pe.wait_ge(s.yT_done, -(-(n + 1) * PER * P // CAP))
                    if n >= 2:
                        pe.wait_ge(s.y_done, n - 1)
                    for i in range(PER):
                        at = (n * PER + i) * P
                        last = pe.transpose(g.psum[:, BACK + n % 2, i * P:(i + 1) * P], w.yT[:, at:at + P], g.ident[:])
                    last.then_inc(s.y_turned, 1)

                turned = back = 0
                for e in range(E + 2):
                    while e < E and turned < turn_before(min(e + 1, E - 1)):
                        turn(turned)
                        turned += 1
                    if e < E:
                        hidden(e)
                    if 1 <= e <= E:
                        out(e - 1)
                    while back < GROUPS and (back + 1) * PER * P <= (e - 1) * CAP:
                        turn_back(back)
                        back += 1

            @block.scalar
            def _(act):
                turned = 0
                for e in range(E):
                    while turned < turn_before(min(e + 1, E - 1)):
                        act.wait_ge(s.turned, turned + 1)
                        act.activation(w.rT[:, turned * PER * P:(turned + 1) * PER * P], g.psum[:, TURN, :],
                                       ACT.Copy).then_inc(s.rT_done, 1)
                        turned += 1
                    for c in range(FC):
                        n = e * FC + c
                        act.wait_ge(s.hidden_mm, n + 1)
                        if e >= 2:
                            act.wait_ge(s.out_mm, e - 1)
                        act.activation(w.hidden[:, e % 2, c, :], g.psum[:, HIDDEN + n % 3, 0:CAP], ACT.Relu,
                                       bias=u.b1[:, n:n + 1]).then_inc(s.hidden_done, 1)

            @block.vector
            def _(dve):
                back = 0
                for e in range(E + 1):
                    if e < E:
                        dve.wait_ge(s.out_mm, e + 1)
                        dve.tensor_scalar(w.yT[:, e * CAP:(e + 1) * CAP], g.psum[:, OUT + e % 2, 0:CAP], u.b2[:, e:e + 1],
                                          None, ALU.add).then_inc(s.yT_done, 1)
                    while back < GROUPS and (back + 1) * PER * P <= e * CAP:
                        dve.wait_ge(s.y_turned, back + 1)
                        dve.tensor_copy(w.y[:, tiles(back), :], g.psum[:, BACK + back % 2, :]
                                        .rearrange("p (t d) -> p t d", d=D)).then_inc(s.y_done, 1)
                        back += 1

        HALF = NT // 2
        with (
            buffers(nc, got=((P, NT, D), F32)) as w,
            stage_semaphores(nc, "added") as s,
            nc.Block() as block,
        ):
            halves = [g.fetched_first, g.fetched_second]

            @block.gpsimd
            def _(pool):
                for t in range(NT):
                    pool.indirect_dma_start(
                        w.got[:, t, :], None, rows_out,
                        bass.IndirectOffsetOnAxis(ap=u.slot_out[:, t:t + 1].bitcast(U32), axis=0),
                        bounds_check=ROWS - 1, oob_is_err=False).then_inc(halves[t // HALF], 16)

            @block.vector
            def _(dve):
                for t in range(NT):
                    if t % HALF == 0:
                        dve.wait_ge(halves[t // HALF], 16 * HALF)
                    dve.scalar_tensor_tensor(out=g.x[:, t, :], in0=w.got[:, t, :], scalar=u.weight[:, t:t + 1],
                                             in1=g.x[:, t, :], op0=ALU.mult, op1=ALU.add).then_inc(s.added, 1)


def prefetch_experts(nc, g, a):
    I = 88
    with nc.Block() as block:
        @block.sync
        def _(sp):
            sp.dma_start(g.w13[:, :, 0:I], a["L0_ffn_w1T"]).then_inc(g.prefetched, 16)
            sp.dma_start(g.w13[:, :, I:2 * I], a["L0_ffn_w3T"]).then_inc(g.prefetched, 16)
            sp.dma_start(g.w2[:], a["L0_ffn_w2T"]).then_inc(g.prefetched, 16)


def layer0_ffn(nc, g, a):
    E, K, CAP, I, SI = 64, 6, 64, 88, 176
    ROWS = E * CAP
    FAR = float(1 << 20)
    layernorm(nc, g)
    rows_in, rows_out = g.moe_in, g.moe_out
    with buffers(nc, gate=((P, E), F32), gate_b=((1, E), F32),
                 ws1=((P, SI), F32), ws3=((P, SI), F32), ws2=((P, 2, D), F32), slot_in=((P, NT, K), I32),
                 slot_out=((P, NT, K), I32), weight=((P, NT, K), F32)) as u:
        load(nc, [(u.gate[:], a["L0_ffn_gate_wT"]), (u.gate_b[:], row(a["L0_ffn_gate_b"])), (u.ws1[:], a["L0_ffn_ws1T"]),
                  (u.ws3[:], a["L0_ffn_ws3T"]), (u.ws2[:, 0, :], a["L0_ffn_ws2T"][0:P, :]),
                  (u.ws2[0:SI - P, 1, :], a["L0_ffn_ws2T"][P:SI, :])])
        with buffers(nc, ex=((P, NT, E), F32), inv_z=((P, NT), F32), pick=((P, K, NT, E), F32), chosen=((P, NT, E), BF16),
                     pos=((P, NT, E), F32), kept=((P, NT, E), F32), tmp=((P, NT, E), F32), slotf=((P, NT, K), F32),
                     first=((P, E), I32)) as w:
            route(nc, g, w, E, K, u.gate, u.gate_b, False)
            with stage_semaphores(nc, "step", "zeroed", "cleared") as s, nc.Block() as block:
                @block.vector
                def _(dve):
                    steps = [0]

                    def done(ins):
                        steps[0] += 1
                        ins.then_inc(s.step, 1)
                        dve.wait_ge(s.step, steps[0])

                    done(dve.tensor_tensor(w.kept[:], w.pick[:, 0], w.pick[:, 1], ALU.add))
                    for k in range(2, K):
                        done(dve.tensor_tensor(w.kept[:], w.kept[:], w.pick[:, k], ALU.add))
                    done(dve.tensor_copy(w.chosen[:], w.kept[:]))
                    dve.memset(w.tmp[:], 0.0).then_inc(s.zeroed, 1)

                @block.sync
                def _(sp):
                    sp.wait_ge(s.zeroed, 1)
                    view = rows_in.rearrange("(p n) d -> p (n d)", p=P)
                    wide = NT * E
                    for n in range(0, ROWS // P * D, wide):
                        sp.dma_start(view[:, n:n + wide], w.tmp[:].rearrange("p t e -> p (t e)")).then_inc(s.cleared, 16)
                    sp.wait_ge(s.cleared, 16 * (ROWS // P * D // wide))
            count_before(nc, g, w, E, w.chosen, w.pos)
            with stage_semaphores(nc, "step", "first_done") as s, nc.Block() as block:
                @block.gpsimd
                def _(pool):
                    pool.iota(w.first[:], pattern=[[CAP, E]], base=0, channel_multiplier=0).then_inc(s.first_done, 1)

                @block.vector
                def _(dve):
                    steps = [0]

                    def done(ins):
                        steps[0] += 1
                        ins.then_inc(s.step, 1)
                        dve.wait_ge(s.step, steps[0])

                    spread = [P, NT, E]
                    done(dve.tensor_scalar(w.kept[:], w.pos[:], float(CAP), None, ALU.is_lt))
                    done(dve.tensor_tensor(w.ex[:], w.ex[:], w.kept[:], ALU.mult))
                    done(dve.tensor_scalar(w.kept[:], w.kept[:], -FAR, FAR, ALU.mult, ALU.add))
                    done(dve.tensor_tensor(w.pos[:], w.pos[:], w.kept[:], ALU.add))
                    dve.wait_ge(s.first_done, 1)
                    done(dve.tensor_tensor(w.pos[:], w.pos[:], w.first[:].unsqueeze(1).to_broadcast(spread), ALU.add))
                    for k in range(K):
                        done(dve.tensor_tensor(w.tmp[:], w.pick[:, k], w.ex[:], ALU.mult))
                        done(dve.tensor_reduce(u.weight[:, :, k], w.tmp[:], AX.X, ALU.add))
                        done(dve.tensor_tensor(w.tmp[:], w.pick[:, k], w.pos[:], ALU.mult))
                        done(dve.tensor_reduce(w.slotf[:, :, k], w.tmp[:], AX.X, ALU.add))
                    done(dve.tensor_copy(u.slot_in[:], w.slotf[:]))
                    done(dve.tensor_scalar(w.slotf[:], w.slotf[:], float(ROWS - 1), None, ALU.min))
                    done(dve.tensor_copy(u.slot_out[:], w.slotf[:]))

        UN = QT
        PS = g.psum
        parts = [(0, P), (P, SI - P)]
        with (
            buffers(nc, tile=((P, UN, D), F32), slots=((P, UN, K), I32), gated=((P, 2, S), F32), h=((P, 2, S), F32)) as w,
            nc.Fori(0, B) as b,
            stage_semaphores(nc, "fixed", "hidden_mm", "silu_done", "h_done", "out_mm", "added") as s,
            nc.Block() as block,
        ):
            @block.gpsimd
            def _(pool):
                pool.wait_ge(s.fixed, 2)
                for i in range(UN):
                    for k in range(K):
                        pool.indirect_dma_start(
                            rows_in, bass.IndirectOffsetOnAxis(ap=w.slots[:, i, k:k + 1].bitcast(U32), axis=0),
                            w.tile[:, i, :], None, bounds_check=ROWS - 1, oob_is_err=False).then_inc(g.scattered, 16)
                pool.wait_ge(g.scattered, b * (16 * K * UN) + 16 * K * UN)

            @block.tensor
            def _(pe):
                src = g.xnT[:, bass.ds(b * S, S)]
                for c, (at, rows) in enumerate(parts):
                    pe.matmul(PS[0:rows, 2 * c, :], u.ws1[:, at:at + rows], src, start=True, stop=True)
                    pe.matmul(PS[0:rows, 2 * c + 1, :], u.ws3[:, at:at + rows], src, start=True,
                              stop=True).then_inc(s.hidden_mm, 1)
                pe.wait_ge(s.h_done, 2)
                for j in range(QT):
                    for c, (_, rows) in enumerate(parts):
                        last = pe.matmul(PS[:, 4, j * D:(j + 1) * D], w.h[0:rows, c, j * P:(j + 1) * P], u.ws2[0:rows, c, :],
                                         start=c == 0, stop=c == 1)
                last.then_inc(s.out_mm, 1)

            @block.scalar
            def _(act):
                for c, (_, rows) in enumerate(parts):
                    act.wait_ge(s.hidden_mm, c + 1)
                    act.activation(w.gated[0:rows, c, :], PS[0:rows, 2 * c, :], ACT.Silu).then_inc(s.silu_done, 1)

            @block.vector
            def _(dve):
                dve.tensor_copy(w.slots[:], u.slot_in[:, bass.ds(b * UN, UN), :]).then_inc(s.fixed, 1)
                dve.tensor_copy(w.tile[:], g.xn[:, bass.ds(b * UN, UN), :]).then_inc(s.fixed, 1)
                for c, (_, rows) in enumerate(parts):
                    dve.wait_ge(s.silu_done, c + 1)
                    dve.tensor_tensor(w.h[0:rows, c, :], w.gated[0:rows, c, :], PS[0:rows, 2 * c + 1, :],
                                      ALU.mult).then_inc(s.h_done, 1)
                dve.wait_ge(s.out_mm, 1)
                at = g.x[:, bass.ds(b * QT, QT), :]
                dve.tensor_tensor(at, at, PS[:, 4, :].rearrange("p (t d) -> p t d", d=D), ALU.add).then_inc(s.added, 1)

        EB = 8
        with (
            buffers(nc, rows=((CAP, EB, D), F32), rT=((P, EB * CAP), F32), gated=((CAP, EB, I), F32),
                    h=((CAP, EB, I), F32), hT=((I, EB * CAP), F32), y=((CAP, EB, D), F32)) as w,
            nc.Fori(0, E // EB) as n,
            stage_semaphores(nc, "rows_in", "turned", "rT_done", "hidden_mm", "silu_done", "h_done", "h_turned",
                             "hT_done", "out_mm", "y_done", "rows_saved") as s,
            nc.Block() as block,
        ):
            @block.sync
            def _(sp):
                sp.wait_ge(g.prefetched, 16 * 3)
                sp.dma_start(w.rows[:], rows_in.rearrange("(e c) d -> c e d", c=CAP)[:, bass.ds(n * EB, EB), :]).then_inc(s.rows_in, 16)
                sp.wait_ge(s.y_done, 2)
                sp.dma_start(rows_out.rearrange("(e c) d -> c e d", c=CAP)[:, bass.ds(n * EB, EB), :],
                             w.y[:]).then_inc(s.rows_saved, 16)
                sp.wait_ge(s.rows_saved, 16)

            def hid(e):
                return PS[0:CAP, 1 + e // 2, (e % 2) * 2 * I:(e % 2 + 1) * 2 * I]

            @block.tensor
            def _(pe):
                pe.wait_ge(s.rows_in, 16)
                for e in range(EB):
                    last = pe.transpose(PS[:, 0, e * CAP:(e + 1) * CAP], w.rows[:, e, :], g.ident[0:CAP, 0:CAP])
                last.then_inc(s.turned, 1)
                pe.wait_ge(s.rT_done, 1)
                for e in range(EB):
                    pe.matmul(hid(e).unsqueeze(1), w.rT[:, e * CAP:(e + 1) * CAP], g.w13[:, bass.ds(n * EB + e, 1), :],
                              start=True, stop=True).then_inc(s.hidden_mm, 1)
                for e in range(EB):
                    pe.wait_ge(s.h_done, e // 2 + 1)
                    last = pe.transpose(PS[0:I, 5, e * CAP:(e + 1) * CAP], w.h[:, e, :], g.ident[0:CAP, 0:CAP])
                last.then_inc(s.h_turned, 1)
                pe.wait_ge(s.hT_done, 1)
                for e in range(EB):
                    pe.matmul(PS[0:CAP, 6 + e // 4, (e % 4) * D:(e % 4 + 1) * D].unsqueeze(1), w.hT[:, e * CAP:(e + 1) * CAP],
                              g.w2[:, bass.ds(n * EB + e, 1), :], start=True, stop=True).then_inc(s.out_mm, 1)

            @block.scalar
            def _(act):
                act.wait_ge(s.turned, 1)
                act.activation(w.rT[:], PS[:, 0, :], ACT.Copy).then_inc(s.rT_done, 1)
                for m in range(EB // 2):
                    act.wait_ge(s.hidden_mm, 2 * m + 2)
                    both = PS[0:CAP, 1 + m, 0:4 * I].rearrange("p (e w i) -> p e w i", e=2, w=2)
                    act.activation(w.gated[:, 2 * m:2 * m + 2, :], both[:, :, 0, :], ACT.Silu).then_inc(s.silu_done, 1)
                act.wait_ge(s.h_turned, 1)
                act.activation(w.hT[:], PS[0:I, 5, :], ACT.Copy).then_inc(s.hT_done, 1)
                act.wait_ge(s.out_mm, 4)
                act.activation(w.y[:, 0:4, :], PS[0:CAP, 6, :].rearrange("p (e d) -> p e d", d=D), ACT.Copy).then_inc(s.y_done, 1)

            @block.vector
            def _(dve):
                for m in range(EB // 2):
                    dve.wait_ge(s.silu_done, m + 1)
                    both = PS[0:CAP, 1 + m, 0:4 * I].rearrange("p (e w i) -> p e w i", e=2, w=2)
                    dve.tensor_tensor(w.h[:, 2 * m:2 * m + 2, :], w.gated[:, 2 * m:2 * m + 2, :], both[:, :, 1, :],
                                      ALU.mult).then_inc(s.h_done, 1)
                dve.wait_ge(s.out_mm, 8)
                dve.tensor_copy(w.y[:, 4:8, :], PS[0:CAP, 7, :].rearrange("p (e d) -> p e d", d=D)).then_inc(s.y_done, 1)

        HALF = UN // 2
        with (
            buffers(nc, got=((P, UN, K, D), F32), slots=((P, UN, K), I32), wt=((P, UN, K), F32)) as w,
            nc.Fori(0, NT // UN) as t,
            stage_semaphores(nc, "fixed", "added") as s,
            nc.Block() as block,
        ):
            halves = [g.gathered_first, g.gathered_second]

            @block.gpsimd
            def _(pool):
                pool.wait_ge(s.fixed, 2)
                for i in range(UN):
                    for k in range(K):
                        pool.indirect_dma_start(
                            w.got[:, i, k, :], None, rows_out,
                            bass.IndirectOffsetOnAxis(ap=w.slots[:, i, k:k + 1].bitcast(U32), axis=0),
                            bounds_check=ROWS - 1, oob_is_err=False).then_inc(halves[i // HALF], 16)

            @block.vector
            def _(dve):
                dve.tensor_copy(w.slots[:], u.slot_out[:, bass.ds(t * UN, UN), :]).then_inc(s.fixed, 1)
                dve.tensor_copy(w.wt[:], u.weight[:, bass.ds(t * UN, UN), :]).then_inc(s.fixed, 1)
                dve.wait_ge(s.fixed, 2)
                for i in range(0, UN, HALF):
                    dve.wait_ge(halves[i // HALF], t * (16 * K * HALF) + 16 * K * HALF)
                    for k in range(K):
                        if k:
                            dve.wait_ge(s.added, i * K + k * HALF)
                        for j in range(i, i + HALF):
                            at = g.x[:, bass.ds(t * UN + j, 1), :]
                            dve.scalar_tensor_tensor(out=at, in0=w.got[:, j, k:k + 1, :], scalar=w.wt[:, j, k:k + 1],
                                                     in1=at, op0=ALU.mult, op1=ALU.add).then_inc(s.added, 1)


def layer2_warp(nc, g, a):
    W = 16
    KB = S // W
    TIMES = SC + KB - 1
    UNIT = 5
    PADDED = -(-TIMES // (2 * UNIT)) * 2 * UNIT
    BIG = 1e30
    BACK = 4
    layernorm(nc, g)
    with buffers(nc, table=((P, PADDED + 1, W + 1), F32), first=((P, 1), F32), last=((P, 1), F32),
                 inner=((P, 1), F32)) as u:
        with stage_semaphores(nc, "marked") as s, nc.Block() as block:
            @block.vector
            def _(dve):
                dve.tensor_reduce(u.first[:], g.ident[:, 0:P:KB], AX.X, ALU.add).then_inc(s.marked, 1)
                dve.tensor_reduce(u.last[:], g.ident[:, KB - 1:P:KB], AX.X, ALU.add).then_inc(s.marked, 1)
                dve.wait_ge(s.marked, 2)
                dve.tensor_scalar(u.inner[:], u.last[:], -1.0, 1.0, ALU.mult, ALU.add).then_inc(s.marked, 1)
                dve.wait_ge(s.marked, 3)

        with buffers(nc, skewed=((P, PADDED, W + 1), F32)) as v:
            PERB = 3
            with (
                buffers(nc, xsq=((P, NT * P), F32), csq=((P, B * SC), F32), cm2=((P, B * SC), F32),
                        dist=((P, SC, W), F32), wide=((P, PADDED * W), F32)) as w,
                stage_semaphores(nc, "squared", "product_done", "floored", "rooted", "filled", "placed", "spread",
                                 "read") as s,
                nc.Block() as block,
            ):
                @block.gpsimd
                def _(pool):
                    pool.memset(w.wide[:], BIG).then_inc(s.filled, 1)

                @block.vector
                def _(dve):
                    dve.tensor_tensor(w.xsq[:], g.xnT[:], g.xnT[:], ALU.mult).then_inc(s.squared, 1)
                    dve.tensor_tensor(w.csq[:], g.ctxT[:], g.ctxT[:], ALU.mult).then_inc(s.squared, 1)
                    dve.tensor_scalar(w.cm2[:], g.ctxT[:], -2.0, None, ALU.mult).then_inc(s.squared, 1)
                    for n in range(0, W, PERB):
                        m = min(PERB, W - n)
                        dve.wait_ge(s.product_done, n // PERB + 1)
                        dve.tensor_scalar(w.dist[:, :, n:n + m].rearrange("p i j -> p j i"),
                                          g.psum[:, n // PERB, 0:m * SC].rearrange("p (j i) -> p j i", i=SC), 0.0, None,
                                          ALU.max).then_inc(s.floored, 1)
                    dve.wait_ge(s.read, 16)
                    dve.tensor_copy(v.skewed[:, :, 1:W + 1], w.wide[:].rearrange("p (t j) -> p t j", j=W)).then_inc(s.spread, 1)
                    dve.memset(v.skewed[:, :, 0], BIG).then_inc(s.spread, 1)
                    dve.wait_ge(s.spread, 2)
                    dve.tensor_scalar(v.skewed[:, :, 0], v.skewed[:, :, 0], u.first[:, 0:1], None, ALU.mult).then_inc(s.spread, 1)

                @block.tensor
                def _(pe):
                    pe.wait_ge(s.squared, 3)
                    for n in range(W):
                        for b in range(B):
                            rows = slice(KB * b, KB * (b + 1))
                            out = g.psum[rows, n // PERB, (n % PERB) * SC:(n % PERB + 1) * SC]
                            x = slice(b * S + n, (b + 1) * S, W)
                            c = slice(b * SC, (b + 1) * SC)
                            at = (0, KB * b)
                            pe.matmul(out, g.xnT[:, x], w.cm2[:, c], start=True, stop=False, tile_position=at)
                            pe.matmul(out, w.xsq[:, x], g.ones[:, 0:1].to_broadcast([P, SC]), start=False, stop=False,
                                      tile_position=at)
                            last = pe.matmul(out, g.ones[:, 0:KB], w.csq[:, c], start=False, stop=True, tile_position=at)
                        if n % PERB == PERB - 1 or n == W - 1:
                            last.then_inc(s.product_done, 1)

                @block.scalar
                def _(act):
                    act.wait_ge(s.floored, -(-W // PERB))
                    act.activation(w.dist[:], w.dist[:], ACT.Sqrt).then_inc(s.rooted, 1)

                @block.sync
                def _(sp):
                    far = g.warp_skew
                    sp.wait_ge(s.filled, 1)
                    sp.dma_start(far[0:P, :], w.wide[:]).then_inc(s.placed, 16)
                    sp.wait_ge(s.placed, 16)
                    sp.wait_ge(s.rooted, 1)
                    for b in range(B):
                        dst = bass.AP(tensor=far.tensor, offset=far.offset + b * KB * PADDED * W,
                                      ap=[[(PADDED + 1) * W, KB], [1, SC * W]])
                        sp.dma_start(dst, w.dist[KB * b:KB * (b + 1), :, :].rearrange("p i j -> p (i j)")).then_inc(s.placed, 16)
                    sp.wait_ge(s.placed, 16 * (1 + B))
                    sp.dma_start(w.wide[:], far[0:P, :]).then_inc(s.read, 16)

            from_left = [max(0, k - 1) for k in range(KB)]
            with (
                buffers(nc, ring=((P, 2 * UNIT, W + 1), F32), best=((P, W + 1), F32)) as w,
                stage_semaphores(nc, "row_done", "best_done", "free0", "free1") as s,
                nc.Block() as block,
            ):
                free = [s.free0, s.free1]

                @block.vector
                def _(dve):
                    start = w.ring[:, 2 * UNIT - 1, :]
                    dve.memset(start, BIG).then_inc(s.row_done, 1)
                    dve.wait_ge(s.row_done, 1)
                    dve.tensor_scalar(start[:, 0:1], u.first[:], -BIG, BIG, ALU.mult, ALU.add).then_inc(s.row_done, 1)
                    dve.wait_ge(s.row_done, 2)
                    dve.tensor_copy(u.table[:, 0, :], start).then_inc(s.free0, 1)
                    dve.tensor_copy(w.best[:, 0:1], start[:, 0:1]).then_inc(s.free1, 1)
                    dve.wait_ge(s.free0, 1)
                    dve.wait_ge(s.free1, 1)
                    with dve.Fori(0, PADDED // (2 * UNIT)) as it:
                        for n in range(2 * UNIT):
                            before, now = w.ring[:, (n - 1) % (2 * UNIT), :], w.ring[:, n, :]
                            dve.wait_ge(s.row_done, it * (2 * UNIT) + n + 2)
                            dve.tensor_tensor(w.best[:, 1:W + 1], before[:, 0:W], before[:, 1:W + 1],
                                              ALU.min).then_inc(s.best_done, 1)
                            dve.stream_shuffle(w.best[:, 0:1], before[:, W:W + 1], from_left).then_inc(s.best_done, 1)
                            if n % UNIT == 0:
                                dve.wait_ge(free[n // UNIT], it + 1)
                            dve.wait_ge(s.best_done, it * (4 * UNIT) + 2 * n + 2)
                            dve.tensor_tensor_scan(now, w.best[:], v.skewed[:, bass.ds(it * (2 * UNIT) + n, 1), :]
                                                   .rearrange("p a w -> p (a w)"), BIG, ALU.min,
                                                   ALU.add).then_inc(s.row_done, 1)

                @block.scalar
                def _(act):
                    with act.Fori(0, PADDED // (2 * UNIT)) as it:
                        for half in range(2):
                            act.wait_ge(s.row_done, it * (2 * UNIT) + UNIT * (half + 1) + 2)
                            act.activation(u.table[:, bass.ds(it * (2 * UNIT) + UNIT * half + 1, UNIT), :],
                                           w.ring[:, UNIT * half:UNIT * (half + 1), :], ACT.Copy).then_inc(free[half], 1)

        with buffers(nc, take=((P, PADDED, 2 * W), F32), keep=((P, PADDED, 2 * W), F32), path=((P, PADDED, W), F32),
                     unskewed=((P, SC, W), F32)) as v:
            from_right = [min(KB - 1, k + 1) for k in range(KB)]
            with (
                buffers(nc, least=((P, PADDED, W), F32), diag=((P, PADDED, W + 1), F32), up=((P, PADDED, W), F32),
                        left=((P, PADDED, W + 1), F32), edge=((P, PADDED), F32)) as w,
                stage_semaphores(nc, "step") as s,
                nc.Block() as block,
            ):
                @block.vector
                def _(dve):
                    steps = [0]

                    def done(ins):
                        steps[0] += 1
                        ins.then_inc(s.step, 1)
                        dve.wait_ge(s.step, steps[0])

                    R = u.table
                    cd, cu, cl = R[:, 0:PADDED, 0:W], R[:, 0:PADDED, 1:W + 1], R[:, 1:PADDED + 1, 0:W]
                    diag, left = w.diag[:, :, 0:W], w.left[:, :, 0:W]
                    done(dve.tensor_tensor(w.least[:], cu, cl, ALU.min))
                    done(dve.tensor_tensor(diag, cd, w.least[:], ALU.is_le))
                    done(dve.tensor_tensor(w.up[:], cu, cl, ALU.is_le))
                    done(dve.tensor_tensor(w.least[:], w.up[:], diag, ALU.mult))
                    done(dve.tensor_tensor(w.up[:], w.up[:], w.least[:], ALU.subtract))
                    done(dve.tensor_tensor(w.least[:], w.up[:], diag, ALU.add))
                    done(dve.tensor_scalar(left, w.least[:], -1.0, 1.0, ALU.mult, ALU.add))
                    for m in (w.diag, w.left):
                        done(dve.memset(m[:, PADDED - 1, W:W + 1], 0.0))
                        done(dve.tensor_copy(w.edge[:], m[:, :, 0]))
                        done(dve.stream_shuffle(w.edge[:], w.edge[:], from_right))
                        done(dve.tensor_scalar(m[:, 0:PADDED - 1, W], w.edge[:, 1:PADDED], u.inner[:, 0:1], None, ALU.mult))
                    for r in range(W):
                        c = W - r
                        dve.tensor_copy(v.take[:, :, 2 * r], w.diag[:, :, c]).then_inc(s.step, 1)
                        dve.tensor_copy(v.take[:, :, 2 * r + 1], w.up[:, :, c - 1]).then_inc(s.step, 1)
                        dve.tensor_copy(v.keep[:, :, 2 * r], w.left[:, :, c]).then_inc(s.step, 1)
                    dve.memset(v.keep[:].rearrange("p t (r two) -> p t r two", two=2)[:, :, :, 1], 1.0).then_inc(s.step, 1)
                    steps[0] += 3 * W + 1
                    dve.wait_ge(s.step, steps[0])

            RW = 2 * W + 2
            with (
                buffers(nc, ring=((P, 2 * BACK, RW), F32), shares=((P, 2 * W), F32)) as w,
                stage_semaphores(nc, "row_done", "share_done", "free0", "free1", "set_up") as s,
                nc.Block() as block,
            ):
                free = [s.free0, s.free1]
                ring = w.ring[:]
                STEPS = TIMES - 1
                assert STEPS % (2 * BACK) == 0

                def pairs_of(n):
                    return bass.AP(tensor=ring.tensor, offset=ring.offset + n * RW + 1,
                                   ap=[[2 * BACK * RW, P], [2, W], [2, 2]])

                @block.vector
                def _(dve):
                    dve.memset(w.ring[:], 0.0).then_inc(s.set_up, 1)
                    dve.memset(w.shares[:], 0.0).then_inc(s.set_up, 1)
                    dve.wait_ge(s.set_up, 2)
                    dve.tensor_copy(w.shares[:, 1:2], u.last[:]).then_inc(s.set_up, 1)
                    dve.wait_ge(s.set_up, 3)
                    first = w.ring[:, 2 * BACK - 1, :]
                    dve.tensor_tensor_scan(first[:, 2:RW], v.keep[:, TIMES - 1, :], w.shares[:], 0.0, ALU.mult,
                                           ALU.add).then_inc(s.row_done, 1)
                    dve.wait_ge(s.row_done, 1)
                    dve.tensor_copy(v.path[:, TIMES - 1, :], first[:, 3:RW:2]).then_inc(s.free0, 1)
                    dve.tensor_copy(w.shares[:, 0:1], u.last[:]).then_inc(s.free1, 1)
                    dve.wait_ge(s.free0, 1)
                    dve.wait_ge(s.free1, 1)
                    with dve.Fori(0, STEPS // (2 * BACK)) as it:
                        for n in range(2 * BACK):
                            before = (n - 1) % (2 * BACK)
                            time = TIMES - 2 - n
                            dve.wait_ge(s.row_done, it * (2 * BACK) + n + 1)
                            if n % BACK == 0:
                                dve.wait_ge(free[n // BACK], it + 1)
                            dve.tensor_tensor(w.shares[:].rearrange("p (r two) -> p r two", two=2), pairs_of(before),
                                              v.take[:, bass.ds(it * (-2 * BACK) + time + 1, 1), :]
                                              .rearrange("p a (r two) -> p (a r) two", two=2), ALU.mult).then_inc(s.share_done, 1)
                            dve.stream_shuffle(w.ring[:, n, 1:2], w.ring[:, before, RW - 1:RW],
                                               from_right).then_inc(s.share_done, 1)
                            dve.wait_ge(s.share_done, it * (4 * BACK) + 2 * n + 2)
                            dve.tensor_tensor_scan(w.ring[:, n, 2:RW], v.keep[:, bass.ds(it * (-2 * BACK) + time, 1), :]
                                                   .rearrange("p a w -> p (a w)"), w.shares[:], w.ring[:, n, 1:2],
                                                   ALU.mult, ALU.add).then_inc(s.row_done, 1)

                @block.scalar
                def _(act):
                    with act.Fori(0, STEPS // (2 * BACK)) as it:
                        for half in range(2):
                            act.wait_ge(s.row_done, it * (2 * BACK) + BACK * (half + 1) + 1)
                            for n in range(BACK * half, BACK * (half + 1)):
                                ins = act.activation(v.path[:, bass.ds(it * (-2 * BACK) + TIMES - 2 - n, 1), :],
                                                     w.ring[:, n:n + 1, 3:RW:2], ACT.Copy)
                            ins.then_inc(free[half], 1)

            with (
                buffers(nc, onT=((P, 2, B, KB, W), F32), ctx=((P, 2, B, D), F32)) as w,
                stage_semaphores(nc, "saved", "read", "ctx_in", "turned", "on_done", "summed", "added") as s,
                nc.Block() as block,
            ):
                parts = ctx_tiles()

                @block.sync
                def _(sp):
                    for h, (at, rows) in enumerate(parts):
                        sp.dma_start(w.ctx[0:rows, h, :, :], a["ctx"][:, at:at + rows, :].rearrange("b i d -> i b d")).then_inc(s.ctx_in, 16)
                    far = g.warp_skew
                    sp.dma_start(far[0:P, 0:TIMES * W], v.path[:, 0:TIMES, :].rearrange("p t j -> p (t j)")).then_inc(s.saved, 16)
                    sp.wait_ge(s.saved, 16)
                    for b in range(B):
                        src = bass.AP(tensor=far.tensor, offset=far.offset + b * KB * PADDED * W,
                                      ap=[[(PADDED + 1) * W, KB], [1, SC * W]])
                        sp.dma_start(v.unskewed[KB * b:KB * (b + 1), :, :].rearrange("p i j -> p (i j)"), src).then_inc(s.read, 16)

                turns = [(h, r0) for h in range(2) for r0 in range(0, W, 4)]

                @block.tensor
                def _(pe):
                    pe.wait_ge(s.read, 16 * B)
                    for n, (h, r0) in enumerate(turns):
                        at, rows = parts[h]
                        if n >= 4:
                            pe.wait_ge(s.on_done, n - 3)
                        for r in range(r0, r0 + 4):
                            last = pe.transpose(g.psum[0:rows, n % 4, (r - r0) * P:(r - r0 + 1) * P],
                                                v.unskewed[:, at:at + rows, r], g.ident[:])
                        last.then_inc(s.turned, 1)
                    pe.wait_ge(s.on_done, len(turns))
                    pe.wait_ge(s.ctx_in, 32)
                    for b in range(B):
                        for j in range(QT):
                            for h, (_, rows) in enumerate(parts):
                                cells = w.onT[0:rows, h, b, :, :].rearrange("p k w -> p (k w)")[:, j * P:(j + 1) * P]
                                last = pe.matmul(g.psum[:, 4 + b, j * D:(j + 1) * D], cells, w.ctx[0:rows, h, b, :],
                                                 start=h == 0, stop=h == 1)
                        last.then_inc(s.summed, 1)

                @block.vector
                def _(dve):
                    for n, (h, r0) in enumerate(turns):
                        rows = parts[h][1]
                        dve.wait_ge(s.turned, n + 1)
                        for r in range(r0, r0 + 4):
                            ins = dve.tensor_copy(w.onT[0:rows, h, :, :, W - 1 - r],
                                                  g.psum[0:rows, n % 4, (r - r0) * P:(r - r0 + 1) * P]
                                                  .rearrange("p (b k) -> p b k", k=KB))
                        ins.then_inc(s.on_done, 1)
                    for b in range(B):
                        dve.wait_ge(s.summed, b + 1)
                        at = g.x[:, b * QT:(b + 1) * QT, :]
                        dve.tensor_tensor(at, at, g.psum[:, 4 + b, :].rearrange("p (t d) -> p t d", d=D), ALU.add).then_inc(s.added, 1)


def fp4_steps(dve, done, x, out, amax, inv, mag, N):
    spread = [x.shape[0], N, 16]
    done(dve.tensor_reduce(amax, x, AX.X, ALU.max, apply_absolute_value=True))
    done(dve.tensor_scalar(amax, amax, 1.0 / 6.0, 1e-12, ALU.mult, ALU.max))
    done(dve.reciprocal(inv, amax))
    done(dve.tensor_tensor(mag, x, inv.unsqueeze(2).to_broadcast(spread), ALU.mult))
    done(dve.scalar_tensor_tensor(out=mag, in0=mag, scalar=-1.0, in1=mag, op0=ALU.mult, op1=ALU.max))
    done(dve.tensor_scalar(x, x, 0.0, None, ALU.is_ge))
    done(dve.tensor_scalar(out, mag, 5.0, 2.0, ALU.is_gt, ALU.mult))
    for mid in (3.5, 2.5):
        done(dve.scalar_tensor_tensor(out=out, in0=mag, scalar=mid, in1=out, op0=ALU.is_gt, op1=ALU.add))
    done(dve.tensor_scalar(out, out, 2.0, None, ALU.mult))
    for mid in (1.75, 1.25, 0.75, 0.25):
        done(dve.scalar_tensor_tensor(out=out, in0=mag, scalar=mid, in1=out, op0=ALU.is_gt, op1=ALU.add))
    done(dve.scalar_tensor_tensor(out=out, in0=x, scalar=-0.5, in1=out, op0=ALU.add, op1=ALU.mult))
    done(dve.tensor_tensor(out, out, amax.unsqueeze(2).to_broadcast(spread), ALU.mult))


def layer3_ffn(nc, g, a):
    I, Q = 352, 16
    parts = [(0, P), (P, P), (2 * P, I - 2 * P)]
    layernorm(nc, g)
    PS = g.psum
    with buffers(nc, wgT=((P, I), F32), wuT=((P, I), F32), wdT=((P, 3, D), F32), xq=((P, NT, D), F32),
                 xqT=((P, NT * P), F32)) as u:
        NW = 2 * 3 * D // Q + I // Q
        with (
            buffers(nc, w=((P, NW, Q), F32), wq=((P, NW, Q), F32), amax=((P, NW), F32), inv=((P, NW), F32),
                    mag=((P, NW, Q), F32)) as w,
            stage_semaphores(nc, "zeroed", "loaded", "step", "turned", "out_done") as s,
            nc.Block() as block,
        ):
            flat = w.w[:].rearrange("p n q -> p (n q)")
            flatq = w.wq[:].rearrange("p n q -> p (n q)")
            STEPS = 16

            @block.sync
            def _(sp):
                sp.wait_ge(s.zeroed, 1)
                for m, name in enumerate(("L3_ffn_w_gate", "L3_ffn_w_up")):
                    for c, (at, rows) in enumerate(parts):
                        sp.dma_start(flat[0:rows, (3 * m + c) * D:(3 * m + c + 1) * D], a[name][at:at + rows, :]).then_inc(s.loaded, 16)
                sp.dma_start(flat[:, 6 * D:6 * D + I], a["L3_ffn_w_down"]).then_inc(s.loaded, 16)

            @block.vector
            def _(dve):
                dve.memset(w.w[:], 0.0).then_inc(s.zeroed, 1)
                dve.wait_ge(s.loaded, 16 * 7)
                steps = [0]

                def done(ins):
                    steps[0] += 1
                    ins.then_inc(s.step, 1)
                    dve.wait_ge(s.step, steps[0])

                fp4_steps(dve, done, w.w[:], w.wq[:], w.amax[:], w.inv[:], w.mag[:], NW)
                assert steps[0] == STEPS
                dve.wait_ge(s.turned, 1)
                dve.tensor_copy(u.wgT[:], PS[:, 0, 0:I]).then_inc(s.out_done, 1)
                dve.tensor_copy(u.wuT[:], PS[:, 1, 0:I]).then_inc(s.out_done, 1)
                for c, (_, rows) in enumerate(parts):
                    dve.tensor_copy(u.wdT[0:rows, c, :], PS[0:rows, 2, c * P:(c + 1) * P]).then_inc(s.out_done, 1)
                dve.wait_ge(s.out_done, 5)

            @block.tensor
            def _(pe):
                pe.wait_ge(s.step, STEPS)
                for m in range(2):
                    for c, (at, rows) in enumerate(parts):
                        pe.transpose(PS[:, m, at:at + rows], flatq[0:rows, (3 * m + c) * D:(3 * m + c + 1) * D],
                                     g.ident[0:rows, 0:rows])
                for c, (at, rows) in enumerate(parts):
                    last = pe.transpose(PS[0:rows, 2, c * P:(c + 1) * P], flatq[:, 6 * D + at:6 * D + at + rows], g.ident[:])
                last.then_inc(s.turned, 1)

        NX = NT * D // Q
        with (
            buffers(nc, x=((P, NX, Q), F32), amax=((P, NX), F32), inv=((P, NX), F32), mag=((P, NX, Q), F32)) as w,
            stage_semaphores(nc, "step") as s,
            nc.Block() as block,
        ):
            @block.vector
            def _(dve):
                steps = [0]

                def done(ins):
                    steps[0] += 1
                    ins.then_inc(s.step, 1)
                    dve.wait_ge(s.step, steps[0])

                done(dve.tensor_copy(w.x[:].rearrange("p n q -> p (n q)"), g.xn[:].rearrange("p t d -> p (t d)")))
                fp4_steps(dve, done, w.x[:], u.xq[:].rearrange("p t (m q) -> p (t m) q", q=Q), w.amax[:], w.inv[:],
                          w.mag[:], NX)
        turn_to_features(nc, g, u.xq, u.xqT)

        NH = QT * I // Q
        with (
            buffers(nc, src=((P, S), F32), gated=((P, QT, I), F32), h=((P, QT, I), F32), hq=((P, QT, I), F32),
                    hqT=((P, 3, S), F32), amax=((P, NH), F32), inv=((P, NH), F32), mag=((P, NH, Q), F32)) as w,
            nc.Fori(0, B) as b,
            stage_semaphores(nc, "src_done", "hidden_mm", "silu_done", "h_done", "step", "h_turned", "hT_done", "out_mm",
                             "added") as s,
            nc.Block() as block,
        ):
            STEPS = 16

            @block.tensor
            def _(pe):
                pe.wait_ge(s.src_done, 1)
                for j in range(QT):
                    pe.matmul(PS[:, 2 * j, 0:I], w.src[:, j * P:(j + 1) * P], u.wgT[:], start=True, stop=True)
                    pe.matmul(PS[:, 2 * j + 1, 0:I], w.src[:, j * P:(j + 1) * P], u.wuT[:], start=True,
                              stop=True).then_inc(s.hidden_mm, 1)
                pe.wait_ge(s.step, STEPS)
                for c, (at, rows) in enumerate(parts):
                    for j in range(QT):
                        last = pe.transpose(PS[0:rows, c, j * P:(j + 1) * P], w.hq[:, j, at:at + rows], g.ident[:])
                    last.then_inc(s.h_turned, 1)
                pe.wait_ge(s.hT_done, 3)
                for j in range(QT):
                    for c, (_, rows) in enumerate(parts):
                        last = pe.matmul(PS[:, 4, j * D:(j + 1) * D], w.hqT[0:rows, c, j * P:(j + 1) * P],
                                         u.wdT[0:rows, c, :], start=c == 0, stop=c == 2)
                last.then_inc(s.out_mm, 1)

            @block.scalar
            def _(act):
                for j in range(QT):
                    act.wait_ge(s.hidden_mm, j + 1)
                    act.activation(w.gated[:, j, :], PS[:, 2 * j, 0:I], ACT.Silu).then_inc(s.silu_done, 1)
                for c, (_, rows) in enumerate(parts):
                    act.wait_ge(s.h_turned, c + 1)
                    act.activation(w.hqT[0:rows, c, :], PS[0:rows, c, :], ACT.Copy).then_inc(s.hT_done, 1)

            @block.vector
            def _(dve):
                dve.tensor_copy(w.src[:], u.xqT[:, bass.ds(b * S, S)]).then_inc(s.src_done, 1)
                for j in range(QT):
                    dve.wait_ge(s.silu_done, j + 1)
                    dve.tensor_tensor(w.h[:, j, :], w.gated[:, j, :], PS[:, 2 * j + 1, 0:I], ALU.mult).then_inc(s.h_done, 1)
                dve.wait_ge(s.h_done, QT)
                steps = [0]

                def done(ins):
                    steps[0] += 1
                    ins.then_inc(s.step, 1)
                    dve.wait_ge(s.step, steps[0])

                fp4_steps(dve, done, w.h[:].rearrange("p j (m q) -> p (j m) q", q=Q),
                          w.hq[:].rearrange("p j (m q) -> p (j m) q", q=Q), w.amax[:], w.inv[:], w.mag[:], NH)
                dve.wait_ge(s.out_mm, 1)
                at = g.x[:, bass.ds(b * QT, QT), :]
                dve.tensor_tensor(at, at, PS[:, 4, :].rearrange("p (t d) -> p t d", d=D), ALU.add).then_inc(s.added, 1)


LAYERS = [layer0_attention, slots_from_context, layer0_ffn, layer1_attention, layer1_cross, layer1_ffn,
          layer2_attention, layer2_warp, layer2_ffn, layer3_attention, layer3_cross, layer3_ffn]


def decoder(nc, a, out, layers=None):
    with ExitStack() as held:
        def sb(name, shape, dt=F32):
            return held.enter_context(nc.sbuf_tensor(name, shape, dt))

        g = named(
            x=sb("x_tokens", [P, NT, D]), xn=sb("xn_tokens", [P, NT, D]), xnT=sb("xn_features", [P, NT * P]),
            ctxT=sb("ctx_features", [P, B * SC]), ident=sb("ident", [P, P]), ones=sb("ones", [P, P]),
            ident_bf=sb("ident_bf", [P, P], BF16), ones_bf=sb("ones_bf", [P, P], BF16),
            before=sb("before", [P, P], BF16), causal=sb("causal", [P, P], BF16), eta=sb("eta", [P, 1]),
            minus_e0=sb("minus_e0", [P, 1]),
            qs=sb("q_stacks", [P, H16, S], BF16), ks=sb("k_stacks", [P, H16, S], BF16),
            q_parts=nc.dram_tensor("q_parts", (B + 1, PARTS, P, S), BF16).ap(),
            k_parts=nc.dram_tensor("k_parts", (B + 1, PARTS, P, S), BF16).ap(),
            scattered=held.enter_context(nc.semaphore("scattered")), gathered_first=held.enter_context(nc.semaphore("gathered_first")),
            gathered_second=held.enter_context(nc.semaphore("gathered_second")), prefetched=held.enter_context(nc.semaphore("prefetched")),
            scattered_rows=held.enter_context(nc.semaphore("scattered_rows")),
            fetched_first=held.enter_context(nc.semaphore("fetched_first")),
            fetched_second=held.enter_context(nc.semaphore("fetched_second")),
            w13=None, w2=None,
            warp_skew=nc.dram_tensor("warp_skew", (P + 1, 190 * 16), F32).ap(),
            moe_in=nc.dram_tensor("expert_rows_in", (64 * 64, D), F32).ap(),
            moe_out=nc.dram_tensor("expert_rows_out", (64 * 64, D), F32).ap(),
            psum=held.enter_context(nc.psum_tensor("psum", [P, 8, 512], F32)))
        xs = a["x"].rearrange("b (t p) d -> p (b t) d", p=P)
        load(nc, [(g.x[:], xs), (g.ctxT[:], a["ctxT"])])
        constants(nc, g)
        prepare_stacks(nc, g)
        for n, layer in enumerate(LAYERS):
            if layers is not None and n not in layers:
                continue
            if layer is layer0_ffn:
                continue
            if layer is slots_from_context:
                with buffers(nc, w13=((P, 64, 2 * 88), F32), w2=((88, 64, D), F32)) as weights:
                    ge = g._replace(w13=weights.w13, w2=weights.w2)
                    prefetch_experts(nc, ge, a)
                    slots_from_context(nc, ge, a)
                    layer0_ffn(nc, ge, a)
            else:
                layer(nc, g, a)
        with stage_semaphores(nc, "saved") as s, nc.Block() as block:
            @block.sync
            def _(sp):
                sp.dma_start(out.rearrange("b (t p) d -> p (b t) d", p=P), g.x[:]).then_inc(s.saved, 16)
                sp.wait_ge(s.saved, 16)


_TURNED = ["L0_attn_W1", "L0_attn_W2", "L0_attn_Wq", "L0_attn_Wk", "L0_attn_Wv", "L0_attn_Wo",
           "L0_xattn_Wq", "L0_xattn_Wk", "L0_xattn_Wv", "L0_xattn_gru_wih", "L0_xattn_gru_whh", "L1_attn_phase",
           "L0_ffn_gate_w", "L0_ffn_ws1", "L0_ffn_ws2", "L0_ffn_ws3", "L2_ffn_gate_w",
           "L1_xattn_W_Q", "L1_xattn_W_K", "L1_xattn_W_V", "L1_xattn_W_O", "L3_attn_Wq", "L3_attn_Wk", "L3_attn_Wv",
           "L3_attn_Wo"]


def laid_out(inputs):
    c = np.ascontiguousarray
    a = {k: np.asarray(v) for k, v in inputs.items()}
    for k in _TURNED:
        a[k + "T"] = c(a.pop(k).T)
    for k in "QKV":
        a[f"L2_attn_{k}T"] = a.pop(f"L2_attn_{k}").transpose(1, 2, 0).reshape(D, -1)
    for k in ("w1", "w2", "w3"):
        a[f"L0_ffn_{k}T"] = a.pop(f"L0_ffn_{k}").transpose(2, 0, 1)
    a["L2_attn_WT"] = a.pop("L2_attn_W").transpose(2, 1, 0).reshape(-1, D)
    for k in ("mask_BxSxS2_bf0", "mask_SxS2_bk1"):
        a[k + "T"] = np.swapaxes(a[k], -1, -2)
    ctx = a.pop("ctx_1024")
    a["ctx"] = ctx
    a["ctxT"] = c(ctx.reshape(B * SC, D).T)
    return {k: c(v) for k, v in a.items()}


def kernel(**inputs):
    import concourse.bacc as _bacc
    from concourse.bass_utils import run_bass_kernel_spmd as _run

    nc = _bacc.Bacc("TRN2", target_bir_lowering=False, num_devices=1)
    arrays = laid_out(inputs)
    aps = {k: nc.dram_tensor("in_" + k, v.shape, mybir.dt.from_np(v.dtype), kind="ExternalInput").ap()
           for k, v in arrays.items()}
    out = nc.dram_tensor("out_0", (B, S, D), F32, kind="ExternalOutput").ap()
    decoder(nc, aps, out)
    r = _run(nc, [{"in_" + k: v for k, v in arrays.items()}], core_ids=[0])
    return r.results[0]["out_0"]
```

```python
from collections import namedtuple
from contextlib import ExitStack, contextmanager
from itertools import count

import numpy as np

import concourse.bass as bass
from concourse import mybir

ALU = mybir.AluOpType
ACT = mybir.ActivationFunctionType
AX = mybir.AxisListType
F32 = mybir.dt.float32
BF16 = mybir.dt.bfloat16
U32 = mybir.dt.uint32
I32 = mybir.dt.int32
U8 = mybir.dt.uint8

P = 128
D = 128
B = 4
S = 512
QT = S // P
NT = B * QT
SC = 154
SERIAL = count()
ALL_KEYS = [(t * P, P) for t in range(QT)]
MASKED = -1.0e30


def named(**items):
    return namedtuple("Named", list(items))(**items)


def ctx_tiles():
    return [(0, P), (P, SC - P)]


@contextmanager
def stage_semaphores(nc, *names):
    with ExitStack() as held:
        sems = {n: held.enter_context(nc.semaphore(n)) for n in names}
        yield named(**sems)
        with nc.Block() as block:
            @block.sync
            def _(sp):
                for s in sems.values():
                    sp.sem_clear(s)


@contextmanager
def buffers(nc, **shapes):
    stage = next(SERIAL)
    with ExitStack() as held:
        yield named(**{n: held.enter_context(nc.sbuf_tensor(f"{n}_{stage}", list(s), t))
                                 for n, (s, t) in shapes.items()})


@contextmanager
def zeroed(nc, tile):
    with stage_semaphores(nc, "zeros_in") as s, nc.Block() as block:
        @block.vector
        def _(dve):
            dve.memset(tile[:], 0.0).then_inc(s.zeros_in, 1)
            dve.wait_ge(s.zeros_in, 1)
    yield tile


def load(nc, pairs):
    with stage_semaphores(nc, "loaded") as s, nc.Block() as block:
        @block.sync
        def _(sp):
            for dst, src in pairs:
                sp.dma_start(dst, src).then_inc(s.loaded, 16)
            sp.wait_ge(s.loaded, 16 * len(pairs))


def constants(nc, g):
    with stage_semaphores(nc, "filled", "selected") as s:
        with nc.Block() as block:
            @block.gpsimd
            def _(pool):
                pool.memset(g.ident[:], 0.0).then_inc(s.filled, 1)
                pool.memset(g.ones[:], 1.0).then_inc(s.filled, 1)
                pool.memset(g.ones_bf[:], 1.0).then_inc(s.filled, 1)
                pool.memset(g.before[:], 1.0).then_inc(s.filled, 1)
                pool.memset(g.causal[:], 0.0).then_inc(s.filled, 1)
                pool.memset(g.eta[:], 1.0).then_inc(s.filled, 1)
                pool.memset(g.minus_e0[:], 0.0).then_inc(s.filled, 1)
                pool.wait_ge(s.filled, 7)
                pool.affine_select(out=g.ident[:], in_=g.ident[:], compare_op=ALU.not_equal, fill=1.0, base=0,
                                   pattern=[[-1, P]], channel_multiplier=1).then_inc(s.selected, 1)
                pool.affine_select(out=g.before[:], in_=g.before[:], compare_op=ALU.is_gt, fill=0.0, base=0,
                                   pattern=[[1, P]], channel_multiplier=-1).then_inc(s.selected, 1)
                pool.affine_select(out=g.causal[:], in_=g.causal[:], compare_op=ALU.is_ge, fill=MASKED, base=0,
                                   pattern=[[-1, P]], channel_multiplier=1).then_inc(s.selected, 1)
                pool.memset(g.eta[0:1, 0:1], -1.0).then_inc(s.filled, 1)
                pool.memset(g.minus_e0[0:1, :], -1.0).then_inc(s.filled, 1)
                pool.wait_ge(s.selected, 1)
                pool.tensor_copy(g.ident_bf[:], g.ident[:]).then_inc(s.selected, 1)
                pool.wait_ge(s.selected, 4)
                pool.wait_ge(s.filled, 9)


def layernorm(nc, g, loads=()):
    with (
        buffers(nc, stats=((P, NT, 6), F32), mv=((P, NT, 2), F32), rstd=((P, NT), F32)) as u,
        stage_semaphores(nc, "stats_done", "mean_done", "var_done", "sd_done", "rstd_done", "normed_done",
                         "turned", "feature_major_done", "loaded") as s,
        nc.Block() as block,
    ):
        @block.sync
        def _(sp):
            for dst, src in loads:
                sp.dma_start(dst, src, allow_slow_non_contiguous=True).then_inc(s.loaded, 16)
            if loads:
                sp.wait_ge(s.loaded, 16 * len(loads))

        def tiles(b):
            return range(b * QT, (b + 1) * QT)

        @block.vector
        def _(dve):
            for b in range(B + 1):
                if b < B:
                    for t in tiles(b):
                        dve.bn_stats(u.stats[:, t, :], g.x[:, t, :]).then_inc(s.stats_done, 1)
                    for t in tiles(b):
                        dve.wait_ge(s.stats_done, t + 1)
                        dve.bn_aggr(u.mv[:, t, :], u.stats[:, t, :]).then_inc(s.mean_done, 1)
                    dve.wait_ge(s.mean_done, QT * (b + 1))
                    dve.tensor_scalar(u.rstd[:, b * QT:(b + 1) * QT], u.mv[:, b * QT:(b + 1) * QT, 1], 1e-5, None,
                                      ALU.add).then_inc(s.var_done, 1)
                if b >= 1:
                    last = slice((b - 1) * QT, b * QT)
                    dve.wait_ge(s.sd_done, b)
                    dve.reciprocal(u.rstd[:, last], u.rstd[:, last]).then_inc(s.rstd_done, 1)
                    dve.wait_ge(s.rstd_done, b)
                    for t in tiles(b - 1):
                        dve.tensor_scalar(g.xn[:, t, :], g.x[:, t, :], u.mv[:, t, 0:1], u.rstd[:, t:t + 1],
                                          ALU.subtract, ALU.mult).then_inc(s.normed_done, 1)

        @block.scalar
        def _(act):
            for b in range(B + 1):
                if b < B:
                    act.wait_ge(s.var_done, b + 1)
                    act.activation(u.rstd[:, b * QT:(b + 1) * QT], u.rstd[:, b * QT:(b + 1) * QT],
                                   ACT.Sqrt).then_inc(s.sd_done, 1)
                if b >= 1:
                    act.wait_ge(s.turned, b)
                    act.activation(g.xnT[:, (b - 1) * S:b * S], g.psum[:, b - 1, :],
                                   ACT.Copy).then_inc(s.feature_major_done, 1)

        @block.tensor
        def _(pe):
            for b in range(B):
                for j in range(QT):
                    pe.wait_ge(s.normed_done, b * QT + j + 1)
                    last = pe.transpose(g.psum[:, b, j * P:(j + 1) * P], g.xn[:, b * QT + j, :], g.ident[:])
                last.then_inc(s.turned, 1)


def turn_to_features(nc, g, src, dstT):
    with (
        buffers(nc, fixed=((P, QT, D), F32)) as u,
        nc.Fori(0, B) as b,
        stage_semaphores(nc, "fixed_done", "turned", "feature_major_done") as s,
        nc.Block() as block,
    ):
        @block.vector
        def _(dve):
            dve.tensor_copy(u.fixed[:], src[:, bass.ds(b * QT, QT), :]).then_inc(s.fixed_done, 1)

        @block.tensor
        def _(pe):
            pe.wait_ge(s.fixed_done, 1)
            for j in range(QT):
                last = pe.transpose(g.psum[:, 0, j * P:(j + 1) * P], u.fixed[:, j, :], g.ident[:])
            last.then_inc(s.turned, 1)

        @block.scalar
        def _(act):
            act.wait_ge(s.turned, 1)
            act.activation(dstT[:, bass.ds(b * S, S)], g.psum[:, 0, :], ACT.Copy).then_inc(s.feature_major_done, 1)


def wide_attention(nc, g, *, w, H, dh, scale, out_scale):
    hp = dh
    keys = ALL_KEYS
    G = H * hp // P
    per = P // hp
    dv = dh
    HV = H * dv
    OC = HV // P
    HH = H // 2
    HC = OC // 2
    assert HH * dv == 512
    KT = len(keys)
    SK = keys[-1][0] + keys[-1][1]
    VN = max(1, HV // 512)
    VW = HV // VN
    jobs_v = [(t, n) for t in range(KT) for n in range(VN)]
    NQK = 2 * G
    NJOBS = NQK + len(jobs_v)
    NB = QT * H

    shapes = dict(src=((P, S), F32), qT=((P, G, S), F32), kT=((P, H, SK), F32),
                  v=((P, KT, HV), F32), probs=((P, 3, S), F32), probsT=((P, 2, KT * P), F32),
                  nmax=((P, QT, H), F32), rsum=((P, QT, H), F32), rinv=((P, 2, H), F32),
                  o=((P, 2, HV), F32), oT=((P, 2, HV), F32))
    with (
        buffers(nc, **shapes) as u,
        zeroed(nc, u.kT),
        nc.Fori(0, B) as b,
        stage_semaphores(nc, "src_done", "product_done", "even_out", "odd_out", "scores_done", "max_done", "probs_done",
                         "probs_turned", "probsT_done", "heads_done", "rinv_done", "o_done", "o_turned", "oT_done",
                         "projected", "stored") as s,
    ):
        with nc.Block() as block:
            @block.vector
            def _(dve):
                dve.tensor_copy(u.src[:], g.xnT[:, bass.ds(b * S, S)]).then_inc(s.src_done, 1)
                for n in range(1, NJOBS, 2):
                    dve.wait_ge(s.product_done, n + 1)
                    if n < NQK:
                        i = n // 2
                        for j in range(per):
                            rows = slice(j * hp, (j + 1) * hp)
                            ins = dve.tensor_copy(u.kT[rows, i * per + j, :], g.psum[rows, n % 8, 0:SK])
                    else:
                        t, c = jobs_v[n - NQK]
                        rows = keys[t][1]
                        ins = dve.tensor_copy(u.v[0:rows, t, c * VW:(c + 1) * VW], g.psum[0:rows, n % 8, 0:VW])
                    ins.then_inc(s.odd_out, 1)

            @block.scalar
            def _(act):
                for n in range(0, NJOBS, 2):
                    act.wait_ge(s.product_done, n + 1)
                    if n < NQK:
                        i = n // 2
                        ins = act.activation(u.qT[:, i, :], g.psum[:, n % 8, :], ACT.Identity, scale=scale)
                    else:
                        t, c = jobs_v[n - NQK]
                        rows = keys[t][1]
                        ins = act.activation(u.v[0:rows, t, c * VW:(c + 1) * VW], g.psum[0:rows, n % 8, 0:VW], ACT.Copy)
                    ins.then_inc(s.even_out, 1)

            @block.tensor
            def _(pe):
                pe.wait_ge(s.src_done, 1)
                for n in range(NJOBS):
                    if n >= 8 and n % 2 == 0:
                        pe.wait_ge(s.even_out, n // 2 - 3)
                    if n >= 8 and n % 2 == 1:
                        pe.wait_ge(s.odd_out, n // 2 - 3)
                    if n < NQK:
                        i = n // 2
                        if n % 2 == 0:
                            last = pe.matmul(g.psum[:, n % 8, :], w.wq[:, i, :], u.src[:], start=True, stop=True)
                        else:
                            last = pe.matmul(g.psum[:, n % 8, 0:SK], w.wk[:, i, :], u.src[:], start=True, stop=True)
                    else:
                        t, c = jobs_v[n - NQK]
                        at, rows = keys[t]
                        out = g.psum[0:rows, n % 8, 0:VW]
                        last = pe.matmul(out, u.src[:, at:at + rows], w.wv[:, c * VW:(c + 1) * VW],
                                         start=True, stop=True)
                    last.then_inc(s.product_done, 1)

        SCORES, TURNED, OUT, OTURN, FINAL = 0, 2, 4, 6, 7

        def width(n):
            return (n // H + 1) * P

        def tiles(n):
            return n // H + 1

        with nc.Block() as block:
            @block.tensor
            def _(pe):
                def scores(n):
                    q, h = n // H, n % H
                    N = width(n)
                    if n >= 2:
                        pe.wait_ge(s.probs_done, n - 1)
                    out = g.psum[:, SCORES + n % 2, 0:N]
                    pe.matmul(out, u.qT[:, h // per, q * P:(q + 1) * P], u.kT[:, h, 0:N], start=True, stop=False)
                    pe.matmul(g.psum[:, SCORES + n % 2, N - P:N], g.ident_bf[:], g.causal[:], start=False,
                              stop=True).then_inc(s.scores_done, 1)

                def turn(n):
                    pe.wait_ge(s.probs_done, n + 1)
                    if n >= 2:
                        pe.wait_ge(s.probsT_done, n - 1)
                    for t in range(tiles(n)):
                        at, rows = keys[t]
                        last = pe.transpose(g.psum[0:rows, TURNED + n % 2, t * P:(t + 1) * P],
                                            u.probs[:, n % 3, at:at + rows], g.ident[:])
                    last.then_inc(s.probs_turned, 1)

                def heads(n):
                    q, h = n // H, n % H
                    pe.wait_ge(s.probsT_done, n + 1)
                    if h % HH == 0 and n >= H:
                        pe.wait_ge(s.o_done, n // HH - 1)
                    for t in range(tiles(n)):
                        rows = keys[t][1]
                        last = pe.matmul(g.psum[:, OUT + h // HH, h % HH * dv:(h % HH + 1) * dv], u.probsT[0:rows, n % 2, t * P:(t + 1) * P],
                                         u.v[0:rows, t, h * dv:(h + 1) * dv], start=t == 0, stop=t == tiles(n) - 1)
                    last.then_inc(s.heads_done, 1)

                def turn_outputs(m):
                    pe.wait_ge(s.o_done, m + 1)
                    if m >= 1:
                        pe.wait_ge(s.oT_done, m)
                    for c in range(HC):
                        at = (m % 2 * HC + c) * P
                        last = pe.transpose(g.psum[:, OTURN, c * P:(c + 1) * P], u.o[:, m // 2 % 2, at:at + P], g.ident[:])
                    last.then_inc(s.o_turned, 1)

                def project(q):
                    pe.wait_ge(s.oT_done, 2 * (q + 1))
                    if q >= 1:
                        pe.wait_ge(s.stored, q)
                    for c in range(OC):
                        last = pe.matmul(g.psum[:, FINAL, 0:D], u.oT[:, q % 2, c * P:(c + 1) * P], w.wo[:, c, :],
                                         start=c == 0, stop=c == OC - 1)
                    last.then_inc(s.projected, 1)

                for n in range(NB + 3):
                    if n < NB:
                        scores(n)
                    if 2 <= n < NB + 2:
                        turn(n - 2)
                    if n >= 3:
                        heads(n - 3)
                    if n >= 5 and (n - 5) % HH == HH - 1:
                        turn_outputs((n - 5) // HH)
                    if n >= 8 and (n - 8) % H == H - 1:
                        project((n - 8) // H)
                turn_outputs(2 * QT - 1)
                project(QT - 1)

            @block.vector
            def _(dve):
                def maximum(n):
                    dve.wait_ge(s.scores_done, n + 1)
                    dve.tensor_reduce(u.nmax[:, n // H, n % H:n % H + 1], g.psum[:, SCORES + n % 2, 0:width(n)], AX.X,
                                      ALU.max, negate=True).then_inc(s.max_done, 1)

                def copy_turned(n):
                    dve.wait_ge(s.probs_turned, n + 1)
                    if n >= 2:
                        dve.wait_ge(s.heads_done, n - 1)
                    some = tiles(n) * P
                    ins = dve.tensor_copy(u.probsT[:, n % 2, 0:some], g.psum[:, TURNED + n % 2, 0:some])
                    ins.then_inc(s.probsT_done, 1)

                def normalise(m):
                    q, hs = m // 2, slice(m % 2 * HH, (m % 2 + 1) * HH)
                    dve.wait_ge(s.heads_done, HH * (m + 1))
                    if m >= 4:
                        dve.wait_ge(s.o_turned, m - 3)
                    dve.wait_ge(s.probs_done, HH * (m + 1))
                    dve.reciprocal(u.rinv[:, q % 2, hs], u.rsum[:, q, hs]).then_inc(s.rinv_done, 1)
                    dve.wait_ge(s.rinv_done, m + 1)
                    dve.tensor_tensor(u.o[:, q % 2, hs.start * dv:hs.stop * dv].rearrange("p (h d) -> p h d", d=dv),
                                      g.psum[:, OUT + m % 2, :].rearrange("p (h d) -> p h d", d=dv),
                                      u.rinv[:, q % 2, hs].unsqueeze(2).to_broadcast([P, HH, dv]),
                                      ALU.mult).then_inc(s.o_done, 1)

                def put(q):
                    dve.wait_ge(s.projected, q + 1)
                    at = g.x[:, bass.ds(b * QT + q, 1), :]
                    dve.scalar_tensor_tensor(out=at, in0=g.psum[:, FINAL, 0:D].unsqueeze(1), scalar=out_scale, in1=at,
                                             op0=ALU.mult, op1=ALU.add).then_inc(s.stored, 1)

                for n in range(NB + 3):
                    if n < NB:
                        maximum(n)
                    if 2 <= n < NB + 2:
                        copy_turned(n - 2)
                    if n >= 3 and (n - 3) % HH == HH - 1:
                        normalise((n - 3) // HH)
                    if n >= 10 and (n - 10) % H == H - 1:
                        put((n - 10) // H)
                put(QT - 1)

            @block.scalar
            def _(act):
                def copy_outputs(m):
                    act.wait_ge(s.o_turned, m + 1)
                    if m >= 4:
                        act.wait_ge(s.projected, m // 2 - 1)
                    act.activation(u.oT[:, m // 2 % 2, m % 2 * HC * P:(m % 2 + 1) * HC * P], g.psum[:, OTURN, 0:HC * P],
                                   ACT.Copy).then_inc(s.oT_done, 1)

                for n in range(NB + 3):
                    if n < NB:
                        act.wait_ge(s.max_done, n + 1)
                        if n >= 3:
                            act.wait_ge(s.probs_turned, n - 2)
                        act.activation(u.probs[:, n % 3, 0:width(n)], g.psum[:, SCORES + n % 2, 0:width(n)], ACT.Exp,
                                       bias=u.nmax[:, n // H, n % H:n % H + 1],
                                       accum_out=u.rsum[:, n // H, n % H:n % H + 1]).then_inc(s.probs_done, 1)
                    if n >= 6 and (n - 6) % HH == HH - 1:
                        copy_outputs((n - 6) // HH)
                copy_outputs(2 * QT - 1)


def log_map(nc, g, dst):
    EPS = 1e-6
    with (
        buffers(nc, sq=((P, NT, D), F32), n2=((P, NT), F32), y0=((P, NT), F32), z=((P, NT), F32), t0=((P, NT), F32),
                a=((P, NT), F32), c=((P, NT), F32)) as u,
        stage_semaphores(nc, "step", "rooted") as s,
        nc.Block() as block,
    ):
        @block.vector
        def _(dve):
            steps = [0]

            def done(ins):
                steps[0] += 1
                ins.then_inc(s.step, 1)
                dve.wait_ge(s.step, steps[0])

            tail = dst[:, :, 1:D]
            done(dve.tensor_scalar(tail, g.xn[:, :, 1:D], -8.0, 8.0, ALU.max, ALU.min))
            done(dve.tensor_tensor(u.sq[:, :, 1:D], tail, tail, ALU.mult))
            done(dve.tensor_reduce(u.n2[:], u.sq[:, :, 1:D], AX.X, ALU.add))
            done(dve.tensor_scalar(u.y0[:], u.n2[:], 1.0, EPS, ALU.add, ALU.add))
            dve.wait_ge(s.rooted, 1)
            done(dve.tensor_scalar(u.z[:], u.y0[:], 1.0 + EPS, None, ALU.max))
            done(dve.tensor_tensor(u.t0[:], u.y0[:], u.z[:], ALU.subtract))
            done(dve.tensor_tensor(u.c[:], u.t0[:], u.t0[:], ALU.mult))
            done(dve.tensor_tensor(u.c[:], u.n2[:], u.c[:], ALU.subtract))
            done(dve.tensor_scalar(u.c[:], u.c[:], EPS, None, ALU.max))
            done(dve.tensor_tensor(u.a[:], u.z[:], u.z[:], ALU.mult))
            done(dve.tensor_scalar(u.a[:], u.a[:], -1.0, None, ALU.add))
            dve.wait_ge(s.rooted, 3)
            done(dve.tensor_tensor(u.a[:], u.a[:], u.z[:], ALU.add))
            dve.wait_ge(s.rooted, 4)
            done(dve.tensor_scalar(u.a[:], u.a[:], 1e-3, None, ALU.max))
            done(dve.tensor_scalar(u.c[:], u.c[:], EPS, None, ALU.add))
            done(dve.reciprocal(u.c[:], u.c[:]))
            done(dve.tensor_tensor(u.a[:], u.a[:], u.c[:], ALU.mult))
            done(dve.tensor_copy(dst[:, :, 0], u.t0[:]))
            done(dve.tensor_tensor(dst[:], dst[:], u.a[:].unsqueeze(2).to_broadcast([P, NT, D]), ALU.mult))

        @block.scalar
        def _(act):
            act.wait_ge(s.step, 4)
            act.activation(u.y0[:], u.y0[:], ACT.Sqrt).then_inc(s.rooted, 1)
            act.wait_ge(s.step, 11)
            act.activation(u.c[:], u.c[:], ACT.Sqrt).then_inc(s.rooted, 1)
            act.activation(u.a[:], u.a[:], ACT.Sqrt).then_inc(s.rooted, 1)
            act.wait_ge(s.step, 12)
            act.activation(u.a[:], u.a[:], ACT.Ln).then_inc(s.rooted, 1)


def project_and_add(nc, g, o):
    EPS = 1e-6
    with (
        buffers(nc, sq=((P, NT, D), F32), n2=((P, NT), F32)) as u,
        stage_semaphores(nc, "step", "rooted") as s,
        nc.Block() as block,
    ):
        @block.vector
        def _(dve):
            dve.tensor_scalar(o[:, :, 1:D], o[:, :, 1:D], -8.0, 8.0, ALU.max, ALU.min).then_inc(s.step, 1)
            dve.wait_ge(s.step, 1)
            dve.tensor_tensor(u.sq[:, :, 1:D], o[:, :, 1:D], o[:, :, 1:D], ALU.mult).then_inc(s.step, 1)
            dve.wait_ge(s.step, 2)
            dve.tensor_reduce(u.n2[:], u.sq[:, :, 1:D], AX.X, ALU.add).then_inc(s.step, 1)
            dve.wait_ge(s.step, 3)
            dve.tensor_scalar(u.n2[:], u.n2[:], 1.0, EPS, ALU.add, ALU.add).then_inc(s.step, 1)
            dve.wait_ge(s.rooted, 1)
            dve.tensor_tensor(g.x[:], g.x[:], o[:], ALU.add).then_inc(s.step, 1)

        @block.scalar
        def _(act):
            act.wait_ge(s.step, 4)
            act.activation(o[:, :, 0], u.n2[:], ACT.Sqrt).then_inc(s.rooted, 1)


H16, DH8, G4 = 16, 8, 4
HG = H16 // G4
HW = P // HG
PARTS = 3
PAIRED = [(0, 0), (0, 1), (1, 0), (0, 2), (1, 1), (2, 0)]
STACK_DMAS = 2 * len(PAIRED)
MAX_AT = 96
MAX_END = MAX_AT + PARTS * HG


def split_projections(nc, g, w, q_src, kv_src, scale, SK, bq, bk, metric):
    LANES = 4 if metric is None else 2
    lanes = range(LANES)
    shapes = dict(q=((P, LANES, S), F32), k=((P, LANES, SK), F32), q_left=((P, LANES, S), F32),
                  k_left=((P, LANES, SK), F32), q_parts=((P, LANES, PARTS, S), BF16),
                  k_parts=((P, LANES, PARTS, SK), BF16))
    if metric is not None:
        shapes.update(metric_src=((P, LANES, S), F32), hidden=((P, LANES, 2, S), F32), gx=((P, LANES, S), F32))
    K, Q, HID, GX = 0, 1, 2, 0
    with (
        buffers(nc, **shapes) as u,
        nc.Fori(0, B // LANES) as pair,
        stage_semaphores(nc, "q_mm", "k_mm", "q_out", "q_ready", "k_ready", "k_first", "k_rest", "k_second", "k_done",
                         "q_first", "q_rest", "q_second", "q_done", "metric_in", "hidden_mm", "hidden_done", "gx_mm",
                         "gx_tanh", "gx_eta", "gx_abs", "written") as s,
        nc.Block() as block,
    ):
        def bank(c, n):
            return g.psum[:, 8 // LANES * c + n, :]

        @block.tensor
        def _(pe):
            for c in lanes:
                pe.matmul(bank(c, K)[:, 0:SK], w.wk[:], kv_src[:, bass.ds((pair * LANES + c) * SK, SK)], start=True,
                          stop=True).then_inc(s.k_mm, 1)
                pe.matmul(bank(c, Q), w.wq[:], q_src[:, bass.ds((pair * LANES + c) * S, S)], start=True,
                          stop=True).then_inc(s.q_mm, 1)
            if metric is not None:
                for c in lanes:
                    pe.wait_ge(s.metric_in, c + 1)
                    for n in range(2):
                        pe.matmul(bank(c, HID + n), metric.w1[:, n, :], u.metric_src[:, c, :], start=True,
                                  stop=True).then_inc(s.hidden_mm, 1)
                for c in lanes:
                    pe.wait_ge(s.k_ready, c + 1)
                    for n in range(2):
                        pe.wait_ge(s.hidden_done, 2 * c + n + 1)
                        last = pe.matmul(bank(c, GX), metric.w2[:, n, :], u.hidden[:, c, n, :], start=n == 0, stop=n == 1)
                    last.then_inc(s.gx_mm, 1)

        @block.scalar
        def _(act):
            for c in lanes:
                act.wait_ge(s.k_mm, c + 1)
                act.activation(u.k[:, c, :], bank(c, K)[:, 0:SK], ACT.Identity,
                               bias=bk[:, 0:1] if bk is not None else 0.0).then_inc(s.k_ready, 1)
                act.wait_ge(s.q_mm, c + 1)
                act.activation(u.q[:, c, :], bank(c, Q), ACT.Identity, bias=bq[:, 0:1] if bq is not None else 0.0,
                               scale=scale).then_inc(s.q_out, 1)
                act.wait_ge(s.k_ready, c + 1)
                act.activation(u.k_parts[:, c, 0, :], u.k[:, c, :], ACT.Copy).then_inc(s.k_first, 1)
            if metric is not None:
                for c in lanes:
                    for n in range(2):
                        act.wait_ge(s.hidden_mm, 2 * c + n + 1)
                        act.activation(u.hidden[:, c, n, :], bank(c, HID + n), ACT.Tanh,
                                       bias=metric.b1[:, n:n + 1]).then_inc(s.hidden_done, 1)
                for c in lanes:
                    act.wait_ge(s.gx_mm, c + 1)
                    act.activation(u.gx[:, c, :], bank(c, GX), ACT.Tanh, bias=metric.b2[:, 0:1]).then_inc(s.gx_tanh, 1)
            for c in lanes:
                act.wait_ge(s.k_rest, c + 1)
                act.activation(u.k_parts[:, c, 1, :], u.k_left[:, c, :], ACT.Copy).then_inc(s.k_second, 1)
                act.wait_ge(s.q_ready if metric is not None else s.q_out, c + 1)
                act.activation(u.q_parts[:, c, 0, :], u.q[:, c, :], ACT.Copy).then_inc(s.q_first, 1)
            for c in lanes:
                act.wait_ge(s.q_rest, c + 1)
                act.activation(u.q_parts[:, c, 1, :], u.q_left[:, c, :], ACT.Copy).then_inc(s.q_second, 1)

        @block.vector
        def _(dve):
            if metric is not None:
                for c in lanes:
                    dve.tensor_scalar(u.metric_src[:, c, :], g.xnT[:, bass.ds((pair * LANES + c) * S, S)],
                                      g.minus_e0[:, 0:1], None, ALU.add).then_inc(s.metric_in, 1)
            for c in lanes:
                dve.wait_ge(s.k_first, c + 1)
                dve.tensor_tensor(u.k_left[:, c, :], u.k[:, c, :], u.k_parts[:, c, 0, :], ALU.subtract).then_inc(s.k_rest, 1)
            for c in lanes:
                if metric is not None:
                    gx = u.gx[:, c, :]
                    dve.wait_ge(s.gx_tanh, c + 1)
                    dve.tensor_scalar(gx, gx, 0.1, g.eta[:, 0:1], ALU.mult, ALU.add).then_inc(s.gx_eta, 1)
                    dve.wait_ge(s.gx_eta, c + 1)
                    dve.scalar_tensor_tensor(out=gx, in0=gx, scalar=-1.0, in1=gx, op0=ALU.mult,
                                             op1=ALU.max).then_inc(s.gx_abs, 1)
                    dve.wait_ge(s.gx_abs, c + 1)
                    dve.wait_ge(s.q_out, c + 1)
                    dve.scalar_tensor_tensor(out=u.q[:, c, :], in0=gx, scalar=g.eta[:, 0:1], in1=u.q[:, c, :],
                                             op0=ALU.mult, op1=ALU.mult).then_inc(s.q_ready, 1)
                dve.wait_ge(s.k_second, c + 1)
                dve.tensor_tensor(u.k_parts[:, c, 2, :], u.k_left[:, c, :], u.k_parts[:, c, 1, :],
                                  ALU.subtract).then_inc(s.k_done, 1)
            for c in lanes:
                dve.wait_ge(s.q_first, c + 1)
                dve.tensor_tensor(u.q_left[:, c, :], u.q[:, c, :], u.q_parts[:, c, 0, :], ALU.subtract).then_inc(s.q_rest, 1)
            for c in lanes:
                dve.wait_ge(s.q_second, c + 1)
                dve.tensor_tensor(u.q_parts[:, c, 2, :], u.q_left[:, c, :], u.q_parts[:, c, 1, :],
                                  ALU.subtract).then_inc(s.q_done, 1)

        @block.sync
        def _(sp):
            def save(parts, src, N, batch):
                sp.dma_start(parts[batch, :, :, 0:N].rearrange("o c p s -> (o p) c s"), src).then_inc(s.written, 16)

            last = LANES - 1
            for c in lanes:
                sp.wait_ge(s.k_done, c + 1)
                save(g.k_parts, u.k_parts[:, c], SK, bass.ds(pair * LANES + c, 1))
            save(g.k_parts, u.k_parts[:, last], SK, slice(B, B + 1))
            for c in lanes:
                sp.wait_ge(s.q_done, c + 1)
                save(g.q_parts, u.q_parts[:, c], S, bass.ds(pair * LANES + c, 1))
            save(g.q_parts, u.q_parts[:, last], S, slice(B, B + 1))
            sp.wait_ge(s.written, 16 * 2 * (LANES + 1))


def prepare_stacks(nc, g):
    with buffers(nc, sel=((P, HG), F32)) as u, stage_semaphores(nc, "filled", "zeroed", "selected") as s, nc.Block() as block:
        @block.gpsimd
        def _(pool):
            pool.memset(g.ks[32:64], 0.0).then_inc(s.filled, 1)
            pool.wait_ge(s.filled, 1)

        @block.vector
        def _(dve):
            dve.tensor_reduce(u.sel[MAX_AT:MAX_END], g.ident[MAX_AT:MAX_END, MAX_AT:MAX_END].rearrange(
                "p (a j) -> p j a", j=HG), AX.X, ALU.add).then_inc(s.selected, 1)
            dve.memset(g.qs[32:64], 0.0).then_inc(s.zeroed, 1)
            dve.memset(g.qs[64:96], 0.0).then_inc(s.zeroed, 1)
            dve.memset(g.ks[64:96], 0.0).then_inc(s.zeroed, 1)
            dve.wait_ge(s.zeroed, 3)

        @block.scalar
        def _(act):
            act.wait_ge(s.selected, 1)
            for gi in range(G4):
                act.activation(g.ks[MAX_AT:MAX_END, gi * HG:(gi + 1) * HG, :],
                               u.sel[MAX_AT:MAX_END].unsqueeze(2).to_broadcast([PARTS * HG, HG, S]),
                               ACT.Copy).then_inc(s.selected, 1)
            act.wait_ge(s.selected, 1 + G4)


def narrow_attention(nc, g, *, w, keys, kv_src, scale, q_src=None, mask=None, metric=None, add_to=None, store=None,
                     out_scale=1.0, zero_if_all_masked=False, bq=None, bk=None, bv=None, bo=None):
    KT = len(keys)
    SK = keys[-1][0] + keys[-1][1]
    PER = QT // KT
    PERG = KT * HG
    NBLK = G4 * PERG
    LEAD = PERG + HG
    RING = 2 * HG
    q_src = q_src if q_src is not None else g.xnT
    split_projections(nc, g, w, q_src, kv_src, scale, SK, bq, bk, metric)

    shapes = dict(srck=((P, SK), F32), v=((P, KT, H16, HW), F32),
                  probs=((P, RING, S), F32), nmax=((P, G4, QT, HG), F32), left=((P, QT, HG), F32),
                  mp=((P, QT, MAX_END), BF16), outs=((P, 2, S), F32), rinv=((P, 2, QT, HG), F32),
                  o=((P, QT, D), F32), oT=((P, QT * P), F32))
    if mask is not None:
        by_batch = mask[0] == "drop"
        MB = B if by_batch else 1
        shapes.update(mask_add=((P, (MB + 1) * QT, SK), BF16), mask_addT=((P, MB * KT, S), BF16),
                      live=((P, QT, HG), F32))
        if by_batch:
            shapes.update(maskT_now=((P, KT, S), BF16))
    NS, NL = 2, 3
    SCORES, LOGITS, OUT, AUX = 0, NS, NS + NL, 7
    with buffers(nc, **shapes) as u:
        ks = g.ks[:, :, 0:SK]

        with stage_semaphores(nc, "zeroed") as s, nc.Block() as block:
            @block.vector
            def _(dve):
                dve.memset(u.mp[:], 0.0).then_inc(s.zeroed, 1)
                dve.memset(u.v[:], 0.0).then_inc(s.zeroed, 1)
                dve.wait_ge(s.zeroed, 2)
                dve.memset(u.v[:, :, :, DH8:DH8 + 1].rearrange("p k h c -> p (k h) c"), 1.0).then_inc(s.zeroed, 1)
                dve.wait_ge(s.zeroed, 3)

        def load_stack(sp, gi, batch, ready):
            rows = slice(gi * HG * DH8, (gi + 1) * HG * DH8)
            hs = slice(gi * HG, (gi + 1) * HG)
            for n, (qp, kp) in enumerate(PAIRED):
                for stack, parts, part, N in ((g.qs, g.q_parts, qp, S), (ks, g.k_parts, kp, SK)):
                    sp.dma_start(stack[n * DH8:(n + 1) * DH8, hs, :], parts[batch, part, rows, 0:N].rearrange(
                        "o (h d) s -> (o d) h s", d=DH8)).then_inc(ready, 16)

        def score(pe, bank, gi, kt, j, batch):
            for i in range(PER):
                q = kt * PER + i
                out = g.psum[:, bank, i * SK:(i + 1) * SK]
                last = pe.matmul(out, g.qs[0:MAX_AT, gi * HG + j, q * P:(q + 1) * P], ks[0:MAX_AT, gi * HG + j, :],
                                 start=True, stop=mask is None)
                if mask is not None:
                    madd = (u.mask_add[:, q, :] if isinstance(batch, int) or not by_batch
                            else u.mask_add[:, bass.ds(batch * QT + q, 1), :])
                    last = pe.matmul(out, g.ident_bf[:], madd, start=False, stop=True)
            return last

        def maximum(dve, bank, gi, kt, j):
            return dve.tensor_reduce(u.nmax[:, gi, kt * PER:(kt + 1) * PER, j],
                                     g.psum[:, bank, 0:PER * SK].rearrange("p (i k) -> p i k", k=SK), AX.X, ALU.max,
                                     negate=True)

        def split_maxima(dve, gi, split, done, before):
            part = [u.mp[:, :, MAX_AT + a * HG:MAX_AT + (a + 1) * HG] for a in range(PARTS)]
            dve.tensor_copy(part[0], u.nmax[:, gi]).then_inc(split, 1)
            dve.wait_ge(split, before + 1)
            dve.tensor_tensor(u.left[:], u.nmax[:, gi], part[0], ALU.subtract).then_inc(split, 1)
            dve.wait_ge(split, before + 2)
            dve.tensor_copy(part[1], u.left[:]).then_inc(split, 1)
            dve.wait_ge(split, before + 3)
            dve.tensor_tensor(part[2], u.left[:], part[1], ALU.subtract).then_inc(done, 1)

        def turn_maxima(pe):
            for q in range(QT):
                last = pe.matmul(g.psum[0:MAX_END, AUX, q * P:(q + 1) * P], u.mp[:, q, :], g.ident_bf[:],
                                 start=True, stop=True)
            return last

        def copy_maxima(act, h):
            return act.activation(g.qs[MAX_AT:MAX_END, h, :], g.psum[MAX_AT:MAX_END, AUX, :], ACT.Copy)

        with (
            stage_semaphores(nc, "stack0", "stack1", "stack2", "masks_done", "scores_done", "max_done", "split", "parts_done",
                             "maxima_turned", "maxima_done") as s,
            nc.Block() as block,
        ):
            @block.sync
            def _(sp):
                load_stack(sp, 0, slice(0, 1), s.stack0)
                load_stack(sp, 1, slice(0, 1), s.stack1)
                load_stack(sp, 2, slice(0, 1), s.stack2)
                sp.wait_ge(s.stack2, 16 * STACK_DMAS)

            @block.tensor
            def _(pe):
                pe.wait_ge(s.stack0, 16 * STACK_DMAS)
                if mask is not None:
                    pe.wait_ge(s.masks_done, 2 + KT)
                for n in range(LEAD):
                    if n == PERG:
                        pe.wait_ge(s.stack1, 16 * STACK_DMAS)
                    if n >= NS:
                        pe.wait_ge(s.max_done, n - NS + 1)
                    score(pe, SCORES + n % NS, n // PERG, n // HG % KT, n % HG, 0).then_inc(s.scores_done, 1)
                pe.wait_ge(s.parts_done, 1)
                turn_maxima(pe).then_inc(s.maxima_turned, 1)

            @block.vector
            def _(dve):
                if mask is not None:
                    kind, m, mT = mask
                    op = (MASKED, None, ALU.mult) if kind == "drop" else (-1.0, -MASKED, ALU.add, ALU.mult)
                    dve.tensor_scalar(u.mask_add[:, 0:MB * QT, :], m[:], *op).then_inc(s.masks_done, 1)
                    dve.tensor_scalar(u.mask_add[:, MB * QT:(MB + 1) * QT, :], m[:, 0:QT, :], *op).then_inc(s.masks_done, 1)
                    for t, (_, rows) in enumerate(keys):
                        dve.tensor_scalar(u.mask_addT[0:rows].rearrange("p (b t) s -> p b t s", t=KT)[:, :, t, :],
                                          mT[0:rows].rearrange("p (b t) s -> p b t s", t=KT)[:, :, t, :],
                                          *op).then_inc(s.masks_done, 1)
                for n in range(LEAD):
                    dve.wait_ge(s.scores_done, n + 1)
                    maximum(dve, SCORES + n % NS, n // PERG, n // HG % KT, n % HG).then_inc(s.max_done, 1)
                dve.wait_ge(s.max_done, PERG)
                split_maxima(dve, 0, s.split, s.parts_done, 0)

            @block.scalar
            def _(act):
                act.wait_ge(s.maxima_turned, 1)
                for h in range(HG):
                    copy_maxima(act, h).then_inc(s.maxima_done, 1)

        with (
            nc.Fori(0, B) as b,
            stage_semaphores(nc, "stack3", "stack0_next", "stack1_next", "stack2_next", "src_done", "v_mm", "v_done",
                             "scores_done", "max_done", "split", "parts_done", "maxima_turned", "maxima_done",
                             "maskT_done", "logits_done", "probs_done", "heads_done", "outputs_copied", "outputs_turned", "chain",
                             "normalised", "o_turned", "oT_done", "projected", "stored") as s,
            nc.Block() as block,
        ):
            @block.sync
            def _(sp):
                load_stack(sp, 3, bass.ds(b, 1), s.stack3)
                for gi, ready in enumerate((s.stack0_next, s.stack1_next, s.stack2_next)):
                    sp.wait_ge(s.probs_done, PERG * (gi + 1))
                    load_stack(sp, gi, bass.ds(b + 1, 1), ready)
                for ready in (s.stack1_next, s.stack2_next):
                    sp.wait_ge(ready, 16 * STACK_DMAS)

            output_quads = [m for m in range(KT + 2, NBLK // HG) if (m - 2) % KT == 0]

            @block.tensor
            def _(pe):
                def values():
                    pe.wait_ge(s.src_done, 1)
                    for t, (at, rows) in enumerate(keys):
                        out = g.psum[0:rows, AUX, t * P:(t + 1) * P]
                        last = pe.matmul(out, u.srck[:, at:at + rows], w.wv[:], start=True, stop=bv is None)
                        if bv is not None:
                            last = pe.matmul(out, g.ones[0:1, 0:rows], bv[0:1, :], start=False, stop=True)
                    last.then_inc(s.v_mm, 1)

                def scores(n):
                    ahead = (n + LEAD) % NBLK
                    if ahead == PERG * (G4 - 1):
                        pe.wait_ge(s.stack3, 16 * STACK_DMAS)
                    if ahead == 0:
                        pe.wait_ge(s.stack0_next, 16 * STACK_DMAS)
                    if ahead == PERG:
                        pe.wait_ge(s.stack1_next, 16 * STACK_DMAS)
                    if n >= NS:
                        pe.wait_ge(s.max_done, n - NS + 1)
                    score(pe, SCORES + n % NS, ahead // PERG, ahead // HG % KT, ahead % HG,
                          b if n + LEAD < NBLK else b + 1).then_inc(s.scores_done, 1)

                def wait_for_aux(n):
                    if n < PERG:
                        pe.wait_ge(s.v_done, 1)
                    if n >= PERG:
                        pe.wait_ge(s.maxima_done, n // PERG * HG)
                    before = sum(m * HG < n for m in output_quads)
                    if before:
                        pe.wait_ge(s.normalised, before)

                def turn_group(k):
                    pe.wait_ge(s.parts_done, k + 1)
                    wait_for_aux(k * PERG + PERG - HG)
                    turn_maxima(pe).then_inc(s.maxima_turned, 1)

                def logits(n):
                    gi, kt, j = n // PERG, n // HG % KT, n % HG
                    at, rows = keys[kt]
                    if kt == 0 and gi >= 1:
                        pe.wait_ge(s.maxima_done, HG * (gi - 1) + j + 1)
                    if n == 0 and mask is not None and by_batch:
                        pe.wait_ge(s.maskT_done, 1)
                    if n >= NL:
                        pe.wait_ge(s.probs_done, n - NL + 1)
                    out = g.psum[0:rows, LOGITS + n % NL, :]
                    last = pe.matmul(out, ks[0:MAX_END, gi * HG + j, at:at + rows], g.qs[0:MAX_END, gi * HG + j, :],
                                     start=True, stop=mask is None)
                    if mask is not None:
                        maddT = u.maskT_now[0:rows, kt, :] if by_batch else u.mask_addT[0:rows, kt, :]
                        last = pe.matmul(out, g.ident_bf[0:rows, 0:rows], maddT, start=False, stop=True)
                    last.then_inc(s.logits_done, 1)

                def heads(m):
                    gi, kt = m // KT, m % KT
                    rows = keys[kt][1]
                    pe.wait_ge(s.probs_done, HG * (m + 1))
                    if m == 0:
                        pe.wait_ge(s.v_done, 1)
                    if kt == 0 and gi >= 2:
                        pe.wait_ge(s.outputs_copied, gi - 1)
                    for j in range(HG):
                        last = pe.matmul(g.psum[j * HW:(j + 1) * HW, OUT + gi % 2, :], u.v[0:rows, kt, gi * HG + j, :],
                                         u.probs[0:rows, (m * HG + j) % RING, :], start=kt == 0, stop=kt == KT - 1,
                                         tile_position=(0, j * HW))
                    last.then_inc(s.heads_done, 1)

                def turn_outputs(gi):
                    pe.wait_ge(s.outputs_copied, gi + 1)
                    wait_for_aux(output_quads[gi] * HG if gi < len(output_quads) else NBLK)
                    if gi > len(output_quads):
                        pe.wait_ge(s.normalised, gi)
                    for q in range(QT):
                        last = pe.transpose(g.psum[:, AUX, q * P:(q + 1) * P], u.outs[:, gi % 2, q * P:(q + 1) * P],
                                            g.ident[:])
                    last.then_inc(s.outputs_turned, 1)

                values()
                for n in range(NBLK):
                    gi, m = n // PERG, n // HG
                    logits(n)
                    scores(n)
                    if n % HG == HG - 1 and m >= 1:
                        heads(m - 1)
                    if n % HG == 1 and m % KT == KT - 1:
                        turn_group(gi)
                    if n % HG == 1 and m in output_quads:
                        turn_outputs(output_quads.index(m))
                heads(NBLK // HG - 1)
                for gi in range(len(output_quads), G4):
                    turn_outputs(gi)
                pe.wait_ge(s.normalised, G4)
                for q in range(QT):
                    last = pe.transpose(g.psum[:, AUX, q * P:(q + 1) * P], u.o[:, q, :], g.ident[:])
                last.then_inc(s.o_turned, 1)
                pe.wait_ge(s.oT_done, 1)
                for q in range(QT):
                    out = g.psum[:, LOGITS, q * P:(q + 1) * P]
                    last = pe.matmul(out, u.oT[:, q * P:(q + 1) * P], w.wo[:], start=True, stop=bo is None)
                    if bo is not None:
                        last = pe.matmul(out, g.ones[0:1, :], bo[0:1, :], start=False, stop=True)
                last.then_inc(s.projected, 1)

            @block.vector
            def _(dve):
                def normalise(gi):
                    turned = g.psum[:, AUX, :].rearrange("p (q j r) -> p q j r", q=QT, r=HW)
                    rinv = u.rinv[:, gi % 2]
                    steps = 3 if zero_if_all_masked else 1
                    dve.wait_ge(s.outputs_turned, gi + 1)
                    dve.reciprocal(rinv, turned[:, :, :, DH8]).then_inc(s.chain, 1)
                    if zero_if_all_masked:
                        dve.tensor_scalar(u.live[:], u.nmax[:, gi], -MASKED / 2, None, ALU.is_lt).then_inc(s.chain, 1)
                        dve.wait_ge(s.chain, steps * gi + 2)
                        dve.tensor_tensor(rinv, rinv, u.live[:], ALU.mult).then_inc(s.chain, 1)
                    dve.wait_ge(s.chain, steps * (gi + 1))
                    for q in range(QT):
                        ins = dve.tensor_tensor(
                            u.o[:, q, gi * HG * DH8:(gi + 1) * HG * DH8].rearrange("p (j r) -> p j r", r=DH8),
                            turned[:, q, :, 0:DH8], rinv[:, q].unsqueeze(2).to_broadcast([P, HG, DH8]), ALU.mult)
                    ins.then_inc(s.normalised, 1)

                if mask is not None and by_batch:
                    for t, (_, rows) in enumerate(keys):
                        ins = dve.tensor_copy(u.maskT_now[0:rows, t:t + 1, :],
                                              u.mask_addT[0:rows, bass.ds(b * KT + t, 1), :])
                    ins.then_inc(s.maskT_done, 1)
                dve.tensor_copy(u.srck[:], kv_src[:, bass.ds(b * SK, SK)]).then_inc(s.src_done, 1)
                for n in range(NBLK):
                    gi, m = n // PERG, n // HG
                    ahead = (n + LEAD) % NBLK
                    dve.wait_ge(s.scores_done, n + 1)
                    maximum(dve, SCORES + n % NS, ahead // PERG, ahead // HG % KT, ahead % HG).then_inc(s.max_done, 1)
                    if n % HG == HG - 1:
                        if m % KT == KT - 2:
                            dve.wait_ge(s.max_done, n + 1)
                            if gi >= 1:
                                dve.wait_ge(s.maxima_turned, gi)
                            split_maxima(dve, (gi + 1) % G4, s.split, s.parts_done, 3 * gi)
                    if n % HG == 2 and m in output_quads:
                        normalise(output_quads.index(m))
                for gi in range(len(output_quads), G4):
                    normalise(gi)
                dve.wait_ge(s.projected, 1)
                result = g.psum[:, LOGITS, :].rearrange("p (q d) -> p q d", d=D)
                if add_to is not None:
                    at = add_to[:, bass.ds(b * QT, QT), :]
                    dve.tensor_tensor(at, result, at, ALU.add).then_inc(s.stored, 1)
                else:
                    dve.tensor_scalar(store[:, bass.ds(b * QT, QT), :], result, out_scale, None,
                                      ALU.mult).then_inc(s.stored, 1)

            @block.scalar
            def _(act):
                def exponentials(n):
                    rows = keys[n // HG % KT][1]
                    act.wait_ge(s.logits_done, n + 1)
                    if n >= RING:
                        act.wait_ge(s.heads_done, (n - RING) // HG + 1)
                    act.activation(u.probs[0:rows, n % RING, :], g.psum[0:rows, LOGITS + n % NL, :],
                                   ACT.Exp).then_inc(s.probs_done, 1)

                def copy_outputs(gi):
                    act.wait_ge(s.heads_done, KT * (gi + 1))
                    if gi >= 2:
                        act.wait_ge(s.outputs_turned, gi - 1)
                    act.activation(u.outs[:, gi % 2, :], g.psum[:, OUT + gi % 2, :],
                                   ACT.Copy).then_inc(s.outputs_copied, 1)

                act.wait_ge(s.v_mm, 1)
                for t, (_, rows) in enumerate(keys):
                    ins = act.activation(u.v[0:rows, t, :, 0:DH8],
                                         g.psum[0:rows, AUX, t * P:(t + 1) * P].rearrange("p (h d) -> p h d", d=DH8),
                                         ACT.Copy)
                ins.then_inc(s.v_done, 1)
                for n in range(NBLK):
                    gi, m = n // PERG, n // HG
                    exponentials(n)
                    if m % KT == KT - 1 and n % HG >= HG // 2:
                        if n % HG == HG // 2:
                            act.wait_ge(s.maxima_turned, gi + 1)
                        for j in (2 * (n % HG) - HG, 2 * (n % HG) - HG + 1):
                            copy_maxima(act, (gi + 1) % G4 * HG + j).then_inc(s.maxima_done, 1)
                    if n % HG == HG - 1:
                        if m >= KT and m % KT == 0:
                            copy_outputs(m // KT - 1)
                copy_outputs(G4 - 1)
                act.wait_ge(s.o_turned, 1)
                act.activation(u.oT[:], g.psum[:, AUX, :], ACT.Copy).then_inc(s.oT_done, 1)


def row(ap):
    return ap.rearrange("(a n) -> a n", a=1)


def column(ap):
    return ap.rearrange("(n a) -> n a", a=1)


def layer0_attention(nc, g, a):
    with (
        buffers(nc, wq=((P, P), F32), wk=((P, P), F32), wv=((P, D), F32), wo=((P, D), F32),
                w1=((P, 2, P), F32), w2=((P, 2, P), F32), b1=((P, 2), F32), b2=((P, 1), F32),
                vmap=((P, NT, D), F32), vT=((P, NT * P), F32)) as u,
    ):
        layernorm(nc, g, [(u.wv[:], a["L0_attn_WvT"]), (u.wo[:], a["L0_attn_WoT"]),
                          (u.wq[:], a["L0_attn_WqT"]), (u.wk[:], a["L0_attn_WkT"]),
                          (u.w1[:], a["L0_attn_W1T"].rearrange("k (c m) -> k c m", c=2)),
                          (u.b1[:], a["L0_attn_b1"].rearrange("(c p) -> p c", c=2)),
                          (u.w2[:], a["L0_attn_W2T"].rearrange("(c p) m -> p c m", c=2)), (u.b2[:], column(a["L0_attn_b2"]))])
        log_map(nc, g, u.vmap)
        turn_to_features(nc, g, u.vmap, u.vT)
        narrow_attention(nc, g, w=u, keys=ALL_KEYS, kv_src=u.vT, q_src=u.vT, scale=DH8 ** -0.5,
                         metric=named(w1=u.w1, w2=u.w2, b1=u.b1, b2=u.b2), store=u.vmap, out_scale=0.1)
        project_and_add(nc, g, u.vmap)


def layer1_cross(nc, g, a):
    keys = ctx_tiles()
    KT = len(keys)
    with buffers(nc, wq=((P, P), F32), wk=((P, P), F32), wv=((P, D), F32), wo=((P, D), F32),
                 mask=((P, NT, SC), U8), maskT=((P, B * KT, S), U8)) as u:
        maskT = u.maskT[:].rearrange("p (b t) s -> p b t s", t=KT)
        layernorm(nc, g, [(u.wv[:], a["L1_xattn_W_VT"]), (u.wo[:], a["L1_xattn_W_OT"]), (u.wq[:], a["L1_xattn_W_QT"]),
                          (u.wk[:], a["L1_xattn_W_KT"]),
                          (u.mask[:], a["mask_BxSxS2_bf0"].rearrange("b (t p) k -> p (b t) k", p=P))]
                     + [(maskT[0:rows, :, t, :], a["mask_BxSxS2_bf0T"][:, at:at + rows, :].rearrange("b k s -> k b s"))
                        for t, (at, rows) in enumerate(keys)])
        narrow_attention(nc, g, w=u, keys=keys, kv_src=g.ctxT, scale=DH8 ** -0.5,
                         mask=("drop", u.mask, u.maskT), zero_if_all_masked=True, add_to=g.x)


def layer3_attention(nc, g, a):
    with buffers(nc, wq=((P, P), F32), wk=((P, P), F32), wv=((P, D), F32), wo=((P, D), F32),
                 bq=((P, 1), F32), bqs=((P, 1), F32), bk=((P, 1), F32), bv=((1, D), F32), bo=((1, D), F32)) as u:
        layernorm(nc, g, [(u.wv[:], a["L3_attn_WvT"]), (u.wo[:], a["L3_attn_WoT"]), (u.bv[:], row(a["L3_attn_bv"])),
                          (u.bo[:], row(a["L3_attn_bo"])), (u.wq[:], a["L3_attn_WqT"]), (u.wk[:], a["L3_attn_WkT"]),
                          (u.bq[:], column(a["L3_attn_bq"])), (u.bk[:], column(a["L3_attn_bk"]))])
        scale_bias(nc, u.bqs, u.bq, DH8 ** -0.5)
        narrow_attention(nc, g, w=u, keys=ALL_KEYS, kv_src=g.xnT, scale=DH8 ** -0.5, add_to=g.x,
                         bq=u.bqs, bk=u.bk, bv=u.bv, bo=u.bo)


def layer3_cross(nc, g, a):
    keys = ctx_tiles()
    with buffers(nc, wq=((P, P), F32), wk=((P, P), F32), wv=((P, D), F32), wo=((P, D), F32),
                 mask=((P, QT, SC), U8), maskT=((P, len(keys), S), U8), bq=((P, 1), F32), bqs=((P, 1), F32),
                 bk=((P, 1), F32), bv=((1, D), F32), bo=((1, D), F32)) as u:
        layernorm(nc, g, [(u.wv[:], a["L3_xattn_Wv"]), (u.wo[:], a["L3_xattn_Wo"]), (u.bv[:], row(a["L3_xattn_bv"])),
                          (u.bo[:], row(a["L3_xattn_bo"])), (u.wq[:], a["L3_xattn_Wq"]), (u.wk[:], a["L3_xattn_Wk"]),
                          (u.bq[:], column(a["L3_xattn_bq"])), (u.bk[:], column(a["L3_xattn_bk"])),
                          (u.mask[:], a["mask_SxS2_bk1"].rearrange("(t p) k -> p t k", p=P))]
                     + [(u.maskT[0:rows, t, :], a["mask_SxS2_bk1T"][at:at + rows, :]) for t, (at, rows) in enumerate(keys)])
        scale_bias(nc, u.bqs, u.bq, DH8 ** -0.5)
        narrow_attention(nc, g, w=u, keys=keys, kv_src=g.ctxT, scale=DH8 ** -0.5,
                         mask=("keep", u.mask, u.maskT), add_to=g.x, bq=u.bqs, bk=u.bk, bv=u.bv, bo=u.bo)


def layer2_attention(nc, g, a):
    DQ = 64
    with buffers(nc, wq=((P, 8, P), F32), wk=((P, 8, P), F32), wv=((P, H16 * DQ), F32), wo=((P, 8, D), F32)) as u:
        layernorm(nc, g, [(u.wq[:], a["L2_attn_QT"].rearrange("k (g m) -> k g m", g=8)),
                          (u.wk[:], a["L2_attn_KT"].rearrange("k (g m) -> k g m", g=8)),
                          (u.wv[:], a["L2_attn_VT"]), (u.wo[:], a["L2_attn_WT"].rearrange("(c p) d -> p c d", p=P))])
        root = (DQ / D) ** 0.5
        wide_attention(nc, g, w=u, H=H16, dh=DQ, scale=root * root / DQ, out_scale=root * (D / DQ) ** 0.5 / H16)


def scale_bias(nc, dst, src, by):
    with stage_semaphores(nc, "scaled") as s, nc.Block() as block:
        @block.vector
        def _(dve):
            dve.tensor_scalar(dst[:], src[:], by, None, ALU.mult).then_inc(s.scaled, 1)
            dve.wait_ge(s.scaled, 1)


def slots_from_context(nc, g, a):
    ROUNDS, EPS, LANES = 3, 1e-6, 2
    SCALE = D ** -0.5
    STEPS = dict(
        dve=(["h_in", "ctx_in", "ctx_sq", "ctx_eps", "ctx_inv", "ctx_normed"],
             ["sq", "rms_eps", "rms_inv", "rms_diag", "q", "max0", "max1", "sinv0", "sinv1", "vs0", "vs1", "total_eps",
              "total_inv", "total_diag", "update", "rh", "nx", "h_n", "zh_n", "h"]),
        act=(["ctx_root", "k_out", "v0_out", "v1_out"],
             ["q_out", "rms_root", "exp0", "exp1", "update_out", "r", "z", "n"]),
        pe=(["ctx_mean", "kv_mm"], ["q_mm", "mean", "rms_mm", "scores", "update_mm", "total_mm", "r_mm", "z_mm", "n_mm"]))

    def after(engine, name, i=None):
        first, every = STEPS[engine]
        return first.index(name) + 1 if i is None else len(first) + i * len(every) + every.index(name) + 1

    with buffers(nc, wq=((P, D), F32), wk=((P, D), F32), wv=((P, D), F32), wih=((P, 3 * D), F32), whh=((P, 3 * D), F32),
                 bih=((P, 3), F32), bhh=((P, 3), F32), bsum=((P, 3), F32), w_slot=((P, 1), F32), w_in=((P, 1), F32),
                 mean=((P, P), F32), h=((P, LANES, S), F32), cT=((P, LANES, SC), F32), sq=((P, LANES, S), F32),
                 c_inv=((P, LANES, SC), F32), inv=((P, LANES, QT), F32), diag=((P, LANES, QT, P), F32),
                 pn=((P, LANES, SC), F32), kT=((P, LANES, SC), F32), v=((P, LANES, 2, D), F32),
                 vs=((P, LANES, 2, D), F32), qT=((P, LANES, S), F32), nmax=((P, LANES, 2), F32),
                 sums=((P, LANES, 2), F32), at=((P, LANES, 2, S), F32), up=((P, LANES, S), F32),
                 r=((P, LANES, S), F32), z=((P, LANES, S), F32), n=((P, LANES, S), F32), d=((P, LANES, S), F32)) as u:
        layernorm(nc, g, [(u.wq[:], a["L0_xattn_WqT"]), (u.wk[:], a["L0_xattn_WkT"]), (u.wv[:], a["L0_xattn_WvT"]),
                          (u.wih[:], a["L0_xattn_gru_wihT"]), (u.whh[:], a["L0_xattn_gru_whhT"]),
                          (u.bih[:], a["L0_xattn_gru_bih"].rearrange("(c p) -> p c", p=P)),
                          (u.bhh[:], a["L0_xattn_gru_bhh"].rearrange("(c p) -> p c", p=P)),
                          (u.w_slot[:], a["L0_xattn_slot_norm_w"].rearrange("(p a) -> p a", a=1)),
                          (u.w_in[:], a["L0_xattn_input_norm_w"].rearrange("(p a) -> p a", a=1))])
        with stage_semaphores(nc, "set_up") as s, nc.Block() as block:
            @block.vector
            def _(dve):
                dve.memset(u.mean[:], 1.0 / D).then_inc(s.set_up, 1)
                dve.tensor_tensor(u.bsum[:], u.bih[:], u.bhh[:], ALU.add).then_inc(s.set_up, 1)
                dve.tensor_scalar(u.wq[:], u.wq[:], u.w_slot[:, 0:1], None, ALU.mult).then_inc(s.set_up, 1)
                dve.wait_ge(s.set_up, 3)
        keys = ctx_tiles()
        PS = g.psum
        with (
            nc.Fori(0, B // LANES) as pair,
            stage_semaphores(nc, "dve0", "dve1", "act0", "act1", "pe0", "pe1", "turned", "added") as s,
            nc.Block() as block,
        ):
            done = dict(dve=(s.dve0, s.dve1), act=(s.act0, s.act1), pe=(s.pe0, s.pe1))
            lanes = range(LANES)
            BK = [[4 * c + k for k in range(4)] for c in lanes]

            @block.vector
            def _(dve):
                step = done["dve"]

                def wait(c, engine, name, i=None):
                    dve.wait_ge(done[engine][c], after(engine, name, i))

                for c in lanes:
                    batch = pair * LANES + c
                    dve.tensor_copy(u.h[:, c, :], g.xnT[:, bass.ds(batch * S, S)]).then_inc(step[c], 1)
                    dve.tensor_copy(u.cT[:, c, :], g.ctxT[:, bass.ds(batch * SC, SC)]).then_inc(step[c], 1)
                for c in lanes:
                    wait(c, "dve", "ctx_in")
                    dve.tensor_tensor(u.sq[:, c, 0:SC], u.cT[:, c, :], u.cT[:, c, :], ALU.mult).then_inc(step[c], 1)
                for c in lanes:
                    wait(c, "pe", "ctx_mean")
                    dve.tensor_scalar(u.c_inv[:, c, :], PS[:, BK[c][0], 0:SC], EPS, None, ALU.add).then_inc(step[c], 1)
                for c in lanes:
                    wait(c, "act", "ctx_root")
                    dve.reciprocal(u.c_inv[:, c, :], u.c_inv[:, c, :]).then_inc(step[c], 1)
                for c in lanes:
                    wait(c, "dve", "ctx_inv")
                    dve.scalar_tensor_tensor(out=u.pn[:, c, :], in0=u.cT[:, c, :], scalar=u.w_in[:, 0:1],
                                             in1=u.c_inv[:, c, :], op0=ALU.mult, op1=ALU.mult).then_inc(step[c], 1)
                for i in range(ROUNDS):
                    for c in lanes:
                        if i == 0:
                            wait(c, "dve", "ctx_normed")
                        else:
                            wait(c, "dve", "h", i - 1)
                        dve.tensor_tensor(u.sq[:, c, :], u.h[:, c, :], u.h[:, c, :], ALU.mult).then_inc(step[c], 1)
                    for c in lanes:
                        wait(c, "pe", "mean", i)
                        dve.tensor_scalar(u.inv[:, c, :], PS[:, BK[c][0], 0:QT], EPS, None, ALU.add).then_inc(step[c], 1)
                    for c in lanes:
                        wait(c, "act", "rms_root", i)
                        dve.reciprocal(u.inv[:, c, :], u.inv[:, c, :]).then_inc(step[c], 1)
                        wait(c, "dve", "rms_inv", i)
                        dve.tensor_tensor(u.diag[:, c], g.ident[:].unsqueeze(1).to_broadcast([P, QT, P]),
                                          u.inv[:, c, :].unsqueeze(2).to_broadcast([P, QT, P]),
                                          ALU.mult).then_inc(step[c], 1)
                    for c in lanes:
                        wait(c, "act", "q_out", i)
                        wait(c, "pe", "rms_mm", i)
                        dve.tensor_tensor(u.qT[:, c, :], u.qT[:, c, :], PS[:, BK[c][0], :], ALU.mult).then_inc(step[c], 1)
                    for c in lanes:
                        wait(c, "pe", "scores", i)
                        for t, (_, rows) in enumerate(keys):
                            dve.tensor_reduce(u.nmax[0:rows, c, t:t + 1], PS[0:rows, BK[c][2 + t], :], AX.X, ALU.max,
                                              negate=True).then_inc(step[c], 1)
                    for c in lanes:
                        for t, (_, rows) in enumerate(keys):
                            wait(c, "act", f"exp{t}", i)
                            dve.reciprocal(u.sums[0:rows, c, t:t + 1], u.sums[0:rows, c, t:t + 1]).then_inc(step[c], 1)
                        for t, (_, rows) in enumerate(keys):
                            wait(c, "dve", f"sinv{t}", i)
                            dve.tensor_scalar(u.vs[0:rows, c, t, :], u.v[0:rows, c, t, :], u.sums[0:rows, c, t:t + 1],
                                              None, ALU.mult).then_inc(step[c], 1)
                    for c in lanes:
                        wait(c, "pe", "update_mm", i)
                        dve.tensor_scalar(u.inv[:, c, :], PS[:, BK[c][0], 0:QT], EPS, None, ALU.add).then_inc(step[c], 1)
                        wait(c, "dve", "total_eps", i)
                        dve.reciprocal(u.inv[:, c, :], u.inv[:, c, :]).then_inc(step[c], 1)
                        wait(c, "dve", "total_inv", i)
                        dve.tensor_tensor(u.diag[:, c], g.ident[:].unsqueeze(1).to_broadcast([P, QT, P]),
                                          u.inv[:, c, :].unsqueeze(2).to_broadcast([P, QT, P]),
                                          ALU.mult).then_inc(step[c], 1)
                    for c in lanes:
                        wait(c, "act", "update_out", i)
                        wait(c, "pe", "total_mm", i)
                        dve.tensor_tensor(u.up[:, c, :], u.up[:, c, :], PS[:, BK[c][0], :], ALU.mult).then_inc(step[c], 1)
                    for c in lanes:
                        wait(c, "act", "r", i)
                        wait(c, "pe", "n_mm", i)
                        dve.scalar_tensor_tensor(out=u.d[:, c, :], in0=PS[:, BK[c][0], :], scalar=u.bhh[:, 2:3],
                                                 in1=u.r[:, c, :], op0=ALU.add, op1=ALU.mult).then_inc(step[c], 1)
                        wait(c, "dve", "rh", i)
                        dve.tensor_tensor(u.n[:, c, :], u.d[:, c, :], PS[:, BK[c][1], :], ALU.add).then_inc(step[c], 1)
                    for c in lanes:
                        wait(c, "act", "n", i)
                        dve.tensor_tensor(u.d[:, c, :], u.h[:, c, :], u.n[:, c, :], ALU.subtract).then_inc(step[c], 1)
                        wait(c, "act", "z", i)
                        wait(c, "dve", "h_n", i)
                        dve.tensor_tensor(u.d[:, c, :], u.d[:, c, :], u.z[:, c, :], ALU.mult).then_inc(step[c], 1)
                        wait(c, "dve", "zh_n", i)
                        dve.tensor_tensor(u.h[:, c, :], u.n[:, c, :], u.d[:, c, :], ALU.add).then_inc(step[c], 1)
                for c in lanes:
                    dve.wait_ge(s.turned, c + 1)
                    at = g.x[:, bass.ds((pair * LANES + c) * QT, QT), :]
                    dve.tensor_tensor(at, at, PS[:, BK[c][0], :].rearrange("p (t d) -> p t d", d=D),
                                      ALU.add).then_inc(s.added, 1)

            @block.scalar
            def _(act):
                step = done["act"]

                def wait(c, engine, name, i=None):
                    act.wait_ge(done[engine][c], after(engine, name, i))

                for c in lanes:
                    wait(c, "dve", "ctx_eps")
                    act.activation(u.c_inv[:, c, :], u.c_inv[:, c, :], ACT.Sqrt).then_inc(step[c], 1)
                for c in lanes:
                    wait(c, "pe", "kv_mm")
                    act.activation(u.kT[:, c, :], PS[:, BK[c][1], 0:SC], ACT.Copy).then_inc(step[c], 1)
                    for t, (_, rows) in enumerate(keys):
                        act.activation(u.v[0:rows, c, t, :], PS[0:rows, BK[c][2 + t], 0:D],
                                       ACT.Copy).then_inc(step[c], 1)
                for i in range(ROUNDS):
                    for c in lanes:
                        wait(c, "pe", "q_mm", i)
                        act.activation(u.qT[:, c, :], PS[:, BK[c][1], :], ACT.Copy, scale=SCALE).then_inc(step[c], 1)
                    for c in lanes:
                        wait(c, "dve", "rms_eps", i)
                        act.activation(u.inv[:, c, :], u.inv[:, c, :], ACT.Sqrt).then_inc(step[c], 1)
                    for c in lanes:
                        for t, (_, rows) in enumerate(keys):
                            wait(c, "dve", f"max{t}", i)
                            act.activation(u.at[0:rows, c, t, :], PS[0:rows, BK[c][2 + t], :], ACT.Exp,
                                           bias=u.nmax[0:rows, c, t:t + 1],
                                           accum_out=u.sums[0:rows, c, t:t + 1]).then_inc(step[c], 1)
                    for c in lanes:
                        wait(c, "pe", "update_mm", i)
                        act.activation(u.up[:, c, :], PS[:, BK[c][1], :], ACT.Copy).then_inc(step[c], 1)
                    for c in lanes:
                        wait(c, "pe", "r_mm", i)
                        act.activation(u.r[:, c, :], PS[:, BK[c][2], :], ACT.Sigmoid,
                                       bias=u.bsum[:, 0:1]).then_inc(step[c], 1)
                        wait(c, "pe", "z_mm", i)
                        act.activation(u.z[:, c, :], PS[:, BK[c][3], :], ACT.Sigmoid,
                                       bias=u.bsum[:, 1:2]).then_inc(step[c], 1)
                    for c in lanes:
                        wait(c, "dve", "nx", i)
                        act.activation(u.n[:, c, :], u.n[:, c, :], ACT.Tanh, bias=u.bih[:, 2:3]).then_inc(step[c], 1)

            @block.tensor
            def _(pe):
                step = done["pe"]

                def wait(c, engine, name, i=None):
                    pe.wait_ge(done[engine][c], after(engine, name, i))

                for c in lanes:
                    wait(c, "dve", "ctx_sq")
                    pe.matmul(PS[:, BK[c][0], 0:SC], u.mean[:], u.sq[:, c, 0:SC], start=True,
                              stop=True).then_inc(step[c], 1)
                for c in lanes:
                    wait(c, "dve", "ctx_normed")
                    pe.matmul(PS[:, BK[c][1], 0:SC], u.wk[:], u.pn[:, c, :], start=True, stop=True)
                    for t, (at, rows) in enumerate(keys):
                        last = pe.matmul(PS[0:rows, BK[c][2 + t], 0:D], u.pn[:, c, at:at + rows], u.wv[:], start=True,
                                         stop=True)
                    last.then_inc(step[c], 1)
                for i in range(ROUNDS):
                    for c in lanes:
                        if i == 0:
                            wait(c, "act", "v1_out")
                        else:
                            wait(c, "dve", "h", i - 1)
                        pe.matmul(PS[:, BK[c][1], :], u.wq[:], u.h[:, c, :], start=True, stop=True).then_inc(step[c], 1)
                        wait(c, "dve", "sq", i)
                        for j in range(QT):
                            last = pe.matmul(PS[:, BK[c][0], j:j + 1], u.sq[:, c, j * P:(j + 1) * P], u.mean[:, 0:1],
                                             start=True, stop=True)
                        last.then_inc(step[c], 1)
                    for c in lanes:
                        wait(c, "dve", "rms_diag", i)
                        pe.matmul(PS[:, BK[c][0], :], g.ones[:], u.diag[:, c].rearrange("p t k -> p (t k)"), start=True,
                                  stop=True).then_inc(step[c], 1)
                    for c in lanes:
                        wait(c, "dve", "q", i)
                        for t, (at, rows) in enumerate(keys):
                            last = pe.matmul(PS[0:rows, BK[c][2 + t], :], u.kT[:, c, at:at + rows], u.qT[:, c, :],
                                             start=True, stop=True)
                        last.then_inc(step[c], 1)
                    for c in lanes:
                        wait(c, "dve", "vs1", i)
                        for j in range(QT):
                            for t, (_, rows) in enumerate(keys):
                                pe.matmul(PS[:, BK[c][0], j:j + 1], u.at[0:rows, c, t, j * P:(j + 1) * P],
                                          u.sums[0:rows, c, t:t + 1], start=t == 0, stop=t == 1)
                        for t, (_, rows) in enumerate(keys):
                            last = pe.matmul(PS[:, BK[c][1], :], u.vs[0:rows, c, t, :], u.at[0:rows, c, t, :],
                                             start=t == 0, stop=t == 1)
                        last.then_inc(step[c], 1)
                        for k in range(2):
                            pe.matmul(PS[:, BK[c][2 + k], :], u.whh[:, k * D:(k + 1) * D], u.h[:, c, :], start=True,
                                      stop=False)
                    for c in lanes:
                        wait(c, "dve", "total_diag", i)
                        pe.matmul(PS[:, BK[c][0], :], g.ones[:], u.diag[:, c].rearrange("p t k -> p (t k)"), start=True,
                                  stop=True).then_inc(step[c], 1)
                    for c in lanes:
                        wait(c, "dve", "update", i)
                        for k in range(2):
                            pe.matmul(PS[:, BK[c][2 + k], :], u.wih[:, k * D:(k + 1) * D], u.up[:, c, :], start=False,
                                      stop=True).then_inc(step[c], 1)
                        pe.matmul(PS[:, BK[c][0], :], u.whh[:, 2 * D:3 * D], u.h[:, c, :], start=True, stop=True)
                        pe.matmul(PS[:, BK[c][1], :], u.wih[:, 2 * D:3 * D], u.up[:, c, :], start=True,
                                  stop=True).then_inc(step[c], 1)
                for c in lanes:
                    wait(c, "dve", "h", ROUNDS - 1)
                    for j in range(QT):
                        last = pe.transpose(PS[:, BK[c][0], j * P:(j + 1) * P], u.h[:, c, j * P:(j + 1) * P], g.ident[:])
                    last.then_inc(s.turned, 1)


def layer1_attention(nc, g, a):
    H = 4
    PAIRS = H * H
    with buffers(nc, wq=((P, H * D), F32), wk=((P, H * D), F32), wv=((P, H * D), F32), wo=((P, H, D), F32),
                 bq=((P, H), F32), bk=((P, H), F32), bv=((1, H * D), F32), bo=((1, D), F32), phase=((P, H), F32),
                 cos=((P, H), F32), sin=((P, H), F32), turn=((P, H), F32), whole=((P, H), I32), cc=((P, H, H), F32),
                 ss=((P, H, H), F32), pick=((P, PAIRS, PAIRS), F32),
                 src=((P, S), F32), qT=((P, H, S), F32), kT=((P, H, S), F32), v=((P, QT, H * D), F32),
                 prod=((P, 2, S), F32), sT=((PAIRS, S), F32), sc=((P, QT * H, H), F32), mx=((P, QT * H), F32),
                 o=((P, QT, H * D), F32), oT=((P, H, S), F32)) as u:
        layernorm(nc, g, [(u.wq[:], a["L1_attn_Wq"]), (u.wk[:], a["L1_attn_Wk"]), (u.wv[:], a["L1_attn_Wv"]),
                          (u.wo[:], a["L1_attn_Wo"].rearrange("(c p) n -> p c n", p=P)),
                          (u.bq[:], a["L1_attn_bq"].rearrange("(h p) -> p h", p=P)),
                          (u.bk[:], a["L1_attn_bk"].rearrange("(h p) -> p h", p=P)), (u.bv[:], row(a["L1_attn_bv"])),
                          (u.bo[:], row(a["L1_attn_bo"])), (u.phase[:], a["L1_attn_phaseT"])])
        with stage_semaphores(nc, "step", "sined") as s, nc.Block() as block:
            @block.vector
            def _(dve):
                steps = [0]

                def done(ins):
                    steps[0] += 1
                    ins.then_inc(s.step, 1)
                    dve.wait_ge(s.step, steps[0])

                for n, (dst, shift) in enumerate(((u.sin, 0.0), (u.cos, 0.25))):
                    done(dve.tensor_scalar(u.turn[:], u.phase[:], 1 / (2 * np.pi), shift, ALU.mult, ALU.add))
                    done(dve.tensor_copy(u.whole[:], u.turn[:]))
                    done(dve.tensor_copy(dst[:], u.whole[:]))
                    done(dve.tensor_tensor(dst[:], u.turn[:], dst[:], ALU.subtract))
                    done(dve.tensor_scalar(dst[:], dst[:], 0.5, -0.5, ALU.min, ALU.max))
                done(dve.memset(u.pick[:], 0.0))
                dve.wait_ge(s.sined, 2)
                row_of = [P, H, H]
                done(dve.tensor_tensor(u.cc[:], u.cos[:].unsqueeze(2).to_broadcast(row_of),
                                       u.cos[:].unsqueeze(1).to_broadcast(row_of), ALU.mult))
                done(dve.tensor_tensor(u.ss[:], u.sin[:].unsqueeze(2).to_broadcast(row_of),
                                       u.sin[:].unsqueeze(1).to_broadcast(row_of), ALU.mult))
                done(dve.tensor_tensor(u.cc[:], u.cc[:], u.ss[:], ALU.add))
                done(dve.tensor_scalar(u.pick[:].rearrange("p a b -> p (a b)")[:, 0:PAIRS * PAIRS:PAIRS + 1],
                                       u.cc[:].rearrange("p a b -> p (a b)"), D ** -0.5, None, ALU.mult))

            @block.scalar
            def _(act):
                act.wait_ge(s.step, 5)
                act.activation(u.sin[:], u.sin[:], ACT.Sin, scale=float(2 * np.pi * (1 - 2e-7))).then_inc(s.sined, 1)
                act.wait_ge(s.step, 10)
                act.activation(u.cos[:], u.cos[:], ACT.Sin, scale=float(2 * np.pi * (1 - 2e-7))).then_inc(s.sined, 1)
        PS = g.psum
        with (
            nc.Fori(0, B) as b,
            stage_semaphores(nc, "src_done", "q_mm", "q_out", "k_mm", "k_out", "v_mm", "v_out", "prod_done", "pair_mm",
                             "sT_done", "s_turned", "step", "exp_done", "heads_done", "o_turned", "oT_done", "projected",
                             "added") as s,
            nc.Block() as block,
        ):
            @block.tensor
            def _(pe):
                pe.wait_ge(s.src_done, 1)
                for h in range(H):
                    pe.matmul(PS[:, h, :], u.wq[:, h * D:(h + 1) * D], u.src[:], start=True, stop=True).then_inc(s.q_mm, 1)
                for h in range(H):
                    pe.matmul(PS[:, 4 + h, :], u.wk[:, h * D:(h + 1) * D], u.src[:], start=True, stop=True).then_inc(s.k_mm, 1)
                for t in range(QT):
                    pe.wait_ge(s.q_out, t + 1)
                    pe.matmul(PS[:, t, :], u.src[:, t * P:(t + 1) * P], u.wv[:], start=True, stop=False)
                    pe.matmul(PS[:, t, :], g.ones[0:1, :], u.bv[0:1, :], start=False, stop=True).then_inc(s.v_mm, 1)
                pe.wait_ge(s.k_out, 1)
                for p in range(PAIRS):
                    pe.wait_ge(s.prod_done, p + 1)
                    pe.matmul(PS[0:PAIRS, 4, :], u.pick[:, p, :], u.prod[:, p % 2, :], start=p == 0,
                              stop=p == PAIRS - 1).then_inc(s.pair_mm, 1)
                pe.wait_ge(s.sT_done, 1)
                pe.wait_ge(s.k_out, 2)
                for t in range(QT):
                    last = pe.transpose(PS[:, 5, t * PAIRS:(t + 1) * PAIRS], u.sT[:, t * P:(t + 1) * P],
                                        g.ident[0:PAIRS, 0:PAIRS])
                last.then_inc(s.s_turned, 1)
                pe.wait_ge(s.v_out, QT)
                for t in range(QT):
                    pe.wait_ge(s.heads_done, H * (t + 1))
                    for h in range(H):
                        last = pe.transpose(PS[:, t, h * P:(h + 1) * P], u.o[:, t, h * D:(h + 1) * D], g.ident[:])
                    last.then_inc(s.o_turned, 1)
                pe.wait_ge(s.oT_done, QT)
                pe.wait_ge(s.step, 1)
                pe.wait_ge(s.k_out, 4)
                for h in range(H):
                    out = PS[:, 6, h * D:(h + 1) * D]
                    for c in range(H):
                        pe.matmul(out, u.oT[:, h, c:S:H], u.wo[:, c, :], start=c == 0, stop=False)
                    last = pe.matmul(out, g.ones[0:1, :], u.bo[0:1, :], start=False, stop=True)
                last.then_inc(s.projected, 1)

            @block.scalar
            def _(act):
                for h in range(H):
                    act.wait_ge(s.q_mm, h + 1)
                    act.activation(u.qT[:, h, :], PS[:, h, :], ACT.Identity, bias=u.bq[:, h:h + 1]).then_inc(s.q_out, 1)
                for t in range(QT):
                    act.wait_ge(s.v_mm, t + 1)
                    act.activation(u.v[:, t, :], PS[:, t, :], ACT.Copy).then_inc(s.v_out, 1)
                act.wait_ge(s.pair_mm, PAIRS)
                act.activation(u.sT[:], PS[0:PAIRS, 4, :], ACT.Copy).then_inc(s.sT_done, 1)
                act.wait_ge(s.step, 2)
                act.activation(u.sc[:], u.sc[:], ACT.Exp).then_inc(s.exp_done, 1)
                for t in range(QT):
                    act.wait_ge(s.o_turned, t + 1)
                    act.activation(u.oT[:, :, t * P:(t + 1) * P], PS[:, t, :].rearrange("p (h m) -> p h m", h=H),
                                   ACT.Copy).then_inc(s.oT_done, 1)

            @block.vector
            def _(dve):
                dve.tensor_copy(u.src[:], g.xnT[:, bass.ds(b * S, S)]).then_inc(s.src_done, 1)
                for h in range(H):
                    dve.wait_ge(s.k_mm, h + 1)
                    dve.tensor_scalar(u.kT[:, h, :], PS[:, 4 + h, :], u.bk[:, h:h + 1], None, ALU.add).then_inc(s.k_out, 1)
                dve.wait_ge(s.k_out, H)
                for p in range(PAIRS):
                    dve.wait_ge(s.q_out, p // H + 1)
                    if p >= 2:
                        dve.wait_ge(s.pair_mm, p - 1)
                    dve.tensor_tensor(u.prod[:, p % 2, :], u.qT[:, p // H, :], u.kT[:, p % H, :],
                                      ALU.mult).then_inc(s.prod_done, 1)
                steps = [0]

                def done(ins):
                    steps[0] += 1
                    ins.then_inc(s.step, 1)
                    dve.wait_ge(s.step, steps[0])

                wide = [P, QT * H, H]
                scores = PS[:, 5, 0:QT * PAIRS].rearrange("p (q e) -> p q e", e=H)
                dve.wait_ge(s.s_turned, 1)
                done(dve.tensor_reduce(u.mx[:], scores, AX.X, ALU.max))
                done(dve.tensor_tensor(u.sc[:], scores, u.mx[:].unsqueeze(2).to_broadcast(wide), ALU.subtract))
                dve.wait_ge(s.exp_done, 1)
                done(dve.tensor_reduce(u.mx[:], u.sc[:], AX.X, ALU.add))
                done(dve.reciprocal(u.mx[:], u.mx[:]))
                done(dve.tensor_tensor(u.sc[:], u.sc[:], u.mx[:].unsqueeze(2).to_broadcast(wide), ALU.mult))
                for t in range(QT):
                    dve.wait_ge(s.v_out, t + 1)
                    for e in range(H):
                        for h in range(H):
                            out, val = u.o[:, t, h * D:(h + 1) * D], u.v[:, t, e * D:(e + 1) * D]
                            wt = u.sc[:, t * H + h, e:e + 1]
                            if e == 0:
                                ins = dve.tensor_scalar(out, val, wt, None, ALU.mult)
                            else:
                                ins = dve.scalar_tensor_tensor(out=out, in0=val, scalar=wt, in1=out, op0=ALU.mult,
                                                               op1=ALU.add)
                            if e == H - 1:
                                ins.then_inc(s.heads_done, 1)
                            else:
                                ins.then_inc(s.step, 1)
                                steps[0] += 1
                        if e < H - 1:
                            dve.wait_ge(s.step, steps[0])
                dve.wait_ge(s.projected, 1)
                at = g.x[:, bass.ds(b * QT, QT), :]
                dve.tensor_tensor(at, at, PS[:, 6, :].rearrange("p (t d) -> p t d", d=D), ALU.add).then_inc(s.added, 1)


def route(nc, g, u, E, K, gate, gate_b, bias_in_logits):
    PER = 512 // E
    with (
        buffers(nc, top=((P, NT, 8), F32), where=((P, NT, 8), U32), wheref=((P, NT, 8), F32),
                select=((P, NT, E), F32), mx=((P, NT), F32), which=((P, E), I32), whichf=((P, E), F32)) as w,
        stage_semaphores(nc, "logits_done", "step", "exp_done", "top_done", "found", "counted") as s,
        nc.Block() as block,
    ):
        banks = [g.psum[:, n, :].rearrange("p (t e) -> p t e", e=E) for n in range(-(-NT // PER))]
        spread = [P, NT, E]

        @block.tensor
        def _(pe):
            for t in range(NT):
                out = banks[t // PER][:, t % PER, :]
                last = pe.matmul(out, g.xnT[:, t * P:(t + 1) * P], gate[:], start=True, stop=not bias_in_logits)
                if bias_in_logits:
                    last = pe.matmul(out, g.ones[0:1, :], gate_b[0:1, :], start=False, stop=True)
            if gate_b is not None and not bias_in_logits:
                last = pe.matmul(g.psum[:, 7, 0:E], g.ones[0:1, :], gate_b[0:1, :], start=True, stop=True)
            last.then_inc(s.logits_done, 1)

        @block.gpsimd
        def _(pool):
            pool.iota(w.which[:], pattern=[[1, E]], base=0, channel_multiplier=0).then_inc(s.counted, 1)
            pool.wait_ge(s.counted, 1)
            pool.tensor_copy(w.whichf[:], w.which[:]).then_inc(s.counted, 1)

        @block.scalar
        def _(act):
            act.wait_ge(s.step, 2 * len(banks))
            act.activation(u.ex[:], u.ex[:], ACT.Exp).then_inc(s.exp_done, 1)

        @block.vector
        def _(dve):
            steps = [0]

            def done(ins):
                steps[0] += 1
                ins.then_inc(s.step, 1)
                dve.wait_ge(s.step, steps[0])

            dve.wait_ge(s.logits_done, 1)
            for n, bank in enumerate(banks):
                some = slice(n * PER, min(NT, (n + 1) * PER))
                wide = some.stop - some.start
                done(dve.tensor_reduce(w.mx[:, some], bank[:, 0:wide, :], AX.X, ALU.max))
                done(dve.tensor_tensor(u.ex[:, some, :], bank[:, 0:wide, :],
                                       w.mx[:, some].unsqueeze(2).to_broadcast([P, wide, E]), ALU.subtract))
            dve.wait_ge(s.exp_done, 1)
            done(dve.tensor_reduce(u.inv_z[:], u.ex[:], AX.X, ALU.add))
            done(dve.reciprocal(u.inv_z[:], u.inv_z[:]))
            if bias_in_logits or gate_b is None:
                for n, bank in enumerate(banks):
                    some = slice(n * PER, min(NT, (n + 1) * PER))
                    done(dve.tensor_copy(w.select[:, some, :], bank[:, 0:some.stop - some.start, :]))
            else:
                done(dve.tensor_tensor(u.ex[:], u.ex[:], u.inv_z[:].unsqueeze(2).to_broadcast(spread), ALU.mult))
                done(dve.tensor_tensor(w.select[:], u.ex[:], g.psum[:, 7, 0:E].unsqueeze(1).to_broadcast(spread), ALU.add))
            for t in range(NT):
                dve.max(w.top[:, t, :], w.select[:, t, :]).then_inc(s.top_done, 1)
            for t in range(NT):
                dve.wait_ge(s.top_done, t + 1)
                dve.max_index(w.where[:, t, :], w.top[:, t, :], w.select[:, t, :]).then_inc(s.found, 1)
            dve.wait_ge(s.found, NT)
            done(dve.tensor_copy(w.wheref[:], w.where[:]))
            dve.wait_ge(s.counted, 2)
            for k in range(K):
                ins = dve.tensor_tensor(u.pick[:, k, :, :], w.whichf[:].unsqueeze(1).to_broadcast(spread),
                                        w.wheref[:, :, k].unsqueeze(2).to_broadcast(spread), ALU.is_equal)
                ins.then_inc(s.step, 1)
            steps[0] += K
            dve.wait_ge(s.step, steps[0])


def count_before(nc, g, u, E, chosen, pos, after=None):
    N = NT * E
    with (
        buffers(nc, prefix=((P, NT, E), BF16), total=((P, E), F32), total_bf=((P, E), BF16)) as w,
        stage_semaphores(nc, "prefix_done", "total_done", "counted", "pos_done") as s,
        nc.Block() as block,
    ):
        @block.vector
        def _(dve):
            dve.memset(w.prefix[:, 0, :], 0.0).then_inc(s.prefix_done, 1)
            for t in range(1, NT):
                dve.wait_ge(s.prefix_done, t)
                dve.tensor_tensor(w.prefix[:, t, :], w.prefix[:, t - 1, :], chosen[:, t - 1, :],
                                  ALU.add).then_inc(s.prefix_done, 1)
            if after is not None:
                dve.tensor_reduce(w.total[:], after[:].rearrange("p t e -> p e t"), AX.X, ALU.add).then_inc(s.total_done, 1)
                dve.wait_ge(s.total_done, 1)
                dve.tensor_copy(w.total_bf[:], w.total[:]).then_inc(s.total_done, 1)
            for n in range(0, N, 512):
                wide = min(512, N - n)
                dve.wait_ge(s.counted, n // 512 + 1)
                dve.tensor_copy(pos[:].rearrange("p t e -> p (t e)")[:, n:n + wide],
                                g.psum[:, n // 512, 0:wide]).then_inc(s.pos_done, 1)

        @block.tensor
        def _(pe):
            pe.wait_ge(s.prefix_done, NT)
            if after is not None:
                pe.wait_ge(s.total_done, 2)
            for n in range(0, N, 512):
                wide = min(512, N - n)
                out = g.psum[:, n // 512, 0:wide]
                pe.matmul(out, g.before[:], chosen[:].rearrange("p t e -> p (t e)")[:, n:n + wide], start=True, stop=False)
                last = pe.matmul(out, g.ones_bf[:], w.prefix[:].rearrange("p t e -> p (t e)")[:, n:n + wide],
                                 start=False, stop=after is None)
                if after is not None:
                    last = pe.matmul(out, g.ones_bf[:], w.total_bf[:].unsqueeze(1).to_broadcast([P, wide // E, E]),
                                     start=False, stop=True)
                last.then_inc(s.counted, 1)


def experts(nc, g, u, E, F, func):
    FC = F // P
    with (
        buffers(nc, src=((P, S), F32), coef=((P, QT, E), F32), hidden=((P, 2, FC, S), F32), acc=((P, QT, D), F32),
                coefT=((E, S), F32)) as w,
        nc.Fori(0, B) as b,
        stage_semaphores(nc, "src_done", "coef_done", "coef_turned", "coefT_done", "bias_mm", "hidden_mm", "hidden_done",
                         "out_mm", "acc_done", "added") as s,
        nc.Block() as block,
    ):
        @block.tensor
        def _(pe):
            def hidden(e):
                for c in range(FC):
                    n = e * FC + c
                    if n >= 3:
                        pe.wait_ge(s.hidden_done, n - 2)
                    pe.matmul(g.psum[:, n % 3, :], u.w1[:, e, c * P:(c + 1) * P], w.src[:], start=True,
                              stop=True).then_inc(s.hidden_mm, 1)

            def out(e):
                pe.wait_ge(s.hidden_done, FC * (e + 1))
                if e >= 2:
                    pe.wait_ge(s.acc_done, QT * (e - 1))
                for j in range(QT):
                    o = g.psum[:, 4 + e % 2, j * D:(j + 1) * D]
                    for c in range(FC):
                        last = pe.matmul(o, w.hidden[:, e % 2, c, j * P:(j + 1) * P], u.w2[:, e, c, :], start=c == 0,
                                         stop=c == FC - 1)
                last.then_inc(s.out_mm, 1)

            pe.wait_ge(s.src_done, 1)
            hidden(0)
            pe.wait_ge(s.coef_done, 1)
            for j in range(QT):
                last = pe.transpose(g.psum[0:E, 6, j * P:(j + 1) * P], w.coef[:, j, :], g.ident[:])
            last.then_inc(s.coef_turned, 1)
            pe.wait_ge(s.coefT_done, 1)
            for j in range(QT):
                last = pe.matmul(g.psum[:, 7, j * D:(j + 1) * D], w.coefT[:, j * P:(j + 1) * P], u.b2[:], start=True, stop=True)
            last.then_inc(s.bias_mm, 1)
            for e in range(E + 1):
                if 0 < e < E:
                    hidden(e)
                if e >= 1:
                    out(e - 1)

        @block.scalar
        def _(act):
            for n in range(E * FC):
                e, c = n // FC, n % FC
                act.wait_ge(s.hidden_mm, n + 1)
                if e >= 2:
                    act.wait_ge(s.out_mm, e - 1)
                act.activation(w.hidden[:, e % 2, c, :], g.psum[:, n % 3, :], func,
                               bias=u.b1[:, n:n + 1]).then_inc(s.hidden_done, 1)

        @block.vector
        def _(dve):
            dve.tensor_copy(w.src[:], g.xnT[:, bass.ds(b * S, S)]).then_inc(s.src_done, 1)
            dve.tensor_copy(w.coef[:], u.coef[:, bass.ds(b * QT, QT), :]).then_inc(s.coef_done, 1)
            dve.wait_ge(s.coef_turned, 1)
            dve.tensor_copy(w.coefT[:], g.psum[0:E, 6, :]).then_inc(s.coefT_done, 1)
            dve.wait_ge(s.bias_mm, 1)
            dve.tensor_copy(w.acc[:], g.psum[:, 7, :].rearrange("p (t d) -> p t d", d=D)).then_inc(s.coef_done, 1)
            dve.wait_ge(s.coef_done, 2)
            for e in range(E):
                dve.wait_ge(s.out_mm, e + 1)
                if e >= 1:
                    dve.wait_ge(s.acc_done, QT * e)
                for j in range(QT):
                    dve.scalar_tensor_tensor(out=w.acc[:, j, :], in0=g.psum[:, 4 + e % 2, j * D:(j + 1) * D],
                                             scalar=w.coef[:, j, e:e + 1], in1=w.acc[:, j, :], op0=ALU.mult,
                                             op1=ALU.add).then_inc(s.acc_done, 1)
            dve.wait_ge(s.acc_done, QT * E)
            at = g.x[:, bass.ds(b * QT, QT), :]
            dve.tensor_tensor(at, at, w.acc[:], ALU.add).then_inc(s.added, 1)


def mixture8(nc, g, a, K, capacity, names, func):
    E, F = 8, 512
    gate, gate_b, w1, b1, w2, b2 = names
    with buffers(nc, w1=((P, E, F), F32), w2=((P, E, F // P, D), F32), b1=((P, E * F // P), F32), b2=((E, D), F32),
                 gate=((P, E), F32), gate_b=((1, E), F32), ex=((P, NT, E), F32), inv_z=((P, NT), F32),
                 pick=((P, K, NT, E), F32), coef=((P, NT, E), F32)) as u:
        pairs = [(u.w1[:], a[w1].rearrange("e k f -> k e f")), (u.w2[:], a[w2].rearrange("e (c p) d -> p e c d", p=P)),
                 (u.b1[:], a[b1].rearrange("e (c p) -> p (e c)", p=P)), (u.b2[:], a[b2]),
                 (u.gate[:], a[gate])]
        if gate_b:
            pairs.append((u.gate_b[:], row(a[gate_b])))
        layernorm(nc, g, pairs)
        route(nc, g, u, E, K, u.gate, u.gate_b if gate_b else None, bool(gate_b))
        with buffers(nc, chosen=((P, K, NT, E), BF16), pos=((P, K, NT, E), F32), g1=((P, NT), F32), g2=((P, NT), F32),
                     den=((P, NT), F32), tmp=((P, NT, E), F32)) as w:
            with stage_semaphores(nc, "chosen_done") as s, nc.Block() as block:
                @block.vector
                def _(dve):
                    dve.tensor_copy(w.chosen[:], u.pick[:]).then_inc(s.chosen_done, 1)
                    dve.wait_ge(s.chosen_done, 1)
            for k in range(K):
                count_before(nc, g, u, E, w.chosen[:, k], w.pos[:, k], after=w.chosen[:, 0] if k else None)
            with stage_semaphores(nc, "step") as s, nc.Block() as block:
                @block.vector
                def _(dve):
                    steps = [0]

                    def done(ins):
                        steps[0] += 1
                        ins.then_inc(s.step, 1)
                        dve.wait_ge(s.step, steps[0])

                    spread = [P, NT, E]
                    done(dve.scalar_tensor_tensor(out=u.pick[:], in0=w.pos[:], scalar=float(capacity), in1=u.pick[:],
                                                  op0=ALU.is_lt, op1=ALU.mult))
                    if K == 1:
                        done(dve.tensor_tensor(u.coef[:], u.pick[:, 0], u.inv_z[:].unsqueeze(2).to_broadcast(spread), ALU.mult))
                    else:
                        done(dve.tensor_tensor(w.tmp[:], u.ex[:], w.chosen[:, 1], ALU.mult))
                        done(dve.tensor_reduce(w.g2[:], w.tmp[:], AX.X, ALU.add))
                        done(dve.tensor_tensor(w.g2[:], w.g2[:], u.inv_z[:], ALU.mult))
                        done(dve.tensor_tensor(w.den[:], w.g2[:], u.inv_z[:], ALU.add))
                        done(dve.tensor_scalar(w.den[:], w.den[:], 1e-9, None, ALU.add))
                        done(dve.reciprocal(w.den[:], w.den[:]))
                        done(dve.tensor_tensor(w.g1[:], u.inv_z[:], w.den[:], ALU.mult))
                        done(dve.tensor_tensor(w.g2[:], w.g2[:], w.den[:], ALU.mult))
                        done(dve.tensor_tensor(u.coef[:], u.pick[:, 0], w.g1[:].unsqueeze(2).to_broadcast(spread), ALU.mult))
                        done(dve.tensor_tensor(w.tmp[:], u.pick[:, 1], w.g2[:].unsqueeze(2).to_broadcast(spread), ALU.mult))
                        done(dve.tensor_tensor(u.coef[:], u.coef[:], w.tmp[:], ALU.add))
        experts(nc, g, u, E, F, func)


def layer1_ffn(nc, g, a):
    mixture8(nc, g, a, 2, 2 * 2 * NT * P // 8, ("L1_ffn_Wg", None, "L1_ffn_W1", "L1_ffn_b1", "L1_ffn_W2", "L1_ffn_b2"),
             ACT.Gelu)


def layer2_ffn(nc, g, a):
    E, F, K = 8, 512, 1
    FC = F // P
    CAP = -(-5 * NT * P // (4 * E))
    ROWS = E * CAP
    RT = ROWS // P
    FAR = float(1 << 20)
    PER = 4
    GROUPS = RT // PER
    assert RT * P == ROWS and GROUPS * PER == RT
    rows_in, rows_out = g.moe_in[0:ROWS, :], g.moe_out[0:ROWS, :]
    with buffers(nc, w1=((P, E, F), F32), w2=((P, E, FC, D), F32), b1=((P, E * FC), F32), b2=((P, E), F32),
                 gate=((P, E), F32), gate_b=((1, E), F32), ex=((P, NT, E), F32), inv_z=((P, NT), F32),
                 pick=((P, K, NT, E), F32), slot_in=((P, NT), I32), slot_out=((P, NT), I32), weight=((P, NT), F32)) as u:
        layernorm(nc, g, [(u.w1[:], a["L2_ffn_w1"].rearrange("e k f -> k e f")),
                          (u.w2[:], a["L2_ffn_w2"].rearrange("e (c p) d -> p e c d", p=P)),
                          (u.b1[:], a["L2_ffn_b1"].rearrange("e (c p) -> p (e c)", p=P)),
                          (u.b2[:], a["L2_ffn_b2"].rearrange("e d -> d e")), (u.gate[:], a["L2_ffn_gate_wT"]),
                          (u.gate_b[:], row(a["L2_ffn_gate_b"]))])
        route(nc, g, u, E, K, u.gate, u.gate_b, True)
        with buffers(nc, chosen=((P, NT, E), BF16), pos=((P, NT, E), F32), tmp=((P, NT, E), F32), kept=((P, NT), F32),
                     slotf=((P, NT), F32), far=((P, NT), F32), first=((P, E), I32), zeros=((P, RT * D), F32)) as w:
            with stage_semaphores(nc, "chosen_done", "first_done", "cleared") as s, nc.Block() as block:
                @block.vector
                def _(dve):
                    dve.tensor_copy(w.chosen[:], u.pick[:, 0]).then_inc(s.chosen_done, 1)
                    dve.memset(w.zeros[:], 0.0).then_inc(s.chosen_done, 1)

                @block.gpsimd
                def _(pool):
                    pool.iota(w.first[:], pattern=[[CAP, E]], base=0, channel_multiplier=0).then_inc(s.first_done, 1)

                @block.sync
                def _(sp):
                    sp.wait_ge(s.chosen_done, 2)
                    sp.dma_start(rows_in.rearrange("(p n) d -> p (n d)", p=P), w.zeros[:]).then_inc(s.cleared, 16)
                    sp.wait_ge(s.cleared, 16)
            count_before(nc, g, u, E, w.chosen, w.pos)
            with stage_semaphores(nc, "step") as s, nc.Block() as block:
                @block.vector
                def _(dve):
                    steps = [0]

                    def done(ins):
                        steps[0] += 1
                        ins.then_inc(s.step, 1)
                        dve.wait_ge(s.step, steps[0])

                    done(dve.scalar_tensor_tensor(out=u.pick[:, 0], in0=w.pos[:], scalar=float(CAP), in1=u.pick[:, 0],
                                                  op0=ALU.is_lt, op1=ALU.mult))
                    done(dve.tensor_tensor(w.tmp[:], w.pos[:], w.first[:].unsqueeze(1).to_broadcast([P, NT, E]), ALU.add))
                    done(dve.tensor_tensor(w.tmp[:], w.tmp[:], u.pick[:, 0], ALU.mult))
                    done(dve.tensor_reduce(w.slotf[:], w.tmp[:], AX.X, ALU.add))
                    done(dve.tensor_reduce(w.kept[:], u.pick[:, 0], AX.X, ALU.add))
                    done(dve.tensor_tensor(u.weight[:], w.kept[:], u.inv_z[:], ALU.mult))
                    done(dve.tensor_scalar(w.far[:], w.kept[:], -FAR, FAR, ALU.mult, ALU.add))
                    done(dve.tensor_tensor(w.slotf[:], w.slotf[:], w.far[:], ALU.add))
                    done(dve.tensor_copy(u.slot_in[:], w.slotf[:]))
                    done(dve.tensor_scalar(w.slotf[:], w.slotf[:], float(ROWS - 1), None, ALU.min))
                    done(dve.tensor_copy(u.slot_out[:], w.slotf[:]))

        with nc.Block() as block:
            @block.gpsimd
            def _(pool):
                for t in range(NT):
                    pool.indirect_dma_start(
                        rows_in, bass.IndirectOffsetOnAxis(ap=u.slot_in[:, t:t + 1].bitcast(U32), axis=0),
                        g.xn[:, t, :], None, bounds_check=ROWS - 1, oob_is_err=False).then_inc(g.scattered_rows, 16)
                pool.wait_ge(g.scattered_rows, 16 * NT)

        with (
            buffers(nc, rows=((P, RT, D), F32), rT=((P, ROWS), F32), hidden=((P, 2, FC, CAP), F32), yT=((P, ROWS), F32),
                    y=((P, RT, D), F32)) as w,
            stage_semaphores(nc, "rows_in0", "rows_in1", "rows_in2", "rows_in3", "rows_in4", "turned", "rT_done",
                             "hidden_mm", "hidden_done", "out_mm", "yT_done", "y_turned", "y_done", "rows_saved") as s,
            nc.Block() as block,
        ):
            TURN, HIDDEN, OUT, BACK = 0, 1, 4, 6
            tiled_in = rows_in.rearrange("(t p) d -> p t d", p=P)
            tiled_out = rows_out.rearrange("(t p) d -> p t d", p=P)
            rows_ready = [s.rows_in0, s.rows_in1, s.rows_in2, s.rows_in3, s.rows_in4]

            def tiles(n):
                return slice(n * PER, (n + 1) * PER)

            def turn_before(e):
                return -(-(e + 1) * CAP // (PER * P))

            @block.sync
            def _(sp):
                for n in range(GROUPS):
                    sp.dma_start(w.rows[:, tiles(n), :], tiled_in[:, tiles(n), :]).then_inc(rows_ready[n], 16)
                for n in range(GROUPS):
                    sp.wait_ge(s.y_done, n + 1)
                    sp.dma_start(tiled_out[:, tiles(n), :], w.y[:, tiles(n), :]).then_inc(s.rows_saved, 16)
                sp.wait_ge(s.rows_saved, 16 * GROUPS)

            @block.tensor
            def _(pe):
                def turn(n):
                    pe.wait_ge(rows_ready[n], 16)
                    if n >= 1:
                        pe.wait_ge(s.rT_done, n)
                    for i in range(PER):
                        last = pe.transpose(g.psum[:, TURN, i * P:(i + 1) * P], w.rows[:, n * PER + i, :], g.ident[:])
                    last.then_inc(s.turned, 1)

                def hidden(e):
                    pe.wait_ge(s.rT_done, turn_before(e))
                    for c in range(FC):
                        n = e * FC + c
                        if n >= 3:
                            pe.wait_ge(s.hidden_done, n - 2)
                        pe.matmul(g.psum[:, HIDDEN + n % 3, 0:CAP], u.w1[:, e, c * P:(c + 1) * P],
                                  w.rT[:, e * CAP:(e + 1) * CAP], start=True, stop=True).then_inc(s.hidden_mm, 1)

                def out(e):
                    pe.wait_ge(s.hidden_done, FC * (e + 1))
                    if e >= 2:
                        pe.wait_ge(s.yT_done, e - 1)
                    for c in range(FC):
                        last = pe.matmul(g.psum[:, OUT + e % 2, 0:CAP], u.w2[:, e, c, :], w.hidden[:, e % 2, c, :],
                                         start=c == 0, stop=c == FC - 1)
                    last.then_inc(s.out_mm, 1)

                def turn_back(n):
                    pe.wait_ge(s.yT_done, -(-(n + 1) * PER * P // CAP))
                    if n >= 2:
                        pe.wait_ge(s.y_done, n - 1)
                    for i in range(PER):
                        at = (n * PER + i) * P
                        last = pe.transpose(g.psum[:, BACK + n % 2, i * P:(i + 1) * P], w.yT[:, at:at + P], g.ident[:])
                    last.then_inc(s.y_turned, 1)

                turned = back = 0
                for e in range(E + 2):
                    while e < E and turned < turn_before(min(e + 1, E - 1)):
                        turn(turned)
                        turned += 1
                    if e < E:
                        hidden(e)
                    if 1 <= e <= E:
                        out(e - 1)
                    while back < GROUPS and (back + 1) * PER * P <= (e - 1) * CAP:
                        turn_back(back)
                        back += 1

            @block.scalar
            def _(act):
                turned = 0
                for e in range(E):
                    while turned < turn_before(min(e + 1, E - 1)):
                        act.wait_ge(s.turned, turned + 1)
                        act.activation(w.rT[:, turned * PER * P:(turned + 1) * PER * P], g.psum[:, TURN, :],
                                       ACT.Copy).then_inc(s.rT_done, 1)
                        turned += 1
                    for c in range(FC):
                        n = e * FC + c
                        act.wait_ge(s.hidden_mm, n + 1)
                        if e >= 2:
                            act.wait_ge(s.out_mm, e - 1)
                        act.activation(w.hidden[:, e % 2, c, :], g.psum[:, HIDDEN + n % 3, 0:CAP], ACT.Relu,
                                       bias=u.b1[:, n:n + 1]).then_inc(s.hidden_done, 1)

            @block.vector
            def _(dve):
                back = 0
                for e in range(E + 1):
                    if e < E:
                        dve.wait_ge(s.out_mm, e + 1)
                        dve.tensor_scalar(w.yT[:, e * CAP:(e + 1) * CAP], g.psum[:, OUT + e % 2, 0:CAP], u.b2[:, e:e + 1],
                                          None, ALU.add).then_inc(s.yT_done, 1)
                    while back < GROUPS and (back + 1) * PER * P <= e * CAP:
                        dve.wait_ge(s.y_turned, back + 1)
                        dve.tensor_copy(w.y[:, tiles(back), :], g.psum[:, BACK + back % 2, :]
                                        .rearrange("p (t d) -> p t d", d=D)).then_inc(s.y_done, 1)
                        back += 1

        HALF = NT // 2
        with (
            buffers(nc, got=((P, NT, D), F32)) as w,
            stage_semaphores(nc, "added") as s,
            nc.Block() as block,
        ):
            halves = [g.fetched_first, g.fetched_second]

            @block.gpsimd
            def _(pool):
                for t in range(NT):
                    pool.indirect_dma_start(
                        w.got[:, t, :], None, rows_out,
                        bass.IndirectOffsetOnAxis(ap=u.slot_out[:, t:t + 1].bitcast(U32), axis=0),
                        bounds_check=ROWS - 1, oob_is_err=False).then_inc(halves[t // HALF], 16)

            @block.vector
            def _(dve):
                for t in range(NT):
                    if t % HALF == 0:
                        dve.wait_ge(halves[t // HALF], 16 * HALF)
                    dve.scalar_tensor_tensor(out=g.x[:, t, :], in0=w.got[:, t, :], scalar=u.weight[:, t:t + 1],
                                             in1=g.x[:, t, :], op0=ALU.mult, op1=ALU.add).then_inc(s.added, 1)


def prefetch_experts(nc, g, a):
    I = 88
    with nc.Block() as block:
        @block.sync
        def _(sp):
            sp.dma_start(g.w13[:, :, 0:I], a["L0_ffn_w1T"]).then_inc(g.prefetched, 16)
            sp.dma_start(g.w13[:, :, I:2 * I], a["L0_ffn_w3T"]).then_inc(g.prefetched, 16)
            sp.dma_start(g.w2[:], a["L0_ffn_w2T"]).then_inc(g.prefetched, 16)


def expert_eights(nc, g, w, moved, eights_in, eights_out):
    E, CAP, I, EB = 64, 64, 88, 8
    PS = g.psum
    with (
        nc.Fori(0, E // EB) as n,
        stage_semaphores(nc, "rows_ready", "turned", "rT_done", "hidden_mm", "silu_done", "h_done", "h_turned",
                         "hT_done", "out_mm", "y_done") as s,
        nc.Block() as block,
    ):
        @block.sync
        def _(sp):
            sp.wait_ge(s.turned, 1)
            sp.dma_start(w.rows[:], eights_in[:, bass.ds(n * EB + EB, EB), :]).then_inc(moved.rows_in, 16)
            sp.wait_ge(s.y_done, 2)
            sp.dma_start(eights_out[:, bass.ds(n * EB, EB), :], w.y[:]).then_inc(moved.rows_saved, 16)

        def hid(e):
            return PS[0:CAP, 1 + e // 2, (e % 2) * 2 * I:(e % 2 + 1) * 2 * I]

        @block.tensor
        def _(pe):
            pe.wait_ge(s.rows_ready, 1)
            for e in range(EB):
                last = pe.transpose(PS[:, 0, e * CAP:(e + 1) * CAP], w.rows[:, e, :], g.ident[0:CAP, 0:CAP])
            last.then_inc(s.turned, 1)
            pe.wait_ge(s.rT_done, 1)
            for e in range(EB):
                pe.matmul(hid(e).unsqueeze(1), w.rT[:, e * CAP:(e + 1) * CAP], g.w13[:, bass.ds(n * EB + e, 1), :],
                          start=True, stop=True).then_inc(s.hidden_mm, 1)
            for e in range(EB):
                pe.wait_ge(s.h_done, e // 2 + 1)
                last = pe.transpose(PS[0:I, 5, e * CAP:(e + 1) * CAP], w.h[:, e, :], g.ident[0:CAP, 0:CAP])
            last.then_inc(s.h_turned, 1)
            pe.wait_ge(s.hT_done, 1)
            for e in range(EB):
                pe.matmul(PS[0:CAP, 6 + e // 4, (e % 4) * D:(e % 4 + 1) * D].unsqueeze(1), w.hT[:, e * CAP:(e + 1) * CAP],
                          g.w2[:, bass.ds(n * EB + e, 1), :], start=True, stop=True).then_inc(s.out_mm, 1)

        @block.scalar
        def _(act):
            act.wait_ge(s.turned, 1)
            act.activation(w.rT[:], PS[:, 0, :], ACT.Copy).then_inc(s.rT_done, 1)
            for m in range(EB // 2):
                act.wait_ge(s.hidden_mm, 2 * m + 2)
                both = PS[0:CAP, 1 + m, 0:4 * I].rearrange("p (e w i) -> p e w i", e=2, w=2)
                act.activation(w.gated[:, 2 * m:2 * m + 2, :], both[:, :, 0, :], ACT.Silu).then_inc(s.silu_done, 1)
            act.wait_ge(s.h_turned, 1)
            act.activation(w.hT[:], PS[0:I, 5, :], ACT.Copy).then_inc(s.hT_done, 1)
            act.wait_ge(s.out_mm, 4)
            act.wait_ge(moved.rows_saved, n * 16)
            act.activation(w.y[:, 0:4, :], PS[0:CAP, 6, :].rearrange("p (e d) -> p e d", d=D), ACT.Copy).then_inc(s.y_done, 1)

        @block.vector
        def _(dve):
            dve.wait_ge(moved.rows_in, n * 16 + 16)
            dve.tensor_copy(w.seen[:], g.ident[:, 0:1]).then_inc(s.rows_ready, 1)
            for m in range(EB // 2):
                dve.wait_ge(s.silu_done, m + 1)
                both = PS[0:CAP, 1 + m, 0:4 * I].rearrange("p (e w i) -> p e w i", e=2, w=2)
                dve.tensor_tensor(w.h[:, 2 * m:2 * m + 2, :], w.gated[:, 2 * m:2 * m + 2, :], both[:, :, 1, :],
                                  ALU.mult).then_inc(s.h_done, 1)
            dve.wait_ge(s.out_mm, 8)
            dve.wait_ge(moved.rows_saved, n * 16)
            dve.tensor_copy(w.y[:, 4:8, :], PS[0:CAP, 7, :].rearrange("p (e d) -> p e d", d=D)).then_inc(s.y_done, 1)


def layer0_ffn(nc, g, a):
    E, K, CAP, I, SI = 64, 6, 64, 88, 176
    ROWS = E * CAP
    FAR = float(1 << 20)
    rows_in, rows_out = g.moe_in, g.moe_out
    with buffers(nc, gate=((P, E), F32), gate_b=((1, E), F32),
                 ws1=((P, SI), F32), ws3=((P, SI), F32), ws2=((P, 2, D), F32), slot_in=((P, NT, K), I32),
                 slot_out=((P, NT, K), I32), weight=((P, NT, K), F32)) as u:
        layernorm(nc, g, [(u.gate[:], a["L0_ffn_gate_wT"]), (u.gate_b[:], row(a["L0_ffn_gate_b"])), (u.ws1[:], a["L0_ffn_ws1T"]),
                          (u.ws3[:], a["L0_ffn_ws3T"]), (u.ws2[:, 0, :], a["L0_ffn_ws2T"][0:P, :]),
                          (u.ws2[0:SI - P, 1, :], a["L0_ffn_ws2T"][P:SI, :])])
        with buffers(nc, ex=((P, NT, E), F32), inv_z=((P, NT), F32), pick=((P, K, NT, E), F32), chosen=((P, NT, E), BF16),
                     pos=((P, NT, E), F32), kept=((P, NT, E), F32), tmp=((P, NT, E), F32), slotf=((P, NT, K), F32),
                     first=((P, E), I32)) as w:
            route(nc, g, w, E, K, u.gate, u.gate_b, False)
            with stage_semaphores(nc, "step", "zeroed", "cleared") as s, nc.Block() as block:
                @block.vector
                def _(dve):
                    steps = [0]

                    def done(ins):
                        steps[0] += 1
                        ins.then_inc(s.step, 1)
                        dve.wait_ge(s.step, steps[0])

                    done(dve.tensor_tensor(w.kept[:], w.pick[:, 0], w.pick[:, 1], ALU.add))
                    for k in range(2, K):
                        done(dve.tensor_tensor(w.kept[:], w.kept[:], w.pick[:, k], ALU.add))
                    done(dve.tensor_copy(w.chosen[:], w.kept[:]))
                    dve.memset(w.tmp[:], 0.0).then_inc(s.zeroed, 1)

                @block.sync
                def _(sp):
                    sp.wait_ge(s.zeroed, 1)
                    view = rows_in.rearrange("(p n) d -> p (n d)", p=P)
                    wide = NT * E
                    zeros = w.tmp[:].rearrange("p t e -> p (t e)")
                    starts = range(0, view.shape[1], wide)
                    for n in starts:
                        some = min(wide, view.shape[1] - n)
                        sp.dma_start(view[:, n:n + some], zeros[:, 0:some]).then_inc(s.cleared, 16)
                    sp.wait_ge(s.cleared, 16 * len(starts))
            count_before(nc, g, w, E, w.chosen, w.pos)
            with stage_semaphores(nc, "step", "first_done") as s, nc.Block() as block:
                @block.gpsimd
                def _(pool):
                    pool.iota(w.first[:], pattern=[[CAP, E]], base=0, channel_multiplier=0).then_inc(s.first_done, 1)

                @block.vector
                def _(dve):
                    steps = [0]

                    def done(ins):
                        steps[0] += 1
                        ins.then_inc(s.step, 1)
                        dve.wait_ge(s.step, steps[0])

                    spread = [P, NT, E]
                    done(dve.tensor_scalar(w.kept[:], w.pos[:], float(CAP), None, ALU.is_lt))
                    done(dve.tensor_tensor(w.ex[:], w.ex[:], w.kept[:], ALU.mult))
                    done(dve.tensor_scalar(w.kept[:], w.kept[:], -FAR, FAR, ALU.mult, ALU.add))
                    done(dve.tensor_tensor(w.pos[:], w.pos[:], w.kept[:], ALU.add))
                    dve.wait_ge(s.first_done, 1)
                    done(dve.tensor_tensor(w.pos[:], w.pos[:], w.first[:].unsqueeze(1).to_broadcast(spread), ALU.add))
                    for k in range(K):
                        done(dve.tensor_tensor(w.tmp[:], w.pick[:, k], w.ex[:], ALU.mult))
                        done(dve.tensor_reduce(u.weight[:, :, k], w.tmp[:], AX.X, ALU.add))
                        done(dve.tensor_tensor(w.tmp[:], w.pick[:, k], w.pos[:], ALU.mult))
                        done(dve.tensor_reduce(w.slotf[:, :, k], w.tmp[:], AX.X, ALU.add))
                    done(dve.tensor_copy(u.slot_in[:], w.slotf[:]))
                    done(dve.tensor_scalar(w.slotf[:], w.slotf[:], float(ROWS - 1), None, ALU.min))
                    done(dve.tensor_copy(u.slot_out[:], w.slotf[:]))

        UN = QT
        PS = g.psum
        parts = [(0, P), (P, SI - P)]
        with (
            buffers(nc, tile=((P, UN, D), F32), slots=((P, UN, K), I32), gated=((P, 2, S), F32), h=((P, 2, S), F32)) as w,
            nc.Fori(0, B) as b,
            stage_semaphores(nc, "fixed", "hidden_mm", "silu_done", "h_done", "out_mm", "added") as s,
            nc.Block() as block,
        ):
            @block.gpsimd
            def _(pool):
                pool.wait_ge(s.fixed, 2)
                for i in range(UN):
                    for k in range(K):
                        pool.indirect_dma_start(
                            rows_in, bass.IndirectOffsetOnAxis(ap=w.slots[:, i, k:k + 1].bitcast(U32), axis=0),
                            w.tile[:, i, :], None, bounds_check=ROWS - 1, oob_is_err=False).then_inc(g.scattered, 16)
                pool.wait_ge(g.scattered, b * (16 * K * UN) + 16 * K * UN)

            @block.tensor
            def _(pe):
                src = g.xnT[:, bass.ds(b * S, S)]
                for c, (at, rows) in enumerate(parts):
                    pe.matmul(PS[0:rows, 2 * c, :], u.ws1[:, at:at + rows], src, start=True, stop=True)
                    pe.matmul(PS[0:rows, 2 * c + 1, :], u.ws3[:, at:at + rows], src, start=True,
                              stop=True).then_inc(s.hidden_mm, 1)
                pe.wait_ge(s.h_done, 2)
                for j in range(QT):
                    for c, (_, rows) in enumerate(parts):
                        last = pe.matmul(PS[:, 4, j * D:(j + 1) * D], w.h[0:rows, c, j * P:(j + 1) * P], u.ws2[0:rows, c, :],
                                         start=c == 0, stop=c == 1)
                last.then_inc(s.out_mm, 1)

            @block.scalar
            def _(act):
                for c, (_, rows) in enumerate(parts):
                    act.wait_ge(s.hidden_mm, c + 1)
                    act.activation(w.gated[0:rows, c, :], PS[0:rows, 2 * c, :], ACT.Silu).then_inc(s.silu_done, 1)

            @block.vector
            def _(dve):
                dve.tensor_copy(w.slots[:], u.slot_in[:, bass.ds(b * UN, UN), :]).then_inc(s.fixed, 1)
                dve.tensor_copy(w.tile[:], g.xn[:, bass.ds(b * UN, UN), :]).then_inc(s.fixed, 1)
                for c, (_, rows) in enumerate(parts):
                    dve.wait_ge(s.silu_done, c + 1)
                    dve.tensor_tensor(w.h[0:rows, c, :], w.gated[0:rows, c, :], PS[0:rows, 2 * c + 1, :],
                                      ALU.mult).then_inc(s.h_done, 1)
                dve.wait_ge(s.out_mm, 1)
                at = g.x[:, bass.ds(b * QT, QT), :]
                dve.tensor_tensor(at, at, PS[:, 4, :].rearrange("p (t d) -> p t d", d=D), ALU.add).then_inc(s.added, 1)

        EB = 8
        with (
            buffers(nc, rows=((CAP, EB, D), F32), rT=((P, EB * CAP), F32), gated=((CAP, EB, I), F32),
                    h=((CAP, EB, I), F32), hT=((I, EB * CAP), F32), y=((CAP, EB, D), F32), seen=((P, 1), F32)) as w,
            stage_semaphores(nc, "rows_in", "rows_saved") as moved,
        ):
            eights_in = rows_in.rearrange("(e c) d -> c e d", c=CAP)
            eights_out = rows_out.rearrange("(e c) d -> c e d", c=CAP)
            with nc.Block() as block:
                @block.sync
                def _(sp):
                    sp.dma_start(w.rows[:], eights_in[:, 0:EB, :]).then_inc(moved.rows_in, 16)
                    sp.wait_ge(g.prefetched, 16 * 3)
            expert_eights(nc, g, w, moved, eights_in, eights_out)
            with nc.Block() as block:
                @block.sync
                def _(sp):
                    sp.wait_ge(moved.rows_in, 16 * (E // EB + 1))
                    sp.wait_ge(moved.rows_saved, 16 * (E // EB))

        HALF = UN // 2
        with (
            buffers(nc, got=((P, UN, K, D), F32), slots=((P, UN, K), I32), wt=((P, UN, K), F32)) as w,
            nc.Fori(0, NT // UN) as t,
            stage_semaphores(nc, "fixed", "added") as s,
            nc.Block() as block,
        ):
            halves = [g.gathered_first, g.gathered_second]

            @block.gpsimd
            def _(pool):
                pool.wait_ge(s.fixed, 2)
                for i in range(UN):
                    for k in range(K):
                        pool.indirect_dma_start(
                            w.got[:, i, k, :], None, rows_out,
                            bass.IndirectOffsetOnAxis(ap=w.slots[:, i, k:k + 1].bitcast(U32), axis=0),
                            bounds_check=ROWS - 1, oob_is_err=False).then_inc(halves[i // HALF], 16)

            @block.vector
            def _(dve):
                dve.tensor_copy(w.slots[:], u.slot_out[:, bass.ds(t * UN, UN), :]).then_inc(s.fixed, 1)
                dve.tensor_copy(w.wt[:], u.weight[:, bass.ds(t * UN, UN), :]).then_inc(s.fixed, 1)
                dve.wait_ge(s.fixed, 2)
                for i in range(0, UN, HALF):
                    dve.wait_ge(halves[i // HALF], t * (16 * K * HALF) + 16 * K * HALF)
                    for k in range(K):
                        if k:
                            dve.wait_ge(s.added, i * K + k * HALF)
                        for j in range(i, i + HALF):
                            at = g.x[:, bass.ds(t * UN + j, 1), :]
                            dve.scalar_tensor_tensor(out=at, in0=w.got[:, j, k:k + 1, :], scalar=w.wt[:, j, k:k + 1],
                                                     in1=at, op0=ALU.mult, op1=ALU.add).then_inc(s.added, 1)


def layer2_warp(nc, g, a):
    W = 16
    KB = S // W
    TIMES = SC + KB - 1
    PADDED = TIMES
    BIG = 1e30
    layernorm(nc, g)
    with buffers(nc, table=((P, PADDED + 1, W + 1), F32), first=((P, 1), F32), last=((P, 1), F32),
                 inner=((P, 1), F32)) as u:
        with stage_semaphores(nc, "marked") as s, nc.Block() as block:
            @block.vector
            def _(dve):
                dve.tensor_reduce(u.first[:], g.ident[:, 0:P:KB], AX.X, ALU.add).then_inc(s.marked, 1)
                dve.tensor_reduce(u.last[:], g.ident[:, KB - 1:P:KB], AX.X, ALU.add).then_inc(s.marked, 1)
                dve.wait_ge(s.marked, 2)
                dve.tensor_scalar(u.inner[:], u.last[:], -1.0, 1.0, ALU.mult, ALU.add).then_inc(s.marked, 1)
                dve.wait_ge(s.marked, 3)

        with buffers(nc, skewed=((P, PADDED, W + 1), F32)) as v:
            PERB = 3
            with (
                buffers(nc, xsq=((P, NT * P), F32), csq=((P, B * SC), F32), cm2=((P, B * SC), F32),
                        dist=((P, SC, W), F32), wide=((P, PADDED * W), F32)) as w,
                stage_semaphores(nc, "squared", "product_done", "floored", "rooted", "filled", "placed", "spread",
                                 "read") as s,
                nc.Block() as block,
            ):
                @block.gpsimd
                def _(pool):
                    pool.memset(w.wide[:], BIG).then_inc(s.filled, 1)

                @block.vector
                def _(dve):
                    dve.tensor_tensor(w.xsq[:], g.xnT[:], g.xnT[:], ALU.mult).then_inc(s.squared, 1)
                    dve.tensor_tensor(w.csq[:], g.ctxT[:], g.ctxT[:], ALU.mult).then_inc(s.squared, 1)
                    dve.tensor_scalar(w.cm2[:], g.ctxT[:], -2.0, None, ALU.mult).then_inc(s.squared, 1)
                    for n in range(0, W, PERB):
                        m = min(PERB, W - n)
                        dve.wait_ge(s.product_done, n // PERB + 1)
                        dve.tensor_scalar(w.dist[:, :, n:n + m].rearrange("p i j -> p j i"),
                                          g.psum[:, n // PERB, 0:m * SC].rearrange("p (j i) -> p j i", i=SC), 0.0, None,
                                          ALU.max).then_inc(s.floored, 1)
                    dve.wait_ge(s.read, 16)
                    dve.tensor_copy(v.skewed[:, :, 1:W + 1], w.wide[:].rearrange("p (t j) -> p t j", j=W)).then_inc(s.spread, 1)
                    dve.memset(v.skewed[:, :, 0], BIG).then_inc(s.spread, 1)
                    dve.wait_ge(s.spread, 2)
                    dve.tensor_scalar(v.skewed[:, :, 0], v.skewed[:, :, 0], u.first[:, 0:1], None, ALU.mult).then_inc(s.spread, 1)

                @block.tensor
                def _(pe):
                    pe.wait_ge(s.squared, 3)
                    for n in range(W):
                        for b in range(B):
                            rows = slice(KB * b, KB * (b + 1))
                            out = g.psum[rows, n // PERB, (n % PERB) * SC:(n % PERB + 1) * SC]
                            x = slice(b * S + n, (b + 1) * S, W)
                            c = slice(b * SC, (b + 1) * SC)
                            at = (0, KB * b)
                            pe.matmul(out, g.xnT[:, x], w.cm2[:, c], start=True, stop=False, tile_position=at)
                            pe.matmul(out, w.xsq[:, x], g.ones[:, 0:1].to_broadcast([P, SC]), start=False, stop=False,
                                      tile_position=at)
                            last = pe.matmul(out, g.ones[:, 0:KB], w.csq[:, c], start=False, stop=True, tile_position=at)
                        if n % PERB == PERB - 1 or n == W - 1:
                            last.then_inc(s.product_done, 1)

                @block.scalar
                def _(act):
                    act.wait_ge(s.floored, -(-W // PERB))
                    act.activation(w.dist[:], w.dist[:], ACT.Sqrt).then_inc(s.rooted, 1)

                @block.sync
                def _(sp):
                    far = g.warp_skew
                    sp.wait_ge(s.filled, 1)
                    sp.dma_start(far[0:P, :], w.wide[:]).then_inc(s.placed, 16)
                    sp.wait_ge(s.placed, 16)
                    sp.wait_ge(s.rooted, 1)
                    for b in range(B):
                        dst = bass.AP(tensor=far.tensor, offset=far.offset + b * KB * PADDED * W,
                                      ap=[[(PADDED + 1) * W, KB], [1, SC * W]])
                        sp.dma_start(dst, w.dist[KB * b:KB * (b + 1), :, :].rearrange("p i j -> p (i j)")).then_inc(s.placed, 16)
                    sp.wait_ge(s.placed, 16 * (1 + B))
                    sp.dma_start(w.wide[:], far[0:P, :]).then_inc(s.read, 16)

            from_left = [max(0, k - 1) for k in range(KB)]
            with (
                buffers(nc, best=((P, W + 1), F32)) as w,
                stage_semaphores(nc, "row_done", "best_done") as s,
                nc.Block() as block,
            ):
                @block.vector
                def _(dve):
                    start = u.table[:, 0, :]
                    dve.memset(start, BIG).then_inc(s.row_done, 1)
                    dve.wait_ge(s.row_done, 1)
                    dve.tensor_scalar(start[:, 0:1], u.first[:], -BIG, BIG, ALU.mult, ALU.add).then_inc(s.row_done, 1)
                    dve.wait_ge(s.row_done, 2)
                    for n in range(TIMES):
                        before, now = u.table[:, n, :], u.table[:, n + 1, :]
                        dve.wait_ge(s.row_done, n + 2)
                        dve.tensor_tensor(w.best[:, 1:W + 1], before[:, 0:W], before[:, 1:W + 1],
                                          ALU.min).then_inc(s.best_done, 1)
                        dve.stream_shuffle(w.best[:, 0:1], before[:, W:W + 1], from_left).then_inc(s.best_done, 1)
                        dve.wait_ge(s.best_done, 2 * n + 2)
                        dve.tensor_tensor_scan(now, w.best[:], v.skewed[:, n, :], BIG, ALU.min,
                                               ALU.add).then_inc(s.row_done, 1)

        with buffers(nc, take=((P, PADDED, 2 * W), F32), keep=((P, PADDED, 2 * W), F32), path=((P, PADDED, W), F32),
                     unskewed=((P, SC, W), F32)) as v:
            from_right = [min(KB - 1, k + 1) for k in range(KB)]
            with (
                buffers(nc, least=((P, PADDED, W), F32), diag=((P, PADDED, W + 1), F32), up=((P, PADDED, W), F32),
                        left=((P, PADDED, W + 1), F32), edge=((P, PADDED), F32)) as w,
                stage_semaphores(nc, "step") as s,
                nc.Block() as block,
            ):
                @block.vector
                def _(dve):
                    steps = [0]

                    def done(ins):
                        steps[0] += 1
                        ins.then_inc(s.step, 1)
                        dve.wait_ge(s.step, steps[0])

                    R = u.table
                    cd, cu, cl = R[:, 0:PADDED, 0:W], R[:, 0:PADDED, 1:W + 1], R[:, 1:PADDED + 1, 0:W]
                    diag, left = w.diag[:, :, 0:W], w.left[:, :, 0:W]
                    done(dve.tensor_tensor(w.least[:], cu, cl, ALU.min))
                    done(dve.tensor_tensor(diag, cd, w.least[:], ALU.is_le))
                    done(dve.tensor_tensor(w.up[:], cu, cl, ALU.is_le))
                    done(dve.tensor_tensor(w.least[:], w.up[:], diag, ALU.mult))
                    done(dve.tensor_tensor(w.up[:], w.up[:], w.least[:], ALU.subtract))
                    done(dve.tensor_tensor(w.least[:], w.up[:], diag, ALU.add))
                    done(dve.tensor_scalar(left, w.least[:], -1.0, 1.0, ALU.mult, ALU.add))
                    for m in (w.diag, w.left):
                        done(dve.memset(m[:, PADDED - 1, W:W + 1], 0.0))
                        done(dve.tensor_copy(w.edge[:], m[:, :, 0]))
                        done(dve.stream_shuffle(w.edge[:], w.edge[:], from_right))
                        done(dve.tensor_scalar(m[:, 0:PADDED - 1, W], w.edge[:, 1:PADDED], u.inner[:, 0:1], None, ALU.mult))
                    for r in range(W):
                        c = W - r
                        dve.tensor_copy(v.take[:, :, 2 * r], w.diag[:, :, c]).then_inc(s.step, 1)
                        dve.tensor_copy(v.take[:, :, 2 * r + 1], w.up[:, :, c - 1]).then_inc(s.step, 1)
                        dve.tensor_copy(v.keep[:, :, 2 * r], w.left[:, :, c]).then_inc(s.step, 1)
                    dve.memset(v.keep[:].rearrange("p t (r two) -> p t r two", two=2)[:, :, :, 1], 1.0).then_inc(s.step, 1)
                    steps[0] += 3 * W + 1
                    dve.wait_ge(s.step, steps[0])

            RW = 2 * W + 2
            PIECE = 37
            assert TIMES % PIECE == 0
            with (
                buffers(nc, on=((P, TIMES, RW), F32), shares=((P, 2 * W), F32)) as w,
                stage_semaphores(nc, "row_done", "share_done", "set_up", "path_done") as s,
                nc.Block() as block,
            ):
                on = w.on[:]

                def pairs_of(time):
                    return bass.AP(tensor=on.tensor, offset=on.offset + time * RW + 1,
                                   ap=[[TIMES * RW, P], [2, W], [2, 2]])

                @block.vector
                def _(dve):
                    first = w.on[:, TIMES - 1, :]
                    dve.memset(first, 0.0).then_inc(s.set_up, 1)
                    dve.memset(w.shares[:], 0.0).then_inc(s.set_up, 1)
                    dve.wait_ge(s.set_up, 2)
                    dve.tensor_copy(w.shares[:, 1:2], u.last[:]).then_inc(s.set_up, 1)
                    dve.wait_ge(s.set_up, 3)
                    dve.tensor_tensor_scan(first[:, 2:RW], v.keep[:, TIMES - 1, :], w.shares[:], 0.0, ALU.mult,
                                           ALU.add).then_inc(s.row_done, 1)
                    for n in range(1, TIMES):
                        time = TIMES - 1 - n
                        now = w.on[:, time, :]
                        dve.wait_ge(s.row_done, n)
                        dve.tensor_tensor(w.shares[:].rearrange("p (r two) -> p r two", two=2), pairs_of(time + 1),
                                          v.take[:, time + 1, :].rearrange("p (r two) -> p r two", two=2),
                                          ALU.mult).then_inc(s.share_done, 1)
                        dve.stream_shuffle(now[:, 1:2], w.on[:, time + 1, RW - 1:RW], from_right).then_inc(s.share_done, 1)
                        dve.wait_ge(s.share_done, 2 * n)
                        dve.tensor_tensor_scan(now[:, 2:RW], v.keep[:, time, :], w.shares[:], now[:, 1:2],
                                               ALU.mult, ALU.add).then_inc(s.row_done, 1)

                @block.scalar
                def _(act):
                    for at in range(TIMES - PIECE, -1, -PIECE):
                        act.wait_ge(s.row_done, TIMES - at)
                        act.activation(v.path[:, at:at + PIECE, :], w.on[:, at:at + PIECE, 3:RW:2],
                                       ACT.Copy).then_inc(s.path_done, 1)

            with (
                buffers(nc, onT=((P, 2, B, KB, W), F32), ctx=((P, 2, B, D), F32)) as w,
                stage_semaphores(nc, "saved", "read", "ctx_in", "turned", "on_done", "summed", "added") as s,
                nc.Block() as block,
            ):
                parts = ctx_tiles()

                @block.sync
                def _(sp):
                    for h, (at, rows) in enumerate(parts):
                        sp.dma_start(w.ctx[0:rows, h, :, :], a["ctx"][:, at:at + rows, :].rearrange("b i d -> i b d")).then_inc(s.ctx_in, 16)
                    far = g.warp_skew
                    sp.dma_start(far[0:P, 0:TIMES * W], v.path[:, 0:TIMES, :].rearrange("p t j -> p (t j)")).then_inc(s.saved, 16)
                    sp.wait_ge(s.saved, 16)
                    for b in range(B):
                        src = bass.AP(tensor=far.tensor, offset=far.offset + b * KB * PADDED * W,
                                      ap=[[(PADDED + 1) * W, KB], [1, SC * W]])
                        sp.dma_start(v.unskewed[KB * b:KB * (b + 1), :, :].rearrange("p i j -> p (i j)"), src).then_inc(s.read, 16)

                turns = [(h, r0) for h in range(2) for r0 in range(0, W, 4)]

                @block.tensor
                def _(pe):
                    pe.wait_ge(s.read, 16 * B)
                    for n, (h, r0) in enumerate(turns):
                        at, rows = parts[h]
                        if n >= 4:
                            pe.wait_ge(s.on_done, n - 3)
                        for r in range(r0, r0 + 4):
                            last = pe.transpose(g.psum[0:rows, n % 4, (r - r0) * P:(r - r0 + 1) * P],
                                                v.unskewed[:, at:at + rows, r], g.ident[:])
                        last.then_inc(s.turned, 1)
                    pe.wait_ge(s.on_done, len(turns))
                    pe.wait_ge(s.ctx_in, 32)
                    for b in range(B):
                        for j in range(QT):
                            for h, (_, rows) in enumerate(parts):
                                cells = w.onT[0:rows, h, b, :, :].rearrange("p k w -> p (k w)")[:, j * P:(j + 1) * P]
                                last = pe.matmul(g.psum[:, 4 + b, j * D:(j + 1) * D], cells, w.ctx[0:rows, h, b, :],
                                                 start=h == 0, stop=h == 1)
                        last.then_inc(s.summed, 1)

                @block.vector
                def _(dve):
                    for n, (h, r0) in enumerate(turns):
                        rows = parts[h][1]
                        dve.wait_ge(s.turned, n + 1)
                        for r in range(r0, r0 + 4):
                            ins = dve.tensor_copy(w.onT[0:rows, h, :, :, W - 1 - r],
                                                  g.psum[0:rows, n % 4, (r - r0) * P:(r - r0 + 1) * P]
                                                  .rearrange("p (b k) -> p b k", k=KB))
                        ins.then_inc(s.on_done, 1)
                    for b in range(B):
                        dve.wait_ge(s.summed, b + 1)
                        at = g.x[:, b * QT:(b + 1) * QT, :]
                        dve.tensor_tensor(at, at, g.psum[:, 4 + b, :].rearrange("p (t d) -> p t d", d=D), ALU.add).then_inc(s.added, 1)


FP4_STEPS = 13


def fp4_steps(dve, done, x, out, amax, inv, mag, parted, read):
    spread = [x.shape[0], x.shape[1], 16]
    dve.tensor_reduce(amax, x, AX.X, ALU.max, apply_absolute_value=True).then_inc(read, 1)
    dve.wait_ge(read, 1)
    done(dve.tensor_scalar(amax, amax, 1.0 / 6.0, 1e-12, ALU.mult, ALU.max))
    done(dve.reciprocal(inv, amax))
    dve.wait_ge(parted, 1)
    done(dve.tensor_tensor(mag, mag, inv.unsqueeze(2).to_broadcast(spread), ALU.mult))
    done(dve.tensor_scalar(out, mag, 5.0, 2.0, ALU.is_gt, ALU.mult))
    for mid in (3.5, 2.5):
        done(dve.scalar_tensor_tensor(out=out, in0=mag, scalar=mid, in1=out, op0=ALU.is_gt, op1=ALU.add))
    done(dve.tensor_scalar(out, out, 2.0, None, ALU.mult))
    for mid in (1.75, 1.25, 0.75, 0.25):
        done(dve.scalar_tensor_tensor(out=out, in0=mag, scalar=mid, in1=out, op0=ALU.is_gt, op1=ALU.add))
    dve.wait_ge(parted, 2)
    done(dve.scalar_tensor_tensor(out=out, in0=out, scalar=0.5, in1=x, op0=ALU.mult, op1=ALU.mult))
    done(dve.tensor_tensor(out, out, amax.unsqueeze(2).to_broadcast(spread), ALU.mult))


def layer3_ffn(nc, g, a):
    I, Q = 352, 16
    parts = [(0, P), (P, P), (2 * P, I - 2 * P)]
    layernorm(nc, g)
    PS = g.psum
    with buffers(nc, wgT=((P, I), F32), wuT=((P, I), F32), wdT=((P, 3, D), F32), xq=((P, NT, D), F32),
                 xqT=((P, NT * P), F32)) as u:
        NW = 2 * 3 * D // Q + I // Q
        with (
            buffers(nc, w=((P, NW, Q), F32), wq=((P, NW, Q), F32), amax=((P, NW), F32), inv=((P, NW), F32),
                    mag=((P, NW, Q), F32)) as w,
            stage_semaphores(nc, "zeroed", "loaded", "step", "turned", "out_done", "parted", "read") as s,
            nc.Block() as block,
        ):
            flat = w.w[:].rearrange("p n q -> p (n q)")
            flatq = w.wq[:].rearrange("p n q -> p (n q)")
            STEPS = FP4_STEPS

            @block.sync
            def _(sp):
                sp.wait_ge(s.zeroed, 1)
                for m, name in enumerate(("L3_ffn_w_gate", "L3_ffn_w_up")):
                    for c, (at, rows) in enumerate(parts):
                        sp.dma_start(flat[0:rows, (3 * m + c) * D:(3 * m + c + 1) * D], a[name][at:at + rows, :]).then_inc(s.loaded, 16)
                sp.dma_start(flat[:, 6 * D:6 * D + I], a["L3_ffn_w_down"]).then_inc(s.loaded, 16)

            @block.vector
            def _(dve):
                dve.memset(w.w[:], 0.0).then_inc(s.zeroed, 1)
                dve.wait_ge(s.loaded, 16 * 7)
                steps = [0]

                def done(ins):
                    steps[0] += 1
                    ins.then_inc(s.step, 1)
                    dve.wait_ge(s.step, steps[0])

                fp4_steps(dve, done, w.w[:], w.wq[:], w.amax[:], w.inv[:], w.mag[:], s.parted, s.read)
                assert steps[0] == STEPS
                dve.wait_ge(s.turned, 1)
                dve.tensor_copy(u.wgT[:], PS[:, 0, 0:I]).then_inc(s.out_done, 1)
                dve.tensor_copy(u.wuT[:], PS[:, 1, 0:I]).then_inc(s.out_done, 1)
                for c, (_, rows) in enumerate(parts):
                    dve.tensor_copy(u.wdT[0:rows, c, :], PS[0:rows, 2, c * P:(c + 1) * P]).then_inc(s.out_done, 1)
                dve.wait_ge(s.out_done, 5)

            @block.scalar
            def _(act):
                act.wait_ge(s.loaded, 16 * 7)
                act.wait_ge(s.zeroed, 1)
                act.activation(w.mag[:], w.w[:], ACT.Abs).then_inc(s.parted, 1)
                act.wait_ge(s.parted, 1)
                act.wait_ge(s.read, 1)
                act.activation(w.w[:], w.w[:], ACT.Sign).then_inc(s.parted, 1)

            @block.tensor
            def _(pe):
                pe.wait_ge(s.step, STEPS)
                for m in range(2):
                    for c, (at, rows) in enumerate(parts):
                        pe.transpose(PS[:, m, at:at + rows], flatq[0:rows, (3 * m + c) * D:(3 * m + c + 1) * D],
                                     g.ident[0:rows, 0:rows])
                for c, (at, rows) in enumerate(parts):
                    last = pe.transpose(PS[0:rows, 2, c * P:(c + 1) * P], flatq[:, 6 * D + at:6 * D + at + rows], g.ident[:])
                last.then_inc(s.turned, 1)

        NX = NT * D // Q
        with (
            buffers(nc, x=((P, NX, Q), F32), amax=((P, NX), F32), inv=((P, NX), F32), mag=((P, NX, Q), F32)) as w,
            stage_semaphores(nc, "copied", "step", "parted", "read") as s,
            nc.Block() as block,
        ):
            @block.vector
            def _(dve):
                steps = [0]

                def done(ins):
                    steps[0] += 1
                    ins.then_inc(s.step, 1)
                    dve.wait_ge(s.step, steps[0])

                dve.tensor_copy(w.x[:].rearrange("p n q -> p (n q)"),
                                g.xn[:].rearrange("p t d -> p (t d)")).then_inc(s.copied, 1)
                dve.wait_ge(s.copied, 1)
                fp4_steps(dve, done, w.x[:], u.xq[:].rearrange("p t (m q) -> p (t m) q", q=Q), w.amax[:], w.inv[:],
                          w.mag[:], s.parted, s.read)

            @block.scalar
            def _(act):
                act.wait_ge(s.copied, 1)
                act.activation(w.mag[:], w.x[:], ACT.Abs).then_inc(s.parted, 1)
                act.wait_ge(s.parted, 1)
                act.wait_ge(s.read, 1)
                act.activation(w.x[:], w.x[:], ACT.Sign).then_inc(s.parted, 1)
        turn_to_features(nc, g, u.xq, u.xqT)

        NH = QT * I // Q
        with (
            buffers(nc, src=((P, S), F32), gated=((P, QT, I), F32), h=((P, QT, I), F32), hq=((P, QT, I), F32),
                    hqT=((P, 3, S), F32), amax=((P, NH), F32), inv=((P, NH), F32), mag=((P, NH, Q), F32)) as w,
            nc.Fori(0, B) as b,
            stage_semaphores(nc, "src_done", "hidden_mm", "silu_done", "h_done", "step", "h_turned", "hT_done", "out_mm",
                             "added", "parted", "read") as s,
            nc.Block() as block,
        ):
            STEPS = FP4_STEPS

            @block.tensor
            def _(pe):
                pe.wait_ge(s.src_done, 1)
                for j in range(QT):
                    pe.matmul(PS[:, 2 * j, 0:I], w.src[:, j * P:(j + 1) * P], u.wgT[:], start=True, stop=True)
                    pe.matmul(PS[:, 2 * j + 1, 0:I], w.src[:, j * P:(j + 1) * P], u.wuT[:], start=True,
                              stop=True).then_inc(s.hidden_mm, 1)
                pe.wait_ge(s.step, STEPS)
                for c, (at, rows) in enumerate(parts):
                    for j in range(QT):
                        last = pe.transpose(PS[0:rows, c, j * P:(j + 1) * P], w.hq[:, j, at:at + rows], g.ident[:])
                    last.then_inc(s.h_turned, 1)
                pe.wait_ge(s.hT_done, 3)
                for j in range(QT):
                    for c, (_, rows) in enumerate(parts):
                        last = pe.matmul(PS[:, 4, j * D:(j + 1) * D], w.hqT[0:rows, c, j * P:(j + 1) * P],
                                         u.wdT[0:rows, c, :], start=c == 0, stop=c == 2)
                last.then_inc(s.out_mm, 1)

            @block.scalar
            def _(act):
                for j in range(QT):
                    act.wait_ge(s.hidden_mm, j + 1)
                    act.activation(w.gated[:, j, :], PS[:, 2 * j, 0:I], ACT.Silu).then_inc(s.silu_done, 1)
                blocks = w.h[:].rearrange("p j (m q) -> p (j m) q", q=Q)
                act.wait_ge(s.h_done, QT)
                act.activation(w.mag[:], blocks, ACT.Abs).then_inc(s.parted, 1)
                act.wait_ge(s.parted, 1)
                act.wait_ge(s.read, 1)
                act.activation(blocks, blocks, ACT.Sign).then_inc(s.parted, 1)
                for c, (_, rows) in enumerate(parts):
                    act.wait_ge(s.h_turned, c + 1)
                    act.activation(w.hqT[0:rows, c, :], PS[0:rows, c, :], ACT.Copy).then_inc(s.hT_done, 1)

            @block.vector
            def _(dve):
                dve.tensor_copy(w.src[:], u.xqT[:, bass.ds(b * S, S)]).then_inc(s.src_done, 1)
                for j in range(QT):
                    dve.wait_ge(s.silu_done, j + 1)
                    dve.tensor_tensor(w.h[:, j, :], w.gated[:, j, :], PS[:, 2 * j + 1, 0:I], ALU.mult).then_inc(s.h_done, 1)
                dve.wait_ge(s.h_done, QT)
                steps = [0]

                def done(ins):
                    steps[0] += 1
                    ins.then_inc(s.step, 1)
                    dve.wait_ge(s.step, steps[0])

                fp4_steps(dve, done, w.h[:].rearrange("p j (m q) -> p (j m) q", q=Q),
                          w.hq[:].rearrange("p j (m q) -> p (j m) q", q=Q), w.amax[:], w.inv[:], w.mag[:], s.parted, s.read)
                dve.wait_ge(s.out_mm, 1)
                at = g.x[:, bass.ds(b * QT, QT), :]
                dve.tensor_tensor(at, at, PS[:, 4, :].rearrange("p (t d) -> p t d", d=D), ALU.add).then_inc(s.added, 1)


def layer0_slots_and_ffn(nc, g, a):
    with buffers(nc, w13=((P, 64, 2 * 88), F32), w2=((88, 64, D), F32)) as weights:
        g = g._replace(w13=weights.w13, w2=weights.w2)
        prefetch_experts(nc, g, a)
        slots_from_context(nc, g, a)
        layer0_ffn(nc, g, a)


LAYERS = [layer0_attention, layer0_slots_and_ffn, layer1_attention, layer1_cross, layer1_ffn,
          layer2_attention, layer2_warp, layer2_ffn, layer3_attention, layer3_cross, layer3_ffn]


def decoder(nc, a, out):
    with ExitStack() as held:
        def sb(name, shape, dt=F32):
            return held.enter_context(nc.sbuf_tensor(name, shape, dt))

        g = named(
            x=sb("x_tokens", [P, NT, D]), xn=sb("xn_tokens", [P, NT, D]), xnT=sb("xn_features", [P, NT * P]),
            ctxT=sb("ctx_features", [P, B * SC]), ident=sb("ident", [P, P]), ones=sb("ones", [P, P]),
            ident_bf=sb("ident_bf", [P, P], BF16), ones_bf=sb("ones_bf", [P, P], BF16),
            before=sb("before", [P, P], BF16), causal=sb("causal", [P, P], BF16), eta=sb("eta", [P, 1]),
            minus_e0=sb("minus_e0", [P, 1]),
            qs=sb("q_stacks", [P, H16, S], BF16), ks=sb("k_stacks", [P, H16, S], BF16),
            q_parts=nc.dram_tensor("q_parts", (B + 1, PARTS, P, S), BF16).ap(),
            k_parts=nc.dram_tensor("k_parts", (B + 1, PARTS, P, S), BF16).ap(),
            scattered=held.enter_context(nc.semaphore("scattered")),
            gathered_first=held.enter_context(nc.semaphore("gathered_first")),
            gathered_second=held.enter_context(nc.semaphore("gathered_second")),
            prefetched=held.enter_context(nc.semaphore("prefetched")),
            scattered_rows=held.enter_context(nc.semaphore("scattered_rows")),
            fetched_first=held.enter_context(nc.semaphore("fetched_first")),
            fetched_second=held.enter_context(nc.semaphore("fetched_second")),
            w13=None, w2=None,
            warp_skew=nc.dram_tensor("warp_skew", (P + 1, (SC + 31) * 16), F32).ap(),
            moe_in=nc.dram_tensor("expert_rows_in", ((64 + 8) * 64, D), F32).ap(),
            moe_out=nc.dram_tensor("expert_rows_out", (64 * 64, D), F32).ap(),
            psum=held.enter_context(nc.psum_tensor("psum", [P, 8, 512], F32)))
        xs = a["x"].rearrange("b (t p) d -> p (b t) d", p=P)
        load(nc, [(g.x[:], xs), (g.ctxT[:], a["ctxT"])])
        constants(nc, g)
        prepare_stacks(nc, g)
        for layer in LAYERS:
            layer(nc, g, a)
        with stage_semaphores(nc, "saved") as s, nc.Block() as block:
            @block.sync
            def _(sp):
                sp.dma_start(out.rearrange("b (t p) d -> p (b t) d", p=P), g.x[:]).then_inc(s.saved, 16)
                sp.wait_ge(s.saved, 16)


_TURNED = ["L0_attn_W1", "L0_attn_W2", "L0_attn_Wq", "L0_attn_Wk", "L0_attn_Wv", "L0_attn_Wo",
           "L0_xattn_Wq", "L0_xattn_Wk", "L0_xattn_Wv", "L0_xattn_gru_wih", "L0_xattn_gru_whh", "L1_attn_phase",
           "L0_ffn_gate_w", "L0_ffn_ws1", "L0_ffn_ws2", "L0_ffn_ws3", "L2_ffn_gate_w",
           "L1_xattn_W_Q", "L1_xattn_W_K", "L1_xattn_W_V", "L1_xattn_W_O", "L3_attn_Wq", "L3_attn_Wk", "L3_attn_Wv",
           "L3_attn_Wo"]


def laid_out(inputs):
    c = np.ascontiguousarray
    a = {k: np.asarray(v) for k, v in inputs.items()}
    for k in _TURNED:
        a[k + "T"] = c(a.pop(k).T)
    for k in "QKV":
        a[f"L2_attn_{k}T"] = a.pop(f"L2_attn_{k}").transpose(1, 2, 0).reshape(D, -1)
    for k in ("w1", "w2", "w3"):
        a[f"L0_ffn_{k}T"] = a.pop(f"L0_ffn_{k}").transpose(2, 0, 1)
    a["L2_attn_WT"] = a.pop("L2_attn_W").transpose(2, 1, 0).reshape(-1, D)
    for k in ("mask_BxSxS2_bf0", "mask_SxS2_bk1"):
        a[k + "T"] = np.swapaxes(a[k], -1, -2)
    ctx = a.pop("ctx_1024")
    a["ctx"] = ctx
    a["ctxT"] = c(ctx.reshape(B * SC, D).T)
    return {k: c(v) for k, v in a.items()}


def kernel(**inputs):
    import concourse.bacc as _bacc
    from concourse.bass_utils import run_bass_kernel_spmd as _run

    nc = _bacc.Bacc("TRN2", target_bir_lowering=False, num_devices=1)
    arrays = laid_out(inputs)
    aps = {k: nc.dram_tensor("in_" + k, v.shape, mybir.dt.from_np(v.dtype), kind="ExternalInput").ap()
           for k, v in arrays.items()}
    out = nc.dram_tensor("out_0", (B, S, D), F32, kind="ExternalOutput").ap()
    decoder(nc, aps, out)
    r = _run(nc, [{"in_" + k: v for k, v in arrays.items()}], core_ids=[0])
    return r.results[0]["out_0"]
```
